# Optimizing a Trainium2 kernel written in Bass

```python
import numpy as np
import jax
import jax.numpy as jnp

def _softmax(x, axis=-1):
    return jax.nn.softmax(x, axis=axis)

def _gelu(x):
    return jax.nn.gelu(x, approximate=True)

def _silu(x):
    return jax.nn.silu(x)

def _sigmoid(x):
    return jax.nn.sigmoid(x)

def _layernorm(x, axis=-1, eps=1e-05):
    m = jnp.mean(x, axis=axis, keepdims=True)
    v = jnp.var(x, axis=axis, keepdims=True)
    return (x - m) / jnp.sqrt(v + eps)

def _scatter_add(tgt, idx, src, axis=0):
    return tgt.at[idx].add(src)

def _segment_sum(src, seg, n):
    return jax.ops.segment_sum(src, seg, n)
kernel_name = 'mk_perceiver_d4_seqx_r4_0d954c'

def setup_inputs(seed: int=0):
    np.random.seed(seed)
    _w = jnp.asarray

    def _rec_inputs():
        import jax
        import jax.numpy as jnp
        _rk = jax.random.key(seed)
        x = -0.0003929 + 0.9999 * jax.random.normal(jax.random.fold_in(_rk, 1), (16, 64, 256), jnp.float32)
        _lenS = 64 - jax.random.randint(jax.random.fold_in(_rk, 7), (16,), 0, max(1, 64 // 4) + 1, jnp.int32)
        _lenS2 = 1601 - jax.random.randint(jax.random.fold_in(_rk, 8), (16,), 0, max(1, 1601 // 4) + 1, jnp.int32)
        _ctx_768P = jax.random.normal(jax.random.fold_in(_rk, 11), (16, 16, 192), jnp.float32)
        _ctx_768c = jax.random.dirichlet(jax.random.fold_in(_rk, 511), 0.3 * jnp.ones((16,), jnp.float32), (16, 1601))
        _ctx_768t = jnp.einsum('bsk,bkd->bsd', _ctx_768c, _ctx_768P)
        _ctx_768t = _ctx_768t * jax.lax.rsqrt(jnp.mean(jnp.square(_ctx_768t)) + 1e-12) * 0.953939
        ctx_768 = -0.00055796 + 0.999787 * (_ctx_768t + 0.3 * jax.random.normal(jax.random.fold_in(_rk, 611), (16, 1601, 192), jnp.float32))
        _validS = jnp.arange(64)[None, :] < _lenS[:, None]
        _validS2 = jnp.arange(1601)[None, :] < _lenS2[:, None]
        _causal = jnp.tril(jnp.ones((64, 64), dtype=bool))
        mask_BxS2_bk0 = jnp.logical_not(jnp.broadcast_to(_validS2[:, :], (16, 1601)))
        return (x, ctx_768, mask_BxS2_bk0)
    x, ctx_768, mask_BxS2_bk0 = _rec_inputs()

    def _L0_xattn_setup():
        import jax, jax.numpy as jnp
        import numpy as np
        HEADS = 16
        DIM_HEAD = 64
        SCALE = DIM_HEAD ** (-0.5)
        key = jax.random.key(seed)
        ks = jax.random.split(key, 6)
        B, N, C = (4, 1024, 256)
        M, Cc = (128, 192)
        inner = HEADS * DIM_HEAD
        s = lambda d: d ** (-0.5)
        return {'x': jax.random.normal(ks[0], (B, N, C), jnp.float32), 'context': jax.random.normal(ks[1], (B, M, Cc), jnp.float32), 'Wq': jax.random.normal(ks[2], (C, inner), jnp.float32) * s(C), 'Wk': jax.random.normal(ks[3], (Cc, inner), jnp.float32) * s(Cc), 'Wv': jax.random.normal(ks[4], (Cc, inner), jnp.float32) * s(Cc), 'Wo': jax.random.normal(ks[5], (inner, C), jnp.float32) * s(inner), 'bo': jnp.zeros((C,), jnp.float32)}
    _L0_xattn_all = _L0_xattn_setup()
    _L0_xattn_in = {k: v for k, v in _L0_xattn_all.items() if k in ('Wq', 'Wk', 'Wv', 'Wo', 'bo')}
    del _L0_xattn_all

    def _L0_attn_setup():
        import jax, jax.numpy as jnp
        import numpy as np
        N_HEAD = 16
        PAGE_SIZE = 64
        ROPE_THETA = 10000.0

        def _rope_tables(T, D, dtype):
            inv = 1.0 / ROPE_THETA ** (np.arange(0, D, 2, dtype=np.float32) / D)
            ang = np.outer(np.arange(T, dtype=np.float32), inv)
            return (jnp.asarray(np.cos(ang), dtype), jnp.asarray(np.sin(ang), dtype))

        def _apply_rope(x, cos, sin):
            x1 = x[..., 0::2]
            x2 = x[..., 1::2]
            c = cos[None, :, None, :]
            s = sin[None, :, None, :]
            out = jnp.stack([x1 * c - x2 * s, x1 * s + x2 * c], axis=-1)
            return out.reshape(x.shape)
        key = jax.random.key(seed)
        ks = jax.random.split(key, 6)
        B, T, E = (2, 512, 256)
        L = E // 2
        sc = lambda fan: 1.0 / np.sqrt(fan)
        return {'x': jax.random.normal(ks[0], (B, T, E), jnp.float32), 'wq': jax.random.normal(ks[1], (E, E), jnp.float32) * sc(E), 'w_down': jax.random.normal(ks[2], (E, L), jnp.float32) * sc(E), 'wk_up': jax.random.normal(ks[3], (L, E), jnp.float32) * sc(L), 'wv_up': jax.random.normal(ks[4], (L, E), jnp.float32) * sc(L), 'wo': jax.random.normal(ks[5], (E, E), jnp.float32) * sc(E)}
    _L0_attn_all = _L0_attn_setup()
    _L0_attn_in = {k: v for k, v in _L0_attn_all.items() if k in ('wq', 'w_down', 'wk_up', 'wv_up', 'wo')}
    del _L0_attn_all

    def _L0_ffn_setup():
        import jax, jax.numpy as jnp
        import numpy as np
        B, T, D = (4, 512, 256)
        H, DH, E, SEL = (8, 64, 5, 2)

        def _topk_mask(logits, k):
            _, idx = jax.lax.top_k(logits, k)
            return jnp.sum(jax.nn.one_hot(idx, logits.shape[-1], dtype=logits.dtype), axis=-2)
        key = jax.random.key(seed)
        ks = jax.random.split(key, 7)
        s = 0.02
        x = jax.random.normal(ks[0], (B, T, D), dtype=jnp.float32)
        Wq = jax.random.normal(ks[1], (D, H * DH), dtype=jnp.float32) * s
        Wk = jax.random.normal(ks[2], (D, H * DH), dtype=jnp.float32) * s
        Ws = jax.random.normal(ks[3], (D, H * E), dtype=jnp.float32) * s
        Wd = jax.random.normal(ks[4], (D, H * E), dtype=jnp.float32) * s
        Wv = jax.random.normal(ks[5], (E, D, DH), dtype=jnp.float32) * s
        Wo = jax.random.normal(ks[6], (E, DH, D), dtype=jnp.float32) * s
        return {'x': x, 'Wq': Wq, 'Wk': Wk, 'Ws': Ws, 'Wd': Wd, 'Wv': Wv, 'Wo': Wo}
    _L0_ffn_all = _L0_ffn_setup()
    _L0_ffn_in = {k: v for k, v in _L0_ffn_all.items() if k in ('Wq', 'Wk', 'Ws', 'Wd', 'Wv', 'Wo')}
    del _L0_ffn_all

    def _L1_xattn_setup():
        import jax, jax.numpy as jnp
        import numpy as np
        DIM_IN, DIM_LAT, DIM_HEAD = (192, 256, 64)
        INNER = max(DIM_LAT, DIM_IN)
        HEADS = INNER // DIM_HEAD
        SCALE = DIM_HEAD ** (-0.5)
        RMS_EPS = 1e-08
        LN_EPS = 1e-05

        def layernorm(x, g, b):
            mu = jnp.mean(x, axis=-1, keepdims=True)
            var = jnp.mean((x - mu) ** 2, axis=-1, keepdims=True)
            return (x - mu) * jax.lax.rsqrt(var + LN_EPS) * g + b

        def rmsnorm(x, gamma):
            norm = jnp.sqrt(jnp.sum(x * x, axis=-1, keepdims=True)) * x.shape[-1] ** (-0.5)
            return x / jnp.maximum(norm, RMS_EPS) * gamma
        key = jax.random.key(seed)
        ks = jax.random.split(key, 12)
        b, n, m = (4, 1024, 128)
        x = jax.random.normal(ks[0], (b, n, DIM_IN), jnp.float32)
        latents = jax.random.normal(ks[1], (b, m, DIM_LAT), jnp.float32)
        mask = jax.random.randint(ks[2], (b, n), 0, 2).astype(bool)
        s = lambda k, sh, fan: jax.random.normal(k, sh, jnp.float32) * fan ** (-0.5)
        return {'x': x, 'latents': latents, 'mask': mask, 'ln_x_g': jnp.ones((DIM_IN,), jnp.float32), 'ln_x_b': jnp.zeros((DIM_IN,), jnp.float32), 'ln_l_g': jnp.ones((DIM_LAT,), jnp.float32), 'ln_l_b': jnp.zeros((DIM_LAT,), jnp.float32), 'qn_g': jnp.ones((DIM_HEAD,), jnp.float32), 'kn_g': jnp.ones((DIM_HEAD,), jnp.float32), 'Wq': s(ks[3], (INNER, DIM_LAT), DIM_LAT), 'Wkv': s(ks[4], (2 * INNER, DIM_IN), DIM_IN), 'Wlkv': s(ks[5], (2 * INNER, DIM_LAT), DIM_LAT), 'Wo': s(ks[6], (DIM_LAT, INNER), INNER), 'bo': jnp.zeros((DIM_LAT,), jnp.float32)}
    _L1_xattn_all = _L1_xattn_setup()
    _L1_xattn_in = {k: v for k, v in _L1_xattn_all.items() if k in ('ln_x_g', 'ln_x_b', 'ln_l_g', 'ln_l_b', 'qn_g', 'kn_g', 'Wq', 'Wkv', 'Wlkv', 'Wo', 'bo')}
    del _L1_xattn_all

    def _L1_attn_setup():
        import jax, jax.numpy as jnp
        import numpy as np
        B, S, E, H = (4, 512, 256, 16)
        HD = E // H
        key = jax.random.key(seed)
        ks = jax.random.split(key, 5)
        scale = 1.0 / np.sqrt(E)
        x = jax.random.normal(ks[0], (B, S, E), dtype=jnp.float32)
        Wqkv = jax.random.uniform(ks[1], (E, 3 * E), dtype=jnp.float32, minval=-scale, maxval=scale)
        bqkv = jax.random.uniform(ks[2], (3 * E,), dtype=jnp.float32, minval=-scale, maxval=scale)
        Wout = jax.random.uniform(ks[3], (E, E), dtype=jnp.float32, minval=-scale, maxval=scale)
        bout = jax.random.uniform(ks[4], (E,), dtype=jnp.float32, minval=-scale, maxval=scale)
        return {'x': x, 'Wqkv': Wqkv, 'bqkv': bqkv, 'Wout': Wout, 'bout': bout}
    _L1_attn_all = _L1_attn_setup()
    _L1_attn_in = {k: v for k, v in _L1_attn_all.items() if k in ('Wqkv', 'bqkv', 'Wout', 'bout')}
    del _L1_attn_all

    def _L1_ffn_setup():
        import jax, jax.numpy as jnp
        import numpy as np
        CAPACITY_FACTOR = 0.5
        key = jax.random.key(seed)
        ks = jax.random.split(key, 5)
        B, S, D, F = (4, 1024, 256, 1024)
        scale_in = 1.0 / np.sqrt(D)
        scale_ff = 1.0 / np.sqrt(F)
        return {'hidden_states': jax.random.normal(ks[0], (B, S, D), dtype=jnp.float32), 'w_router': jax.random.normal(ks[1], (D,), dtype=jnp.float32) * scale_in, 'W1': jax.random.normal(ks[2], (D, F), dtype=jnp.float32) * scale_in, 'b1': jnp.zeros((F,), dtype=jnp.float32), 'W2': jax.random.normal(ks[3], (F, D), dtype=jnp.float32) * scale_ff, 'b2': jnp.zeros((D,), dtype=jnp.float32)}
    _L1_ffn_all = _L1_ffn_setup()
    _L1_ffn_in = {k: v for k, v in _L1_ffn_all.items() if k in ('w_router', 'W1', 'b1', 'W2', 'b2')}
    del _L1_ffn_all

    def _L2_xattn_setup():
        import math
        import jax, jax.numpy as jnp
        import numpy as np
        B, SQ, SKV = (4, 512, 512)
        D_EMBED, D_CROSS, D_ATT, N_HEADS = (256, 192, 256, 16)
        D_HEAD = D_ATT // N_HEADS

        def _split_heads(t):
            b, s, _ = t.shape
            return t.reshape(b, s, N_HEADS, D_HEAD).transpose(0, 2, 1, 3)
        key = jax.random.key(seed)
        ks = jax.random.split(key, 10)
        s_e = 1.0 / math.sqrt(D_EMBED)
        s_c = 1.0 / math.sqrt(D_CROSS)
        s_a = 1.0 / math.sqrt(D_ATT)
        return {'x': jax.random.normal(ks[0], (B, SQ, D_EMBED), jnp.float32), 'y': jax.random.normal(ks[1], (B, SKV, D_CROSS), jnp.float32), 'Wq': jax.random.normal(ks[2], (D_EMBED, D_ATT), jnp.float32) * s_e, 'bq': jax.random.normal(ks[3], (D_ATT,), jnp.float32) * 0.01, 'Wk': jax.random.normal(ks[4], (D_CROSS, D_ATT), jnp.float32) * s_c, 'bk': jax.random.normal(ks[5], (D_ATT,), jnp.float32) * 0.01, 'Wv': jax.random.normal(ks[6], (D_CROSS, D_ATT), jnp.float32) * s_c, 'bv': jax.random.normal(ks[7], (D_ATT,), jnp.float32) * 0.01, 'Wo': jax.random.normal(ks[8], (D_ATT, D_EMBED), jnp.float32) * s_a, 'bo': jax.random.normal(ks[9], (D_EMBED,), jnp.float32) * 0.01}
    _L2_xattn_all = _L2_xattn_setup()
    _L2_xattn_in = {k: v for k, v in _L2_xattn_all.items() if k in ('Wq', 'bq', 'Wk', 'bk', 'Wv', 'bv', 'Wo', 'bo')}
    del _L2_xattn_all

    def _L2_attn_setup():
        import jax, jax.numpy as jnp
        import numpy as np
        D_MODEL = 256
        N_HEADS = 16
        CHUNK = 64
        EPS = 1e-06

        def elu_plus_1(x):
            return jax.nn.elu(x) + 1.0
        key = jax.random.key(seed)
        kx, kq, kk, kv, ko = jax.random.split(key, 5)
        B, T = (4, 1024)
        lim = float(np.sqrt(6.0 / (D_MODEL + D_MODEL)))
        mk = lambda k: jax.random.uniform(k, (D_MODEL, D_MODEL), jnp.float32, -lim, lim)
        return {'x': jax.random.normal(kx, (B, T, D_MODEL), jnp.float32), 'W_q': mk(kq), 'W_k': mk(kk), 'W_v': mk(kv), 'W_o': mk(ko)}
    _L2_attn_all = _L2_attn_setup()
    _L2_attn_in = {k: v for k, v in _L2_attn_all.items() if k in ('W_q', 'W_k', 'W_v', 'W_o')}
    del _L2_attn_all

    def _L2_ffn_setup():
        import jax, jax.numpy as jnp
        import numpy as np
        B, S, D = (2, 512, 256)
        I = 128
        E = 16
        TOP_K = 2

        def _mlp(x, wg, wu, wd):
            return jnp.einsum('bsi,id->bsd', jax.nn.silu(x @ wg) * (x @ wu), wd)
        key = jax.random.key(seed)
        ks = jax.random.split(key, 10)
        sc_d = 1.0 / np.sqrt(D)
        sc_i = 1.0 / np.sqrt(I)
        return {'x': jax.random.normal(ks[0], (B, S, D), dtype=jnp.float32), 'gate_w': jax.random.normal(ks[1], (D, E), dtype=jnp.float32) * sc_d, 'gate_b': jnp.zeros((E,), dtype=jnp.float32), 'shared_wg': jax.random.normal(ks[2], (D, I), dtype=jnp.float32) * sc_d, 'shared_wu': jax.random.normal(ks[3], (D, I), dtype=jnp.float32) * sc_d, 'shared_wd': jax.random.normal(ks[4], (I, D), dtype=jnp.float32) * sc_i, 'experts_wg': jax.random.normal(ks[5], (E, D, I), dtype=jnp.float32) * sc_d, 'experts_wu': jax.random.normal(ks[6], (E, D, I), dtype=jnp.float32) * sc_d, 'experts_wd': jax.random.normal(ks[7], (E, I, D), dtype=jnp.float32) * sc_i}
    _L2_ffn_all = _L2_ffn_setup()
    _L2_ffn_in = {k: v for k, v in _L2_ffn_all.items() if k in ('gate_w', 'gate_b', 'shared_wg', 'shared_wu', 'shared_wd', 'experts_wg', 'experts_wu', 'experts_wd')}
    del _L2_ffn_all

    def _L3_xattn_setup():
        import jax, jax.numpy as jnp
        import numpy as np
        N_HEADS = 16
        DIMS = 256
        D_CTX = 192
        HEAD = DIMS // N_HEADS
        key = jax.random.key(seed)
        ks = jax.random.split(key, 10)
        s_q = 1.0 / np.sqrt(DIMS)
        s_c = 1.0 / np.sqrt(D_CTX)
        return {'x': jax.random.normal(ks[0], (2, 512, DIMS), jnp.float32), 'context': jax.random.normal(ks[1], (2, 512, D_CTX), jnp.float32), 'w_q': jax.random.normal(ks[2], (DIMS, DIMS), jnp.float32) * s_q, 'b_q': jax.random.normal(ks[3], (DIMS,), jnp.float32) * 0.01, 'w_k': jax.random.normal(ks[4], (D_CTX, DIMS), jnp.float32) * s_c, 'b_k': jax.random.normal(ks[5], (DIMS,), jnp.float32) * 0.01, 'w_v': jax.random.normal(ks[6], (D_CTX, DIMS), jnp.float32) * s_c, 'b_v': jax.random.normal(ks[7], (DIMS,), jnp.float32) * 0.01, 'w_o': jax.random.normal(ks[8], (DIMS, DIMS), jnp.float32) * s_q, 'b_o': jax.random.normal(ks[9], (DIMS,), jnp.float32) * 0.01}
    _L3_xattn_all = _L3_xattn_setup()
    _L3_xattn_in = {k: v for k, v in _L3_xattn_all.items() if k in ('w_q', 'b_q', 'w_k', 'b_k', 'w_v', 'b_v', 'w_o', 'b_o')}
    del _L3_xattn_all

    def _L3_attn_setup():
        import jax, jax.numpy as jnp
        import numpy as np
        import math
        B, L, D, N2 = (8, 1024, 256, 32)

        def s4d_kernel(log_dt, log_A_real, A_imag, C_real, C_imag, length):
            dt = jnp.exp(log_dt)[:, None]
            A = -jnp.exp(log_A_real) + 1j * A_imag
            dtA = A * dt
            C = (C_real + 1j * C_imag) * (jnp.exp(dtA) - 1.0) / A
            t = jnp.arange(length, dtype=jnp.float32)
            vand = jnp.exp(dtA[:, :, None] * t)
            K = 2.0 * jnp.einsum('dn,dnl->dl', C, vand).real
            return K
        key = jax.random.key(seed)
        ks = jax.random.split(key, 6)
        x = jax.random.normal(ks[0], (B, L, D), dtype=jnp.float32)
        log_dt = jax.random.uniform(ks[1], (D,), minval=math.log(0.001), maxval=math.log(0.1)).astype(jnp.float32)
        log_A_real = jnp.log(0.5 * jnp.ones((D, N2), jnp.float32))
        A_imag = math.pi * jnp.broadcast_to(jnp.arange(N2, dtype=jnp.float32), (D, N2))
        C_real = jax.random.normal(ks[2], (D, N2), dtype=jnp.float32)
        C_imag = jax.random.normal(ks[3], (D, N2), dtype=jnp.float32)
        W = jax.random.normal(ks[4], (D, D), dtype=jnp.float32) / jnp.sqrt(jnp.float32(D))
        b = jax.random.normal(ks[5], (D,), dtype=jnp.float32) * 0.01
        return dict(x=x, log_dt=log_dt, log_A_real=log_A_real, A_imag=A_imag, C_real=C_real, C_imag=C_imag, W=W, b=b)
    _L3_attn_all = _L3_attn_setup()
    _L3_attn_in = {k: v for k, v in _L3_attn_all.items() if k in ('log_dt', 'log_A_real', 'A_imag', 'C_real', 'C_imag', 'W', 'b')}
    del _L3_attn_all

    def _L3_ffn_setup():
        import jax, jax.numpy as jnp
        from jax import lax
        import numpy as np
        D_MODEL = 256
        HIDDEN = 128
        N_EXPERTS = 32
        TOP_K = 2
        B, S = (1, 1024)

        def _moe_group(x2, router_w, wg, wu, wd, top_k):
            T = x2.shape[0]
            n_experts = router_w.shape[1]
            logits = x2 @ router_w
            scores = jax.nn.softmax(logits, axis=-1)
            expert_weights, expert_indices = lax.top_k(scores, top_k)
            flat_e = expert_indices.reshape(-1)
            flat_w = expert_weights.reshape(-1)
            flat_t = jnp.repeat(jnp.arange(T), top_k)
            order = jnp.argsort(flat_e)
            tok = flat_t[order]
            xs = x2[tok]
            group_sizes = jnp.bincount(flat_e, length=n_experts).astype(jnp.int32)
            gate = lax.ragged_dot(xs, wg, group_sizes)
            up = lax.ragged_dot(xs, wu, group_sizes)
            ys = lax.ragged_dot(jax.nn.silu(gate) * up, wd, group_sizes)
            ys = ys * flat_w[order][:, None]
            return jnp.zeros_like(x2).at[tok].add(ys)
        key = jax.random.key(seed)
        ks = jax.random.split(key, 9)
        w = lambda k, shape: jax.random.normal(k, shape, dtype=jnp.float32) * 0.02
        return {'x': jax.random.normal(ks[0], (B, S, D_MODEL), dtype=jnp.float32), 'router_w0': w(ks[1], (D_MODEL, N_EXPERTS)), 'wg0': w(ks[2], (N_EXPERTS, D_MODEL, HIDDEN)), 'wu0': w(ks[3], (N_EXPERTS, D_MODEL, HIDDEN)), 'wd0': w(ks[4], (N_EXPERTS, HIDDEN, D_MODEL)), 'router_w1': w(ks[5], (D_MODEL, N_EXPERTS)), 'wg1': w(ks[6], (N_EXPERTS, D_MODEL, HIDDEN)), 'wu1': w(ks[7], (N_EXPERTS, D_MODEL, HIDDEN)), 'wd1': w(ks[8], (N_EXPERTS, HIDDEN, D_MODEL))}
    _L3_ffn_all = _L3_ffn_setup()
    _L3_ffn_in = {k: v for k, v in _L3_ffn_all.items() if k in ('router_w0', 'wg0', 'wu0', 'wd0', 'router_w1', 'wg1', 'wu1', 'wd1')}
    del _L3_ffn_all
    return {'x': x, 'ctx_768': ctx_768, 'mask_BxS2_bk0': mask_BxS2_bk0, 'L0_xattn_Wq': _L0_xattn_in['Wq'], 'L0_xattn_Wk': _L0_xattn_in['Wk'], 'L0_xattn_Wv': _L0_xattn_in['Wv'], 'L0_xattn_Wo': _L0_xattn_in['Wo'], 'L0_xattn_bo': _L0_xattn_in['bo'], 'L0_attn_wq': _L0_attn_in['wq'], 'L0_attn_w_down': _L0_attn_in['w_down'], 'L0_attn_wk_up': _L0_attn_in['wk_up'], 'L0_attn_wv_up': _L0_attn_in['wv_up'], 'L0_attn_wo': _L0_attn_in['wo'], 'L0_ffn_Wq': _L0_ffn_in['Wq'], 'L0_ffn_Wk': _L0_ffn_in['Wk'], 'L0_ffn_Ws': _L0_ffn_in['Ws'], 'L0_ffn_Wd': _L0_ffn_in['Wd'], 'L0_ffn_Wv': _L0_ffn_in['Wv'], 'L0_ffn_Wo': _L0_ffn_in['Wo'], 'L1_xattn_ln_x_g': _L1_xattn_in['ln_x_g'], 'L1_xattn_ln_x_b': _L1_xattn_in['ln_x_b'], 'L1_xattn_ln_l_g': _L1_xattn_in['ln_l_g'], 'L1_xattn_ln_l_b': _L1_xattn_in['ln_l_b'], 'L1_xattn_qn_g': _L1_xattn_in['qn_g'], 'L1_xattn_kn_g': _L1_xattn_in['kn_g'], 'L1_xattn_Wq': _L1_xattn_in['Wq'], 'L1_xattn_Wkv': _L1_xattn_in['Wkv'], 'L1_xattn_Wlkv': _L1_xattn_in['Wlkv'], 'L1_xattn_Wo': _L1_xattn_in['Wo'], 'L1_xattn_bo': _L1_xattn_in['bo'], 'L1_attn_Wqkv': _L1_attn_in['Wqkv'], 'L1_attn_bqkv': _L1_attn_in['bqkv'], 'L1_attn_Wout': _L1_attn_in['Wout'], 'L1_attn_bout': _L1_attn_in['bout'], 'L1_ffn_w_router': _L1_ffn_in['w_router'], 'L1_ffn_W1': _L1_ffn_in['W1'], 'L1_ffn_b1': _L1_ffn_in['b1'], 'L1_ffn_W2': _L1_ffn_in['W2'], 'L1_ffn_b2': _L1_ffn_in['b2'], 'L2_xattn_Wq': _L2_xattn_in['Wq'], 'L2_xattn_bq': _L2_xattn_in['bq'], 'L2_xattn_Wk': _L2_xattn_in['Wk'], 'L2_xattn_bk': _L2_xattn_in['bk'], 'L2_xattn_Wv': _L2_xattn_in['Wv'], 'L2_xattn_bv': _L2_xattn_in['bv'], 'L2_xattn_Wo': _L2_xattn_in['Wo'], 'L2_xattn_bo': _L2_xattn_in['bo'], 'L2_attn_W_q': _L2_attn_in['W_q'], 'L2_attn_W_k': _L2_attn_in['W_k'], 'L2_attn_W_v': _L2_attn_in['W_v'], 'L2_attn_W_o': _L2_attn_in['W_o'], 'L2_ffn_gate_w': _L2_ffn_in['gate_w'], 'L2_ffn_gate_b': _L2_ffn_in['gate_b'], 'L2_ffn_shared_wg': _L2_ffn_in['shared_wg'], 'L2_ffn_shared_wu': _L2_ffn_in['shared_wu'], 'L2_ffn_shared_wd': _L2_ffn_in['shared_wd'], 'L2_ffn_experts_wg': _L2_ffn_in['experts_wg'], 'L2_ffn_experts_wu': _L2_ffn_in['experts_wu'], 'L2_ffn_experts_wd': _L2_ffn_in['experts_wd'], 'L3_xattn_w_q': _L3_xattn_in['w_q'], 'L3_xattn_b_q': _L3_xattn_in['b_q'], 'L3_xattn_w_k': _L3_xattn_in['w_k'], 'L3_xattn_b_k': _L3_xattn_in['b_k'], 'L3_xattn_w_v': _L3_xattn_in['w_v'], 'L3_xattn_b_v': _L3_xattn_in['b_v'], 'L3_xattn_w_o': _L3_xattn_in['w_o'], 'L3_xattn_b_o': _L3_xattn_in['b_o'], 'L3_attn_log_dt': _L3_attn_in['log_dt'], 'L3_attn_log_A_real': _L3_attn_in['log_A_real'], 'L3_attn_A_imag': _L3_attn_in['A_imag'], 'L3_attn_C_real': _L3_attn_in['C_real'], 'L3_attn_C_imag': _L3_attn_in['C_imag'], 'L3_attn_W': _L3_attn_in['W'], 'L3_attn_b': _L3_attn_in['b'], 'L3_ffn_router_w0': _L3_ffn_in['router_w0'], 'L3_ffn_wg0': _L3_ffn_in['wg0'], 'L3_ffn_wu0': _L3_ffn_in['wu0'], 'L3_ffn_wd0': _L3_ffn_in['wd0'], 'L3_ffn_router_w1': _L3_ffn_in['router_w1'], 'L3_ffn_wg1': _L3_ffn_in['wg1'], 'L3_ffn_wu1': _L3_ffn_in['wu1'], 'L3_ffn_wd1': _L3_ffn_in['wd1']}

def reference(x, ctx_768, mask_BxS2_bk0, L0_xattn_Wq, L0_xattn_Wk, L0_xattn_Wv, L0_xattn_Wo, L0_xattn_bo, L0_attn_wq, L0_attn_w_down, L0_attn_wk_up, L0_attn_wv_up, L0_attn_wo, L0_ffn_Wq, L0_ffn_Wk, L0_ffn_Ws, L0_ffn_Wd, L0_ffn_Wv, L0_ffn_Wo, L1_xattn_ln_x_g, L1_xattn_ln_x_b, L1_xattn_ln_l_g, L1_xattn_ln_l_b, L1_xattn_qn_g, L1_xattn_kn_g, L1_xattn_Wq, L1_xattn_Wkv, L1_xattn_Wlkv, L1_xattn_Wo, L1_xattn_bo, L1_attn_Wqkv, L1_attn_bqkv, L1_attn_Wout, L1_attn_bout, L1_ffn_w_router, L1_ffn_W1, L1_ffn_b1, L1_ffn_W2, L1_ffn_b2, L2_xattn_Wq, L2_xattn_bq, L2_xattn_Wk, L2_xattn_bk, L2_xattn_Wv, L2_xattn_bv, L2_xattn_Wo, L2_xattn_bo, L2_attn_W_q, L2_attn_W_k, L2_attn_W_v, L2_attn_W_o, L2_ffn_gate_w, L2_ffn_gate_b, L2_ffn_shared_wg, L2_ffn_shared_wu, L2_ffn_shared_wd, L2_ffn_experts_wg, L2_ffn_experts_wu, L2_ffn_experts_wd, L3_xattn_w_q, L3_xattn_b_q, L3_xattn_w_k, L3_xattn_b_k, L3_xattn_w_v, L3_xattn_b_v, L3_xattn_w_o, L3_xattn_b_o, L3_attn_log_dt, L3_attn_log_A_real, L3_attn_A_imag, L3_attn_C_real, L3_attn_C_imag, L3_attn_W, L3_attn_b, L3_ffn_router_w0, L3_ffn_wg0, L3_ffn_wu0, L3_ffn_wd0, L3_ffn_router_w1, L3_ffn_wg1, L3_ffn_wu1, L3_ffn_wd1):
    import jax
    import jax.numpy as jnp

    def _L0_xattn_ref(x, context, Wq, Wk, Wv, Wo, bo):
        import jax, jax.numpy as jnp
        import numpy as np
        HEADS = 16
        DIM_HEAD = 64
        SCALE = DIM_HEAD ** (-0.5)
        B, N, _ = x.shape
        M = context.shape[1]
        q = (x @ Wq).reshape(B, N, HEADS, DIM_HEAD).transpose(0, 2, 1, 3)
        k = (context @ Wk).reshape(B, M, HEADS, DIM_HEAD).transpose(0, 2, 1, 3)
        v = (context @ Wv).reshape(B, M, HEADS, DIM_HEAD).transpose(0, 2, 1, 3)
        dots = jnp.einsum('bhnd,bhmd->bhnm', q, k) * SCALE
        attn = jax.nn.softmax(dots, axis=-1)
        out = jnp.einsum('bhnm,bhmd->bhnd', attn, v)
        out = out.transpose(0, 2, 1, 3).reshape(B, N, HEADS * DIM_HEAD)
        return out @ Wo + bo

    def _L0_attn_ref(x, wq, w_down, wk_up, wv_up, wo):
        import jax, jax.numpy as jnp
        import numpy as np
        N_HEAD = 16
        PAGE_SIZE = 64
        ROPE_THETA = 10000.0

        def _rope_tables(T, D, dtype):
            inv = 1.0 / ROPE_THETA ** (np.arange(0, D, 2, dtype=np.float32) / D)
            ang = np.outer(np.arange(T, dtype=np.float32), inv)
            return (jnp.asarray(np.cos(ang), dtype), jnp.asarray(np.sin(ang), dtype))

        def _apply_rope(x, cos, sin):
            x1 = x[..., 0::2]
            x2 = x[..., 1::2]
            c = cos[None, :, None, :]
            s = sin[None, :, None, :]
            out = jnp.stack([x1 * c - x2 * s, x1 * s + x2 * c], axis=-1)
            return out.reshape(x.shape)
        B, T, E = x.shape
        H = N_HEAD
        D = E // H
        q = (x @ wq).reshape(B, T, H, D)
        lat = x @ w_down
        k = (lat @ wk_up).reshape(B, T, H, D)
        v = (lat @ wv_up).reshape(B, T, H, D)
        cos, sin = _rope_tables(T, D, x.dtype)
        q = _apply_rope(q, cos, sin)
        k = _apply_rope(k, cos, sin)
        scale = 1.0 / jnp.sqrt(jnp.asarray(D, x.dtype))
        scores = jnp.einsum('bqhd,bkhd->bhqk', q, k) * scale
        pages = jnp.arange(T) // PAGE_SIZE
        allowed = pages[None, :] <= pages[:, None]
        scores = jnp.where(allowed[None, None], scores, jnp.finfo(scores.dtype).min)
        attn = jax.nn.softmax(scores, axis=-1)
        out = jnp.einsum('bhqk,bkhd->bqhd', attn, v).reshape(B, T, E)
        return out @ wo

    def _L0_ffn_ref(x, Wq, Wk, Ws, Wd, Wv, Wo):
        import jax, jax.numpy as jnp
        import numpy as np
        B, T, D = (4, 512, 256)
        H, DH, E, SEL = (8, 64, 5, 2)

        def _topk_mask(logits, k):
            _, idx = jax.lax.top_k(logits, k)
            return jnp.sum(jax.nn.one_hot(idx, logits.shape[-1], dtype=logits.dtype), axis=-2)
        e, d, dh = Wv.shape
        h = Wq.shape[1] // dh
        b, t, _ = x.shape
        scale = dh ** (-0.5)
        q = (x @ Wq).reshape(b, t, h, dh).transpose(0, 2, 1, 3)
        k = (x @ Wk).reshape(b, t, h, dh).transpose(0, 2, 1, 3)
        gl_v = (x @ Ws).reshape(b, t, h, e)
        wv = _topk_mask(gl_v, SEL) * jax.nn.sigmoid(gl_v)
        xv = jnp.einsum('btd,edk->btek', x, Wv)
        v = jnp.einsum('bthe,btek->bhtk', wv, xv)
        scores = jnp.einsum('bhid,bhjd->bhij', q * scale, k)
        probs = jax.nn.softmax(scores, axis=-1)
        attn = jnp.einsum('bhij,bhjd->bihd', probs, v)
        gl_o = (x @ Wd).reshape(b, t, h, e)
        mask_o = _topk_mask(gl_o, SEL)
        out = jnp.einsum('bthe,bthk,ekd->btd', mask_o, attn, Wo)
        return out

    def _L1_xattn_ref(x, latents, mask, ln_x_g, ln_x_b, ln_l_g, ln_l_b, qn_g, kn_g, Wq, Wkv, Wlkv, Wo, bo):
        import jax, jax.numpy as jnp
        import numpy as np
        DIM_IN, DIM_LAT, DIM_HEAD = (192, 256, 64)
        INNER = max(DIM_LAT, DIM_IN)
        HEADS = INNER // DIM_HEAD
        SCALE = DIM_HEAD ** (-0.5)
        RMS_EPS = 1e-08
        LN_EPS = 1e-05

        def layernorm(x, g, b):
            mu = jnp.mean(x, axis=-1, keepdims=True)
            var = jnp.mean((x - mu) ** 2, axis=-1, keepdims=True)
            return (x - mu) * jax.lax.rsqrt(var + LN_EPS) * g + b

        def rmsnorm(x, gamma):
            norm = jnp.sqrt(jnp.sum(x * x, axis=-1, keepdims=True)) * x.shape[-1] ** (-0.5)
            return x / jnp.maximum(norm, RMS_EPS) * gamma
        b, n, _ = x.shape
        m = latents.shape[1]
        xn = layernorm(x, ln_x_g, ln_x_b)
        ln = layernorm(latents, ln_l_g, ln_l_b)
        q = ln @ Wq.T
        kv = jnp.concatenate([xn @ Wkv.T, ln @ Wlkv.T], axis=1)
        k, v = (kv[..., :INNER], kv[..., INNER:])
        split_heads = lambda t: t.reshape(t.shape[0], t.shape[1], HEADS, DIM_HEAD).transpose(0, 2, 1, 3)
        q, k, v = (split_heads(q), split_heads(k), split_heads(v))
        qn = rmsnorm(q, qn_g) * SCALE
        kn = rmsnorm(k, kn_g)
        attn = jnp.einsum('bhid,bhjd->bhij', qn, kn)
        full_mask = jnp.pad(mask, ((0, 0), (0, m)), constant_values=True)
        attn = jnp.where(full_mask[:, None, None, :], attn, -jnp.finfo(attn.dtype).max)
        attn = jax.nn.softmax(attn, axis=-1)
        out = jnp.einsum('bhij,bhjd->bhid', attn, v)
        out = out.transpose(0, 2, 1, 3).reshape(b, m, INNER)
        return out @ Wo.T + bo

    def _L1_attn_ref(x, Wqkv, bqkv, Wout, bout):
        import jax, jax.numpy as jnp
        import numpy as np
        B, S, E, H = (4, 512, 256, 16)
        HD = E // H
        b, s, e = x.shape
        qkv = x @ Wqkv + bqkv
        qkv = qkv.reshape(b, s, H, 3 * HD)
        q, k, v = (qkv[..., :HD], qkv[..., HD:2 * HD], qkv[..., 2 * HD:])
        scores = jnp.einsum('bqhd,bkhd->bhqk', q, k) / jnp.sqrt(jnp.float32(HD))
        attn = jax.nn.softmax(scores, axis=-1)
        out = jnp.einsum('bhqk,bkhd->bqhd', attn, v).reshape(b, s, e)
        return out @ Wout + bout

    def _L1_ffn_ref(hidden_states, w_router, W1, b1, W2, b2):
        import jax, jax.numpy as jnp
        import numpy as np
        CAPACITY_FACTOR = 0.5
        'Mixture-of-Depths block: route top-k tokens through an FFN inner block,\n            scatter back with sigmoid router weights; bypassed tokens pass through.'
        B, S, D = hidden_states.shape
        k = int(S * CAPACITY_FACTOR)
        scores = jnp.einsum('bsd,d->bs', hidden_states, w_router)
        top_scores, top_idx = jax.lax.top_k(scores, k)
        weights = jax.nn.sigmoid(top_scores)
        selected = jnp.take_along_axis(hidden_states, top_idx[:, :, None], axis=1)
        h = jax.nn.gelu(jnp.einsum('bkd,df->bkf', selected, W1) + b1)
        processed = jnp.einsum('bkf,fd->bkd', h, W2) + b2
        update = weights[:, :, None] * processed

        def scatter_one(xb, ib, ub):
            return xb.at[ib].add(ub)
        output = jax.vmap(scatter_one)(hidden_states, top_idx, update)
        return output

    def _L2_xattn_ref(x, y, Wq, bq, Wk, bk, Wv, bv, Wo, bo):
        import math
        import jax, jax.numpy as jnp
        import numpy as np
        B, SQ, SKV = (4, 512, 512)
        D_EMBED, D_CROSS, D_ATT, N_HEADS = (256, 192, 256, 16)
        D_HEAD = D_ATT // N_HEADS

        def _split_heads(t):
            b, s, _ = t.shape
            return t.reshape(b, s, N_HEADS, D_HEAD).transpose(0, 2, 1, 3)
        q = _split_heads(x @ Wq + bq)
        k = _split_heads(y @ Wk + bk)
        v = _split_heads(y @ Wv + bv)
        scale = 1.0 / math.sqrt(D_HEAD)
        scores = jnp.einsum('bhqd,bhkd->bhqk', q, k) * scale
        weights = jax.nn.softmax(scores, axis=-1)
        out = jnp.einsum('bhqk,bhkd->bhqd', weights, v)
        out = out.transpose(0, 2, 1, 3).reshape(x.shape[0], x.shape[1], D_ATT)
        return out @ Wo + bo

    def _L2_attn_ref(x, W_q, W_k, W_v, W_o):
        import jax, jax.numpy as jnp
        import numpy as np
        D_MODEL = 256
        N_HEADS = 16
        CHUNK = 64
        EPS = 1e-06

        def elu_plus_1(x):
            return jax.nn.elu(x) + 1.0
        B, T, D = x.shape
        H = N_HEADS
        dk = D // H
        dv = dk
        C = CHUNK
        N = T // C
        q = (x @ W_q.T).reshape(B, T, H, dk)
        k = (x @ W_k.T).reshape(B, T, H, dk)
        v = (x @ W_v.T).reshape(B, T, H, dv)
        phi_q = elu_plus_1(q).reshape(B, N, C, H, dk)
        phi_k = elu_plus_1(k).reshape(B, N, C, H, dk)
        vc = v.reshape(B, N, C, H, dv)
        KV = jnp.einsum('bnchk,bnchv->bnhkv', phi_k, vc)
        Ksum = phi_k.sum(axis=2)
        KV_cum = jnp.cumsum(KV, axis=1)
        Ksum_cum = jnp.cumsum(Ksum, axis=1)
        S_prefix = jnp.concatenate([jnp.zeros_like(KV_cum[:, :1]), KV_cum[:, :-1]], axis=1)
        z_prefix = jnp.concatenate([jnp.zeros_like(Ksum_cum[:, :1]), Ksum_cum[:, :-1]], axis=1)
        inter = jnp.einsum('bnchk,bnhkv->bnchv', phi_q, S_prefix)
        z_inter = jnp.einsum('bnchk,bnhk->bnch', phi_q, z_prefix)
        mask = jnp.tril(jnp.ones((C, C), dtype=x.dtype))
        attn = jnp.einsum('bnihk,bnjhk->bnhij', phi_q, phi_k) * mask
        intra = jnp.einsum('bnhij,bnjhv->bnihv', attn, vc)
        z_intra = attn.sum(axis=-1).transpose(0, 1, 3, 2)
        denom = jnp.clip((z_inter + z_intra)[..., None], 1e-06, None)
        y = (inter + intra) / denom
        y = y.reshape(B, T, H * dv)
        return y @ W_o.T

    def _L2_ffn_ref(x, gate_w, gate_b, shared_wg, shared_wu, shared_wd, experts_wg, experts_wu, experts_wd):
        import jax, jax.numpy as jnp
        import numpy as np
        B, S, D = (2, 512, 256)
        I = 128
        E = 16
        TOP_K = 2

        def _mlp(x, wg, wu, wd):
            return jnp.einsum('bsi,id->bsd', jax.nn.silu(x @ wg) * (x @ wu), wd)
        router_logits = jax.nn.sigmoid(x @ gate_w + gate_b)
        expert_values, expert_indices = jax.lax.top_k(router_logits, k=TOP_K)
        expert_values = expert_values / jnp.sum(expert_values, axis=-1, keepdims=True)
        hg = jnp.einsum('bsd,edi->bsei', x, experts_wg)
        hu = jnp.einsum('bsd,edi->bsei', x, experts_wu)
        all_outputs = jnp.einsum('bsei,eid->bsed', jax.nn.silu(hg) * hu, experts_wd)
        selected = jnp.take_along_axis(all_outputs, expert_indices[..., None], axis=2)
        expert_weighted = jnp.sum(expert_values[..., None] * selected, axis=2)
        return x + _mlp(x, shared_wg, shared_wu, shared_wd) + expert_weighted

    def _L3_xattn_ref(x, context, w_q, b_q, w_k, b_k, w_v, b_v, w_o, b_o):
        import jax, jax.numpy as jnp
        import numpy as np
        N_HEADS = 16
        DIMS = 256
        D_CTX = 192
        HEAD = DIMS // N_HEADS
        B, Lq, D = x.shape
        q = x @ w_q + b_q
        k = context @ w_k + b_k
        v = context @ w_v + b_v
        q = q.reshape(B, Lq, N_HEADS, HEAD)
        k = k.reshape(B, -1, N_HEADS, HEAD)
        v = v.reshape(B, -1, N_HEADS, HEAD)
        scale = 1.0 / np.sqrt(HEAD).astype(np.float32)
        scores = jnp.einsum('bqhd,bkhd->bhqk', q, k) * scale
        weights = jax.nn.softmax(scores, axis=-1)
        out = jnp.einsum('bhqk,bkhd->bqhd', weights, v).reshape(B, Lq, D)
        return out @ w_o + b_o

    def _L3_attn_ref(x, log_dt, log_A_real, A_imag, C_real, C_imag, W, b):
        import jax, jax.numpy as jnp
        import numpy as np
        import math
        B, L, D, N2 = (8, 1024, 256, 32)

        def s4d_kernel(log_dt, log_A_real, A_imag, C_real, C_imag, length):
            dt = jnp.exp(log_dt)[:, None]
            A = -jnp.exp(log_A_real) + 1j * A_imag
            dtA = A * dt
            C = (C_real + 1j * C_imag) * (jnp.exp(dtA) - 1.0) / A
            t = jnp.arange(length, dtype=jnp.float32)
            vand = jnp.exp(dtA[:, :, None] * t)
            K = 2.0 * jnp.einsum('dn,dnl->dl', C, vand).real
            return K
        Bb, Ll, Dd = x.shape
        K = s4d_kernel(log_dt, log_A_real, A_imag, C_real, C_imag, Ll)
        n_fft = 2 * Ll
        x_t = jnp.transpose(x, (0, 2, 1))
        k_f = jnp.fft.rfft(K, n=n_fft)
        x_f = jnp.fft.rfft(x_t, n=n_fft)
        y = jnp.fft.irfft(x_f * k_f[None], n=n_fft)[:, :, :Ll]
        y = jnp.transpose(y, (0, 2, 1))
        y = jax.nn.gelu(y, approximate=False)
        return y @ W.T + b

    def _L3_ffn_ref(x, router_w0, wg0, wu0, wd0, router_w1, wg1, wu1, wd1):
        import jax, jax.numpy as jnp
        from jax import lax
        import numpy as np
        D_MODEL = 256
        HIDDEN = 128
        N_EXPERTS = 32
        TOP_K = 2
        B, S = (1, 1024)

        def _moe_group(x2, router_w, wg, wu, wd, top_k):
            T = x2.shape[0]
            n_experts = router_w.shape[1]
            logits = x2 @ router_w
            scores = jax.nn.softmax(logits, axis=-1)
            expert_weights, expert_indices = lax.top_k(scores, top_k)
            flat_e = expert_indices.reshape(-1)
            flat_w = expert_weights.reshape(-1)
            flat_t = jnp.repeat(jnp.arange(T), top_k)
            order = jnp.argsort(flat_e)
            tok = flat_t[order]
            xs = x2[tok]
            group_sizes = jnp.bincount(flat_e, length=n_experts).astype(jnp.int32)
            gate = lax.ragged_dot(xs, wg, group_sizes)
            up = lax.ragged_dot(xs, wu, group_sizes)
            ys = lax.ragged_dot(jax.nn.silu(gate) * up, wd, group_sizes)
            ys = ys * flat_w[order][:, None]
            return jnp.zeros_like(x2).at[tok].add(ys)
        b, s, d = x.shape
        x2 = x.reshape(-1, d)
        out0 = _moe_group(x2, router_w0, wg0, wu0, wd0, TOP_K)
        out1 = _moe_group(x2, router_w1, wg1, wu1, wd1, TOP_K)
        out = (out0 * TOP_K + out1 * TOP_K) / (TOP_K + TOP_K)
        return out.reshape(b, s, d)
    x = x + _L0_xattn_ref(_layernorm(x, axis=-1), ctx_768, L0_xattn_Wq, L0_xattn_Wk, L0_xattn_Wv, L0_xattn_Wo, L0_xattn_bo)
    x = x + _L0_attn_ref(_layernorm(x, axis=-1), L0_attn_wq, L0_attn_w_down, L0_attn_wk_up, L0_attn_wv_up, L0_attn_wo)
    x = x + _L0_ffn_ref(_layernorm(x, axis=-1), L0_ffn_Wq, L0_ffn_Wk, L0_ffn_Ws, L0_ffn_Wd, L0_ffn_Wv, L0_ffn_Wo)
    x = x + _L1_xattn_ref(ctx_768, _layernorm(x, axis=-1), mask_BxS2_bk0, L1_xattn_ln_x_g, L1_xattn_ln_x_b, L1_xattn_ln_l_g, L1_xattn_ln_l_b, L1_xattn_qn_g, L1_xattn_kn_g, L1_xattn_Wq, L1_xattn_Wkv, L1_xattn_Wlkv, L1_xattn_Wo, L1_xattn_bo)
    x = x + _L1_attn_ref(_layernorm(x, axis=-1), L1_attn_Wqkv, L1_attn_bqkv, L1_attn_Wout, L1_attn_bout)
    x = x + _L1_ffn_ref(_layernorm(x, axis=-1), L1_ffn_w_router, L1_ffn_W1, L1_ffn_b1, L1_ffn_W2, L1_ffn_b2)
    x = x + _L2_xattn_ref(_layernorm(x, axis=-1), ctx_768, L2_xattn_Wq, L2_xattn_bq, L2_xattn_Wk, L2_xattn_bk, L2_xattn_Wv, L2_xattn_bv, L2_xattn_Wo, L2_xattn_bo)
    x = x + _L2_attn_ref(_layernorm(x, axis=-1), L2_attn_W_q, L2_attn_W_k, L2_attn_W_v, L2_attn_W_o)
    x = x + _L2_ffn_ref(_layernorm(x, axis=-1), L2_ffn_gate_w, L2_ffn_gate_b, L2_ffn_shared_wg, L2_ffn_shared_wu, L2_ffn_shared_wd, L2_ffn_experts_wg, L2_ffn_experts_wu, L2_ffn_experts_wd)
    x = x + _L3_xattn_ref(_layernorm(x, axis=-1), ctx_768, L3_xattn_w_q, L3_xattn_b_q, L3_xattn_w_k, L3_xattn_b_k, L3_xattn_w_v, L3_xattn_b_v, L3_xattn_w_o, L3_xattn_b_o)
    x = x + _L3_attn_ref(_layernorm(x, axis=-1), L3_attn_log_dt, L3_attn_log_A_real, L3_attn_A_imag, L3_attn_C_real, L3_attn_C_imag, L3_attn_W, L3_attn_b)
    x = x + _L3_ffn_ref(_layernorm(x, axis=-1), L3_ffn_router_w0, L3_ffn_wg0, L3_ffn_wu0, L3_ffn_wd0, L3_ffn_router_w1, L3_ffn_wg1, L3_ffn_wu1, L3_ffn_wd1)
    return x

_drawn_inputs = setup_inputs


def setup_inputs(seed=0):
    import zlib

    import numpy as np

    out = dict(_drawn_inputs(seed))
    spreads = {'L0_xattn_bo': (0.0, 0.1),
     'L1_xattn_ln_x_g': (1.0, 0.2),
     'L1_xattn_ln_x_b': (0.0, 0.1),
     'L1_xattn_ln_l_g': (1.0, 0.2),
     'L1_xattn_ln_l_b': (0.0, 0.1),
     'L1_xattn_qn_g': (1.0, 0.2),
     'L1_xattn_kn_g': (1.0, 0.2),
     'L1_xattn_bo': (0.0, 0.1),
     'L1_ffn_b1': (0.0, 0.396),
     'L1_ffn_b2': (0.0, 0.272),
     'L2_ffn_gate_b': (0.0, 0.1),
     'L3_attn_log_A_real': (-0.6931471824645996, 0.6)}
    factors = {'L0_ffn_Wq': 8.0,
     'L0_ffn_Wk': 7.37,
     'L2_xattn_bq': 8.0,
     'L2_xattn_bk': 64.0,
     'L2_xattn_bv': 6.323,
     'L2_xattn_bo': 6.522,
     'L2_attn_W_q': 5.686,
     'L2_attn_W_k': 3.588,
     'L3_xattn_b_q': 25.256,
     'L3_xattn_b_k': 64.0,
     'L3_xattn_b_v': 8.0,
     'L3_xattn_b_o': 8.0,
     'L3_attn_b': 8.0,
     'L3_ffn_router_w0': 8.0,
     'L3_ffn_wg0': 8.0,
     'L3_ffn_wu0': 8.0,
     'L3_ffn_wd0': 8.0,
     'L3_ffn_router_w1': 8.0,
     'L3_ffn_wg1': 8.0,
     'L3_ffn_wu1': 8.0,
     'L3_ffn_wd1': 8.0}
    for name, (base, spread) in spreads.items():
        noise = np.random.default_rng([zlib.crc32(name.encode()), seed]).standard_normal(out[name].shape)
        drawn = base * np.exp(spread * noise) if base else spread * noise
        out[name] = jnp.asarray(drawn.astype(out[name].dtype))
    for name, factor in factors.items():
        out[name] = (out[name] * factor).astype(out[name].dtype)
    return out
```

```python
from contextlib import ExitStack, contextmanager

import concourse.bass as bass
import numpy as np
from concourse import mybir

F32 = mybir.dt.float32
BF16 = mybir.dt.bfloat16
I32 = mybir.dt.int32
ALU = mybir.AluOpType
ACT = mybir.ActivationFunctionType
AX = mybir.AxisListType

FIRST_LAYER, LAST_LAYER = 0, 11

P = 128
BATCH, SEQ, D = 16, 64, 256
KEYS, DC = 1601, 192
TOK = BATCH * SEQ
TT = TOK // P
KD = D // P
MT = -(-KEYS // P)
MPAD = MT * P
CA = DC + 1
CL = CA - P
HALF = 512
LN_EPS = 1e-5
CLIP = 1e-6


class Mem:
    pass


def alloc_memory(nc, ctx):
    m = Mem()
    m.ctx = ctx

    def sb(name, shape, dt=F32):
        return ctx.enter_context(nc.sbuf_tensor(name, shape, dt))

    m.x = sb("x_tok", [P, TT, D])
    m.xn = sb("xn_tok", [P, TT, D])
    m.xnT = sb("xn_T", [P, KD, TOK])
    m.featT = sb("feat_T", [P, 8, TOK])
    m.wo = sb("w_out", [P, 8, D])
    m.bo = sb("b_out", [1, D])
    m.ident = sb("ident", [P, P])
    m.ones = sb("ones_row", [1, P])
    m.held = ctx.enter_context(nc.semaphore("held"))
    m.n_blocks = 0
    m.retired = []
    return m


def scope(nc, m):
    m.n_blocks += 1
    tag = f"b{m.n_blocks}_"
    ctx = ExitStack()

    def sb(name, shape, dt=F32):
        return ctx.enter_context(nc.sbuf_tensor(tag + name, shape, dt))

    def ps(name, shape, dt=F32):
        return ctx.enter_context(nc.psum_tensor(tag + name, shape, dt))

    def sem(name):
        s = nc.alloc_semaphore(name=tag + name)
        own.append(s)
        return s

    own = []
    ctx.callback(lambda: m.retired.extend(own))
    return ctx, sb, ps, sem


@contextmanager
def engines_block(nc, m):
    cleared, m.retired = m.retired, []
    for s in cleared:
        nc.gpsimd.sem_clear(s)
    with nc.Block() as block:
        yield block
    for s in cleared:
        nc.release_semaphore(s)


class Chain:

    def __init__(self, eng, sem, base=None, per=None):
        self.eng, self.sem, self.base, self.n, self.per = eng, sem, base, 0, per

    def step(self, ins):
        self.n += 1
        ins.then_inc(self.sem, 1)
        self.eng.wait_ge(self.sem, self.n if self.base is None else self.base + self.n)

    def close(self):
        assert self.n == self.per, (self.n, self.per)


def hold_waits(eng, m):
    eng.sem_inc(m.held, 1)


def flat(ap):
    return ap.rearrange("p a b -> p (a b)")


def load_x_block(nc, m, x_in, ident_in):
    ctx, sb, ps, sem = scope(nc, m)
    with ctx:
        loaded = sem("loaded")
        with engines_block(nc, m) as block:

            @block.sync
            def _(sp):
                sp.dma_start(m.x[:, :, :], x_in).then_inc(loaded, 16)
                sp.dma_start(m.ident[:, :], ident_in).then_inc(loaded, 16)
                sp.wait_ge(loaded, 32)

            @block.vector
            def _(dve):
                nc.vector.memset(m.ones[:, :], 1.0)


def store_x_block(nc, m, x_out):
    ctx, sb, ps, sem = scope(nc, m)
    with ctx:
        stored = sem("stored")
        with engines_block(nc, m) as block:

            @block.sync
            def _(sp):
                sp.dma_start(x_out, m.x[:, :, :]).then_inc(stored, 16)
                sp.wait_ge(stored, 16)


def project_and_norm_block(nc, m, chunks, last_rows=P, bias=False, gated=None, norm=True):
    ctx, sb, ps, sem = scope(nc, m)
    with ctx:
        stats = sb("stats", [P, TT, 6])
        mv = sb("mean_var", [P, TT, 2])
        rstd = sb("rstd", [P, TT])
        proj = [ps(f"proj{i}", [P, D]) for i in range(2)]
        tps = [ps(f"tps{i}", [P, KD, P]) for i in range(2)]
        projected = sem("projected")
        added = sem("added")
        vec = sem("vec")
        var_ready = sem("var_ready")
        std_ready = sem("std_ready")
        xn_ready = sem("xn_ready")
        transposed = sem("transposed")
        evacuated = sem("evacuated")
        with engines_block(nc, m) as block:

            @block.tensor
            def _(pe):
                if chunks:
                    for t in range(TT):
                        if t >= 2:
                            pe.wait_ge(added, t - 1)
                        for c in range(chunks):
                            k = last_rows if c == chunks - 1 else P
                            last = nc.tensor.matmul(
                                proj[t % 2][:, :], m.featT[0:k, c, t * P:(t + 1) * P], m.wo[0:k, c, :],
                                start=(c == 0), stop=(c == chunks - 1 and not bias))
                        if bias:
                            last = nc.tensor.matmul(proj[t % 2][:, :], m.ones[0:1, :], m.bo[0:1, :],
                                                    start=False, stop=True)
                        last.then_inc(projected, 1)
                if norm:
                    for t in range(TT):
                        pe.wait_ge(xn_ready, t + 1)
                        if t >= 2:
                            pe.wait_ge(evacuated, t - 1)
                        for k in range(KD):
                            last = nc.tensor.transpose(tps[t % 2][:, k, :], m.xn[:, t, k * P:(k + 1) * P],
                                                       m.ident[:, :])
                        last.then_inc(transposed, 1)

            @block.vector
            def _(dve):
                chain = Chain(dve, vec)
                for t in range(TT):
                    if chunks:
                        dve.wait_ge(projected, t + 1)
                        if gated is not None:
                            chain.step(nc.vector.tensor_tensor(m.x[:, t, :], m.x[:, t, :], m.xn[:, t, :], ALU.add))
                            nc.vector.scalar_tensor_tensor(m.x[:, t, :], proj[t % 2][:, :], gated[:, t:t + 1],
                                                           m.x[:, t, :], ALU.mult, ALU.add).then_inc(added, 1)
                        else:
                            nc.vector.tensor_tensor(m.x[:, t, :], m.x[:, t, :], proj[t % 2][:, :],
                                                    ALU.add).then_inc(added, 1)
                        dve.wait_ge(added, t + 1)
                    if norm:
                        chain.step(nc.vector.bn_stats(stats[:, t, :], m.x[:, t, :]))
                        last = nc.vector.bn_aggr(mv[:, t, :], stats[:, t, :])
                if norm:
                    chain.step(last)
                    nc.vector.tensor_scalar(rstd[:, :], mv[:, :, 1], LN_EPS, None, ALU.add).then_inc(var_ready, 1)
                    dve.wait_ge(std_ready, 1)
                    chain.step(nc.vector.reciprocal(rstd[:, :], rstd[:, :]))
                    for t in range(TT):
                        nc.vector.tensor_scalar(m.xn[:, t, :], m.x[:, t, :], mv[:, t, 0:1], rstd[:, t:t + 1],
                                                ALU.subtract, ALU.mult).then_inc(xn_ready, 1)

            @block.scalar
            def _(act):
                if norm:
                    act.wait_ge(var_ready, 1)
                    nc.scalar.activation(rstd[:, :], rstd[:, :], ACT.Sqrt).then_inc(std_ready, 1)
                    for t in range(TT):
                        act.wait_ge(transposed, t + 1)
                        nc.scalar.copy(m.xnT[:, :, t * P:(t + 1) * P], tps[t % 2][:, :, :]).then_inc(evacuated, 1)


def feature_major_block(nc, m, jobs, loads):
    ctx, sb, ps, sem = scope(nc, m)
    pieces = [(j, c, h) for j in range(len(jobs)) for c in range(jobs[j][1]) for h in range(TOK // HALF)]
    on_act = [jobs[j][5][0] == "gelu" or (jobs[j][5][0] == "linear" and n % 2 == 0)
              for n, (j, c, h) in enumerate(pieces)]
    done_before = [sum(1 for k in range(n) if on_act[k] == on_act[n]) for n in range(len(pieces))]
    with ctx:
        ring = [ps(f"ring{i}", [P, HALF]) for i in range(4)]
        low = sb("low", [P, 2, HALF])
        loaded = sem("loaded")
        filled = sem("filled")
        act_done = sem("act_done")
        dve_done = sem("dve_done")
        vec = sem("vec")
        low_ready = sem("low_ready")
        exp_ready = sem("exp_ready")
        with engines_block(nc, m) as block:

            @block.sync
            def _(sp):
                for buf, dram in loads:
                    sp.dma_start(buf, dram).then_inc(loaded, 16)

            @block.tensor
            def _(pe):
                if loads:
                    pe.wait_ge(loaded, 16 * len(loads))
                for n, (j, c, h) in enumerate(pieces):
                    dst, chunks, w, src, kc, post = jobs[j]
                    if j and c == 0 and h == 0 and src is jobs[j - 1][0]:
                        for q in (k for k in range(n) if pieces[k][0] == j - 1):
                            pe.wait_ge(act_done if on_act[q] else dve_done, done_before[q] + 1)
                    if n >= 4:
                        pe.wait_ge(act_done if on_act[n - 4] else dve_done, done_before[n - 4] + 1)
                    for k in range(kc):
                        last = nc.tensor.matmul(ring[n % 4][:, :], w[:, k, c * P:(c + 1) * P],
                                                src[:, k, h * HALF:(h + 1) * HALF],
                                                start=(k == 0), stop=(k == kc - 1))
                    last.then_inc(filled, 1)

            @block.scalar
            def _(act):
                if loads:
                    act.wait_ge(loaded, 16 * len(loads))
                n_low = 0
                for n, (j, c, h) in enumerate(pieces):
                    dst, chunks, w, src, kc, post = jobs[j]
                    out = dst[:, c, h * HALF:(h + 1) * HALF]
                    if post[0] == "elu1":
                        n_low += 1
                        act.wait_ge(low_ready, n_low)
                        nc.scalar.activation(low[:, (n_low - 1) % 2, :], low[:, (n_low - 1) % 2, :],
                                             ACT.Exp).then_inc(exp_ready, 1)
                    if not on_act[n]:
                        continue
                    act.wait_ge(filled, n + 1)
                    if post[0] == "gelu":
                        nc.scalar.activation(out, ring[n % 4][:, :], ACT.Gelu_apprx_tanh,
                                             bias=post[1][:, c:c + 1]).then_inc(act_done, 1)
                    else:
                        nc.scalar.activation(out, ring[n % 4][:, :], ACT.Copy,
                                             scale=float(post[1])).then_inc(act_done, 1)

            @block.vector
            def _(dve):
                if loads:
                    dve.wait_ge(loaded, 16 * len(loads))
                n_low = 0
                for n, (j, c, h) in enumerate(pieces):
                    if on_act[n]:
                        continue
                    dst, chunks, w, src, kc, post = jobs[j]
                    out = dst[:, c, h * HALF:(h + 1) * HALF]
                    dve.wait_ge(filled, n + 1)
                    if post[0] == "bias":
                        nc.vector.tensor_scalar(out, ring[n % 4][:, :], post[1][:, c:c + 1], float(post[2]),
                                                ALU.add, ALU.mult).then_inc(dve_done, 1)
                    elif post[0] == "elu1":
                        nc.vector.tensor_scalar(low[:, n_low % 2, :], ring[n % 4][:, :], 0.0, None,
                                                ALU.min).then_inc(low_ready, 1)
                        n_low += 1
                        dve.wait_ge(exp_ready, n_low)
                        nc.vector.scalar_tensor_tensor(out, ring[n % 4][:, :], 0.0, low[:, (n_low - 1) % 2, :],
                                                       ALU.max, ALU.add).then_inc(dve_done, 1)
                    else:
                        nc.vector.tensor_scalar(out, ring[n % 4][:, :], float(post[1]), None,
                                                ALU.mult).then_inc(dve_done, 1)


def cross_attention_blocks(nc, m, heads, dh, d, ctx_T1, ctx_T2, ctx_tok, consts):
    nch = heads * dh // P
    hpc = P // dh
    scale = dh ** -0.5
    ctx, sb, ps, sem = scope(nc, m)
    with ctx:
        wq = sb("wq", [P, KD, heads * dh])
        wk = sb("wk", [P, heads, CA])
        wv1 = sb("wv1", [P, heads * dh])
        wv2 = sb("wv2", [CL, heads * dh])
        bq = sb("bq", [P, nch])
        qT = m.featT
        loads = [(wq[:, :, :], d["wq"])]
        if d["bq"] is not None:
            loads.append((bq[:, :], d["bq"]))
        feature_major_block(
            nc, m, [(qT, nch, wq, m.xnT, KD, ("bias", bq, scale) if d["bq"] is not None else ("linear", scale))],
            loads)

        cT1 = sb("ctx_T1", [P, 2, MPAD])
        cT2 = sb("ctx_T2", [CL, 2, MPAD])
        ctok = sb("ctx_tok", [P, 2, MT, CA])
        cb1 = sb("ctx_bf1", [P, MPAD], BF16)
        cb2 = sb("ctx_bf2", [CL, MPAD], BF16)
        q1 = sb("q1", [P, TOK])
        q2 = sb("q2", [CL, TOK])
        qb1 = sb("q_bf1", [P, TOK], BF16)
        qb2 = sb("q_bf2", [CL, TOK], BF16)
        e = sb("exp", [P, 2, TOK])
        pt1 = sb("pooled1", [P, TOK])
        pt2 = sb("pooled2", [CL, TOK])
        mx = sb("max_parts", [P, 8, 2])
        nmx = sb("neg_max", [P, 8])
        rsum = sb("rsum", [SEQ, heads])
        o = sb("o_tok", [SEQ, heads * dh])
        e64 = sb("sum_col", [CL, 1])
        ringA = ps("ringA", [P, 2, HALF])
        ringB = ps("ringB", [P, 2, HALF])
        acc1 = ps("acc1", [P, 2, HALF])
        acc2 = ps("acc2", [CL, 2, HALF])

        weights_in = sem("weights_in")
        ctx_in = [sem(f"ctx_in{u}") for u in range(2)]
        cast_done = sem("cast_done")
        qcast_done = sem("qcast_done")
        fullA, freeA = sem("fullA"), sem("freeA")
        fullB, freeB = sem("fullB"), sem("freeB")
        negmax_ready = sem("negmax_ready")
        e_used = sem("e_used")
        pooled_out = sem("pooled_out")
        NA = 1 + 8 + 1 + (MT + 1) // 2 + 1
        NB = 1 + 8 + MT // 2 + 2
        REST = KEYS - TOK
        with engines_block(nc, m) as block:

            @block.sync
            def _(sp):
                for buf, dram in ((wk[:, :, :], d["wk"]), (wv1[:, :], d["wv1"]), (wv2[:, :], d["wv2"]),
                                  (m.wo[:, 0:nch, :], d["wo"]), (m.bo[:, :], d["bo"]), (e64[:, :], consts["e64"])):
                    sp.dma_start(buf, dram).then_inc(weights_in, 16)
                with sp.Fori(0, BATCH // 2) as i:
                    for u in range(2):
                        b = i * 2 + u
                        sp.wait_ge(pooled_out, b * 2 + 2)
                        sp.dma_start(cT1[:, u, :], ctx_T1[bass.ds(b, 1)].rearrange("o p n -> p (o n)")).then_inc(ctx_in[u], 16)
                        sp.dma_start(cT2[:, u, :], ctx_T2[bass.ds(b, 1)].rearrange("o p n -> p (o n)")).then_inc(ctx_in[u], 16)
                        sp.dma_start(flat(ctok[:, u, :, :]), ctx_tok[bass.ds(b, 1)].rearrange("o p t n -> p (o t n)")).then_inc(ctx_in[u], 16)

            @block.gpsimd
            def _(pool):
                pool.sem_inc(negmax_ready, 1)
                pool.sem_inc(freeA, 1)
                pool.sem_inc(freeB, 1)
                with pool.Fori(0, BATCH // 2) as i:
                    for u in range(2):
                        b = i * 2 + u
                        pool.wait_ge(negmax_ready, b + 1)
                        pool.wait_ge(ctx_in[u], i * 48 + 48)
                        hold_waits(pool, m)
                        nc.gpsimd.tensor_copy(cb1[:, :], cT1[:, u, :]).then_inc(cast_done, 1)
                        nc.gpsimd.tensor_copy(cb2[:, :], cT2[:, u, :]).then_inc(cast_done, 1)
                        pool.wait_ge(freeA, b * NA + 2)
                        pool.wait_ge(freeB, b * NB + 2)
                        hold_waits(pool, m)
                        nc.gpsimd.tensor_copy(qb1[:, :], q1[:, :]).then_inc(qcast_done, 1)
                        nc.gpsimd.tensor_copy(qb2[:, :], q2[:, :]).then_inc(qcast_done, 1)

            @block.tensor
            def _(pe):
                pe.wait_ge(weights_in, 6 * 16)
                with pe.Fori(0, BATCH // 2) as i:
                    for u in range(2):
                        b = i * 2 + u
                        nA, nB = b * NA, b * NB

                        pe.wait_ge(freeA, nA + 1)
                        for h in range(heads):
                            src = qT[:, h // hpc, bass.ds(b * SEQ, SEQ)]
                            last = nc.tensor.matmul(ringA[:, h // 8, (h % 8) * SEQ:(h % 8 + 1) * SEQ],
                                                    wk[:, h, 0:P], src, start=True, stop=True)
                        last.then_inc(fullA, 1)
                        pe.wait_ge(freeB, nB + 1)
                        for h in range(heads):
                            src = qT[:, h // hpc, bass.ds(b * SEQ, SEQ)]
                            last = nc.tensor.matmul(ringB[0:CL, h // 8, (h % 8) * SEQ:(h % 8 + 1) * SEQ],
                                                    wk[:, h, P:CA], src, start=True, stop=True)
                        last.then_inc(fullB, 1)

                        pe.wait_ge(cast_done, b * 2 + 2)
                        pe.wait_ge(qcast_done, b * 2 + 2)
                        for j in range(8):
                            pe.wait_ge(freeA, nA + j + 2)
                            for h in range(2):
                                for q, c, s in ((qb1, cb1, True), (qb2, cb2, False)):
                                    last = nc.tensor.matmul(ringA[:, h, :], q[:, j * P:(j + 1) * P],
                                                            c[:, h * HALF:(h + 1) * HALF], start=s, stop=not s)
                            last.then_inc(fullA, 1)
                            pe.wait_ge(freeB, nB + j + 2)
                            for h, a, z in ((0, TOK, TOK + HALF), (1, TOK + HALF, KEYS)):
                                for q, c, s in ((qb1, cb1, True), (qb2, cb2, False)):
                                    last = nc.tensor.matmul(ringB[:, h, 0:z - a], q[:, j * P:(j + 1) * P],
                                                            c[:, a:z], start=s, stop=not s)
                            last.then_inc(fullB, 1)

                        pe.wait_ge(negmax_ready, b + 2)
                        pe.wait_ge(freeA, nA + 10)
                        for j in range(8):
                            last = nc.tensor.matmul(flat(ringA[0:1, :, :])[:, j * P:(j + 1) * P],
                                                    nmx[:, j:j + 1], m.ident[:, :], start=True, stop=True)
                        last.then_inc(fullA, 1)

                        def scores(t):
                            ring = ringA if t % 2 == 0 else ringB
                            if t % 2 == 0:
                                pe.wait_ge(freeA, nA + 11 + t // 2)
                            else:
                                pe.wait_ge(freeB, nB + 10 + t // 2)
                            for h in range(2):
                                nc.tensor.matmul(ring[:, h, :], cT1[:, u, t * P:(t + 1) * P],
                                                 q1[:, h * HALF:(h + 1) * HALF], start=True, stop=False)
                                last = nc.tensor.matmul(ring[:, h, :], cT2[:, u, t * P:(t + 1) * P],
                                                        q2[:, h * HALF:(h + 1) * HALF], start=False, stop=True)
                            last.then_inc(fullA if t % 2 == 0 else fullB, 1)

                        def pool_tile(t):
                            if t % 2 == 0:
                                pe.wait_ge(freeA, nA + 12 + t // 2)
                            else:
                                pe.wait_ge(freeB, nB + 11 + t // 2)
                            if t == 0:
                                pe.wait_ge(pooled_out, b * 2 + 4)
                            for h in range(2):
                                nc.tensor.matmul(acc1[:, h, :], ctok[:, u, t, 0:P], e[:, t % 2, h * HALF:(h + 1) * HALF],
                                                 start=(t == 0), stop=(t == MT - 1))
                                last = nc.tensor.matmul(acc2[:, h, :], ctok[:, u, t, P:CA],
                                                        e[:, t % 2, h * HALF:(h + 1) * HALF],
                                                        start=(t == 0), stop=(t == MT - 1))
                            last.then_inc(e_used, 1)

                        scores(0)
                        for t in range(1, MT):
                            scores(t)
                            pool_tile(t - 1)
                        pool_tile(MT - 1)

                        pe.wait_ge(pooled_out, b * 2 + 6)
                        pe.wait_ge(freeA, nA + NA)
                        for h in range(heads):
                            col = h * dh
                            dst = flat(ringA[0:SEQ, :, :])[:, col:col + dh]
                            nc.tensor.matmul(dst, pt1[:, h * SEQ:(h + 1) * SEQ], wv1[:, col:col + dh], start=True, stop=False)
                            last = nc.tensor.matmul(dst, pt2[:, h * SEQ:(h + 1) * SEQ], wv2[:, col:col + dh],
                                                    start=False, stop=True)
                        last.then_inc(fullA, 1)
                        pe.wait_ge(freeB, nB + NB - 1)
                        for h in range(heads):
                            last = nc.tensor.matmul(ringB[0:SEQ, 0, h:h + 1], pt2[:, h * SEQ:(h + 1) * SEQ], e64[:, :],
                                                    start=True, stop=True)
                        last.then_inc(fullB, 1)
                        pe.wait_ge(freeA, nA + NA + 1)
                        pe.wait_ge(freeB, nB + NB)
                        hold_waits(pe, m)
                        for c in range(nch):
                            last = nc.tensor.transpose(ringB[:, 1, c * SEQ:(c + 1) * SEQ], o[:, c * P:(c + 1) * P],
                                                       m.ident[0:SEQ, 0:SEQ])
                        last.then_inc(fullB, 1)

            @block.scalar
            def _(act):
                act.sem_inc(e_used, 2)
                act.sem_inc(pooled_out, 4)
                with act.Fori(0, BATCH // 2) as i:
                    for u in range(2):
                        b = i * 2 + u
                        nA, nB = b * NA, b * NB
                        act.wait_ge(fullA, nA + 1)
                        nc.scalar.copy(q1[:, :], flat(ringA[:, :, :])).then_inc(freeA, 1)
                        for t in range(MT):
                            act.wait_ge(e_used, b * MT + (t + 1 if t else 2))
                            if t % 2 == 0:
                                act.wait_ge(fullA, nA + 11 + t // 2)
                            else:
                                act.wait_ge(fullB, nB + 10 + t // 2)
                            nc.scalar.activation(e[:, t % 2, :], flat((ringA if t % 2 == 0 else ringB)[:, :, :]),
                                                 ACT.Exp).then_inc(freeA if t % 2 == 0 else freeB, 1)
                        act.wait_ge(e_used, b * MT + MT + 2)
                        nc.scalar.copy(pt1[:, :], flat(acc1[:, :, :])).then_inc(pooled_out, 1)
                        act.wait_ge(fullB, nB + NB)
                        nc.scalar.copy(m.featT[:, 0:nch, bass.ds(b * SEQ, SEQ)],
                                       ringB[:, 1, 0:nch * SEQ].rearrange("p (c n) -> p c n", c=nch)).then_inc(freeB, 1)

            @block.vector
            def _(dve):
                with dve.Fori(0, BATCH // 2) as i:
                    for u in range(2):
                        b = i * 2 + u
                        nA, nB = b * NA, b * NB
                        dve.wait_ge(fullB, nB + 1)
                        nc.vector.tensor_copy(q2[:, :], flat(ringB[0:CL, :, :])).then_inc(freeB, 1)
                        for j in range(8):
                            dve.wait_ge(fullA, nA + j + 2)
                            nc.vector.tensor_reduce(mx[:, j, 0:1], flat(ringA[:, :, :]), AX.X, ALU.max).then_inc(freeA, 1)
                            dve.wait_ge(fullB, nB + j + 2)
                            ins = nc.vector.tensor_reduce(mx[:, j, 1:2], flat(ringB[:, :, :])[:, 0:REST], AX.X, ALU.max)
                            ins.then_inc(freeB, 1)
                        dve.wait_ge(freeB, nB + 10)
                        dve.wait_ge(freeA, nA + 10)
                        nc.vector.tensor_reduce(nmx[:, :], mx[:, :, :], AX.X, ALU.max, negate=True).then_inc(negmax_ready, 1)
                        dve.wait_ge(fullA, nA + 10)
                        ins = nc.vector.tensor_tensor(q2[CL - 1:CL, :], q2[CL - 1:CL, :], flat(ringA[0:1, :, :]), ALU.add)
                        ins.then_inc(freeA, 1)
                        dve.wait_ge(e_used, b * MT + MT + 2)
                        nc.vector.tensor_copy(pt2[:, :], flat(acc2[:, :, :])).then_inc(pooled_out, 1)
                        dve.wait_ge(fullB, nB + NB - 1)
                        ins = nc.vector.reciprocal(rsum[:, :], ringB[0:SEQ, 0, 0:heads])
                        ins.then_inc(freeB, 1)
                        dve.wait_ge(freeB, nB + NB)
                        dve.wait_ge(fullA, nA + NA)
                        ins = nc.vector.tensor_tensor(
                            o[:, :].rearrange("p (h d) -> p h d", h=heads),
                            flat(ringA[0:SEQ, :, :])[:, 0:heads * dh].rearrange("p (h d) -> p h d", h=heads),
                            rsum[:, :].unsqueeze(2).to_broadcast([SEQ, heads, dh]), ALU.mult)
                        ins.then_inc(freeA, 1)


def token_major_block(nc, m, jobs, loads):
    ctx, sb, ps, sem = scope(nc, m)
    with ctx:
        ring = [ps(f"ring{i}", [P, HALF]) for i in range(4)]
        loaded = sem("loaded")
        filled = sem("filled")
        act_done = sem("act_done")
        dve_done = sem("dve_done")
        pieces = [(j, t) for t in range(TT) for j in range(len(jobs))]
        with engines_block(nc, m) as block:

            @block.sync
            def _(sp):
                for buf, dram in loads:
                    sp.dma_start(buf, dram).then_inc(loaded, 16)

            @block.tensor
            def _(pe):
                if loads:
                    pe.wait_ge(loaded, 16 * len(loads))
                for n, (j, t) in enumerate(pieces):
                    dst, w, src, kc, bias = jobs[j]
                    cols = dst.shape[-1]
                    if n >= 4:
                        pe.wait_ge(act_done if n % 2 == 0 else dve_done, (n - 4) // 2 + 1)
                    for k in range(kc):
                        last = nc.tensor.matmul(ring[n % 4][:, 0:cols], src[:, k, t * P:(t + 1) * P], w[:, k, :],
                                                start=(k == 0), stop=(k == kc - 1 and bias is None))
                    if bias is not None:
                        last = nc.tensor.matmul(ring[n % 4][:, 0:cols], m.ones[0:1, :], bias, start=False, stop=True)
                    last.then_inc(filled, 1)

            @block.scalar
            def _(act):
                for n, (j, t) in enumerate(pieces):
                    if n % 2 == 0:
                        dst = jobs[j][0]
                        act.wait_ge(filled, n + 1)
                        nc.scalar.copy(dst[:, t, :], ring[n % 4][:, 0:dst.shape[-1]]).then_inc(act_done, 1)

            @block.vector
            def _(dve):
                for n, (j, t) in enumerate(pieces):
                    if n % 2 == 1:
                        dst = jobs[j][0]
                        dve.wait_ge(filled, n + 1)
                        nc.vector.tensor_copy(dst[:, t, :], ring[n % 4][:, 0:dst.shape[-1]]).then_inc(dve_done, 1)


def self_attention_block(nc, m, heads, dh, qT, kT, v, loads, mask_dram, causal_dram=None, o_out=None):
    nch = heads * dh // P
    hpc = P // dh
    W = heads * SEQ
    ctx, sb, ps, sem = scope(nc, m)
    with ctx:
        own = sb("own_head", [P, hpc, SEQ])
        qs = sb("q_now", [P, nch, P])
        kz = sb("k_by_head", [P, 2, nch, hpc * SEQ])
        vz = sb("v_by_head", [P, 2, heads // 2, 2 * dh])
        ex = sb("weights", [P, heads, SEQ])
        exT = sb("weights_T", [P, heads // 2, P])
        o = sb("o_now", [P, heads, dh])
        mx = sb("row_max", [P, heads])
        rs = sb("row_sum", [P, heads])
        tri = sb("causal", [P, SEQ]) if causal_dram is not None else None
        s_ps = ps("scores", [P, W])
        t_ps = ps("weights_T_ps", [P, W])
        o_ps = ps("o_ps", [P, heads * dh])
        ot_ps = ps("oT_ps", [P, nch, P]) if o_out is None else None
        loaded = sem("loaded")
        zeroed = sem("zeroed")
        qk_ready = sem("qk_ready")
        v_ready = sem("v_ready")
        scored = sem("scored")
        shifted = sem("shifted")
        exped = sem("exped")
        transposed = sem("transposed")
        exT_ready = sem("exT_ready")
        weighed = sem("weighed")
        o_ready = sem("o_ready")
        o_transposed = sem("o_transposed")
        o_out_done = sem("o_out_done")
        vec = sem("vec")
        n_loads = len(loads) + 1 + (causal_dram is not None)
        VSTEPS = 3
        with engines_block(nc, m) as block:

            @block.sync
            def _(sp):
                sp.dma_start(own[:, :, :], mask_dram).then_inc(loaded, 16)
                if causal_dram is not None:
                    sp.dma_start(tri[:, :], causal_dram).then_inc(loaded, 16)
                for buf, dram in loads:
                    sp.dma_start(buf, dram).then_inc(loaded, 16)

            @block.gpsimd
            def _(pool):
                pool.sem_inc(scored, 1)
                pool.sem_inc(weighed, 1)
                pool.wait_ge(loaded, 16 * n_loads)
                nc.gpsimd.memset(vz[:, :, :, :], 0.0).then_inc(zeroed, 1)
                with pool.Fori(0, TT) as i:
                    pool.wait_ge(scored, i + 1)
                    for e in range(2):
                        for c in range(nch):
                            last = nc.gpsimd.tensor_tensor(
                                kz[:, e, c, :].rearrange("p (h n) -> p h n", h=hpc),
                                kT[:, c, bass.ds(i * P + e * SEQ, SEQ)].unsqueeze(1).to_broadcast([P, hpc, SEQ]),
                                own[:, :, :], ALU.mult)
                            if e == 1 and c == nch - 1:
                                last.then_inc(qk_ready, 1)

            @block.tensor
            def _(pe):
                with pe.Fori(0, TT) as i:
                    pe.wait_ge(qk_ready, i * 2 + 2)
                    pe.wait_ge(shifted, i + 1)
                    for e in range(2):
                        for c in range(nch):
                            last = nc.tensor.matmul(s_ps[e * SEQ:(e + 1) * SEQ, c * hpc * SEQ:(c + 1) * hpc * SEQ],
                                                    qs[:, c, e * SEQ:(e + 1) * SEQ], kz[:, e, c, :],
                                                    start=True, stop=True)
                    last.then_inc(scored, 1)
                    pe.wait_ge(exT_ready, i + 1)
                    if causal_dram is None:
                        pe.wait_ge(exped, i + 1)
                    else:
                        pe.wait_ge(shifted, i + 2)
                    for j in range(heads // 2):
                        last = nc.tensor.transpose(t_ps[:, j * P:(j + 1) * P],
                                                   ex[:, 2 * j:2 * j + 2, :].rearrange("p h n -> p (h n)"), m.ident[:, :])
                    last.then_inc(transposed, 1)
                    pe.wait_ge(v_ready, i + 1)
                    pe.wait_ge(o_ready, i + 1)
                    pe.wait_ge(exT_ready, i + 2)
                    hold_waits(pe, m)
                    for e in range(2):
                        for j in range(heads // 2):
                            last = nc.tensor.matmul(o_ps[e * SEQ:(e + 1) * SEQ, j * 2 * dh:(j + 1) * 2 * dh],
                                                    exT[:, j, e * SEQ:(e + 1) * SEQ], vz[:, e, j, :],
                                                    start=True, stop=True)
                    last.then_inc(weighed, 1)
                    if o_out is None:
                        pe.wait_ge(o_out_done, i + 1)
                        pe.wait_ge(o_ready, i + 2)
                        for c in range(nch):
                            last = nc.tensor.transpose(
                                ot_ps[:, c, :], o[:, c * hpc:(c + 1) * hpc, :].rearrange("p h d -> p (h d)"), m.ident[:, :])
                        last.then_inc(o_transposed, 1)

            @block.scalar
            def _(act):
                act.wait_ge(zeroed, 1)
                act.sem_inc(exT_ready, 1)
                act.sem_inc(o_out_done, 1)
                with act.Fori(0, TT) as i:
                    act.wait_ge(scored, i + 1)
                    nc.scalar.copy(qs[:, :, :], qT[:, 0:nch, bass.ds(i * P, P)]).then_inc(qk_ready, 1)
                    act.wait_ge(weighed, i + 1)
                    for e in range(2):
                        for par in range(2):
                            src = v[e * SEQ:(e + 1) * SEQ, bass.ds(i, 1), :].rearrange(
                                "p o (j two d) -> p (o j) two d", two=2, d=dh)[:, :, par, :]
                            last = nc.scalar.copy(
                                vz[par * SEQ:(par + 1) * SEQ, e, :, par * dh:(par + 1) * dh], src)
                            if e == 1 and par == 1:
                                last.then_inc(v_ready, 1)
                    if causal_dram is None:
                        act.wait_ge(shifted, i + 2)
                        nc.scalar.activation(ex[:, :, :], ex[:, :, :], ACT.Exp).then_inc(exped, 1)
                    act.wait_ge(transposed, i + 1)
                    act.wait_ge(weighed, i + 1)
                    nc.scalar.copy(flat(exT[:, :, :]), t_ps[:, :]).then_inc(exT_ready, 1)
                    if o_out is None:
                        act.wait_ge(o_transposed, i + 1)
                        nc.scalar.copy(m.featT[:, 0:nch, bass.ds(i * P, P)], ot_ps[:, :, :]).then_inc(o_out_done, 1)

            @block.vector
            def _(dve):
                dve.sem_inc(shifted, 1)
                dve.sem_inc(o_ready, 1)
                if causal_dram is not None:
                    dve.wait_ge(loaded, 16 * n_loads)
                s3 = s_ps[:, :].rearrange("p (h n) -> p h n", h=heads)
                with dve.Fori(0, TT) as i:
                    chain = Chain(dve, vec, i * VSTEPS, VSTEPS)
                    dve.wait_ge(scored, i + 2)
                    if causal_dram is None:
                        chain.step(nc.vector.tensor_reduce(mx[:, :], s3, AX.X, ALU.max))
                        dve.wait_ge(weighed, i + 1)
                        nc.vector.tensor_tensor(ex[:, :, :], s3, mx[:, :].unsqueeze(2).to_broadcast([P, heads, SEQ]),
                                                ALU.subtract).then_inc(shifted, 1)
                        dve.wait_ge(exped, i + 1)
                        chain.step(nc.vector.tensor_reduce(rs[:, :], ex[:, :, :], AX.X, ALU.add))
                    else:
                        dve.wait_ge(weighed, i + 1)
                        nc.vector.tensor_tensor(ex[:, :, :], s3, tri[:, :].unsqueeze(1).to_broadcast([P, heads, SEQ]),
                                                ALU.mult).then_inc(shifted, 1)
                        dve.wait_ge(shifted, i + 2)
                        chain.step(nc.vector.tensor_reduce(mx[:, :], ex[:, :, :], AX.X, ALU.add))
                        chain.step(nc.vector.tensor_scalar(rs[:, :], mx[:, :], CLIP, None, ALU.max))
                    chain.step(nc.vector.reciprocal(rs[:, :], rs[:, :]))
                    chain.close()
                    dve.wait_ge(weighed, i + 2)
                    if o_out is None:
                        dve.wait_ge(o_out_done, i + 1)
                        dst = o[:, :, :]
                    else:
                        dst = o_out[:, bass.ds(i, 1), :].rearrange("p o (h d) -> p (o h) d", h=heads)
                    nc.vector.tensor_tensor(dst, o_ps[:, :].rearrange("p (h d) -> p h d", h=heads),
                                            rs[:, :].unsqueeze(2).to_broadcast([P, heads, dh]), ALU.mult).then_inc(o_ready, 1)


def qkv_memory(nc, m, nch, cols):
    ctx, sb, ps, sem = scope(nc, m)
    return ctx, sb, sb("qT", [P, nch, TOK]), sb("kT", [P, nch, TOK]), sb("v", [P, TT, cols])


def latent_attention_layer(nc, m, t):
    ctx, sb, qT, kT, v = qkv_memory(nc, m, KD, D)
    with ctx:
        wq, wqs, wd = (sb(n, [P, KD, c]) for n, c in (("wq", D), ("wqs", D), ("wd", P)))
        wk, wks, wv = (sb(n, [P, 1, D]) for n in ("wk", "wks", "wv"))
        qsT, ksT = sb("qsT", [P, KD, TOK]), sb("ksT", [P, KD, TOK])
        lat = sb("lat", [P, 1, TOK])
        cos, sin = sb("cos", [P, SEQ]), sb("sin", [P, SEQ])
        scale = 0.25
        feature_major_block(
            nc, m,
            [(qT, KD, wq, m.xnT, KD, ("linear", scale)), (qsT, KD, wqs, m.xnT, KD, ("linear", scale)),
             (lat, 1, wd, m.xnT, KD, ("linear", 1.0)), (kT, KD, wk, lat, 1, ("linear", 1.0)),
             (ksT, KD, wks, lat, 1, ("linear", 1.0))],
            [(wq[:, :, :], t["b_wq"]), (wqs[:, :, :], t["b_wqs"]), (wd[:, :, :], t["b_wd"]), (wk[:, :, :], t["b_wk"]),
             (wks[:, :, :], t["b_wks"]), (wv[:, :, :], t["b_wv"]), (cos[:, :], t["rope_cos"]), (sin[:, :], t["rope_sin"])])
        rotate_block(nc, m, qT, qsT, kT, ksT, cos, sin)
        token_major_block(nc, m, [(v, wv, lat, 1, None)], [])
        self_attention_block(nc, m, 16, 16, qT, kT, v, [(m.wo[:, 0:KD, :], t["b_wo"])], t["own16"])


def rotate_block(nc, m, qT, qsT, kT, ksT, cos, sin):
    ctx, sb, ps, sem = scope(nc, m)

    def rows(x, c):
        return x[:, c, :].rearrange("p (b n) -> p b n", b=BATCH)

    def table(x):
        return x[:, :].unsqueeze(1).to_broadcast([P, BATCH, SEQ])

    with ctx:
        q_steps, k_steps = sem("q_steps"), sem("k_steps")
        with engines_block(nc, m) as block:

            @block.vector
            def _(dve):
                chain = Chain(dve, q_steps)
                for c in range(KD):
                    nc.vector.tensor_tensor(rows(qT, c), rows(qT, c), table(cos), ALU.mult).then_inc(q_steps, 1)
                    chain.n += 1
                    chain.step(nc.vector.tensor_tensor(rows(qsT, c), rows(qsT, c), table(sin), ALU.mult))
                    chain.step(nc.vector.tensor_tensor(qT[:, c, :], qT[:, c, :], qsT[:, c, :], ALU.add))

            @block.gpsimd
            def _(pool):
                chain = Chain(pool, k_steps)
                for c in range(KD):
                    nc.gpsimd.tensor_tensor(rows(kT, c), rows(kT, c), table(cos), ALU.mult).then_inc(k_steps, 1)
                    chain.n += 1
                    chain.step(nc.gpsimd.tensor_tensor(rows(ksT, c), rows(ksT, c), table(sin), ALU.mult))
                    chain.step(nc.gpsimd.tensor_tensor(kT[:, c, :], kT[:, c, :], ksT[:, c, :], ALU.add))


def biased_attention_layer(nc, m, t):
    ctx, sb, qT, kT, v = qkv_memory(nc, m, KD, D)
    with ctx:
        wq, wk, wv = (sb(n, [P, KD, D]) for n in ("wq", "wk", "wv"))
        bq, bk, bv = sb("bq", [P, KD]), sb("bk", [P, KD]), sb("bv", [1, D])
        feature_major_block(
            nc, m, [(qT, KD, wq, m.xnT, KD, ("bias", bq, 0.25)), (kT, KD, wk, m.xnT, KD, ("bias", bk, 1.0))],
            [(wq[:, :, :], t["e_wq"]), (wk[:, :, :], t["e_wk"]), (wv[:, :, :], t["e_wv"]), (bq[:, :], t["e_bq"]),
             (bk[:, :], t["e_bk"]), (bv[:, :], t["e_bv"]), (m.bo[:, :], t["e_bo"])])
        token_major_block(nc, m, [(v, wv, m.xnT, KD, bv[0:1, :])], [])
        self_attention_block(nc, m, 16, 16, qT, kT, v, [(m.wo[:, 0:KD, :], t["e_wo"])], t["own16"])


def linear_attention_layer(nc, m, t):
    ctx, sb, qT, kT, v = qkv_memory(nc, m, KD, D)
    with ctx:
        wq, wk, wv = (sb(n, [P, KD, D]) for n in ("wq", "wk", "wv"))
        feature_major_block(
            nc, m, [(qT, KD, wq, m.xnT, KD, ("elu1",)), (kT, KD, wk, m.xnT, KD, ("elu1",))],
            [(wq[:, :, :], t["h_wq"]), (wk[:, :, :], t["h_wk"]), (wv[:, :, :], t["h_wv"])])
        token_major_block(nc, m, [(v, wv, m.xnT, KD, None)], [])
        self_attention_block(nc, m, 16, 16, qT, kT, v, [(m.wo[:, 0:KD, :], t["h_wo"])], t["own16"], t["causal"])

FAR = 3.0e38


def top2_steps(nc, chain, logits, rev, masks, tmp, eq, mx):
    _, groups, n = logits.shape

    def spread(x):
        return x[:, :].unsqueeze(2).to_broadcast([P, groups, n])

    ranks = rev[:, :].unsqueeze(1).to_broadcast([P, groups, n])
    for k, (src, out) in enumerate(((logits, masks), (tmp, eq))):
        chain.step(nc.vector.tensor_reduce(mx[:, :], src, AX.X, ALU.max))
        chain.step(nc.vector.tensor_tensor(eq, src, spread(mx), ALU.is_equal))
        chain.step(nc.vector.tensor_tensor(eq, eq, ranks, ALU.mult))
        chain.step(nc.vector.tensor_reduce(mx[:, :], eq, AX.X, ALU.max))
        chain.step(nc.vector.tensor_tensor(out, eq, spread(mx), ALU.is_equal))
        if k == 0:
            chain.step(nc.vector.scalar_tensor_tensor(tmp, out, -FAR, logits, ALU.mult, ALU.add))
    chain.step(nc.vector.tensor_tensor(masks, masks, eq, ALU.add))


def switch_head_layer(nc, m, t):
    H, DH, E = 8, 64, 5
    NX = E * DH
    NG = H * E
    with ExitStack() as whole:
        def big(name, shape):
            return whole.enter_context(nc.sbuf_tensor(name, shape, F32))

        qT, kT = big("c_qT", [P, 4, TOK]), big("c_kT", [P, 4, TOK])
        v = big("c_v", [P, TT, H * DH])
        xvg = big("c_xvg", [P, TT, NX + 2 * NG])
        mask = big("c_mask", [P, TT * 2 * H, E])
        o = big("c_o", [P, TT, H * DH])
        rev = big("c_rev", [P, E])
        wv = big("c_wv", [P, TT, NG])
        ctx, sb, ps, sem = scope(nc, m)
        with ctx:
            wq, wk = sb("wq", [P, KD, H * DH]), sb("wk", [P, KD, H * DH])
            wx = sb("wx", [P, KD, NX + 2 * NG])
            feature_major_block(
                nc, m, [(qT, 4, wq, m.xnT, KD, ("linear", DH ** -0.5)), (kT, 4, wk, m.xnT, KD, ("linear", 1.0))],
                [(wq[:, :, :], t["c_wq"]), (wk[:, :, :], t["c_wk"]), (wx[:, :, :], t["c_wx"]), (rev[:, :], t["rev5"])])
            token_major_block(nc, m, [(xvg, wx, m.xnT, KD, None)], [])
        switch_gates_block(nc, m, xvg, mask, wv, rev, H, E, NX)
        switch_mix_block(nc, m, H, DH, E, "values",
                         lambda i: xvg[:, bass.ds(i, 1), 0:NX].rearrange("p o (e d) -> p (o e) d", e=E)
                         .unsqueeze(2).to_broadcast([P, E, H, DH]),
                         lambda i: wv[:, bass.ds(i, 1), :].rearrange("p o (h e) -> p (o e) h", e=E)
                         .unsqueeze(3).to_broadcast([P, E, H, DH]),
                         "p e h d -> p (h d) e", v)
        self_attention_block(nc, m, H, DH, qT, kT, v, [(m.wo[:, 0:3, :], t["c_wo"])], t["own64"], None, o)
        ctx, sb, ps, sem = scope(nc, m)
        with ctx:
            a = sb("by_expert", [P, TT, NX])
            switch_mix_block(nc, m, H, DH, E, "outputs",
                             lambda i: o[:, bass.ds(i, 1), :].rearrange("p o (h d) -> p o h d", h=H)
                             .to_broadcast([P, E, H, DH]),
                             lambda i: mask[:, bass.ds(i * (2 * H) + H, H), :].rearrange("p h e -> p e h")
                             .unsqueeze(3).to_broadcast([P, E, H, DH]),
                             "p e h d -> p e d h", a)
            to_features_block(nc, m, a, NX)


def switch_gates_block(nc, m, xvg, mask, wv, rev, H, E, NX):
    G = TT * 2 * H
    ctx, sb, ps, sem = scope(nc, m)
    with ctx:
        logits, tmp, eq = (sb(n, [P, G, E]) for n in ("logits", "tmp", "eq"))
        mx = sb("mx", [P, G])
        gathered, gated = sem("gathered"), sem("gated")
        vec = sem("vec")
        gates = xvg[:, :, NX:NX + 2 * H * E]
        with engines_block(nc, m) as block:

            @block.scalar
            def _(act):
                nc.scalar.copy(logits[:, :, :].rearrange("p (t g) e -> p t (g e)", t=TT), gates).then_inc(gathered, 1)
                nc.scalar.activation(wv[:, :, :], gates[:, :, 0:H * E], ACT.Sigmoid).then_inc(gated, 1)

            @block.vector
            def _(dve):
                dve.wait_ge(gathered, 1)
                chain = Chain(dve, vec)
                top2_steps(nc, chain, logits[:, :, :], rev, mask[:, :, :], tmp[:, :, :], eq[:, :, :], mx)
                dve.wait_ge(gated, 1)
                nc.vector.tensor_tensor(wv[:, :, :], wv[:, :, :],
                                        mask[:, :, :].rearrange("p (t g) e -> p t (g e)", t=TT)[:, :, 0:H * E], ALU.mult)


def switch_mix_block(nc, m, H, DH, E, what, left, right, order, dst):
    ctx, sb, ps, sem = scope(nc, m)
    with ctx:
        prod = sb("prod", [P, 2, E, H, DH])
        multiplied, summed = sem("multiplied"), sem("summed")
        with engines_block(nc, m) as block:

            @block.gpsimd
            def _(pool):
                pool.sem_inc(summed, 2)
                with pool.Fori(0, TT // 2) as i:
                    for u in range(2):
                        n = i * 2 + u
                        pool.wait_ge(summed, n + 1)
                        hold_waits(pool, m)
                        for e in range(E):
                            last = nc.gpsimd.tensor_tensor(prod[:, u, e, :, :], left(n)[:, e], right(n)[:, e], ALU.mult)
                        last.then_inc(multiplied, 1)

            @block.vector
            def _(dve):
                with dve.Fori(0, TT // 2) as i:
                    for u in range(2):
                        n = i * 2 + u
                        dve.wait_ge(multiplied, n + 1)
                        src = prod[:, u, :, :, :].rearrange(order)
                        out = dst[:, bass.ds(n, 1), :]
                        if len(src.shape) == 4:
                            out = out.rearrange("p o (e d) -> p (o e) d", e=E)
                        else:
                            out = out.rearrange("p o n -> p (o n)")
                        nc.vector.tensor_reduce(out, src, AX.X, ALU.add).then_inc(summed, 1)


def to_features_block(nc, m, a, cols):
    chunks = -(-cols // P)
    ctx, sb, ps, sem = scope(nc, m)
    with ctx:
        tps = [ps(f"tps{i}", [P, chunks, P]) for i in range(2)]
        transposed, evacuated = sem("transposed"), sem("evacuated")
        with engines_block(nc, m) as block:

            @block.tensor
            def _(pe):
                for n in range(TT):
                    if n >= 2:
                        pe.wait_ge(evacuated, 2 * (n - 1))
                    for c in range(chunks):
                        k = min(P, cols - c * P)
                        last = nc.tensor.transpose(tps[n % 2][0:k, c, :], a[:, n, c * P:c * P + k], m.ident[:, :])
                    last.then_inc(transposed, 1)

            @block.scalar
            def _(act):
                for n in range(TT):
                    act.wait_ge(transposed, n + 1)
                    full = cols // P
                    nc.scalar.copy(m.featT[:, 0:full, n * P:(n + 1) * P], tps[n % 2][:, 0:full, :]).then_inc(evacuated, 1)
                    k = cols - full * P
                    nc.scalar.copy(m.featT[0:k, full, n * P:(n + 1) * P], tps[n % 2][0:k, full, :]).then_inc(evacuated, 1)


def mixture_of_depths_layer(nc, m, t, factor):
    CAP = SEQ // 2
    ctx, sb, ps, sem = scope(nc, m)
    with ctx:
        w1, b1 = sb("w1", [P, KD, 1024]), sb("b1", [P, 8])
        wr = sb("wr", [P, KD])
        before = sb("before", [P, SEQ])
        feature_major_block(
            nc, m, [(m.featT, 8, w1, m.xnT, KD, ("gelu", b1))],
            [(w1[:, :, :], t["f_w1"]), (b1[:, :], t["f_b1"]), (wr[:, :], t["f_wr"]), (before[:, :], t["before"]),
             (m.wo[:, :, :], t["f_w2"]), (m.bo[:, :], t["f_b2"])])
        row = sb("score_row", [1, TOK])
        col = sb("score_col", [P, TT])
        above, equal = sb("above", [P, TT, SEQ]), sb("equal", [P, TT, SEQ])
        rank = sb("rank", [P, TT])
        row_ps, all_ps, col_ps = ps("row_ps", [1, TOK]), ps("all_ps", [P, TOK]), ps("col_ps", [P, TT])
        row_done, row_ready, spread_done, col_ready, sig_ready = (
            sem(n) for n in ("row_done", "row_ready", "spread_done", "col_ready", "sig_ready"))
        vec = sem("vec")
        with engines_block(nc, m) as block:

            @block.tensor
            def _(pe):
                for h in range(2):
                    for k in range(KD):
                        last = nc.tensor.matmul(row_ps[0:1, h * HALF:(h + 1) * HALF], wr[:, k:k + 1],
                                                m.xnT[:, k, h * HALF:(h + 1) * HALF], start=(k == 0), stop=(k == KD - 1))
                last.then_inc(row_done, 1)
                pe.wait_ge(row_ready, 1)
                for h in range(2):
                    nc.tensor.matmul(all_ps[:, h * HALF:(h + 1) * HALF], m.ones[0:1, :], row[0:1, h * HALF:(h + 1) * HALF],
                                     start=True, stop=True)
                for n in range(TT):
                    last = nc.tensor.matmul(col_ps[:, n:n + 1], row[0:1, n * P:(n + 1) * P], m.ones[0:1, 0:1],
                                            start=True, stop=True)
                last.then_inc(spread_done, 1)

            @block.scalar
            def _(act):
                act.wait_ge(row_done, 1)
                nc.scalar.copy(row[:, :], row_ps[:, :]).then_inc(row_ready, 1)
                act.wait_ge(col_ready, 1)
                nc.scalar.activation(factor[:, :], col[:, :], ACT.Sigmoid).then_inc(sig_ready, 1)

            @block.vector
            def _(dve):
                chain = Chain(dve, vec)
                dve.wait_ge(spread_done, 1)
                nc.vector.tensor_copy(col[:, :], col_ps[:, :]).then_inc(col_ready, 1)
                dve.wait_ge(col_ready, 1)
                for op, dst in ((ALU.is_gt, above), (ALU.is_equal, equal)):
                    for e in range(2):
                        rows = slice(e * SEQ, (e + 1) * SEQ)
                        chain.step(nc.vector.tensor_tensor(
                            dst[rows, :, :], all_ps[rows, :].rearrange("p (t e n) -> p t e n", e=2, n=SEQ)[:, :, e, :],
                            col[rows, :].unsqueeze(2).to_broadcast([SEQ, TT, SEQ]), op))
                chain.step(nc.vector.tensor_tensor(equal[:, :, :], equal[:, :, :],
                                                   before[:, :].unsqueeze(1).to_broadcast([P, TT, SEQ]), ALU.mult))
                chain.step(nc.vector.tensor_tensor(above[:, :, :], above[:, :, :], equal[:, :, :], ALU.add))
                chain.step(nc.vector.tensor_reduce(rank[:, :], above[:, :, :], AX.X, ALU.add))
                dve.wait_ge(sig_ready, 1)
                nc.vector.scalar_tensor_tensor(factor[:, :], rank[:, :], float(CAP), factor[:, :], ALU.is_lt, ALU.mult)


def routing_block(nc, m, w_gate, loads, groups, n, weights, rev, bias=None, softmax=False, shared=False):
    G = TT * groups
    N = groups * n
    ctx, sb, ps, sem = scope(nc, m)
    with ctx:
        logits, tmp, eq, mask, val = (sb(x, [P, G, n]) for x in ("logits", "tmp", "eq", "mask", "val"))
        mx, sums = sb("mx", [P, G]), sb("sums", [P, G])
        lps = ps("lps", [P, TT, N])
        loaded, projected, logits_ready, shifted, valued = (
            sem(x) for x in ("loaded", "projected", "logits_ready", "shifted", "valued"))
        vec = sem("vec")

        def spread(x):
            return x[:, :].unsqueeze(2).to_broadcast([P, G, n])

        with engines_block(nc, m) as block:

            @block.sync
            def _(sp):
                for buf, dram in loads:
                    sp.dma_start(buf, dram).then_inc(loaded, 16)

            @block.tensor
            def _(pe):
                pe.wait_ge(loaded, 16 * len(loads))
                for i in range(TT):
                    for k in range(KD):
                        last = nc.tensor.matmul(lps[:, i, :], m.xnT[:, k, i * P:(i + 1) * P], w_gate[:, k, :],
                                                start=(k == 0), stop=(k == KD - 1 and bias is None))
                    if bias is not None:
                        last = nc.tensor.matmul(lps[:, i, :], m.ones[0:1, :], bias, start=False, stop=True)
                last.then_inc(projected, 1)

            @block.scalar
            def _(act):
                act.wait_ge(projected, 1)
                nc.scalar.copy(logits[:, :, :].rearrange("p g n -> p (g n)"), flat(lps[:, :, :])).then_inc(logits_ready, 1)
                if softmax:
                    act.wait_ge(shifted, 1)
                    nc.scalar.activation(val[:, :, :], val[:, :, :], ACT.Exp).then_inc(valued, 1)
                else:
                    act.wait_ge(logits_ready, 1)
                    nc.scalar.activation(val[:, :, :], logits[:, :, :], ACT.Sigmoid).then_inc(valued, 1)

            @block.vector
            def _(dve):
                chain = Chain(dve, vec)
                dve.wait_ge(logits_ready, 1)
                if loads:
                    dve.wait_ge(loaded, 16 * len(loads))
                if softmax:
                    chain.step(nc.vector.tensor_reduce(mx[:, :], logits[:, :, :], AX.X, ALU.max))
                    nc.vector.tensor_tensor(val[:, :, :], logits[:, :, :], spread(mx), ALU.subtract).then_inc(shifted, 1)
                    dve.wait_ge(shifted, 1)
                top2_steps(nc, chain, logits[:, :, :], rev, mask[:, :, :], tmp[:, :, :], eq[:, :, :], mx)
                dve.wait_ge(valued, 1)
                out = weights[:, :, 0:N].rearrange("p t (g n) -> p t g n", g=groups)
                if softmax:
                    chain.step(nc.vector.tensor_reduce(sums[:, :], val[:, :, :], AX.X, ALU.add))
                    chain.step(nc.vector.reciprocal(sums[:, :], sums[:, :]))
                    chain.step(nc.vector.tensor_tensor(val[:, :, :], val[:, :, :], spread(sums), ALU.mult))
                    chain.step(nc.vector.scalar_tensor_tensor(val[:, :, :], val[:, :, :], 0.5, mask[:, :, :], ALU.mult, ALU.mult))
                else:
                    chain.step(nc.vector.tensor_tensor(val[:, :, :], val[:, :, :], mask[:, :, :], ALU.mult))
                    chain.step(nc.vector.tensor_reduce(sums[:, :], val[:, :, :], AX.X, ALU.add))
                    chain.step(nc.vector.reciprocal(sums[:, :], sums[:, :]))
                    chain.step(nc.vector.tensor_tensor(val[:, :, :], val[:, :, :], spread(sums), ALU.mult))
                chain.step(nc.vector.tensor_copy(out, val[:, :, :].rearrange("p (t g) n -> p t g n", t=TT)))
                if shared:
                    nc.vector.memset(weights[:, :, N:N + 1], 1.0)


def experts_block(nc, m, n_experts, packed, weights, add_xn):
    I = P
    ctx, sb, ps, sem = scope(nc, m)
    with ctx:
        w = sb("w", [P, 2, 6 * P])
        act_g = sb("silu", [P, 2, HALF])
        hT = sb("hT", [P, 2, HALF])
        g_ps, u_ps = ps("g_ps", [P, 2, HALF]), ps("u_ps", [P, 2, HALF])
        y_ps = [ps(f"y{i}", [P, HALF]) for i in range(4)]
        w_in = [sem(f"w_in{u}") for u in range(2)]
        gu_done = sem("gu_done")
        silu_done = sem("silu_done")
        h_ready = sem("h_ready")
        y_done = sem("y_done")
        y_added = sem("y_added")
        xn_added = sem("xn_added")

        def sync_turn(sp, e, i, u):
            sp.wait_ge(y_done, e * TT + 8)
            sp.dma_start(w[:, u, :], packed[bass.ds(e, 1)].rearrange("o p n -> p (o n)")).then_inc(w_in[u], 16)

        def pe_turn(pe, e, i, u):
            pe.wait_ge(w_in[u], i * 16 + 16)
            for h in range(2):
                pe.wait_ge(h_ready, e * 2 + h + 1)
                for dst, col in ((g_ps, 0), (u_ps, 2 * P)):
                    for k in range(KD):
                        last = nc.tensor.matmul(dst[:, h, :], w[:, u, col + k * P:col + (k + 1) * P],
                                                m.xnT[:, k, h * HALF:(h + 1) * HALF], start=(k == 0), stop=(k == KD - 1))
                last.then_inc(gu_done, 1)
            for n in range(TT):
                h = n // 4
                if n % 4 == 0:
                    pe.wait_ge(h_ready, e * 2 + h + 3)
                pe.wait_ge(y_added, e * TT + n + 1)
                nc.tensor.matmul(y_ps[n % 4][:, 0:D], hT[:, h, (n % 4) * P:(n % 4 + 1) * P], w[:, u, 4 * P:6 * P],
                                 start=True, stop=True).then_inc(y_done, 1)

        def act_turn(act, e, i, u):
            for h in range(2):
                act.wait_ge(gu_done, e * 2 + h + 1)
                act.wait_ge(h_ready, e * 2 + h + 1)
                nc.scalar.activation(act_g[:, h, :], g_ps[:, h, :], ACT.Silu).then_inc(silu_done, 1)

        def dve_turn(dve, e, i, u):
            for h in range(2):
                dve.wait_ge(silu_done, e * 2 + h + 1)
                dve.wait_ge(y_done, e * TT + 4 * h + 12)
                nc.vector.tensor_tensor(hT[:, h, :], act_g[:, h, :], u_ps[:, h, :], ALU.mult).then_inc(h_ready, 1)
            for n in range(TT):
                dve.wait_ge(y_done, e * TT + n + 17)
                dve.wait_ge(y_added, e * TT + n + 1)
                nc.vector.scalar_tensor_tensor(m.x[:, n, :], y_ps[n % 4][:, 0:D],
                                               weights[:, n, bass.ds(e, 1)], m.x[:, n, :],
                                               ALU.mult, ALU.add).then_inc(y_added, 1)

        def turns(eng, body):
            with eng.Fori(0, n_experts // 2) as i:
                for u in range(2):
                    body(eng, i * 2 + u, i, u)
            if n_experts % 2:
                body(eng, n_experts - 1, n_experts // 2, 0)

        with engines_block(nc, m) as block:

            @block.sync
            def _(sp):
                sp.sem_inc(y_done, 16)
                turns(sp, sync_turn)

            @block.tensor
            def _(pe):
                turns(pe, pe_turn)

            @block.scalar
            def _(act):
                turns(act, act_turn)

            @block.vector
            def _(dve):
                dve.sem_inc(h_ready, 2)
                dve.sem_inc(y_added, 4)
                if add_xn:
                    nc.vector.tensor_tensor(flat(m.x[:, :, :]), flat(m.x[:, :, :]), flat(m.xn[:, :, :]),
                                            ALU.add).then_inc(xn_added, 1)
                    dve.wait_ge(xn_added, 1)
                turns(dve, dve_turn)


TWO_PI = 2.0 * np.pi
TWO_PI_HI = 6.28125
TWO_PI_LO = TWO_PI - TWO_PI_HI
ROUND = 1.5 * 2.0 ** 23
N2 = 32


def state_space_kernel_block(nc, m, t, kern):
    ctx, sb, ps, sem = scope(nc, m)
    with ctx:
        S = [P, KD, N2]
        ldt, dt = sb("ldt", [P, KD]), sb("dt", [P, KD])
        are, aim, cre, cim = (sb(x, S) for x in ("are", "aim", "cre", "cim"))
        a, th, em1, ang, turns_, sb1, sb2 = (sb(x, S) for x in ("a", "th", "em1", "ang", "turns", "sin1", "sin2"))
        zr, zi, wr, u, v, w, qr, qi = (sb(x, S) for x in ("zr", "zi", "wr", "u", "v", "w", "qr", "qi"))
        Vr, Vi = sb("Vr", [P, KD, SEQ, N2]), sb("Vi", [P, KD, SEQ, N2])
        t1, t2 = sb("t1", [P, KD, SEQ // 2, N2]), sb("t2", [P, KD, SEQ // 2, N2])
        loaded, exp_ready, small_ready, tanh_ready, ang_ready, sin_ready = (
            sem(x) for x in ("loaded", "exp_ready", "small_ready", "tanh_ready", "ang_ready", "sin_ready"))
        vec = sem("vec")
        with engines_block(nc, m) as block:

            @block.sync
            def _(sp):
                for buf, x in ((ldt, "k_ldt"), (are, "k_lar"), (aim, "k_aim"), (cre, "k_cre"), (cim, "k_cim")):
                    dst = buf[:, :] if x == "k_ldt" else buf[:, :, :]
                    sp.dma_start(dst, t[x]).then_inc(loaded, 16)

            @block.scalar
            def _(act):
                act.wait_ge(loaded, 5 * 16)
                nc.scalar.activation(dt[:, :], ldt[:, :], ACT.Exp).then_inc(exp_ready, 1)
                nc.scalar.activation(are[:, :, :], are[:, :, :], ACT.Exp).then_inc(exp_ready, 1)
                act.wait_ge(small_ready, 1)
                nc.scalar.activation(th[:, :, :], a[:, :, :], ACT.Tanh, scale=0.5).then_inc(tanh_ready, 1)
                act.wait_ge(ang_ready, 1)
                nc.scalar.activation(sb1[:, :, :], ang[:, :, :], ACT.Sin).then_inc(sin_ready, 1)
                nc.scalar.activation(sb2[:, :, :], ang[:, :, :], ACT.Sin, scale=0.5).then_inc(sin_ready, 1)

            @block.vector
            def _(dve):
                chain = Chain(dve, vec)

                def tt(out, x, y, op):
                    chain.step(nc.vector.tensor_tensor(out, x, y, op))

                def ts(out, x, s1, s2, op0, op1):
                    chain.step(nc.vector.tensor_scalar(out, x, s1, s2, op0, op1))

                def spread(x):
                    return x[:, :].unsqueeze(2).to_broadcast(S)

                F = (slice(None),) * 3
                dve.wait_ge(exp_ready, 2)
                ts(are[F], are[F], -1.0, None, ALU.mult, ALU.bypass)
                nc.vector.tensor_tensor(a[F], are[F], spread(dt), ALU.mult).then_inc(small_ready, 1)
                tt(ang[F], aim[F], spread(dt), ALU.mult)
                ts(turns_[F], ang[F], 1.0 / TWO_PI, ROUND, ALU.mult, ALU.add)
                ts(turns_[F], turns_[F], -ROUND, None, ALU.add, ALU.bypass)
                chain.step(nc.vector.scalar_tensor_tensor(ang[F], turns_[F], -TWO_PI_HI, ang[F], ALU.mult, ALU.add))
                chain.step(nc.vector.scalar_tensor_tensor(ang[F], turns_[F], -TWO_PI_LO, ang[F], ALU.mult, ALU.add))
                nc.vector.tensor_scalar(ang[F], ang[F], 3.1415925, -3.1415925, ALU.min, ALU.max).then_inc(ang_ready, 1)
                dve.wait_ge(tanh_ready, 1)
                ts(u[F], th[F], -1.0, 1.0, ALU.mult, ALU.add)
                chain.step(nc.vector.reciprocal(u[F], u[F]))
                chain.step(nc.vector.scalar_tensor_tensor(em1[F], th[F], 2.0, u[F], ALU.mult, ALU.mult))
                ts(v[F], em1[F], 1.0, None, ALU.add, ALU.bypass)
                dve.wait_ge(sin_ready, 2)
                tt(zi[F], v[F], sb1[F], ALU.mult)
                tt(w[F], sb2[F], sb2[F], ALU.mult)
                tt(w[F], w[F], v[F], ALU.mult)
                chain.step(nc.vector.scalar_tensor_tensor(wr[F], w[F], -2.0, em1[F], ALU.mult, ALU.add))
                ts(zr[F], wr[F], 1.0, None, ALU.add, ALU.bypass)
                tt(u[F], are[F], are[F], ALU.mult)
                tt(v[F], aim[F], aim[F], ALU.mult)
                tt(u[F], u[F], v[F], ALU.add)
                chain.step(nc.vector.reciprocal(u[F], u[F]))
                tt(v[F], wr[F], are[F], ALU.mult)
                tt(w[F], zi[F], aim[F], ALU.mult)
                tt(v[F], v[F], w[F], ALU.add)
                tt(qr[F], v[F], u[F], ALU.mult)
                tt(v[F], zi[F], are[F], ALU.mult)
                tt(w[F], wr[F], aim[F], ALU.mult)
                tt(v[F], v[F], w[F], ALU.subtract)
                tt(qi[F], v[F], u[F], ALU.mult)

                def product(outr, outi, xr, xi, yr, yi, s1, s2):
                    tt(s1, xr, yr, ALU.mult)
                    tt(s2, xi, yi, ALU.mult)
                    tt(outr, s1, s2, ALU.subtract)
                    tt(s1, xr, yi, ALU.mult)
                    tt(s2, xi, yr, ALU.mult)
                    tt(outi, s1, s2, ALU.add)

                product(Vr[:, :, 0, :], Vi[:, :, 0, :], cre[F], cim[F], qr[F], qi[F], v[F], w[F])
                n = 1
                while n < SEQ:
                    for c in range(KD):
                        yr, yi = (x[:, c, :].unsqueeze(1).to_broadcast([P, n, N2]) for x in (zr, zi))
                        product(Vr[:, c, n:2 * n, :], Vi[:, c, n:2 * n, :], Vr[:, c, 0:n, :], Vi[:, c, 0:n, :], yr, yi,
                                t1[:, c, 0:n, :], t2[:, c, 0:n, :])
                    n *= 2
                    if n < SEQ:
                        product(u[F], qr[F], zr[F], zi[F], zr[F], zi[F], v[F], w[F])
                        chain.step(nc.vector.tensor_copy(zr[F], u[F]))
                        chain.step(nc.vector.tensor_copy(zi[F], qr[F]))
                chain.step(nc.vector.tensor_reduce(kern[:, :, :], Vr[:, :, :, :], AX.X, ALU.add))
                ts(kern[:, :, :], kern[:, :, :], 2.0, None, ALU.mult, ALU.bypass)


def causal_convolution_block(nc, m, t, kern):
    ctx, sb, ps, sem = scope(nc, m)
    with ctx:
        xpad = sb("xpad", [P, KD, BATCH, 2 * SEQ])
        y = sb("y", [P, KD, TOK])
        loaded, padded, zeroed, summed, copied = (sem(x) for x in ("loaded", "padded", "zeroed", "summed", "copied"))
        with engines_block(nc, m) as block:

            @block.sync
            def _(sp):
                sp.dma_start(m.wo[:, 0:KD, :], t["k_w"]).then_inc(loaded, 16)
                sp.dma_start(m.bo[:, :], t["k_b"]).then_inc(loaded, 16)
                sp.wait_ge(loaded, 32)

            @block.gpsimd
            def _(pool):
                for c in range(KD):
                    nc.gpsimd.memset(xpad[:, c, :, 0:SEQ], 0.0).then_inc(padded, 1)
                nc.gpsimd.memset(y[:, :, :], 0.0).then_inc(zeroed, 1)

            @block.scalar
            def _(act):
                for c in range(KD):
                    nc.scalar.copy(xpad[:, c, :, SEQ:2 * SEQ], m.xnT[:, c, :].rearrange("p (b n) -> p b n", b=BATCH)).then_inc(copied, 1)
                for c in range(KD):
                    act.wait_ge(summed, KD * SEQ + 2)
                    nc.scalar.activation(m.featT[:, c, :], y[:, c, :], ACT.Gelu)

            @block.vector
            def _(dve):
                dve.sem_inc(summed, 2)
                dve.wait_ge(copied, KD)
                dve.wait_ge(padded, KD)
                dve.wait_ge(zeroed, 1)
                with dve.Fori(0, SEQ) as s:
                    for c in range(KD):
                        dve.wait_ge(summed, s * KD + c + 1)
                        hold_waits(dve, m)
                        yc = y[:, c, :].rearrange("p (b n) -> p b n", b=BATCH)
                        nc.vector.scalar_tensor_tensor(yc, xpad[:, c, :, bass.ds(SEQ - s, SEQ)], kern[:, c, bass.ds(s, 1)],
                                                       yc, ALU.mult, ALU.add).then_inc(summed, 1)


MASKED = -30000.0
RMS_EPS = 1e-8


def resampler_layer(nc, m, t):
    H, DH = 4, 64
    HD = H * DH
    with ExitStack() as whole:
        def big(name, shape, dt=F32):
            return whole.enter_context(nc.sbuf_tensor("d_" + name, shape, dt))

        lnT = m.featT
        q_tok, kv_tok = big("q_tok", [P, TT, HD]), big("kv_tok", [P, TT, 2 * HD])
        qT, klT = big("qT", [P, KD, TOK]), big("klT", [P, KD, TOK])
        wq, wlkv = big("wq", [P, KD, HD]), big("wlkv", [P, KD, 2 * HD])
        w1, w2 = big("w1", [P, 2 * HD]), big("w2", [CL, 2 * HD])
        wk = big("wk", [P, H, CA])
        gk, gates = big("gk", [P, 4]), big("gates", [P, 6])
        g_row, b_row = big("g_row", [P, DC]), big("b_row", [P, DC])
        mask_in, mbias = big("mask_in", [P, BATCH, MT], I32), big("mbias", [P, BATCH, MT])
        resampler_prepare_block(nc, m, t, lnT, wq, wlkv, w1, w2, wk, gk, gates, g_row, b_row, mask_in, mbias)
        token_major_block(nc, m, [(q_tok, wq, lnT, KD, None), (kv_tok, wlkv, lnT, KD, None)], [])
        unit_rms_block(nc, m, q_tok, kv_tok, qT, klT, gk, H)
        resampler_attention_block(nc, m, t, H, DH, qT, klT, kv_tok, w1, w2, wk, mbias)


def resampler_prepare_block(nc, m, t, lnT, wq, wlkv, w1, w2, wk, gk, gates, g_row, b_row, mask_in, mbias):
    ctx, sb, ps, sem = scope(nc, m)
    H = 4
    with ctx:
        stats, mv, rstd = sb("stats", [P, TT, 6]), sb("mv", [P, TT, 2]), sb("rstd", [P, TT])
        ln = sb("ln", [P, TT, D])
        tmp = sb("tmp", [P, H, DC])
        bcol = sb("bcol", [P, 2])
        tps = [ps(f"tps{i}", [P, KD, P]) for i in range(2)]
        b_ps = ps("b_ps", [1, HALF])
        loaded, var_ready, std_ready, ln_ready, transposed, evacuated, folded = (
            sem(x) for x in ("loaded", "var_ready", "std_ready", "ln_ready", "transposed", "evacuated", "folded"))
        vec = sem("vec")
        loads = ((wq[:, :, :], "d_wq"), (wlkv[:, :, :], "d_wlkv"), (w1[:, :], "d_w1"), (w2[:, :], "d_w2"),
                 (wk[:, :, :], "d_wk"), (gk[:, :], "d_gk"), (gates[:, :], "d_gates"), (g_row[:, :], "d_g_row"),
                 (b_row[:, :], "d_b_row"), (mask_in[:, :, :], "d_mask"), (bcol[:, :], "d_bcol"),
                 (m.wo[:, 0:KD, :], "d_wo"), (m.bo[:, :], "d_bo"))
        with engines_block(nc, m) as block:

            @block.sync
            def _(sp):
                for buf, name in loads:
                    sp.dma_start(buf, t[name]).then_inc(loaded, 16)

            @block.vector
            def _(dve):
                chain = Chain(dve, vec)
                for n in range(TT):
                    chain.step(nc.vector.bn_stats(stats[:, n, :], m.xn[:, n, :]))
                    last = nc.vector.bn_aggr(mv[:, n, :], stats[:, n, :])
                chain.step(last)
                nc.vector.tensor_scalar(rstd[:, :], mv[:, :, 1], LN_EPS, None, ALU.add).then_inc(var_ready, 1)
                dve.wait_ge(loaded, 16 * len(loads))
                nc.vector.tensor_copy(mbias[:, :, :], mask_in[:, :, :]).then_inc(vec, 1)
                chain.n += 1
                for h in range(H):
                    nc.vector.tensor_tensor(tmp[:, h, :], wk[:, h, 0:DC], b_row[:, :], ALU.mult).then_inc(vec, 1)
                    chain.n += 1
                dve.wait_ge(vec, chain.n)
                nc.vector.tensor_reduce(wk[:, :, DC:CA], tmp[:, :, :], AX.X, ALU.add)
                for h in range(H):
                    nc.vector.tensor_tensor(wk[:, h, 0:DC], wk[:, h, 0:DC], g_row[:, :], ALU.mult)
                nc.vector.tensor_scalar(mbias[:, :, :], mbias[:, :, :], -MASKED, MASKED, ALU.mult, ALU.add)
                dve.wait_ge(folded, 1)
                nc.vector.tensor_scalar(w1[:, :], w1[:, :], gates[:, 4:5], None, ALU.mult)
                nc.vector.tensor_scalar(w2[0:CL - 1, :], w2[0:CL - 1, :], gates[0:CL - 1, 5:6], None, ALU.mult)
                nc.vector.tensor_copy(w2[CL - 1:CL, :], b_ps[:, :])
                nc.vector.scalar_tensor_tensor(gk[:, 2:3], gk[:, 0:1], DHEAD_SCALE, gk[:, 1:2], ALU.mult, ALU.mult)
                dve.wait_ge(std_ready, 1)
                chain.step(nc.vector.reciprocal(rstd[:, :], rstd[:, :]))
                for n in range(TT):
                    nc.vector.tensor_scalar(ln[:, n, :], m.xn[:, n, :], mv[:, n, 0:1], rstd[:, n:n + 1],
                                            ALU.subtract, ALU.mult).then_inc(ln_ready, 1)
                for n in range(TT):
                    dve.wait_ge(transposed, n + 1)
                    for k in range(KD):
                        last = nc.vector.tensor_scalar(lnT[:, k, n * P:(n + 1) * P], tps[n % 2][:, k, :],
                                                       gates[:, k:k + 1], gates[:, 2 + k:3 + k], ALU.mult, ALU.add)
                    last.then_inc(evacuated, 1)

            @block.scalar
            def _(act):
                act.wait_ge(var_ready, 1)
                nc.scalar.activation(rstd[:, :], rstd[:, :], ACT.Sqrt).then_inc(std_ready, 1)

            @block.tensor
            def _(pe):
                pe.wait_ge(loaded, 16 * len(loads))
                nc.tensor.matmul(b_ps[:, :], bcol[:, 0:1], w1[:, :], start=True, stop=False)
                nc.tensor.matmul(b_ps[:, :], bcol[0:CL - 1, 1:2], w2[0:CL - 1, :], start=False, stop=True).then_inc(folded, 1)
                for n in range(TT):
                    pe.wait_ge(ln_ready, n + 1)
                    if n >= 2:
                        pe.wait_ge(evacuated, n - 1)
                    for k in range(KD):
                        last = nc.tensor.transpose(tps[n % 2][:, k, :], ln[:, n, k * P:(k + 1) * P], m.ident[:, :])
                    last.then_inc(transposed, 1)


DHEAD_SCALE = 64 ** -0.5


def unit_rms_block(nc, m, q_tok, kv_tok, qT, klT, gk, H):
    ctx, sb, ps, sem = scope(nc, m)
    with ctx:
        HD = H * 64
        sq = sb("sq", [P, 2, TT, HD])
        ss = sb("ss", [P, 2, TT * H])
        tps = [ps(f"tps{i}", [P, 2, KD, P]) for i in range(2)]
        squared, summed, rooted, ready, transposed, evacuated = (
            sem(x) for x in ("squared", "summed", "rooted", "ready", "transposed", "evacuated"))
        vec = sem("vec")
        srcs = (q_tok[:, :, :], kv_tok[:, :, 0:HD])
        with engines_block(nc, m) as block:

            @block.scalar
            def _(act):
                for j in range(2):
                    nc.scalar.activation(sq[:, j, :, :], srcs[j], ACT.Square).then_inc(squared, 1)
                act.wait_ge(summed, 2)
                nc.scalar.activation(ss[:, :, :], ss[:, :, :], ACT.Sqrt, scale=1.0 / 64).then_inc(rooted, 1)

            @block.vector
            def _(dve):
                chain = Chain(dve, vec)
                for j in range(2):
                    dve.wait_ge(squared, j + 1)
                    nc.vector.tensor_reduce(ss[:, j, :], sq[:, j, :, :].rearrange("p t (h d) -> p (t h) d", h=H),
                                            AX.X, ALU.add).then_inc(summed, 1)
                dve.wait_ge(rooted, 1)
                chain.step(nc.vector.tensor_scalar(ss[:, :, :], ss[:, :, :], RMS_EPS, None, ALU.max))
                chain.step(nc.vector.reciprocal(ss[:, :, :], ss[:, :, :]))
                for j in range(2):
                    r = ss[:, j, :].rearrange("p (t h) -> p t h", h=H)
                    for h in range(H):
                        x = srcs[j][:, :, h * 64:(h + 1) * 64]
                        nc.vector.tensor_tensor(x, x, r[:, :, h:h + 1].to_broadcast([P, TT, 64]), ALU.mult).then_inc(ready, 1)
                for n in range(TT):
                    dve.wait_ge(transposed, n + 1)
                    nc.vector.tensor_scalar(qT[:, :, n * P:(n + 1) * P], tps[n % 2][:, 0, :, :], gk[:, 2:3], None, ALU.mult)
                    nc.vector.tensor_copy(klT[:, :, n * P:(n + 1) * P], tps[n % 2][:, 1, :, :]).then_inc(evacuated, 1)

            @block.tensor
            def _(pe):
                pe.wait_ge(ready, 2 * H)
                for n in range(TT):
                    if n >= 2:
                        pe.wait_ge(evacuated, n - 1)
                    for j in range(2):
                        for k in range(KD):
                            last = nc.tensor.transpose(tps[n % 2][:, j, k, :], srcs[j][:, n, k * P:(k + 1) * P], m.ident[:, :])
                    last.then_inc(transposed, 1)


def resampler_attention_block(nc, m, t, H, DH, qT, klT, kv_tok, w1, w2, wk, mbias):
    ctx, sb, ps, sem = scope(nc, m)
    HD = H * DH
    W = H * SEQ
    hpc = P // DH
    with ctx:
        ctok = sb("ctx_tok", [P, 2, MT, CA])
        stats, mv, rstd = sb("stats", [P, MT, 6]), sb("mv", [P, MT, 2]), sb("rstd", [P, MT])
        xT1, xT2 = sb("xT1", [P, MPAD]), sb("xT2", [CL, MPAD])
        q1, q2 = sb("q1", [P, W]), sb("q2", [CL, W])
        qz = sb("q_by_head", [P, KD, hpc, SEQ])
        kl = sb("kl", [P, KD, SEQ])
        vl = sb("vl", [SEQ, HD])
        mb = sb("mask_now", [P, MT])
        sq = sb("sq", [P, 2, HD])
        rk = sb("rk", [P, MT, H])
        sc = sb("scaled", [P, 2, W])
        e = sb("e", [P, 2, W])
        el = sb("e_latents", [SEQ, W])
        pt1, pt2 = sb("pt1", [P, W]), sb("pt2", [CL, W])
        rsum = sb("rsum", [SEQ, H])
        o = sb("o", [SEQ, HD])
        e64 = sb("sum_col", [CL, 1])
        one = sb("one_col", [SEQ, 1])
        own = sb("own_head", [P, hpc, SEQ])
        ringT = [ps(f"ringT{i}", [P, HALF]) for i in range(2)]
        ringK = [ps(f"ringK{i}", [P, HALF]) for i in range(2)]
        acc1, acc2 = ps("acc1", [P, W]), ps("acc2", [CL, W])
        o_ps, misc = ps("o_ps", [SEQ, HALF]), ps("misc", [P, HALF])
        loaded, zeroed = sem("loaded"), sem("zeroed")
        ctx_in = [sem(f"ctx_in{u}") for u in range(2)]
        norm_var, norm_std = sem("norm_var"), sem("norm_std")
        x_ready = sem("x_ready")
        staged = sem("staged")
        v_staged = sem("v_staged")
        t_full, t_free = sem("t_full"), sem("t_free")
        k_full, k_squared = sem("k_full"), sem("k_squared")
        k_summed = sem("k_summed")
        rms_root, rk_ready = sem("rms_root"), sem("rk_ready")
        s_full, s_free = sem("s_full"), sem("s_free")
        e_ready, e_used = sem("e_ready"), sem("e_used")
        lat_full, lat_ready = sem("lat_full"), sem("lat_ready")
        pooled_out = sem("pooled_out")
        o_full, sums_ready = sem("o_full"), sem("sums_ready")
        o_ready = sem("o_ready")
        oT_full, oT_out = sem("oT_full"), sem("oT_out")
        vec = sem("vec")
        NT = MT + 1
        PER = 2 * MT + 3
        with engines_block(nc, m) as block:

            def each_batch(eng, body):
                with eng.Fori(0, BATCH // 2) as i:
                    for u in range(2):
                        body(i * 2 + u, i, u)

            @block.sync
            def _(sp):
                sp.dma_start(e64[:, :], t["e64"]).then_inc(loaded, 16)
                sp.dma_start(own[:, :, :], t["own64"]).then_inc(loaded, 16)

                def body(b, i, u):
                    sp.wait_ge(pooled_out, b * 2 + 2)
                    sp.dma_start(flat(ctok[:, u, :, :]),
                                 t["ctok"][bass.ds(b, 1)].rearrange("o p t n -> p (o t n)")).then_inc(ctx_in[u], 16)

                each_batch(sp, body)

            @block.gpsimd
            def _(pool):
                pool.sem_inc(s_free, 1)
                nc.gpsimd.memset(one[:, :], 1.0).then_inc(zeroed, 1)
                pool.wait_ge(loaded, 32)

                def body(b, i, u):
                    pool.wait_ge(pooled_out, b * 2 + 4)
                    hold_waits(pool, m)
                    now = bass.ds(b * SEQ, SEQ)
                    for c in range(KD):
                        nc.gpsimd.tensor_tensor(qz[:, c, :, :], qT[:, c, now].unsqueeze(1).to_broadcast([P, hpc, SEQ]),
                                                own[:, :, :], ALU.mult)
                    nc.gpsimd.tensor_copy(mb[:, :], mbias[:, bass.ds(b, 1), :].rearrange("p o t -> p (o t)"))
                    nc.gpsimd.tensor_copy(kl[:, :, :], klT[:, :, now]).then_inc(staged, 1)

                each_batch(pool, body)

            @block.tensor
            def _(pe):
                pe.wait_ge(zeroed, 1)
                pe.wait_ge(loaded, 32)

                def body(b, i, u):
                    pe.wait_ge(t_free, b * NT + 1)
                    for h in range(H):
                        src = qT[:, h // hpc, bass.ds(b * SEQ, SEQ)]
                        nc.tensor.matmul(ringT[0][:, h * SEQ:(h + 1) * SEQ], wk[:, h, 0:P], src, start=True, stop=True)
                        last = nc.tensor.matmul(ringT[0][0:CL, W + h * SEQ:W + (h + 1) * SEQ], wk[:, h, P:CA], src,
                                                start=True, stop=True)
                    last.then_inc(t_full, 1)
                    pe.wait_ge(staged, b + 1)
                    pe.wait_ge(oT_out, b + 1)
                    hold_waits(pe, m)
                    for c in range(KD):
                        last = nc.tensor.matmul(misc[0:SEQ, c * P:(c + 1) * P], kl[:, c, :], flat(qz[:, c, :, :]),
                                                start=True, stop=True)
                    last.then_inc(lat_full, 1)

                    def turn(n):
                        pe.wait_ge(x_ready, b * MT + n + 1)
                        pe.wait_ge(t_free, b * NT + n + 2)
                        bank = ringT[(n + 1) % 2]
                        nc.tensor.transpose(bank[:, 0:P], ctok[:, u, n, 0:P], m.ident[:, :])
                        nc.tensor.transpose(bank[0:CL, P:2 * P], ctok[:, u, n, P:CA], m.ident[:, :]).then_inc(t_full, 1)

                    def keys(n):
                        pe.wait_ge(t_free, b * NT + n + 4)
                        if n < 2:
                            pe.wait_ge(s_free, b * MT + 1)
                        else:
                            pe.wait_ge(k_squared, b * MT + n - 1)
                        cols = slice(n * P, (n + 1) * P)
                        nc.tensor.matmul(ringK[n % 2][:, 0:HD], xT1[:, cols], w1[:, 0:HD], start=True, stop=False)
                        nc.tensor.matmul(ringK[n % 2][:, 0:HD], xT2[:, cols], w2[:, 0:HD],
                                         start=False, stop=True).then_inc(k_full, 1)

                    turn(0)
                    for n in range(1, MT):
                        turn(n)
                        keys(n - 1)
                    keys(MT - 1)

                    def scores(n):
                        if n < 2:
                            pe.wait_ge(k_squared, b * MT + MT - 1 + n)
                        else:
                            pe.wait_ge(s_free, b * MT + n)
                        bank = ringK[(MT + n) % 2]
                        cols = slice(n * P, (n + 1) * P)
                        nc.tensor.matmul(bank[:, 0:W], xT1[:, cols], q1[:, :], start=True, stop=False)
                        nc.tensor.matmul(bank[:, 0:W], xT2[:, cols], q2[:, :], start=False, stop=True).then_inc(s_full, 1)

                    def pool_tile(n):
                        pe.wait_ge(e_ready, b * MT + n + 1)
                        if n == 0:
                            pe.wait_ge(pooled_out, b * 2 + 4)
                        nc.tensor.matmul(acc1[:, :], ctok[:, u, n, 0:P], e[:, n % 2, :], start=(n == 0), stop=(n == MT - 1))
                        nc.tensor.matmul(acc2[:, :], ctok[:, u, n, P:CA], e[:, n % 2, :], start=(n == 0),
                                         stop=(n == MT - 1)).then_inc(e_used, 1)

                    scores(0)
                    scores(1)
                    for n in range(MT):
                        pool_tile(n)
                        if n + 2 < MT:
                            scores(n + 2)

                    pe.wait_ge(pooled_out, b * 2 + 6)
                    pe.wait_ge(lat_ready, b + 1)
                    pe.wait_ge(v_staged, b + 1)
                    pe.wait_ge(o_ready, b + 1)
                    hold_waits(pe, m)
                    for h in range(H):
                        rows = slice(h * SEQ, (h + 1) * SEQ)
                        vcols = slice(HD + h * DH, HD + (h + 1) * DH)
                        dst = o_ps[:, h * DH:(h + 1) * DH]
                        nc.tensor.matmul(dst, pt1[:, rows], w1[:, vcols], start=True, stop=False)
                        nc.tensor.matmul(dst, pt2[:, rows], w2[:, vcols], start=False, stop=False)
                        nc.tensor.matmul(dst, el[:, rows], vl[:, h * DH:(h + 1) * DH], start=False, stop=True)
                        dst = o_ps[:, HD + h:HD + h + 1]
                        nc.tensor.matmul(dst, pt2[:, rows], e64[:, :], start=True, stop=False)
                        last = nc.tensor.matmul(dst, el[:, rows], one[:, :], start=False, stop=True)
                    last.then_inc(o_full, 1)
                    pe.wait_ge(o_ready, b + 2)
                    hold_waits(pe, m)
                    for c in range(KD):
                        last = nc.tensor.transpose(misc[:, W + c * SEQ:W + (c + 1) * SEQ], o[:, c * P:(c + 1) * P],
                                                   m.ident[0:SEQ, 0:SEQ])
                    last.then_inc(oT_full, 1)

                each_batch(pe, body)

            @block.scalar
            def _(act):
                act.sem_inc(t_free, 2)
                act.sem_inc(oT_out, 1)
                act.sem_inc(e_used, 2)
                act.sem_inc(pooled_out, 4)

                def body(b, i, u):
                    act.wait_ge(norm_var, b + 1)
                    nc.scalar.activation(rstd[:, :], rstd[:, :], ACT.Sqrt).then_inc(norm_std, 1)
                    act.wait_ge(t_full, b * NT + 1)
                    nc.scalar.copy(q1[:, :], ringT[0][:, 0:W])
                    nc.scalar.copy(q2[:, :], ringT[0][0:CL, W:2 * W]).then_inc(t_free, 1)
                    nc.scalar.copy(vl[:, :], kv_tok[u * SEQ:(u + 1) * SEQ, bass.ds(i, 1), HD:2 * HD]
                                   .rearrange("p o n -> p (o n)")).then_inc(v_staged, 1)

                    def square(n):
                        act.wait_ge(k_full, b * MT + n + 1)
                        act.wait_ge(k_summed, b * MT + n + 1)
                        nc.scalar.activation(sq[:, n % 2, :], ringK[n % 2][:, 0:HD], ACT.Square).then_inc(k_squared, 1)

                    for n in range(MT):
                        act.wait_ge(t_full, b * NT + n + 2)
                        bank = ringT[(n + 1) % 2]
                        nc.scalar.copy(xT1[:, n * P:(n + 1) * P], bank[:, 0:P])
                        nc.scalar.copy(xT2[:, n * P:(n + 1) * P], bank[0:CL, P:2 * P]).then_inc(t_free, 1)
                        if n:
                            square(n - 1)
                    square(MT - 1)
                    act.wait_ge(k_summed, b * MT + MT + 2)
                    nc.scalar.activation(flat(rk[:, :, :]), flat(rk[:, :, :]), ACT.Sqrt, scale=1.0 / DH).then_inc(rms_root, 1)
                    act.wait_ge(lat_full, b + 1)
                    nc.scalar.activation(el[:, :], misc[0:SEQ, 0:W], ACT.Exp).then_inc(lat_ready, 1)
                    for n in range(MT):
                        act.wait_ge(s_free, b * MT + n + 2)
                        act.wait_ge(e_used, b * MT + (n + 1))
                        nc.scalar.activation(e[:, n % 2, :], sc[:, n % 2, :], ACT.Exp,
                                             bias=mb[:, n:n + 1]).then_inc(e_ready, 1)
                    act.wait_ge(e_used, b * MT + MT + 2)
                    nc.scalar.copy(pt1[:, :], acc1[:, :]).then_inc(pooled_out, 1)
                    act.wait_ge(oT_full, b + 1)
                    nc.scalar.copy(m.featT[:, 0:KD, bass.ds(b * SEQ, SEQ)],
                                   misc[:, W:W + KD * SEQ].rearrange("p (c n) -> p c n", c=KD)).then_inc(oT_out, 1)

                each_batch(act, body)

            @block.vector
            def _(dve):
                dve.sem_inc(k_summed, 2)
                dve.sem_inc(o_ready, 1)

                def body(b, i, u):
                    chain = Chain(dve, vec, b * PER, PER)
                    dve.wait_ge(ctx_in[u], i * 16 + 16)
                    for n in range(MT):
                        nc.vector.bn_stats(stats[:, n, :], ctok[:, u, n, 0:DC]).then_inc(vec, 1)
                        chain.n += 1
                    dve.wait_ge(vec, b * PER + MT)
                    hold_waits(dve, m)
                    for n in range(MT):
                        nc.vector.bn_aggr(mv[:, n, :], stats[:, n, :]).then_inc(vec, 1)
                        chain.n += 1
                    dve.wait_ge(vec, b * PER + chain.n)
                    nc.vector.tensor_scalar(rstd[:, :], mv[:, :, 1], LN_EPS, None, ALU.add).then_inc(norm_var, 1)
                    dve.wait_ge(norm_std, b + 1)
                    chain.step(nc.vector.reciprocal(rstd[:, :], rstd[:, :]))
                    for n in range(MT):
                        nc.vector.tensor_scalar(ctok[:, u, n, 0:DC], ctok[:, u, n, 0:DC], mv[:, n, 0:1],
                                                rstd[:, n:n + 1], ALU.subtract, ALU.mult).then_inc(x_ready, 1)
                    for n in range(MT):
                        dve.wait_ge(k_squared, b * MT + n + 1)
                        nc.vector.tensor_reduce(rk[:, n, :], sq[:, n % 2, :].rearrange("p (h d) -> p h d", h=H),
                                                AX.X, ALU.add).then_inc(k_summed, 1)
                    dve.wait_ge(rms_root, b + 1)
                    chain.step(nc.vector.tensor_scalar(flat(rk[:, :, :]), flat(rk[:, :, :]), RMS_EPS, None, ALU.max))
                    chain.step(nc.vector.reciprocal(flat(rk[:, :, :]), flat(rk[:, :, :])))
                    chain.close()
                    for n in range(MT):
                        dve.wait_ge(s_full, b * MT + n + 1)
                        if n >= 2:
                            dve.wait_ge(e_ready, b * MT + n - 1)
                        nc.vector.tensor_tensor(sc[:, n % 2, :].rearrange("p (h n) -> p h n", h=H),
                                                ringK[(MT + n) % 2][:, 0:W].rearrange("p (h n) -> p h n", h=H),
                                                rk[:, n, :].unsqueeze(2).to_broadcast([P, H, SEQ]), ALU.mult).then_inc(s_free, 1)
                    dve.wait_ge(e_used, b * MT + MT + 2)
                    nc.vector.tensor_copy(pt2[:, :], acc2[:, :]).then_inc(pooled_out, 1)
                    dve.wait_ge(o_full, b + 1)
                    nc.vector.reciprocal(rsum[:, :], o_ps[:, HD:HD + H]).then_inc(sums_ready, 1)
                    dve.wait_ge(sums_ready, b + 1)
                    nc.vector.tensor_tensor(o[:, :].rearrange("p (h d) -> p h d", h=H),
                                            o_ps[:, 0:HD].rearrange("p (h d) -> p h d", h=H),
                                            rsum[:, :].unsqueeze(2).to_broadcast([SEQ, H, DH]), ALU.mult).then_inc(o_ready, 1)

                each_batch(dve, body)


def build(nc, t, out):
    with ExitStack() as ctx:
        m = alloc_memory(nc, ctx)
        load_x_block(nc, m, t["x"], t["ident"])
        project_and_norm_block(nc, m, 0)
        for layer in range(FIRST_LAYER, LAST_LAYER + 1):
            last = layer == LAST_LAYER
            if layer == 0:
                cross_attention_blocks(nc, m, 16, 64, dict(wq=t["a_wq"], bq=None, wk=t["a_wk"], wv1=t["a_wv1"],
                                       wv2=t["a_wv2"], wo=t["a_wo"], bo=t["a_bo"]), t["ctxT1"], t["ctxT2"], t["ctok"], t)
                project_and_norm_block(nc, m, 8, bias=True, norm=not last)
            elif layer == 1:
                latent_attention_layer(nc, m, t)
                project_and_norm_block(nc, m, 2, norm=not last)
            elif layer == 4:
                biased_attention_layer(nc, m, t)
                project_and_norm_block(nc, m, 2, bias=True, norm=not last)
            elif layer == 7:
                linear_attention_layer(nc, m, t)
                project_and_norm_block(nc, m, 2, norm=not last)
            elif layer in (6, 9):
                k = "g" if layer == 6 else "j"
                cross_attention_blocks(nc, m, 16, 16, dict(wq=t[k + "_wq"], bq=t[k + "_bq"], wk=t[k + "_wk"],
                                       wv1=t[k + "_wv1"], wv2=t[k + "_wv2"], wo=t[k + "_wo"], bo=t[k + "_bo"]),
                                       t["ctxT1"], t["ctxT2"], t["ctok"], t)
                project_and_norm_block(nc, m, 2, bias=True, norm=not last)
            elif layer == 2:
                switch_head_layer(nc, m, t)
                project_and_norm_block(nc, m, 3, last_rows=64, norm=not last)
            elif layer == 3:
                resampler_layer(nc, m, t)
                project_and_norm_block(nc, m, 2, bias=True, norm=not last)
            elif layer == 5:
                with nc.sbuf_tensor("mod_factor", [P, TT], F32) as factor:
                    mixture_of_depths_layer(nc, m, t, factor)
                    project_and_norm_block(nc, m, 8, bias=True, gated=factor, norm=not last)
            elif layer in (8, 11):
                groups, n, k = (1, 16, "i") if layer == 8 else (2, 32, "l")
                N = groups * n
                total = N + (layer == 8)
                with ExitStack() as own:
                    w_gate, rev, weights = (own.enter_context(nc.sbuf_tensor(f"{k}_{x}", shape, F32)) for x, shape in
                                            (("gate", [P, KD, N]), ("rev", [P, n]), ("weights", [P, TT, total])))
                    b_gate = own.enter_context(nc.sbuf_tensor(f"{k}_bgate", [1, N], F32))
                    loads = [(w_gate[:, :, :], t[k + "_gate"]), (rev[:, :], t[f"rev{n}"])]
                    if layer == 8:
                        loads.append((b_gate[:, :], t["i_bgate"]))
                    routing_block(nc, m, w_gate, loads, groups, n, weights, rev,
                                  bias=b_gate[0:1, :] if layer == 8 else None, softmax=layer == 11, shared=layer == 8)
                    experts_block(nc, m, total, t[k + "_experts"], weights, add_xn=layer == 8)
                if not last:
                    project_and_norm_block(nc, m, 0)
            elif layer == 10:
                with nc.sbuf_tensor("s4d_kernel", [P, KD, SEQ], F32) as kern:
                    state_space_kernel_block(nc, m, t, kern)
                    causal_convolution_block(nc, m, t, kern)
                project_and_norm_block(nc, m, 2, bias=True, norm=not last)
        store_x_block(nc, m, out)


def rows_to_partitions(w):
    w = np.asarray(w)
    return np.ascontiguousarray(w.reshape(w.shape[0] // P, P, w.shape[1]).transpose(1, 0, 2))


def column(b):
    return np.ascontiguousarray(np.asarray(b).reshape(-1, P).T)


def per_head_keys(wk, bk, heads, dh):
    w = np.zeros((CA, heads * dh), np.float32)
    w[:DC] = wk
    if bk is not None:
        w[DC] = bk
    out = np.zeros((P, heads, CA), np.float32)
    for h in range(heads):
        r = (h * dh) % P
        out[r:r + dh, h, :] = w[:, h * dh:(h + 1) * dh].T
    return out


def with_row(w, b):
    out = np.zeros((w.shape[0] + 1, w.shape[1]), np.float32)
    out[:-1] = w
    if b is not None:
        out[-1] = b
    return out


def lay_out(a):
    t = {}
    t["x"] = np.ascontiguousarray(a["x"].reshape(TT, P, D).transpose(1, 0, 2))
    t["ident"] = np.eye(P, dtype=np.float32)
    aug = np.zeros((BATCH, MPAD, CA), np.float32)
    aug[:, :KEYS, :DC] = a["ctx_768"]
    aug[:, :KEYS, DC] = 1.0
    t["ctxT1"] = np.ascontiguousarray(aug.transpose(0, 2, 1)[:, :P])
    t["ctxT2"] = np.ascontiguousarray(aug.transpose(0, 2, 1)[:, P:])
    t["ctok"] = np.ascontiguousarray(aug.reshape(BATCH, MT, P, CA).transpose(0, 2, 1, 3))
    e64 = np.zeros((CL, 1), np.float32)
    e64[-1] = 1.0
    t["e64"] = e64

    t["a_wq"] = rows_to_partitions(a["L0_xattn_Wq"])
    t["a_wk"] = per_head_keys(a["L0_xattn_Wk"], None, 16, 64)
    wv = with_row(a["L0_xattn_Wv"], None)
    t["a_wv1"], t["a_wv2"] = wv[:P], wv[P:]
    t["a_wo"] = rows_to_partitions(a["L0_xattn_Wo"])
    t["a_bo"] = a["L0_xattn_bo"][None, :]

    swap = np.arange(D) ^ 1
    t["b_wq"], t["b_wqs"] = rows_to_partitions(a["L0_attn_wq"]), rows_to_partitions(a["L0_attn_wq"][:, swap])
    t["b_wd"] = rows_to_partitions(a["L0_attn_w_down"])
    t["b_wk"], t["b_wks"] = rows_to_partitions(a["L0_attn_wk_up"]), rows_to_partitions(a["L0_attn_wk_up"][:, swap])
    t["b_wv"] = rows_to_partitions(a["L0_attn_wv_up"])
    t["b_wo"] = rows_to_partitions(a["L0_attn_wo"])
    inv = 1.0 / 10000.0 ** (np.arange(0, 16, 2, dtype=np.float32) / 16)
    ang = np.outer(np.arange(SEQ, dtype=np.float32), inv)
    pair = (np.arange(P) % 16) // 2
    t["rope_cos"] = np.ascontiguousarray(np.cos(ang).astype(np.float32).T[pair])
    sign = np.where(np.arange(P) % 2 == 0, -1.0, 1.0).astype(np.float32)
    t["rope_sin"] = np.ascontiguousarray(np.sin(ang).astype(np.float32).T[pair] * sign[:, None])
    for dh in (16, 64):
        own = np.arange(P)[:, None] // dh == np.arange(P // dh)[None, :]
        t[f"own{dh}"] = np.ascontiguousarray(np.repeat(own[:, :, None], SEQ, 2).astype(np.float32))
    pos = np.arange(P) % SEQ
    t["causal"] = (np.arange(SEQ)[None, :] <= pos[:, None]).astype(np.float32)
    t["before"] = (np.arange(SEQ)[None, :] < pos[:, None]).astype(np.float32)

    order = np.arange(3 * D).reshape(16, 3, 16).transpose(1, 0, 2).reshape(3, D)
    for n, k in enumerate("qkv"):
        t[f"e_w{k}"] = rows_to_partitions(a["L1_attn_Wqkv"][:, order[n]])
    t["e_bq"], t["e_bk"] = column(a["L1_attn_bqkv"][order[0]]), column(a["L1_attn_bqkv"][order[1]])
    t["e_bv"] = a["L1_attn_bqkv"][order[2]][None, :]
    t["e_wo"], t["e_bo"] = rows_to_partitions(a["L1_attn_Wout"]), a["L1_attn_bout"][None, :]

    for k, n, names in (("g", "L2_xattn_", ("Wq", "bq", "Wk", "bk", "Wv", "bv", "Wo", "bo")),
                        ("j", "L3_xattn_", ("w_q", "b_q", "w_k", "b_k", "w_v", "b_v", "w_o", "b_o"))):
        wq, bq, wk, bk, wv, bv, wo, bo = (a[n + x] for x in names)
        t[k + "_wq"], t[k + "_bq"] = rows_to_partitions(wq), column(bq)
        t[k + "_wk"] = per_head_keys(wk, bk, 16, 16)
        w = with_row(wv, bv)
        t[k + "_wv1"], t[k + "_wv2"] = w[:P], w[P:]
        t[k + "_wo"], t[k + "_bo"] = rows_to_partitions(wo), bo[None, :]

    for k in ("q", "k", "v", "o"):
        t["h_w" + k] = rows_to_partitions(a["L2_attn_W_" + k].T)

    t["c_wq"], t["c_wk"] = rows_to_partitions(a["L0_ffn_Wq"]), rows_to_partitions(a["L0_ffn_Wk"])
    wx = a["L0_ffn_Wv"].transpose(1, 0, 2).reshape(D, -1)
    t["c_wx"] = rows_to_partitions(np.concatenate([wx, a["L0_ffn_Ws"], a["L0_ffn_Wd"]], 1))
    wo = np.zeros((3 * P, D), np.float32)
    wo[:5 * 64] = a["L0_ffn_Wo"].reshape(5 * 64, D)
    t["c_wo"] = rows_to_partitions(wo)
    for n in (5, 16, 32):
        t[f"rev{n}"] = np.tile(np.arange(n, 0, -1, dtype=np.float32), (P, 1))

    t["d_wq"], t["d_wlkv"] = rows_to_partitions(a["L1_xattn_Wq"].T), rows_to_partitions(a["L1_xattn_Wlkv"].T)
    w = with_row(a["L1_xattn_Wkv"].T, None)
    t["d_w1"], t["d_w2"] = w[:P], w[P:]
    t["d_wk"] = per_head_keys(a["L1_xattn_Wkv"][:D].T, None, 4, 64)
    gk = np.zeros((P, 4), np.float32)
    gk[:, 0], gk[:, 1] = np.tile(a["L1_xattn_qn_g"], 2), np.tile(a["L1_xattn_kn_g"], 2)
    t["d_gk"] = gk
    two = np.zeros((4, P), np.float32)
    for n, x in enumerate(("g", "b")):
        v = a[f"L1_xattn_ln_x_{x}"]
        two[2 * n], two[2 * n + 1, :DC - P] = v[:P], v[P:]
        t[f"d_{x}_row"] = np.tile(v, (P, 1))
    t["d_gates"] = np.concatenate([column(a["L1_xattn_ln_l_g"]), column(a["L1_xattn_ln_l_b"]), two[:2].T], 1)
    t["d_bcol"] = two[2:].T
    mask = np.zeros((BATCH, MPAD, 4), np.uint8)
    mask[:, :KEYS, 0] = a["mask_BxS2_bk0"].view(np.uint8)
    t["d_mask"] = mask.view(np.int32).reshape(BATCH, MT, P).transpose(2, 0, 1)
    t["d_wo"], t["d_bo"] = rows_to_partitions(a["L1_xattn_Wo"].T), a["L1_xattn_bo"][None, :]

    t["f_w1"], t["f_b1"] = rows_to_partitions(a["L1_ffn_W1"]), column(a["L1_ffn_b1"])
    t["f_wr"] = column(a["L1_ffn_w_router"])
    t["f_w2"], t["f_b2"] = rows_to_partitions(a["L1_ffn_W2"]), a["L1_ffn_b2"][None, :]

    def pack(wg, wu, wd):
        up = [w.reshape(-1, KD, P, P).transpose(0, 2, 1, 3).reshape(-1, P, KD * P) for w in (wg, wu)]
        return np.concatenate([*up, wd], 2)

    t["i_gate"], t["i_bgate"] = rows_to_partitions(a["L2_ffn_gate_w"]), a["L2_ffn_gate_b"][None, :]
    t["i_experts"] = np.concatenate([
        pack(*(a["L2_ffn_experts_" + w] for w in ("wg", "wu", "wd"))),
        pack(*(a["L2_ffn_shared_" + w][None] for w in ("wg", "wu", "wd")))])
    t["l_gate"] = rows_to_partitions(np.concatenate([a["L3_ffn_router_w0"], a["L3_ffn_router_w1"]], 1))
    t["l_experts"] = np.concatenate([pack(*(a[f"L3_ffn_{w}{g}"] for w in ("wg", "wu", "wd"))) for g in range(2)])

    t["k_ldt"] = column(a["L3_attn_log_dt"])
    for k, x in (("lar", "log_A_real"), ("aim", "A_imag"), ("cre", "C_real"), ("cim", "C_imag")):
        t["k_" + k] = rows_to_partitions(a["L3_attn_" + x])
    t["k_w"], t["k_b"] = rows_to_partitions(a["L3_attn_W"].T), a["L3_attn_b"][None, :]
    return t


def kernel(**inputs):
    import concourse.bacc as bacc
    from concourse.bass_utils import run_bass_kernel_spmd

    nc = bacc.Bacc("TRN2", target_bir_lowering=False, num_devices=1)
    arrays, t = {}, {}
    for name, a in lay_out({k: np.asarray(v) for k, v in inputs.items()}).items():
        a = np.ascontiguousarray(a)
        arrays[f"in_{name}_dram"] = a
        t[name] = nc.dram_tensor(f"in_{name}_dram", a.shape, mybir.dt.from_np(a.dtype), kind="ExternalInput").ap()
    out = nc.dram_tensor("out_0_dram", (P, TT, D), F32, kind="ExternalOutput").ap()
    build(nc, t, out)
    r = run_bass_kernel_spmd(nc, [arrays], core_ids=[0])
    got = r.results[0]["out_0_dram"]
    return np.ascontiguousarray(got.transpose(1, 0, 2)).reshape(BATCH, SEQ, D)
```

```python
from contextlib import ExitStack, contextmanager

import concourse.bass as bass
import numpy as np
from concourse import mybir

F32 = mybir.dt.float32
BF16 = mybir.dt.bfloat16
I32 = mybir.dt.int32
ALU = mybir.AluOpType
ACT = mybir.ActivationFunctionType
AX = mybir.AxisListType

FIRST_LAYER, LAST_LAYER = 0, 11

P = 128
BATCH, SEQ, D = 16, 64, 256
KEYS, DC = 1601, 192
TOK = BATCH * SEQ
TT = TOK // P
KD = D // P
MT = -(-KEYS // P)
MPAD = MT * P
CA = DC + 1
CL = CA - P
HALF = 512
LN_EPS = 1e-5
CLIP = 1e-6


class Mem:
    pass


def alloc_memory(nc, ctx):
    m = Mem()
    m.ctx = ctx

    def sb(name, shape, dt=F32):
        return ctx.enter_context(nc.sbuf_tensor(name, shape, dt))

    m.x = sb("x_tok", [P, TT, D])
    m.xn = sb("xn_tok", [P, TT, D])
    m.xnT = sb("xn_T", [P, KD, TOK])
    m.featT = sb("feat_T", [P, 8, TOK])
    m.wo = sb("w_out", [P, 8, D])
    m.bo = sb("b_out", [1, D])
    m.ident = sb("ident", [P, P])
    m.ones = sb("ones_row", [1, P])
    m.bf_in = ctx.enter_context(nc.semaphore("bf_in"))
    m.bf_in_count = 0
    m.held = ctx.enter_context(nc.semaphore("held"))
    m.n_blocks = 0
    m.retired = []
    return m


def scope(nc, m):
    m.n_blocks += 1
    tag = f"b{m.n_blocks}_"
    ctx = ExitStack()

    def sb(name, shape, dt=F32):
        return ctx.enter_context(nc.sbuf_tensor(tag + name, shape, dt))

    def ps(name, shape, dt=F32):
        return ctx.enter_context(nc.psum_tensor(tag + name, shape, dt))

    def sem(name):
        s = nc.alloc_semaphore(name=tag + name)
        own.append(s)
        return s

    own = []
    ctx.callback(lambda: m.retired.extend(own))
    return ctx, sb, ps, sem


@contextmanager
def engines_block(nc, m):
    cleared, m.retired = m.retired, []
    for s in cleared:
        nc.gpsimd.sem_clear(s)
    with nc.Block() as block:
        yield block
    for s in cleared:
        nc.release_semaphore(s)


class Chain:

    def __init__(self, eng, sem, base=None, per=None):
        self.eng, self.sem, self.base, self.n, self.per = eng, sem, base, 0, per

    def step(self, ins):
        self.n += 1
        ins.then_inc(self.sem, 1)
        self.eng.wait_ge(self.sem, self.n if self.base is None else self.base + self.n)

    def close(self):
        assert self.n == self.per, (self.n, self.per)


def hold_waits(eng, m):
    eng.sem_inc(m.held, 1)


def flat(ap):
    return ap.rearrange("p a b -> p (a b)")


def load_x_block(nc, m, x_in, ident_in):
    ctx, sb, ps, sem = scope(nc, m)
    with ctx:
        loaded = sem("loaded")
        with engines_block(nc, m) as block:

            @block.sync
            def _(sp):
                sp.dma_start(m.x[:, :, :], x_in).then_inc(loaded, 16)
                sp.dma_start(m.ident[:, :], ident_in).then_inc(loaded, 16)
                sp.wait_ge(loaded, 32)

            @block.vector
            def _(dve):
                nc.vector.memset(m.ones[:, :], 1.0)


def store_x_block(nc, m, x_out):
    ctx, sb, ps, sem = scope(nc, m)
    with ctx:
        stored = sem("stored")
        with engines_block(nc, m) as block:

            @block.sync
            def _(sp):
                sp.dma_start(x_out, m.x[:, :, :]).then_inc(stored, 16)
                sp.wait_ge(stored, 16)


def project_and_norm_block(nc, m, chunks, last_rows=P, bias=False, gated=None, norm=True):
    ctx, sb, ps, sem = scope(nc, m)
    with ctx:
        stats = sb("stats", [P, TT, 6])
        mv = sb("mean_var", [P, TT, 2])
        rstd = sb("rstd", [P, TT])
        proj = [ps(f"proj{i}", [P, D]) for i in range(2)]
        tps = [ps(f"tps{i}", [P, KD, P]) for i in range(2)]
        projected = sem("projected")
        added = sem("added")
        vec = sem("vec")
        var_ready = sem("var_ready")
        std_ready = sem("std_ready")
        xn_ready = sem("xn_ready")
        transposed = sem("transposed")
        evacuated = sem("evacuated")
        with engines_block(nc, m) as block:

            @block.tensor
            def _(pe):
                if chunks:
                    for t in range(TT):
                        if t >= 2:
                            pe.wait_ge(added, t - 1)
                        for c in range(chunks):
                            k = last_rows if c == chunks - 1 else P
                            last = nc.tensor.matmul(
                                proj[t % 2][:, :], m.featT[0:k, c, t * P:(t + 1) * P], m.wo[0:k, c, :],
                                start=(c == 0), stop=(c == chunks - 1 and not bias))
                        if bias:
                            last = nc.tensor.matmul(proj[t % 2][:, :], m.ones[0:1, :], m.bo[0:1, :],
                                                    start=False, stop=True)
                        last.then_inc(projected, 1)
                if norm:
                    for t in range(TT):
                        pe.wait_ge(xn_ready, t + 1)
                        if t >= 2:
                            pe.wait_ge(evacuated, t - 1)
                        for k in range(KD):
                            last = nc.tensor.transpose(tps[t % 2][:, k, :], m.xn[:, t, k * P:(k + 1) * P],
                                                       m.ident[:, :])
                        last.then_inc(transposed, 1)

            @block.vector
            def _(dve):
                chain = Chain(dve, vec)
                for t in range(TT):
                    if chunks:
                        dve.wait_ge(projected, t + 1)
                        if gated is not None:
                            chain.step(nc.vector.tensor_tensor(m.x[:, t, :], m.x[:, t, :], m.xn[:, t, :], ALU.add))
                            nc.vector.scalar_tensor_tensor(m.x[:, t, :], proj[t % 2][:, :], gated[:, t:t + 1],
                                                           m.x[:, t, :], ALU.mult, ALU.add).then_inc(added, 1)
                        else:
                            nc.vector.tensor_tensor(m.x[:, t, :], m.x[:, t, :], proj[t % 2][:, :],
                                                    ALU.add).then_inc(added, 1)
                        dve.wait_ge(added, t + 1)
                    if norm:
                        chain.step(nc.vector.bn_stats(stats[:, t, :], m.x[:, t, :]))
                        last = nc.vector.bn_aggr(mv[:, t, :], stats[:, t, :])
                if norm:
                    chain.step(last)
                    nc.vector.tensor_scalar(rstd[:, :], mv[:, :, 1], LN_EPS, None, ALU.add).then_inc(var_ready, 1)
                    dve.wait_ge(std_ready, 1)
                    chain.step(nc.vector.reciprocal(rstd[:, :], rstd[:, :]))
                    for t in range(TT):
                        nc.vector.tensor_scalar(m.xn[:, t, :], m.x[:, t, :], mv[:, t, 0:1], rstd[:, t:t + 1],
                                                ALU.subtract, ALU.mult).then_inc(xn_ready, 1)

            @block.scalar
            def _(act):
                if norm:
                    act.wait_ge(var_ready, 1)
                    nc.scalar.activation(rstd[:, :], rstd[:, :], ACT.Sqrt).then_inc(std_ready, 1)
                    for t in range(TT):
                        act.wait_ge(transposed, t + 1)
                        nc.scalar.copy(m.xnT[:, :, t * P:(t + 1) * P], tps[t % 2][:, :, :]).then_inc(evacuated, 1)


def feature_major_block(nc, m, jobs, loads):
    ctx, sb, ps, sem = scope(nc, m)
    pieces = [(j, c, h) for j in range(len(jobs)) for c in range(jobs[j][1]) for h in range(TOK // HALF)]
    on_act = [jobs[j][5][0] == "gelu" or (jobs[j][5][0] == "linear" and n % 2 == 0)
              for n, (j, c, h) in enumerate(pieces)]
    done_before = [sum(1 for k in range(n) if on_act[k] == on_act[n]) for n in range(len(pieces))]
    with ctx:
        ring = [ps(f"ring{i}", [P, HALF]) for i in range(4)]
        low = sb("low", [P, 2, HALF])
        loaded = sem("loaded")
        filled = sem("filled")
        act_done = sem("act_done")
        dve_done = sem("dve_done")
        vec = sem("vec")
        low_ready = sem("low_ready")
        exp_ready = sem("exp_ready")
        with engines_block(nc, m) as block:

            @block.sync
            def _(sp):
                for buf, dram in loads:
                    sp.dma_start(buf, dram).then_inc(loaded, 16)

            @block.tensor
            def _(pe):
                if loads:
                    pe.wait_ge(loaded, 16 * len(loads))
                for n, (j, c, h) in enumerate(pieces):
                    dst, chunks, w, src, kc, post = jobs[j]
                    if j and c == 0 and h == 0 and src is jobs[j - 1][0]:
                        for q in (k for k in range(n) if pieces[k][0] == j - 1):
                            pe.wait_ge(act_done if on_act[q] else dve_done, done_before[q] + 1)
                    if n >= 4:
                        pe.wait_ge(act_done if on_act[n - 4] else dve_done, done_before[n - 4] + 1)
                    for k in range(kc):
                        last = nc.tensor.matmul(ring[n % 4][:, :], w[:, k, c * P:(c + 1) * P],
                                                src[:, k, h * HALF:(h + 1) * HALF],
                                                start=(k == 0), stop=(k == kc - 1))
                    last.then_inc(filled, 1)

            @block.scalar
            def _(act):
                if loads:
                    act.wait_ge(loaded, 16 * len(loads))
                n_low = 0
                for n, (j, c, h) in enumerate(pieces):
                    dst, chunks, w, src, kc, post = jobs[j]
                    out = dst[:, c, h * HALF:(h + 1) * HALF]
                    if post[0] == "elu1":
                        n_low += 1
                        act.wait_ge(low_ready, n_low)
                        nc.scalar.activation(low[:, (n_low - 1) % 2, :], low[:, (n_low - 1) % 2, :],
                                             ACT.Exp).then_inc(exp_ready, 1)
                    if not on_act[n]:
                        continue
                    act.wait_ge(filled, n + 1)
                    if post[0] == "gelu":
                        nc.scalar.activation(out, ring[n % 4][:, :], ACT.Gelu_apprx_tanh,
                                             bias=post[1][:, c:c + 1]).then_inc(act_done, 1)
                    else:
                        nc.scalar.activation(out, ring[n % 4][:, :], ACT.Copy,
                                             scale=float(post[1])).then_inc(act_done, 1)

            @block.vector
            def _(dve):
                if loads:
                    dve.wait_ge(loaded, 16 * len(loads))
                n_low = 0
                for n, (j, c, h) in enumerate(pieces):
                    if on_act[n]:
                        continue
                    dst, chunks, w, src, kc, post = jobs[j]
                    out = dst[:, c, h * HALF:(h + 1) * HALF]
                    dve.wait_ge(filled, n + 1)
                    if post[0] == "bias":
                        nc.vector.tensor_scalar(out, ring[n % 4][:, :], post[1][:, c:c + 1], float(post[2]),
                                                ALU.add, ALU.mult).then_inc(dve_done, 1)
                    elif post[0] == "elu1":
                        nc.vector.tensor_scalar(low[:, n_low % 2, :], ring[n % 4][:, :], 0.0, None,
                                                ALU.min).then_inc(low_ready, 1)
                        n_low += 1
                        dve.wait_ge(exp_ready, n_low)
                        nc.vector.scalar_tensor_tensor(out, ring[n % 4][:, :], 0.0, low[:, (n_low - 1) % 2, :],
                                                       ALU.max, ALU.add).then_inc(dve_done, 1)
                    else:
                        nc.vector.tensor_scalar(out, ring[n % 4][:, :], float(post[1]), None,
                                                ALU.mult).then_inc(dve_done, 1)


RAW = 2 * P + DC


class Ring:

    def __init__(self, first, turn, last, tail):
        assert len(turn) % 2 == 0
        self.turn, self.last = len(turn), last
        self.at = {key: n for n, key in enumerate(first)}
        self.at.update({key: n + len(first) for n, key in enumerate(turn)})
        self.tail = {key: n + self.at[tail[0]] for n, key in enumerate(tail)}

    def __call__(self, i, *key):
        if key[0] == "first":
            n, i = self.at[key], 0
        elif isinstance(i, int) and i == self.last and key in self.tail:
            n = self.tail[key]
        else:
            n = self.at[key]
        return n % 2, i * (self.turn // 2) + n // 2


def cross_attention_blocks(nc, m, heads, dh, d, t):
    F32R = mybir.dt.float32r
    nch = heads * dh // P
    hpc = P // dh
    scale = dh ** -0.5
    biased = d["bq"] is not None
    KT = [min(P, KEYS - n * P) for n in range(MT)]
    ctx, sb, ps, sem = scope(nc, m)
    with ctx:
        wk = sb("wk", [P, heads, 2 * P])
        wv1 = sb("wv1", [P, heads * dh])
        wv2 = sb("wv2", [P, heads * dh])
        wkb = sb("wkb", [P, heads])
        bvb = sb("bv_rows", [P, heads * dh]) if biased else None
        bq = sb("bq", [P, nch])
        qT = m.featT
        inner, sb2, _, _ = scope(nc, m)
        with inner:
            wq = sb2("wq", [P, KD, heads * dh])
            loads = [(wq[:, :, :], d["wq"])]
            if biased:
                loads.append((bq[:, :], d["bq"]))
            feature_major_block(
                nc, m, [(qT, nch, wq, m.xnT, KD, ("bias", bq, scale) if biased else ("linear", scale))], loads)

        raw = sb("raw", [P, 2, RAW])
        kHX = sb("kHX", [P, 2, 2 * P], F32R)
        kL0 = sb("kL0", [P, 2, P], F32R)
        kS = sb("kS", [P, 2, P], F32R)
        vHL = sb("vHL", [P, 2, 3 * P], F32R)
        cb1 = sb("ctx_bf1", [P, KEYS], BF16)
        cb2 = sb("ctx_bf2", [SEQ + 1, KEYS], BF16)
        qb1 = sb("q_bf1", [P, TOK], BF16)
        qb2 = sb("q_bf2", [SEQ + 1, TOK], BF16)
        qH0 = sb("qH0", [P, 2, TOK], F32R)
        qL0 = sb("qL0", [P, 2, TOK], F32R)
        qH1 = sb("qH1", [P, 2, TOK], F32R)
        qS = sb("qS", [P, 2, TOK], F32R)
        shift = sb("shift", [SEQ + 1, TOK])
        e = sb("e", [P, 2, TOK])
        eH = sb("eH", [P, 2, TOK], F32R)
        eL = sb("eL", [P, 2, TOK], F32R)
        es = sb("e_sum", [P, TOK])
        pt1, pt2 = m.xnT[:, 0, :], m.xnT[:, 1, :]
        mx = sb("max_parts", [P, 8, 2])
        nmx = sb("neg_max", [P, 8])
        rsum = sb("rsum", [SEQ, heads])
        o = sb("o_tok", [SEQ, heads * dh])
        ones = sb("ones_col", [P, 1])
        pair = [ps("pair0", [P, 2, HALF]), ps("pair1", [P, 2, HALF])]
        acc1 = ps("acc1", [P, 2, HALF])
        acc2 = ps("acc2", [P, 2, HALF])

        weights_in = sem("weights_in")
        set_up = sem("set_up")
        raw_in = [sem(f"raw_in{k}") for k in range(2)]
        bf_in, bf_before = m.bf_in, m.bf_in_count
        m.bf_in_count += BATCH * 32
        k_hi, k_lo = sem("k_hi"), sem("k_lo")
        v_hi, v_lo = sem("v_hi"), sem("v_lo")
        full = [sem(f"full{p}") for p in range(2)]
        free = [sem(f"free{p}") for p in range(2)]
        q_hi = sem("q_hi")
        bias_row = sem("bias_row")
        q_cast = sem("q_cast")
        max_ready = sem("max_ready")
        shifted = sem("shifted")
        summed = sem("summed")
        eH_ready = sem("eH_ready")
        eL_ready = sem("eL_ready")
        es_added = sem("es_added")
        pooled = sem("pooled")
        pooled_out = sem("pooled_out")
        REST = KEYS - TOK

        def prologue_items():
            return [("first", "qA"), ("first", "qB")] + [("first", "qK")] * biased + \
                   [("first", f"m{h}", j) for j in range(8) for h in range(2)] + [("first", "neg")]

        def batch_items(u, follows):
            for n in range(MT):
                yield (u, "s", n)
                if n == 0 and follows:
                    yield from [(u, "qA"), (u, "qB")] + [(u, "qK")] * biased
                if 1 <= n <= 8 and follows:
                    yield from [(u, "m0", n - 1), (u, "m1", n - 1)]
                if n == 10 and follows:
                    yield (u, "neg")
            yield from [(u, "S"), (u, "O"), (u, "T")]

        ring = Ring(prologue_items(), [x for u in range(2) for x in batch_items(u, True)],
                    BATCH // 2 - 1, list(batch_items(1, False)))

        def each_batch(eng, body):
            with eng.Fori(0, BATCH // 2 - 1) as i:
                for u in range(2):
                    body(i, u, i * 2 + u, True)
            for u in range(2):
                body(BATCH // 2 - 1, u, BATCH - 2 + u, u == 0)

        def tile(i, u, n):
            return i * (2 * MT) + (u * MT + n)

        with engines_block(nc, m) as block:

            @block.sync
            def _(sp):
                for buf, dram in ((wk[:, :, :], d["wk"]), (wv1[:, :], d["wv1"]), (wv2[:, :], d["wv2"]),
                                  (m.wo[:, 0:nch, :], d["wo"]), (m.bo[:, :], d["bo"])):
                    sp.dma_start(buf, dram).then_inc(weights_in, 16)
                if biased:
                    sp.dma_start(wkb[:, :], d["wkb"]).then_inc(weights_in, 16)
                    sp.dma_start(bvb[:, :], d["bvb"]).then_inc(weights_in, 16)
                with sp.Fori(0, BATCH // 2) as i:
                    for k in range(2 * MT):
                        g = i * (2 * MT) + k
                        sp.wait_ge(v_lo, g + 1)
                        sp.dma_start(raw[:, k % 2, :], t["ctx_tiles"][bass.ds(g, 1)]
                                     .rearrange("o p n -> p (o n)")).then_inc(raw_in[k % 2], 16)

            @block.gpsimd
            def _(pool):
                pool.sem_inc(free[0], 1)
                pool.sem_inc(free[1], 1)
                pool.sem_inc(es_added, 2)
                nc.gpsimd.memset(ones[:, :], 1.0).then_inc(set_up, 1)
                for k in range(2):
                    nc.gpsimd.memset(kS[:, k, :].bitcast(F32), 0.0).then_inc(set_up, 1)
                    nc.gpsimd.memset(qS[:, k, :].bitcast(F32), 0.0).then_inc(set_up, 1)
                pool.wait_ge(set_up, 5)
                for row in (SEQ, SEQ + 32):
                    nc.gpsimd.memset(kS[row:row + 1, :, :].bitcast(F32), 1.0).then_inc(set_up, 1)
                nc.gpsimd.memset(cb2[SEQ:SEQ + 1, :], 1.0).then_inc(set_up, 1)

                def load_bf(b):
                    pool.dma_start(cb1[:, :], t["ctxT1"][bass.ds(b, 1)].rearrange("o p n -> p (o n)")).then_inc(bf_in, 16)
                    pool.dma_start(cb2[0:SEQ, :], t["ctxT2"][bass.ds(b, 1)].rearrange("o p n -> p (o n)")).then_inc(bf_in, 16)

                def cast(i, who, b, s):
                    pool.wait_ge(q_hi, b * 2 + 2)
                    hold_waits(pool, m)
                    nc.gpsimd.tensor_copy(qb1[:, :], qH0[:, s, :].bitcast(F32)).then_inc(q_cast, 1)
                    nc.gpsimd.tensor_copy(qb2[0:SEQ, :], qH1[0:SEQ, s, :].bitcast(F32)).then_inc(q_cast, 1)

                load_bf(0)
                cast(0, "first", 0, 0)

                def body(i, u, b, follows):
                    if follows:
                        pool.wait_ge(max_ready, b + 1)
                        load_bf(b + 1)
                    for n in range(MT):
                        p, k = ring(i, u, "s", n)
                        pool.wait_ge(free[p], k + 2)
                        g = tile(i, u, n)
                        if n:
                            pool.wait_ge(es_added, g + 2)
                            nc.gpsimd.tensor_tensor(es[0:KT[n], :], es[0:KT[n], :], e[0:KT[n], (u * MT + n) % 2, :],
                                                    ALU.add).then_inc(es_added, 1)
                        else:
                            pool.wait_ge(es_added, g + 2)
                            hold_waits(pool, m)
                            nc.gpsimd.tensor_copy(es[:, :], e[:, (u * MT + n) % 2, :]).then_inc(es_added, 1)
                        if n == 0 and follows:
                            cast(i, u, b + 1, 1 - u)

                each_batch(pool, body)

            @block.tensor
            def _(pe):
                pe.wait_ge(weights_in, 16 * (7 if biased else 5))
                pe.wait_ge(set_up, 8)

                def fill(i, *key):
                    p, k = ring(i, *key)
                    pe.wait_ge(free[p], k + 1)
                    return pair[p], full[p]

                def project(i, who, b):
                    for name, c0, rows in (("qA", 0, P), ("qB", P, P)) + ((("qK", None, 1),) if biased else ()):
                        dst, done = fill(i, who, name)
                        hold_waits(pe, m)
                        for h in range(heads):
                            w = wkb[:, h:h + 1] if c0 is None else wk[:, h, c0:c0 + P]
                            last = nc.tensor.matmul(dst[0:rows, h // 8, (h % 8) * SEQ:(h % 8 + 1) * SEQ], w,
                                                    qT[:, h // hpc, bass.ds(b * SEQ, SEQ)], start=True, stop=True)
                        last.then_inc(done, 1)

                def max_part(i, who, j, half, b):
                    if j == 0 and half == 0:
                        pe.wait_ge(q_cast, b * 2 + 2)
                        pe.wait_ge(bf_in, b * 32 + bf_before + 32)
                        if biased:
                            pe.wait_ge(bias_row, b * 2 + 2)
                    dst, done = fill(i, who, f"m{half}", j)
                    rows = SEQ + biased
                    for h, a, z in (((0, 0, HALF), (1, HALF, TOK)), ((0, TOK, TOK + HALF), (1, TOK + HALF, KEYS)))[half]:
                        nc.tensor.matmul(dst[:, h, 0:z - a], qb1[:, j * P:(j + 1) * P], cb1[:, a:z], start=True, stop=False)
                        last = nc.tensor.matmul(dst[:, h, 0:z - a], qb2[0:rows, j * P:(j + 1) * P], cb2[0:rows, a:z],
                                                start=False, stop=True)
                    last.then_inc(done, 1)

                def shift_row(i, who, b):
                    pe.wait_ge(max_ready, b + 1)
                    dst, done = fill(i, who, "neg")
                    for j in range(8):
                        last = nc.tensor.matmul(flat(dst[0:1, :, :])[:, j * P:(j + 1) * P], nmx[:, j:j + 1], m.ident[:, :],
                                                start=True, stop=True)
                    last.then_inc(done, 1)

                def scores(i, u, b, n):
                    g, s = tile(i, u, n), (u * MT + n) % 2
                    if n == 0:
                        pe.wait_ge(summed, b + 1)
                    pe.wait_ge(k_lo, g + 1)
                    dst, done = fill(i, u, "s", n)
                    for h in range(2):
                        cols = slice(h * HALF, (h + 1) * HALF)
                        out = dst[0:KT[n], h, :]
                        for x, (w, q) in enumerate((
                                (kHX[:, s, 0:KT[n]], qH0[:, u, cols]), (kHX[:, s, 0:KT[n]], qL0[:, u, cols]),
                                (kL0[:, s, 0:KT[n]], qH0[:, u, cols]), (kHX[:, s, P:P + KT[n]], qH1[:, u, cols]),
                                (kS[0:SEQ + 33, s, 0:KT[n]], qS[0:SEQ + 33, u, cols]))):
                            last = nc.tensor.matmul(out, w, q, start=(x == 0), stop=(x == 4))
                    last.then_inc(done, 1)

                def pool_tile(i, u, b, n):
                    g, s = tile(i, u, n), (u * MT + n) % 2
                    pe.wait_ge(eL_ready, g + 3)
                    pe.wait_ge(v_lo, g + 3)
                    if n == 0:
                        pe.wait_ge(pooled_out, b * 2 + 2)
                    r = slice(0, KT[n])
                    for h in range(2):
                        cols = slice(h * HALF, (h + 1) * HALF)
                        hi, lo = eH[r, s, cols], eL[r, s, cols]
                        low = vHL[r, s, P:2 * P]
                        nc.tensor.matmul(acc1[:, h, :], vHL[r, s, 0:P], hi, start=(n == 0), stop=False)
                        nc.tensor.matmul(acc1[:, h, :], vHL[r, s, 0:P], lo, start=False, stop=False)
                        nc.tensor.matmul(acc1[:, h, :], vHL[r, s, 2 * P:3 * P], hi, start=False, stop=(n == MT - 1))
                        nc.tensor.matmul(acc2[:, h, :], low, hi, start=(n == 0), stop=False)
                        last = nc.tensor.matmul(acc2[:, h, :], low, lo, start=False, stop=(n == MT - 1))
                    last.then_inc(pooled, 1)

                def finish(i, u, b):
                    pe.wait_ge(es_added, tile(i, u, MT - 1) + 3)
                    dst, done = fill(i, u, "S")
                    for h in range(heads):
                        last = nc.tensor.matmul(dst[0:SEQ, 0, h:h + 1], es[:, h * SEQ:(h + 1) * SEQ], ones[:, :],
                                                start=True, stop=True)
                    last.then_inc(done, 1)
                    pe.wait_ge(pooled_out, b * 2 + 4)
                    dst, done = fill(i, u, "O")
                    for h in range(heads):
                        cols, rows = slice(h * dh, (h + 1) * dh), slice(h * SEQ, (h + 1) * SEQ)
                        out = flat(dst[0:SEQ, :, :])[:, cols]
                        nc.tensor.matmul(out, pt1[:, rows], wv1[:, cols], start=True, stop=False)
                        last = nc.tensor.matmul(out, pt2[:, rows], wv2[:, cols], start=False, stop=not biased)
                        if biased:
                            last = nc.tensor.matmul(out, es[:, rows], bvb[:, cols], start=False, stop=True)
                    last.then_inc(done, 1)
                    p, k = ring(i, u, "O")
                    pe.wait_ge(free[p], k + 2)
                    dst, done = fill(i, u, "T")
                    hold_waits(pe, m)
                    for c in range(nch):
                        last = nc.tensor.transpose(dst[:, 0, c * SEQ:(c + 1) * SEQ], o[:, c * P:(c + 1) * P],
                                                   m.ident[0:SEQ, 0:SEQ])
                    last.then_inc(done, 1)

                project(0, "first", 0)
                for j in range(8):
                    max_part(0, "first", j, 0, 0)
                    max_part(0, "first", j, 1, 0)
                shift_row(0, "first", 0)

                def body(i, u, b, follows):
                    for n in range(MT):
                        scores(i, u, b, n)
                        if n == 0 and follows:
                            project(i, u, b + 1)
                        if 1 <= n <= 8 and follows:
                            max_part(i, u, n - 1, 0, b + 1)
                        if n:
                            pool_tile(i, u, b, n - 1)
                        if 1 <= n <= 8 and follows:
                            max_part(i, u, n - 1, 1, b + 1)
                        if n == 10 and follows:
                            shift_row(i, u, b + 1)
                    pool_tile(i, u, b, MT - 1)
                    finish(i, u, b)

                each_batch(pe, body)

            @block.scalar
            def _(act):
                act.sem_inc(pooled_out, 2)
                act.wait_ge(set_up, 8)

                def split_keys(g, s, k):
                    act.wait_ge(raw_in[s], k)
                    nc.scalar.copy(kHX[:, s, :], raw[:, s, 0:2 * P])
                    nc.scalar.copy(kS[0:SEQ, s, :], raw[0:SEQ, s, P:2 * P]).then_inc(k_hi, 1)

                def split_values(g, s):
                    act.wait_ge(pooled, g + 1)
                    nc.scalar.copy(vHL[:, s, 0:DC], raw[:, s, 2 * P:RAW]).then_inc(v_hi, 1)

                def round_q(i, who, b, s):
                    for x, dst in (("qA", qH0), ("qB", qH1)):
                        p, k = ring(i, who, x)
                        act.wait_ge(full[p], k + 1)
                        nc.scalar.copy(dst[:, s, :], flat(pair[p][:, :, :])).then_inc(q_hi, 1)
                    if biased:
                        p, k = ring(i, who, "qK")
                        act.wait_ge(full[p], k + 1)
                        nc.scalar.copy(shift[SEQ:SEQ + 1, :], flat(pair[p][0:1, :, :])).then_inc(bias_row, 1)
                        act.wait_ge(bias_row, b * 2 + 1)
                        nc.scalar.copy(qb2[SEQ:SEQ + 1, :], shift[SEQ:SEQ + 1, :]).then_inc(bias_row, 1)

                round_q(0, "first", 0, 0)
                split_keys(0, 0, 16)
                split_values(0, 0)
                split_keys(1, 1, 16)

                def body(i, u, b, follows):
                    for n in range(MT):
                        g, s = tile(i, u, n), (u * MT + n) % 2
                        r = slice(0, KT[n])
                        p, k = ring(i, u, "s", n)
                        act.wait_ge(full[p], k + 1)
                        act.wait_ge(eL_ready, g + 1)
                        act.wait_ge(es_added, g + 1)
                        nc.scalar.activation(e[r, s, :], flat(pair[p][r, :, :]), ACT.Exp).then_inc(free[p], 1)
                        act.wait_ge(free[p], k + 2)
                        act.wait_ge(pooled, g + 1)
                        nc.scalar.copy(eH[r, s, :], e[r, s, :]).then_inc(eH_ready, 1)
                        if n == 0 and follows:
                            round_q(i, u, b + 1, 1 - u)
                        if follows or n < MT - 2:
                            split_keys(g + 2, s, i * (MT * 16) + ((u * MT + n + 2) // 2 + 1) * 16)
                        if follows or n < MT - 1:
                            split_values(g + 1, 1 - s)
                    act.wait_ge(pooled, tile(i, u, MT - 1) + 3)
                    nc.scalar.copy(pt1, flat(acc1[:, :, :])).then_inc(pooled_out, 1)
                    p, k = ring(i, u, "T")
                    act.wait_ge(full[p], k + 1)
                    nc.scalar.copy(m.featT[:, 0:nch, bass.ds(b * SEQ, SEQ)],
                                   pair[p][:, 0, 0:nch * SEQ].rearrange("p (c n) -> p c n", c=nch)).then_inc(free[p], 1)

                each_batch(act, body)

            @block.vector
            def _(dve):
                dve.sem_inc(v_lo, 2)
                dve.sem_inc(eL_ready, 2)
                dve.sem_inc(pooled, 2)
                dve.wait_ge(set_up, 8)

                def split_keys(g, s):
                    dve.wait_ge(k_hi, g + 1)
                    nc.vector.tensor_tensor(kL0[:, s, :], raw[:, s, 0:P], kHX[:, s, 0:P].bitcast(F32), ALU.subtract)
                    low = kHX[SEQ:P, s, P:2 * P]
                    nc.vector.tensor_tensor(low, raw[SEQ:P, s, P:2 * P], low.bitcast(F32), ALU.subtract).then_inc(k_lo, 1)

                def split_values(g, s):
                    dve.wait_ge(v_hi, g + 1)
                    nc.vector.tensor_tensor(vHL[:, s, 2 * P:3 * P], raw[:, s, 2 * P:3 * P], vHL[:, s, 0:P].bitcast(F32),
                                            ALU.subtract)
                    nc.vector.tensor_tensor(vHL[:, s, DC:2 * P], raw[:, s, 3 * P:RAW], vHL[:, s, P:DC].bitcast(F32),
                                            ALU.subtract).then_inc(v_lo, 1)

                def split_q(i, who, b, s):
                    for x, (name, hi, lo, r) in enumerate((("qA", qH0, qL0, P), ("qB", qH1, qS, SEQ))):
                        p, k = ring(i, who, name)
                        dve.wait_ge(q_hi, b * 2 + x + 1)
                        nc.vector.tensor_tensor(lo[0:r, s, :], flat(pair[p][0:r, :, :]), hi[0:r, s, :].bitcast(F32),
                                                ALU.subtract).then_inc(free[p], 1)
                    if biased:
                        p, k = ring(i, who, "qK")
                        dve.wait_ge(bias_row, b * 2 + 1)
                        dve.sem_inc(free[p], 1)

                def max_part(i, who, j, half):
                    p, k = ring(i, who, f"m{half}", j)
                    dve.wait_ge(full[p], k + 1)
                    nc.vector.tensor_reduce(mx[:, j, half:half + 1], flat(pair[p][:, :, :])[:, 0:(TOK, REST)[half]],
                                            AX.X, ALU.max).then_inc(free[p], 1)

                def max_all(i, who):
                    for half in range(2):
                        p, k = ring(i, who, f"m{half}", 7)
                        dve.wait_ge(free[p], k + 2)
                    nc.vector.tensor_reduce(nmx[:, :], mx[:, :, :], AX.X, ALU.max, negate=True).then_inc(max_ready, 1)

                def shift_row(i, who, b, s):
                    p, k = ring(i, who, "neg")
                    dve.wait_ge(full[p], k + 1)
                    row, hi, lo = shift[SEQ:SEQ + 1, :], qS[SEQ:SEQ + 1, s, :], qS[SEQ + 32:SEQ + 33, s, :]
                    if biased:
                        dve.wait_ge(bias_row, b * 2 + 2)
                        nc.vector.tensor_tensor(row, flat(pair[p][0:1, :, :]), row, ALU.add).then_inc(free[p], 1)
                    else:
                        nc.vector.tensor_copy(row, flat(pair[p][0:1, :, :])).then_inc(free[p], 1)
                    dve.wait_ge(free[p], k + 2)
                    nc.vector.tensor_copy(hi, row).then_inc(shifted, 1)
                    dve.wait_ge(shifted, b + 1)
                    nc.vector.tensor_tensor(lo, row, hi.bitcast(F32), ALU.subtract).then_inc(summed, 1)

                split_q(0, "first", 0, 0)
                split_keys(0, 0)
                split_values(0, 0)
                split_keys(1, 1)
                for j in range(8):
                    max_part(0, "first", j, 0)
                    max_part(0, "first", j, 1)
                max_all(0, "first")
                shift_row(0, "first", 0, 0)

                def body(i, u, b, follows):
                    for n in range(MT):
                        g, s = tile(i, u, n), (u * MT + n) % 2
                        r = slice(0, KT[n])
                        if 1 <= n <= 8 and follows:
                            max_part(i, u, n - 1, 0)
                        dve.wait_ge(eH_ready, g + 1)
                        nc.vector.tensor_tensor(eL[r, s, :], e[r, s, :], eH[r, s, :].bitcast(F32),
                                                ALU.subtract).then_inc(eL_ready, 1)
                        if n == 0 and follows:
                            split_q(i, u, b + 1, 1 - u)
                        if follows or n < MT - 2:
                            split_keys(g + 2, s)
                        if follows or n < MT - 1:
                            split_values(g + 1, 1 - s)
                        if 1 <= n <= 8 and follows:
                            max_part(i, u, n - 1, 1)
                        if n == 8 and follows:
                            max_all(i, u)
                        if n == 10 and follows:
                            shift_row(i, u, b + 1, 1 - u)
                    dve.wait_ge(pooled, tile(i, u, MT - 1) + 3)
                    nc.vector.tensor_copy(pt2, flat(acc2[:, :, :])).then_inc(pooled_out, 1)
                    p, k = ring(i, u, "S")
                    dve.wait_ge(full[p], k + 1)
                    nc.vector.reciprocal(rsum[:, :], pair[p][0:SEQ, 0, 0:heads]).then_inc(free[p], 1)
                    dve.wait_ge(free[p], k + 2)
                    p, k = ring(i, u, "O")
                    dve.wait_ge(full[p], k + 1)
                    nc.vector.tensor_tensor(
                        o[:, :].rearrange("p (h d) -> p h d", h=heads),
                        flat(pair[p][0:SEQ, :, :])[:, 0:heads * dh].rearrange("p (h d) -> p h d", h=heads),
                        rsum[:, :].unsqueeze(2).to_broadcast([SEQ, heads, dh]), ALU.mult).then_inc(free[p], 1)

                each_batch(dve, body)


def token_major_block(nc, m, jobs, loads):
    ctx, sb, ps, sem = scope(nc, m)
    with ctx:
        ring = [ps(f"ring{i}", [P, HALF]) for i in range(4)]
        loaded = sem("loaded")
        filled = sem("filled")
        act_done = sem("act_done")
        dve_done = sem("dve_done")
        pieces = [(j, t) for t in range(TT) for j in range(len(jobs))]
        with engines_block(nc, m) as block:

            @block.sync
            def _(sp):
                for buf, dram in loads:
                    sp.dma_start(buf, dram).then_inc(loaded, 16)

            @block.tensor
            def _(pe):
                if loads:
                    pe.wait_ge(loaded, 16 * len(loads))
                for n, (j, t) in enumerate(pieces):
                    dst, w, src, kc, bias = jobs[j]
                    cols = dst.shape[-1]
                    if n >= 4:
                        pe.wait_ge(act_done if n % 2 == 0 else dve_done, (n - 4) // 2 + 1)
                    for k in range(kc):
                        last = nc.tensor.matmul(ring[n % 4][:, 0:cols], src[:, k, t * P:(t + 1) * P], w[:, k, :],
                                                start=(k == 0), stop=(k == kc - 1 and bias is None))
                    if bias is not None:
                        last = nc.tensor.matmul(ring[n % 4][:, 0:cols], m.ones[0:1, :], bias, start=False, stop=True)
                    last.then_inc(filled, 1)

            @block.scalar
            def _(act):
                for n, (j, t) in enumerate(pieces):
                    if n % 2 == 0:
                        dst = jobs[j][0]
                        act.wait_ge(filled, n + 1)
                        nc.scalar.copy(dst[:, t, :], ring[n % 4][:, 0:dst.shape[-1]]).then_inc(act_done, 1)

            @block.vector
            def _(dve):
                for n, (j, t) in enumerate(pieces):
                    if n % 2 == 1:
                        dst = jobs[j][0]
                        dve.wait_ge(filled, n + 1)
                        nc.vector.tensor_copy(dst[:, t, :], ring[n % 4][:, 0:dst.shape[-1]]).then_inc(dve_done, 1)


def self_attention_block(nc, m, heads, dh, qT, kT, v, loads, mask_dram, causal_dram=None, o_out=None):
    nch = heads * dh // P
    hpc = P // dh
    W = heads * SEQ
    ctx, sb, ps, sem = scope(nc, m)
    with ctx:
        own = sb("own_head", [P, hpc, SEQ])
        qs = sb("q_now", [P, nch, P])
        kz = sb("k_by_head", [P, 2, nch, hpc * SEQ])
        vz = sb("v_by_head", [P, 2, heads // 2, 2 * dh])
        ex = sb("weights", [P, heads, SEQ])
        exT = sb("weights_T", [P, heads // 2, P])
        o = sb("o_now", [P, heads, dh])
        mx = sb("row_max", [P, heads])
        rs = sb("row_sum", [P, heads])
        tri = sb("causal", [P, SEQ]) if causal_dram is not None else None
        s_ps = ps("scores", [P, W])
        t_ps = ps("weights_T_ps", [P, W])
        o_ps = ps("o_ps", [P, heads * dh])
        ot_ps = ps("oT_ps", [P, nch, P]) if o_out is None else None
        loaded = sem("loaded")
        zeroed = sem("zeroed")
        qk_ready = sem("qk_ready")
        v_ready = sem("v_ready")
        scored = sem("scored")
        shifted = sem("shifted")
        exped = sem("exped")
        transposed = sem("transposed")
        exT_ready = sem("exT_ready")
        weighed = sem("weighed")
        o_ready = sem("o_ready")
        o_transposed = sem("o_transposed")
        o_out_done = sem("o_out_done")
        vec = sem("vec")
        n_loads = len(loads) + 1 + (causal_dram is not None)
        VSTEPS = 3
        with engines_block(nc, m) as block:

            @block.sync
            def _(sp):
                sp.dma_start(own[:, :, :], mask_dram).then_inc(loaded, 16)
                if causal_dram is not None:
                    sp.dma_start(tri[:, :], causal_dram).then_inc(loaded, 16)
                for buf, dram in loads:
                    sp.dma_start(buf, dram).then_inc(loaded, 16)

            @block.gpsimd
            def _(pool):
                pool.sem_inc(scored, 1)
                pool.sem_inc(weighed, 1)
                pool.wait_ge(loaded, 16 * n_loads)
                nc.gpsimd.memset(vz[:, :, :, :], 0.0).then_inc(zeroed, 1)
                with pool.Fori(0, TT) as i:
                    pool.wait_ge(scored, i + 1)
                    for e in range(2):
                        for c in range(nch):
                            last = nc.gpsimd.tensor_tensor(
                                kz[:, e, c, :].rearrange("p (h n) -> p h n", h=hpc),
                                kT[:, c, bass.ds(i * P + e * SEQ, SEQ)].unsqueeze(1).to_broadcast([P, hpc, SEQ]),
                                own[:, :, :], ALU.mult)
                            if e == 1 and c == nch - 1:
                                last.then_inc(qk_ready, 1)

            @block.tensor
            def _(pe):
                with pe.Fori(0, TT) as i:
                    pe.wait_ge(qk_ready, i * 2 + 2)
                    pe.wait_ge(shifted, i + 1)
                    for e in range(2):
                        for c in range(nch):
                            last = nc.tensor.matmul(s_ps[e * SEQ:(e + 1) * SEQ, c * hpc * SEQ:(c + 1) * hpc * SEQ],
                                                    qs[:, c, e * SEQ:(e + 1) * SEQ], kz[:, e, c, :],
                                                    start=True, stop=True)
                    last.then_inc(scored, 1)
                    pe.wait_ge(exT_ready, i + 1)
                    if causal_dram is None:
                        pe.wait_ge(exped, i + 1)
                    else:
                        pe.wait_ge(shifted, i + 2)
                    for j in range(heads // 2):
                        last = nc.tensor.transpose(t_ps[:, j * P:(j + 1) * P],
                                                   ex[:, 2 * j:2 * j + 2, :].rearrange("p h n -> p (h n)"), m.ident[:, :])
                    last.then_inc(transposed, 1)
                    pe.wait_ge(v_ready, i + 1)
                    pe.wait_ge(o_ready, i + 1)
                    pe.wait_ge(exT_ready, i + 2)
                    hold_waits(pe, m)
                    for e in range(2):
                        for j in range(heads // 2):
                            last = nc.tensor.matmul(o_ps[e * SEQ:(e + 1) * SEQ, j * 2 * dh:(j + 1) * 2 * dh],
                                                    exT[:, j, e * SEQ:(e + 1) * SEQ], vz[:, e, j, :],
                                                    start=True, stop=True)
                    last.then_inc(weighed, 1)
                    if o_out is None:
                        pe.wait_ge(o_out_done, i + 1)
                        pe.wait_ge(o_ready, i + 2)
                        for c in range(nch):
                            last = nc.tensor.transpose(
                                ot_ps[:, c, :], o[:, c * hpc:(c + 1) * hpc, :].rearrange("p h d -> p (h d)"), m.ident[:, :])
                        last.then_inc(o_transposed, 1)

            @block.scalar
            def _(act):
                act.wait_ge(zeroed, 1)
                act.sem_inc(exT_ready, 1)
                act.sem_inc(o_out_done, 1)
                with act.Fori(0, TT) as i:
                    act.wait_ge(scored, i + 1)
                    nc.scalar.copy(qs[:, :, :], qT[:, 0:nch, bass.ds(i * P, P)]).then_inc(qk_ready, 1)
                    act.wait_ge(weighed, i + 1)
                    for e in range(2):
                        for par in range(2):
                            src = v[e * SEQ:(e + 1) * SEQ, bass.ds(i, 1), :].rearrange(
                                "p o (j two d) -> p (o j) two d", two=2, d=dh)[:, :, par, :]
                            last = nc.scalar.copy(
                                vz[par * SEQ:(par + 1) * SEQ, e, :, par * dh:(par + 1) * dh], src)
                            if e == 1 and par == 1:
                                last.then_inc(v_ready, 1)
                    if causal_dram is None:
                        act.wait_ge(shifted, i + 2)
                        nc.scalar.activation(ex[:, :, :], ex[:, :, :], ACT.Exp).then_inc(exped, 1)
                    act.wait_ge(transposed, i + 1)
                    act.wait_ge(weighed, i + 1)
                    nc.scalar.copy(flat(exT[:, :, :]), t_ps[:, :]).then_inc(exT_ready, 1)
                    if o_out is None:
                        act.wait_ge(o_transposed, i + 1)
                        nc.scalar.copy(m.featT[:, 0:nch, bass.ds(i * P, P)], ot_ps[:, :, :]).then_inc(o_out_done, 1)

            @block.vector
            def _(dve):
                dve.sem_inc(shifted, 1)
                dve.sem_inc(o_ready, 1)
                if causal_dram is not None:
                    dve.wait_ge(loaded, 16 * n_loads)
                s3 = s_ps[:, :].rearrange("p (h n) -> p h n", h=heads)
                with dve.Fori(0, TT) as i:
                    chain = Chain(dve, vec, i * VSTEPS, VSTEPS)
                    dve.wait_ge(scored, i + 2)
                    if causal_dram is None:
                        chain.step(nc.vector.tensor_reduce(mx[:, :], s3, AX.X, ALU.max))
                        dve.wait_ge(weighed, i + 1)
                        nc.vector.tensor_tensor(ex[:, :, :], s3, mx[:, :].unsqueeze(2).to_broadcast([P, heads, SEQ]),
                                                ALU.subtract).then_inc(shifted, 1)
                        dve.wait_ge(exped, i + 1)
                        chain.step(nc.vector.tensor_reduce(rs[:, :], ex[:, :, :], AX.X, ALU.add))
                    else:
                        dve.wait_ge(weighed, i + 1)
                        nc.vector.tensor_tensor(ex[:, :, :], s3, tri[:, :].unsqueeze(1).to_broadcast([P, heads, SEQ]),
                                                ALU.mult).then_inc(shifted, 1)
                        dve.wait_ge(shifted, i + 2)
                        chain.step(nc.vector.tensor_reduce(mx[:, :], ex[:, :, :], AX.X, ALU.add))
                        chain.step(nc.vector.tensor_scalar(rs[:, :], mx[:, :], CLIP, None, ALU.max))
                    chain.step(nc.vector.reciprocal(rs[:, :], rs[:, :]))
                    chain.close()
                    dve.wait_ge(weighed, i + 2)
                    if o_out is None:
                        dve.wait_ge(o_out_done, i + 1)
                        dst = o[:, :, :]
                    else:
                        dst = o_out[:, bass.ds(i, 1), :].rearrange("p o (h d) -> p (o h) d", h=heads)
                    nc.vector.tensor_tensor(dst, o_ps[:, :].rearrange("p (h d) -> p h d", h=heads),
                                            rs[:, :].unsqueeze(2).to_broadcast([P, heads, dh]), ALU.mult).then_inc(o_ready, 1)


def qkv_memory(nc, m, nch, cols):
    ctx, sb, ps, sem = scope(nc, m)
    return ctx, sb, sb("qT", [P, nch, TOK]), sb("kT", [P, nch, TOK]), sb("v", [P, TT, cols])


def latent_attention_layer(nc, m, t):
    ctx, sb, qT, kT, v = qkv_memory(nc, m, KD, D)
    with ctx:
        wq, wqs, wd = (sb(n, [P, KD, c]) for n, c in (("wq", D), ("wqs", D), ("wd", P)))
        wk, wks, wv = (sb(n, [P, 1, D]) for n in ("wk", "wks", "wv"))
        qsT, ksT = sb("qsT", [P, KD, TOK]), sb("ksT", [P, KD, TOK])
        lat = sb("lat", [P, 1, TOK])
        cos, sin = sb("cos", [P, SEQ]), sb("sin", [P, SEQ])
        scale = 0.25
        feature_major_block(
            nc, m,
            [(qT, KD, wq, m.xnT, KD, ("linear", scale)), (qsT, KD, wqs, m.xnT, KD, ("linear", scale)),
             (lat, 1, wd, m.xnT, KD, ("linear", 1.0)), (kT, KD, wk, lat, 1, ("linear", 1.0)),
             (ksT, KD, wks, lat, 1, ("linear", 1.0))],
            [(wq[:, :, :], t["b_wq"]), (wqs[:, :, :], t["b_wqs"]), (wd[:, :, :], t["b_wd"]), (wk[:, :, :], t["b_wk"]),
             (wks[:, :, :], t["b_wks"]), (wv[:, :, :], t["b_wv"]), (cos[:, :], t["rope_cos"]), (sin[:, :], t["rope_sin"])])
        rotate_block(nc, m, qT, qsT, kT, ksT, cos, sin)
        token_major_block(nc, m, [(v, wv, lat, 1, None)], [])
        self_attention_block(nc, m, 16, 16, qT, kT, v, [(m.wo[:, 0:KD, :], t["b_wo"])], t["own16"])


def rotate_block(nc, m, qT, qsT, kT, ksT, cos, sin):
    ctx, sb, ps, sem = scope(nc, m)

    def rows(x, c):
        return x[:, c, :].rearrange("p (b n) -> p b n", b=BATCH)

    def table(x):
        return x[:, :].unsqueeze(1).to_broadcast([P, BATCH, SEQ])

    with ctx:
        q_steps, k_steps = sem("q_steps"), sem("k_steps")
        with engines_block(nc, m) as block:

            @block.vector
            def _(dve):
                chain = Chain(dve, q_steps)
                for c in range(KD):
                    nc.vector.tensor_tensor(rows(qT, c), rows(qT, c), table(cos), ALU.mult).then_inc(q_steps, 1)
                    chain.n += 1
                    chain.step(nc.vector.tensor_tensor(rows(qsT, c), rows(qsT, c), table(sin), ALU.mult))
                    chain.step(nc.vector.tensor_tensor(qT[:, c, :], qT[:, c, :], qsT[:, c, :], ALU.add))

            @block.gpsimd
            def _(pool):
                chain = Chain(pool, k_steps)
                for c in range(KD):
                    nc.gpsimd.tensor_tensor(rows(kT, c), rows(kT, c), table(cos), ALU.mult).then_inc(k_steps, 1)
                    chain.n += 1
                    chain.step(nc.gpsimd.tensor_tensor(rows(ksT, c), rows(ksT, c), table(sin), ALU.mult))
                    chain.step(nc.gpsimd.tensor_tensor(kT[:, c, :], kT[:, c, :], ksT[:, c, :], ALU.add))


def biased_attention_layer(nc, m, t):
    ctx, sb, qT, kT, v = qkv_memory(nc, m, KD, D)
    with ctx:
        wq, wk, wv = (sb(n, [P, KD, D]) for n in ("wq", "wk", "wv"))
        bq, bk, bv = sb("bq", [P, KD]), sb("bk", [P, KD]), sb("bv", [1, D])
        feature_major_block(
            nc, m, [(qT, KD, wq, m.xnT, KD, ("bias", bq, 0.25)), (kT, KD, wk, m.xnT, KD, ("bias", bk, 1.0))],
            [(wq[:, :, :], t["e_wq"]), (wk[:, :, :], t["e_wk"]), (wv[:, :, :], t["e_wv"]), (bq[:, :], t["e_bq"]),
             (bk[:, :], t["e_bk"]), (bv[:, :], t["e_bv"]), (m.bo[:, :], t["e_bo"])])
        token_major_block(nc, m, [(v, wv, m.xnT, KD, bv[0:1, :])], [])
        self_attention_block(nc, m, 16, 16, qT, kT, v, [(m.wo[:, 0:KD, :], t["e_wo"])], t["own16"])


def linear_attention_layer(nc, m, t):
    ctx, sb, qT, kT, v = qkv_memory(nc, m, KD, D)
    with ctx:
        wq, wk, wv = (sb(n, [P, KD, D]) for n in ("wq", "wk", "wv"))
        feature_major_block(
            nc, m, [(qT, KD, wq, m.xnT, KD, ("elu1",)), (kT, KD, wk, m.xnT, KD, ("elu1",))],
            [(wq[:, :, :], t["h_wq"]), (wk[:, :, :], t["h_wk"]), (wv[:, :, :], t["h_wv"])])
        token_major_block(nc, m, [(v, wv, m.xnT, KD, None)], [])
        self_attention_block(nc, m, 16, 16, qT, kT, v, [(m.wo[:, 0:KD, :], t["h_wo"])], t["own16"], t["causal"])

FAR = 3.0e38


def top2_steps(nc, chain, logits, rev, masks, tmp, eq, mx):
    _, groups, n = logits.shape

    def spread(x):
        return x[:, :].unsqueeze(2).to_broadcast([P, groups, n])

    ranks = rev[:, :].unsqueeze(1).to_broadcast([P, groups, n])
    for k, (src, out) in enumerate(((logits, masks), (tmp, eq))):
        chain.step(nc.vector.tensor_reduce(mx[:, :], src, AX.X, ALU.max))
        chain.step(nc.vector.tensor_tensor(eq, src, spread(mx), ALU.is_equal))
        chain.step(nc.vector.tensor_tensor(eq, eq, ranks, ALU.mult))
        chain.step(nc.vector.tensor_reduce(mx[:, :], eq, AX.X, ALU.max))
        chain.step(nc.vector.tensor_tensor(out, eq, spread(mx), ALU.is_equal))
        if k == 0:
            chain.step(nc.vector.scalar_tensor_tensor(tmp, out, -FAR, logits, ALU.mult, ALU.add))
    chain.step(nc.vector.tensor_tensor(masks, masks, eq, ALU.add))


def switch_head_layer(nc, m, t):
    H, DH, E = 8, 64, 5
    NX = E * DH
    NG = H * E
    with ExitStack() as whole:
        def big(name, shape):
            return whole.enter_context(nc.sbuf_tensor(name, shape, F32))

        qT, kT = big("c_qT", [P, 4, TOK]), big("c_kT", [P, 4, TOK])
        v = big("c_v", [P, TT, H * DH])
        xvg = big("c_xvg", [P, TT, NX + 2 * NG])
        mask = big("c_mask", [P, TT * 2 * H, E])
        o = big("c_o", [P, TT, H * DH])
        rev = big("c_rev", [P, E])
        wv = big("c_wv", [P, TT, NG])
        ctx, sb, ps, sem = scope(nc, m)
        with ctx:
            wq, wk = sb("wq", [P, KD, H * DH]), sb("wk", [P, KD, H * DH])
            wx = sb("wx", [P, KD, NX + 2 * NG])
            feature_major_block(
                nc, m, [(qT, 4, wq, m.xnT, KD, ("linear", DH ** -0.5)), (kT, 4, wk, m.xnT, KD, ("linear", 1.0))],
                [(wq[:, :, :], t["c_wq"]), (wk[:, :, :], t["c_wk"]), (wx[:, :, :], t["c_wx"]), (rev[:, :], t["rev5"])])
            token_major_block(nc, m, [(xvg, wx, m.xnT, KD, None)], [])
        switch_gates_block(nc, m, xvg, mask, wv, rev, H, E, NX)
        switch_mix_block(nc, m, H, DH, E, "values",
                         lambda i: xvg[:, bass.ds(i, 1), 0:NX].rearrange("p o (e d) -> p (o e) d", e=E)
                         .unsqueeze(2).to_broadcast([P, E, H, DH]),
                         lambda i: wv[:, bass.ds(i, 1), :].rearrange("p o (h e) -> p (o e) h", e=E)
                         .unsqueeze(3).to_broadcast([P, E, H, DH]),
                         "p e h d -> p (h d) e", v)
        self_attention_block(nc, m, H, DH, qT, kT, v, [(m.wo[:, 0:3, :], t["c_wo"])], t["own64"], None, o)
        ctx, sb, ps, sem = scope(nc, m)
        with ctx:
            a = sb("by_expert", [P, TT, NX])
            switch_mix_block(nc, m, H, DH, E, "outputs",
                             lambda i: o[:, bass.ds(i, 1), :].rearrange("p o (h d) -> p o h d", h=H)
                             .to_broadcast([P, E, H, DH]),
                             lambda i: mask[:, bass.ds(i * (2 * H) + H, H), :].rearrange("p h e -> p e h")
                             .unsqueeze(3).to_broadcast([P, E, H, DH]),
                             "p e h d -> p e d h", a)
            to_features_block(nc, m, a, NX)


def switch_gates_block(nc, m, xvg, mask, wv, rev, H, E, NX):
    G = TT * 2 * H
    ctx, sb, ps, sem = scope(nc, m)
    with ctx:
        logits, tmp, eq = (sb(n, [P, G, E]) for n in ("logits", "tmp", "eq"))
        mx = sb("mx", [P, G])
        gathered, gated = sem("gathered"), sem("gated")
        vec = sem("vec")
        gates = xvg[:, :, NX:NX + 2 * H * E]
        with engines_block(nc, m) as block:

            @block.scalar
            def _(act):
                nc.scalar.copy(logits[:, :, :].rearrange("p (t g) e -> p t (g e)", t=TT), gates).then_inc(gathered, 1)
                nc.scalar.activation(wv[:, :, :], gates[:, :, 0:H * E], ACT.Sigmoid).then_inc(gated, 1)

            @block.vector
            def _(dve):
                dve.wait_ge(gathered, 1)
                chain = Chain(dve, vec)
                top2_steps(nc, chain, logits[:, :, :], rev, mask[:, :, :], tmp[:, :, :], eq[:, :, :], mx)
                dve.wait_ge(gated, 1)
                nc.vector.tensor_tensor(wv[:, :, :], wv[:, :, :],
                                        mask[:, :, :].rearrange("p (t g) e -> p t (g e)", t=TT)[:, :, 0:H * E], ALU.mult)


def switch_mix_block(nc, m, H, DH, E, what, left, right, order, dst):
    ctx, sb, ps, sem = scope(nc, m)
    with ctx:
        prod = sb("prod", [P, 2, E, H, DH])
        multiplied, summed = sem("multiplied"), sem("summed")
        with engines_block(nc, m) as block:

            @block.gpsimd
            def _(pool):
                pool.sem_inc(summed, 2)
                with pool.Fori(0, TT // 2) as i:
                    for u in range(2):
                        n = i * 2 + u
                        pool.wait_ge(summed, n + 1)
                        hold_waits(pool, m)
                        for e in range(E):
                            last = nc.gpsimd.tensor_tensor(prod[:, u, e, :, :], left(n)[:, e], right(n)[:, e], ALU.mult)
                        last.then_inc(multiplied, 1)

            @block.vector
            def _(dve):
                with dve.Fori(0, TT // 2) as i:
                    for u in range(2):
                        n = i * 2 + u
                        dve.wait_ge(multiplied, n + 1)
                        src = prod[:, u, :, :, :].rearrange(order)
                        out = dst[:, bass.ds(n, 1), :]
                        if len(src.shape) == 4:
                            out = out.rearrange("p o (e d) -> p (o e) d", e=E)
                        else:
                            out = out.rearrange("p o n -> p (o n)")
                        nc.vector.tensor_reduce(out, src, AX.X, ALU.add).then_inc(summed, 1)


def to_features_block(nc, m, a, cols):
    chunks = -(-cols // P)
    ctx, sb, ps, sem = scope(nc, m)
    with ctx:
        tps = [ps(f"tps{i}", [P, chunks, P]) for i in range(2)]
        transposed, evacuated = sem("transposed"), sem("evacuated")
        with engines_block(nc, m) as block:

            @block.tensor
            def _(pe):
                for n in range(TT):
                    if n >= 2:
                        pe.wait_ge(evacuated, 2 * (n - 1))
                    for c in range(chunks):
                        k = min(P, cols - c * P)
                        last = nc.tensor.transpose(tps[n % 2][0:k, c, :], a[:, n, c * P:c * P + k], m.ident[:, :])
                    last.then_inc(transposed, 1)

            @block.scalar
            def _(act):
                for n in range(TT):
                    act.wait_ge(transposed, n + 1)
                    full = cols // P
                    nc.scalar.copy(m.featT[:, 0:full, n * P:(n + 1) * P], tps[n % 2][:, 0:full, :]).then_inc(evacuated, 1)
                    k = cols - full * P
                    nc.scalar.copy(m.featT[0:k, full, n * P:(n + 1) * P], tps[n % 2][0:k, full, :]).then_inc(evacuated, 1)


def mixture_of_depths_layer(nc, m, t, factor):
    CAP = SEQ // 2
    ctx, sb, ps, sem = scope(nc, m)
    with ctx:
        w1, b1 = sb("w1", [P, KD, 1024]), sb("b1", [P, 8])
        wr = sb("wr", [P, KD])
        before = sb("before", [P, SEQ])
        feature_major_block(
            nc, m, [(m.featT, 8, w1, m.xnT, KD, ("gelu", b1))],
            [(w1[:, :, :], t["f_w1"]), (b1[:, :], t["f_b1"]), (wr[:, :], t["f_wr"]), (before[:, :], t["before"]),
             (m.wo[:, :, :], t["f_w2"]), (m.bo[:, :], t["f_b2"])])
        row = sb("score_row", [1, TOK])
        col = sb("score_col", [P, TT])
        above, equal = sb("above", [P, TT, SEQ]), sb("equal", [P, TT, SEQ])
        rank = sb("rank", [P, TT])
        row_ps, all_ps, col_ps = ps("row_ps", [1, TOK]), ps("all_ps", [P, TOK]), ps("col_ps", [P, TT])
        row_done, row_ready, spread_done, col_ready, sig_ready = (
            sem(n) for n in ("row_done", "row_ready", "spread_done", "col_ready", "sig_ready"))
        vec = sem("vec")
        with engines_block(nc, m) as block:

            @block.tensor
            def _(pe):
                for h in range(2):
                    for k in range(KD):
                        last = nc.tensor.matmul(row_ps[0:1, h * HALF:(h + 1) * HALF], wr[:, k:k + 1],
                                                m.xnT[:, k, h * HALF:(h + 1) * HALF], start=(k == 0), stop=(k == KD - 1))
                last.then_inc(row_done, 1)
                pe.wait_ge(row_ready, 1)
                for h in range(2):
                    nc.tensor.matmul(all_ps[:, h * HALF:(h + 1) * HALF], m.ones[0:1, :], row[0:1, h * HALF:(h + 1) * HALF],
                                     start=True, stop=True)
                for n in range(TT):
                    last = nc.tensor.matmul(col_ps[:, n:n + 1], row[0:1, n * P:(n + 1) * P], m.ones[0:1, 0:1],
                                            start=True, stop=True)
                last.then_inc(spread_done, 1)

            @block.scalar
            def _(act):
                act.wait_ge(row_done, 1)
                nc.scalar.copy(row[:, :], row_ps[:, :]).then_inc(row_ready, 1)
                act.wait_ge(col_ready, 1)
                nc.scalar.activation(factor[:, :], col[:, :], ACT.Sigmoid).then_inc(sig_ready, 1)

            @block.vector
            def _(dve):
                chain = Chain(dve, vec)
                dve.wait_ge(spread_done, 1)
                nc.vector.tensor_copy(col[:, :], col_ps[:, :]).then_inc(col_ready, 1)
                dve.wait_ge(col_ready, 1)
                for op, dst in ((ALU.is_gt, above), (ALU.is_equal, equal)):
                    for e in range(2):
                        rows = slice(e * SEQ, (e + 1) * SEQ)
                        chain.step(nc.vector.tensor_tensor(
                            dst[rows, :, :], all_ps[rows, :].rearrange("p (t e n) -> p t e n", e=2, n=SEQ)[:, :, e, :],
                            col[rows, :].unsqueeze(2).to_broadcast([SEQ, TT, SEQ]), op))
                chain.step(nc.vector.tensor_tensor(equal[:, :, :], equal[:, :, :],
                                                   before[:, :].unsqueeze(1).to_broadcast([P, TT, SEQ]), ALU.mult))
                chain.step(nc.vector.tensor_tensor(above[:, :, :], above[:, :, :], equal[:, :, :], ALU.add))
                chain.step(nc.vector.tensor_reduce(rank[:, :], above[:, :, :], AX.X, ALU.add))
                dve.wait_ge(sig_ready, 1)
                nc.vector.scalar_tensor_tensor(factor[:, :], rank[:, :], float(CAP), factor[:, :], ALU.is_lt, ALU.mult)


def routing_block(nc, m, w_gate, loads, groups, n, weights, rev, bias=None, softmax=False, shared=False):
    G = TT * groups
    N = groups * n
    ctx, sb, ps, sem = scope(nc, m)
    with ctx:
        logits, tmp, eq, mask, val = (sb(x, [P, G, n]) for x in ("logits", "tmp", "eq", "mask", "val"))
        mx, sums = sb("mx", [P, G]), sb("sums", [P, G])
        lps = ps("lps", [P, TT, N])
        loaded, projected, logits_ready, shifted, valued = (
            sem(x) for x in ("loaded", "projected", "logits_ready", "shifted", "valued"))
        vec = sem("vec")

        def spread(x):
            return x[:, :].unsqueeze(2).to_broadcast([P, G, n])

        with engines_block(nc, m) as block:

            @block.sync
            def _(sp):
                for buf, dram in loads:
                    sp.dma_start(buf, dram).then_inc(loaded, 16)

            @block.tensor
            def _(pe):
                pe.wait_ge(loaded, 16 * len(loads))
                for i in range(TT):
                    for k in range(KD):
                        last = nc.tensor.matmul(lps[:, i, :], m.xnT[:, k, i * P:(i + 1) * P], w_gate[:, k, :],
                                                start=(k == 0), stop=(k == KD - 1 and bias is None))
                    if bias is not None:
                        last = nc.tensor.matmul(lps[:, i, :], m.ones[0:1, :], bias, start=False, stop=True)
                last.then_inc(projected, 1)

            @block.scalar
            def _(act):
                act.wait_ge(projected, 1)
                nc.scalar.copy(logits[:, :, :].rearrange("p g n -> p (g n)"), flat(lps[:, :, :])).then_inc(logits_ready, 1)
                if softmax:
                    act.wait_ge(shifted, 1)
                    nc.scalar.activation(val[:, :, :], val[:, :, :], ACT.Exp).then_inc(valued, 1)
                else:
                    act.wait_ge(logits_ready, 1)
                    nc.scalar.activation(val[:, :, :], logits[:, :, :], ACT.Sigmoid).then_inc(valued, 1)

            @block.vector
            def _(dve):
                chain = Chain(dve, vec)
                dve.wait_ge(logits_ready, 1)
                if loads:
                    dve.wait_ge(loaded, 16 * len(loads))
                if softmax:
                    chain.step(nc.vector.tensor_reduce(mx[:, :], logits[:, :, :], AX.X, ALU.max))
                    nc.vector.tensor_tensor(val[:, :, :], logits[:, :, :], spread(mx), ALU.subtract).then_inc(shifted, 1)
                    dve.wait_ge(shifted, 1)
                top2_steps(nc, chain, logits[:, :, :], rev, mask[:, :, :], tmp[:, :, :], eq[:, :, :], mx)
                dve.wait_ge(valued, 1)
                out = weights[:, :, 0:N].rearrange("p t (g n) -> p t g n", g=groups)
                if softmax:
                    chain.step(nc.vector.tensor_reduce(sums[:, :], val[:, :, :], AX.X, ALU.add))
                    chain.step(nc.vector.reciprocal(sums[:, :], sums[:, :]))
                    chain.step(nc.vector.tensor_tensor(val[:, :, :], val[:, :, :], spread(sums), ALU.mult))
                    chain.step(nc.vector.scalar_tensor_tensor(val[:, :, :], val[:, :, :], 0.5, mask[:, :, :], ALU.mult, ALU.mult))
                else:
                    chain.step(nc.vector.tensor_tensor(val[:, :, :], val[:, :, :], mask[:, :, :], ALU.mult))
                    chain.step(nc.vector.tensor_reduce(sums[:, :], val[:, :, :], AX.X, ALU.add))
                    chain.step(nc.vector.reciprocal(sums[:, :], sums[:, :]))
                    chain.step(nc.vector.tensor_tensor(val[:, :, :], val[:, :, :], spread(sums), ALU.mult))
                chain.step(nc.vector.tensor_copy(out, val[:, :, :].rearrange("p (t g) n -> p t g n", t=TT)))
                if shared:
                    nc.vector.memset(weights[:, :, N:N + 1], 1.0)


def experts_block(nc, m, n_experts, packed, weights, add_xn):
    I = P
    ctx, sb, ps, sem = scope(nc, m)
    with ctx:
        w = sb("w", [P, 2, 6 * P])
        act_g = sb("silu", [P, 2, HALF])
        hT = sb("hT", [P, 2, HALF])
        g_ps, u_ps = ps("g_ps", [P, 2, HALF]), ps("u_ps", [P, 2, HALF])
        y_ps = [ps(f"y{i}", [P, HALF]) for i in range(4)]
        w_in = [sem(f"w_in{u}") for u in range(2)]
        gu_done = sem("gu_done")
        silu_done = sem("silu_done")
        h_ready = sem("h_ready")
        y_done = sem("y_done")
        y_added = sem("y_added")
        xn_added = sem("xn_added")

        def sync_turn(sp, e, i, u):
            sp.wait_ge(y_done, e * TT + 8)
            sp.dma_start(w[:, u, :], packed[bass.ds(e, 1)].rearrange("o p n -> p (o n)")).then_inc(w_in[u], 16)

        def pe_turn(pe, e, i, u):
            pe.wait_ge(w_in[u], i * 16 + 16)
            for h in range(2):
                pe.wait_ge(h_ready, e * 2 + h + 1)
                for dst, col in ((g_ps, 0), (u_ps, 2 * P)):
                    for k in range(KD):
                        last = nc.tensor.matmul(dst[:, h, :], w[:, u, col + k * P:col + (k + 1) * P],
                                                m.xnT[:, k, h * HALF:(h + 1) * HALF], start=(k == 0), stop=(k == KD - 1))
                last.then_inc(gu_done, 1)
            for n in range(TT):
                h = n // 4
                if n % 4 == 0:
                    pe.wait_ge(h_ready, e * 2 + h + 3)
                pe.wait_ge(y_added, e * TT + n + 1)
                nc.tensor.matmul(y_ps[n % 4][:, 0:D], hT[:, h, (n % 4) * P:(n % 4 + 1) * P], w[:, u, 4 * P:6 * P],
                                 start=True, stop=True).then_inc(y_done, 1)

        def act_turn(act, e, i, u):
            for h in range(2):
                act.wait_ge(gu_done, e * 2 + h + 1)
                act.wait_ge(h_ready, e * 2 + h + 1)
                nc.scalar.activation(act_g[:, h, :], g_ps[:, h, :], ACT.Silu).then_inc(silu_done, 1)

        def dve_turn(dve, e, i, u):
            for h in range(2):
                dve.wait_ge(silu_done, e * 2 + h + 1)
                dve.wait_ge(y_done, e * TT + 4 * h + 12)
                nc.vector.tensor_tensor(hT[:, h, :], act_g[:, h, :], u_ps[:, h, :], ALU.mult).then_inc(h_ready, 1)
            for n in range(TT):
                dve.wait_ge(y_done, e * TT + n + 17)
                dve.wait_ge(y_added, e * TT + n + 1)
                nc.vector.scalar_tensor_tensor(m.x[:, n, :], y_ps[n % 4][:, 0:D],
                                               weights[:, n, bass.ds(e, 1)], m.x[:, n, :],
                                               ALU.mult, ALU.add).then_inc(y_added, 1)

        def turns(eng, body):
            with eng.Fori(0, n_experts // 2) as i:
                for u in range(2):
                    body(eng, i * 2 + u, i, u)
            if n_experts % 2:
                body(eng, n_experts - 1, n_experts // 2, 0)

        with engines_block(nc, m) as block:

            @block.sync
            def _(sp):
                sp.sem_inc(y_done, 16)
                turns(sp, sync_turn)

            @block.tensor
            def _(pe):
                turns(pe, pe_turn)

            @block.scalar
            def _(act):
                turns(act, act_turn)

            @block.vector
            def _(dve):
                dve.sem_inc(h_ready, 2)
                dve.sem_inc(y_added, 4)
                if add_xn:
                    nc.vector.tensor_tensor(flat(m.x[:, :, :]), flat(m.x[:, :, :]), flat(m.xn[:, :, :]),
                                            ALU.add).then_inc(xn_added, 1)
                    dve.wait_ge(xn_added, 1)
                turns(dve, dve_turn)


TWO_PI = 2.0 * np.pi
TWO_PI_HI = 6.28125
TWO_PI_LO = TWO_PI - TWO_PI_HI
ROUND = 1.5 * 2.0 ** 23
N2 = 32


def state_space_kernel_block(nc, m, t, kern):
    ctx, sb, ps, sem = scope(nc, m)
    with ctx:
        S = [P, KD, N2]
        ldt, dt = sb("ldt", [P, KD]), sb("dt", [P, KD])
        are, aim, cre, cim = (sb(x, S) for x in ("are", "aim", "cre", "cim"))
        a, th, em1, ang, turns_, sb1, sb2 = (sb(x, S) for x in ("a", "th", "em1", "ang", "turns", "sin1", "sin2"))
        zr, zi, wr, u, v, w, qr, qi = (sb(x, S) for x in ("zr", "zi", "wr", "u", "v", "w", "qr", "qi"))
        Vr, Vi = sb("Vr", [P, KD, SEQ, N2]), sb("Vi", [P, KD, SEQ, N2])
        t1, t2 = sb("t1", [P, KD, SEQ // 2, N2]), sb("t2", [P, KD, SEQ // 2, N2])
        loaded, exp_ready, small_ready, tanh_ready, ang_ready, sin_ready = (
            sem(x) for x in ("loaded", "exp_ready", "small_ready", "tanh_ready", "ang_ready", "sin_ready"))
        vec = sem("vec")
        with engines_block(nc, m) as block:

            @block.sync
            def _(sp):
                for buf, x in ((ldt, "k_ldt"), (are, "k_lar"), (aim, "k_aim"), (cre, "k_cre"), (cim, "k_cim")):
                    dst = buf[:, :] if x == "k_ldt" else buf[:, :, :]
                    sp.dma_start(dst, t[x]).then_inc(loaded, 16)

            @block.scalar
            def _(act):
                act.wait_ge(loaded, 5 * 16)
                nc.scalar.activation(dt[:, :], ldt[:, :], ACT.Exp).then_inc(exp_ready, 1)
                nc.scalar.activation(are[:, :, :], are[:, :, :], ACT.Exp).then_inc(exp_ready, 1)
                act.wait_ge(small_ready, 1)
                nc.scalar.activation(th[:, :, :], a[:, :, :], ACT.Tanh, scale=0.5).then_inc(tanh_ready, 1)
                act.wait_ge(ang_ready, 1)
                nc.scalar.activation(sb1[:, :, :], ang[:, :, :], ACT.Sin).then_inc(sin_ready, 1)
                nc.scalar.activation(sb2[:, :, :], ang[:, :, :], ACT.Sin, scale=0.5).then_inc(sin_ready, 1)

            @block.vector
            def _(dve):
                chain = Chain(dve, vec)

                def tt(out, x, y, op):
                    chain.step(nc.vector.tensor_tensor(out, x, y, op))

                def ts(out, x, s1, s2, op0, op1):
                    chain.step(nc.vector.tensor_scalar(out, x, s1, s2, op0, op1))

                def spread(x):
                    return x[:, :].unsqueeze(2).to_broadcast(S)

                F = (slice(None),) * 3
                dve.wait_ge(exp_ready, 2)
                ts(are[F], are[F], -1.0, None, ALU.mult, ALU.bypass)
                nc.vector.tensor_tensor(a[F], are[F], spread(dt), ALU.mult).then_inc(small_ready, 1)
                tt(ang[F], aim[F], spread(dt), ALU.mult)
                ts(turns_[F], ang[F], 1.0 / TWO_PI, ROUND, ALU.mult, ALU.add)
                ts(turns_[F], turns_[F], -ROUND, None, ALU.add, ALU.bypass)
                chain.step(nc.vector.scalar_tensor_tensor(ang[F], turns_[F], -TWO_PI_HI, ang[F], ALU.mult, ALU.add))
                chain.step(nc.vector.scalar_tensor_tensor(ang[F], turns_[F], -TWO_PI_LO, ang[F], ALU.mult, ALU.add))
                nc.vector.tensor_scalar(ang[F], ang[F], 3.1415925, -3.1415925, ALU.min, ALU.max).then_inc(ang_ready, 1)
                dve.wait_ge(tanh_ready, 1)
                ts(u[F], th[F], -1.0, 1.0, ALU.mult, ALU.add)
                chain.step(nc.vector.reciprocal(u[F], u[F]))
                chain.step(nc.vector.scalar_tensor_tensor(em1[F], th[F], 2.0, u[F], ALU.mult, ALU.mult))
                ts(v[F], em1[F], 1.0, None, ALU.add, ALU.bypass)
                dve.wait_ge(sin_ready, 2)
                tt(zi[F], v[F], sb1[F], ALU.mult)
                tt(w[F], sb2[F], sb2[F], ALU.mult)
                tt(w[F], w[F], v[F], ALU.mult)
                chain.step(nc.vector.scalar_tensor_tensor(wr[F], w[F], -2.0, em1[F], ALU.mult, ALU.add))
                ts(zr[F], wr[F], 1.0, None, ALU.add, ALU.bypass)
                tt(u[F], are[F], are[F], ALU.mult)
                tt(v[F], aim[F], aim[F], ALU.mult)
                tt(u[F], u[F], v[F], ALU.add)
                chain.step(nc.vector.reciprocal(u[F], u[F]))
                tt(v[F], wr[F], are[F], ALU.mult)
                tt(w[F], zi[F], aim[F], ALU.mult)
                tt(v[F], v[F], w[F], ALU.add)
                tt(qr[F], v[F], u[F], ALU.mult)
                tt(v[F], zi[F], are[F], ALU.mult)
                tt(w[F], wr[F], aim[F], ALU.mult)
                tt(v[F], v[F], w[F], ALU.subtract)
                tt(qi[F], v[F], u[F], ALU.mult)

                def product(outr, outi, xr, xi, yr, yi, s1, s2):
                    tt(s1, xr, yr, ALU.mult)
                    tt(s2, xi, yi, ALU.mult)
                    tt(outr, s1, s2, ALU.subtract)
                    tt(s1, xr, yi, ALU.mult)
                    tt(s2, xi, yr, ALU.mult)
                    tt(outi, s1, s2, ALU.add)

                product(Vr[:, :, 0, :], Vi[:, :, 0, :], cre[F], cim[F], qr[F], qi[F], v[F], w[F])
                n = 1
                while n < SEQ:
                    for c in range(KD):
                        yr, yi = (x[:, c, :].unsqueeze(1).to_broadcast([P, n, N2]) for x in (zr, zi))
                        product(Vr[:, c, n:2 * n, :], Vi[:, c, n:2 * n, :], Vr[:, c, 0:n, :], Vi[:, c, 0:n, :], yr, yi,
                                t1[:, c, 0:n, :], t2[:, c, 0:n, :])
                    n *= 2
                    if n < SEQ:
                        product(u[F], qr[F], zr[F], zi[F], zr[F], zi[F], v[F], w[F])
                        chain.step(nc.vector.tensor_copy(zr[F], u[F]))
                        chain.step(nc.vector.tensor_copy(zi[F], qr[F]))
                chain.step(nc.vector.tensor_reduce(kern[:, :, :], Vr[:, :, :, :], AX.X, ALU.add))
                ts(kern[:, :, :], kern[:, :, :], 2.0, None, ALU.mult, ALU.bypass)


def causal_convolution_block(nc, m, t, kern):
    ctx, sb, ps, sem = scope(nc, m)
    with ctx:
        xpad = sb("xpad", [P, KD, BATCH, 2 * SEQ])
        y = sb("y", [P, KD, TOK])
        loaded, padded, zeroed, summed, copied = (sem(x) for x in ("loaded", "padded", "zeroed", "summed", "copied"))
        with engines_block(nc, m) as block:

            @block.sync
            def _(sp):
                sp.dma_start(m.wo[:, 0:KD, :], t["k_w"]).then_inc(loaded, 16)
                sp.dma_start(m.bo[:, :], t["k_b"]).then_inc(loaded, 16)
                sp.wait_ge(loaded, 32)

            @block.gpsimd
            def _(pool):
                for c in range(KD):
                    nc.gpsimd.memset(xpad[:, c, :, 0:SEQ], 0.0).then_inc(padded, 1)
                nc.gpsimd.memset(y[:, :, :], 0.0).then_inc(zeroed, 1)

            @block.scalar
            def _(act):
                for c in range(KD):
                    nc.scalar.copy(xpad[:, c, :, SEQ:2 * SEQ], m.xnT[:, c, :].rearrange("p (b n) -> p b n", b=BATCH)).then_inc(copied, 1)
                for c in range(KD):
                    act.wait_ge(summed, KD * SEQ + 2)
                    nc.scalar.activation(m.featT[:, c, :], y[:, c, :], ACT.Gelu)

            @block.vector
            def _(dve):
                dve.sem_inc(summed, 2)
                dve.wait_ge(copied, KD)
                dve.wait_ge(padded, KD)
                dve.wait_ge(zeroed, 1)
                with dve.Fori(0, SEQ) as s:
                    for c in range(KD):
                        dve.wait_ge(summed, s * KD + c + 1)
                        hold_waits(dve, m)
                        yc = y[:, c, :].rearrange("p (b n) -> p b n", b=BATCH)
                        nc.vector.scalar_tensor_tensor(yc, xpad[:, c, :, bass.ds(SEQ - s, SEQ)], kern[:, c, bass.ds(s, 1)],
                                                       yc, ALU.mult, ALU.add).then_inc(summed, 1)


MASKED = -30000.0
RMS_EPS = 1e-8


def resampler_layer(nc, m, t):
    H, DH = 4, 64
    HD = H * DH
    with ExitStack() as whole:
        def big(name, shape, dt=F32):
            return whole.enter_context(nc.sbuf_tensor("d_" + name, shape, dt))

        lnT = m.featT
        q_tok, kv_tok = big("q_tok", [P, TT, HD]), big("kv_tok", [P, TT, 2 * HD])
        qT, klT = big("qT", [P, KD, TOK]), big("klT", [P, KD, TOK])
        wq, wlkv = big("wq", [P, KD, HD]), big("wlkv", [P, KD, 2 * HD])
        w1, w2 = big("w1", [P, 2 * HD]), big("w2", [CL, 2 * HD])
        wk = big("wk", [P, H, CA])
        gk, gates = big("gk", [P, 4]), big("gates", [P, 6])
        g_row, b_row = big("g_row", [P, DC]), big("b_row", [P, DC])
        mask_in, mbias = big("mask_in", [P, BATCH, MT], I32), big("mbias", [P, BATCH, MT])
        resampler_prepare_block(nc, m, t, lnT, wq, wlkv, w1, w2, wk, gk, gates, g_row, b_row, mask_in, mbias)
        token_major_block(nc, m, [(q_tok, wq, lnT, KD, None), (kv_tok, wlkv, lnT, KD, None)], [])
        unit_rms_block(nc, m, q_tok, kv_tok, qT, klT, gk, H)
        resampler_attention_block(nc, m, t, H, DH, qT, klT, kv_tok, w1, w2, wk, mbias)


def resampler_prepare_block(nc, m, t, lnT, wq, wlkv, w1, w2, wk, gk, gates, g_row, b_row, mask_in, mbias):
    ctx, sb, ps, sem = scope(nc, m)
    H = 4
    with ctx:
        stats, mv, rstd = sb("stats", [P, TT, 6]), sb("mv", [P, TT, 2]), sb("rstd", [P, TT])
        ln = sb("ln", [P, TT, D])
        tmp = sb("tmp", [P, H, DC])
        bcol = sb("bcol", [P, 2])
        tps = [ps(f"tps{i}", [P, KD, P]) for i in range(2)]
        b_ps = ps("b_ps", [1, HALF])
        loaded, var_ready, std_ready, ln_ready, transposed, evacuated, folded = (
            sem(x) for x in ("loaded", "var_ready", "std_ready", "ln_ready", "transposed", "evacuated", "folded"))
        vec = sem("vec")
        loads = ((wq[:, :, :], "d_wq"), (wlkv[:, :, :], "d_wlkv"), (w1[:, :], "d_w1"), (w2[:, :], "d_w2"),
                 (wk[:, :, :], "d_wk"), (gk[:, :], "d_gk"), (gates[:, :], "d_gates"), (g_row[:, :], "d_g_row"),
                 (b_row[:, :], "d_b_row"), (mask_in[:, :, :], "d_mask"), (bcol[:, :], "d_bcol"),
                 (m.wo[:, 0:KD, :], "d_wo"), (m.bo[:, :], "d_bo"))
        with engines_block(nc, m) as block:

            @block.sync
            def _(sp):
                for buf, name in loads:
                    sp.dma_start(buf, t[name]).then_inc(loaded, 16)

            @block.vector
            def _(dve):
                chain = Chain(dve, vec)
                for n in range(TT):
                    chain.step(nc.vector.bn_stats(stats[:, n, :], m.xn[:, n, :]))
                    last = nc.vector.bn_aggr(mv[:, n, :], stats[:, n, :])
                chain.step(last)
                nc.vector.tensor_scalar(rstd[:, :], mv[:, :, 1], LN_EPS, None, ALU.add).then_inc(var_ready, 1)
                dve.wait_ge(loaded, 16 * len(loads))
                nc.vector.tensor_copy(mbias[:, :, :], mask_in[:, :, :]).then_inc(vec, 1)
                chain.n += 1
                for h in range(H):
                    nc.vector.tensor_tensor(tmp[:, h, :], wk[:, h, 0:DC], b_row[:, :], ALU.mult).then_inc(vec, 1)
                    chain.n += 1
                dve.wait_ge(vec, chain.n)
                nc.vector.tensor_reduce(wk[:, :, DC:CA], tmp[:, :, :], AX.X, ALU.add)
                for h in range(H):
                    nc.vector.tensor_tensor(wk[:, h, 0:DC], wk[:, h, 0:DC], g_row[:, :], ALU.mult)
                nc.vector.tensor_scalar(mbias[:, :, :], mbias[:, :, :], -MASKED, MASKED, ALU.mult, ALU.add)
                dve.wait_ge(folded, 1)
                nc.vector.tensor_scalar(w1[:, :], w1[:, :], gates[:, 4:5], None, ALU.mult)
                nc.vector.tensor_scalar(w2[0:CL - 1, :], w2[0:CL - 1, :], gates[0:CL - 1, 5:6], None, ALU.mult)
                nc.vector.tensor_copy(w2[CL - 1:CL, :], b_ps[:, :])
                nc.vector.scalar_tensor_tensor(gk[:, 2:3], gk[:, 0:1], DHEAD_SCALE, gk[:, 1:2], ALU.mult, ALU.mult)
                dve.wait_ge(std_ready, 1)
                chain.step(nc.vector.reciprocal(rstd[:, :], rstd[:, :]))
                for n in range(TT):
                    nc.vector.tensor_scalar(ln[:, n, :], m.xn[:, n, :], mv[:, n, 0:1], rstd[:, n:n + 1],
                                            ALU.subtract, ALU.mult).then_inc(ln_ready, 1)
                for n in range(TT):
                    dve.wait_ge(transposed, n + 1)
                    for k in range(KD):
                        last = nc.vector.tensor_scalar(lnT[:, k, n * P:(n + 1) * P], tps[n % 2][:, k, :],
                                                       gates[:, k:k + 1], gates[:, 2 + k:3 + k], ALU.mult, ALU.add)
                    last.then_inc(evacuated, 1)

            @block.scalar
            def _(act):
                act.wait_ge(var_ready, 1)
                nc.scalar.activation(rstd[:, :], rstd[:, :], ACT.Sqrt).then_inc(std_ready, 1)

            @block.tensor
            def _(pe):
                pe.wait_ge(loaded, 16 * len(loads))
                nc.tensor.matmul(b_ps[:, :], bcol[:, 0:1], w1[:, :], start=True, stop=False)
                nc.tensor.matmul(b_ps[:, :], bcol[0:CL - 1, 1:2], w2[0:CL - 1, :], start=False, stop=True).then_inc(folded, 1)
                for n in range(TT):
                    pe.wait_ge(ln_ready, n + 1)
                    if n >= 2:
                        pe.wait_ge(evacuated, n - 1)
                    for k in range(KD):
                        last = nc.tensor.transpose(tps[n % 2][:, k, :], ln[:, n, k * P:(k + 1) * P], m.ident[:, :])
                    last.then_inc(transposed, 1)


DHEAD_SCALE = 64 ** -0.5


def unit_rms_block(nc, m, q_tok, kv_tok, qT, klT, gk, H):
    ctx, sb, ps, sem = scope(nc, m)
    with ctx:
        HD = H * 64
        sq = sb("sq", [P, 2, TT, HD])
        ss = sb("ss", [P, 2, TT * H])
        tps = [ps(f"tps{i}", [P, 2, KD, P]) for i in range(2)]
        squared, summed, rooted, ready, transposed, evacuated = (
            sem(x) for x in ("squared", "summed", "rooted", "ready", "transposed", "evacuated"))
        vec = sem("vec")
        srcs = (q_tok[:, :, :], kv_tok[:, :, 0:HD])
        with engines_block(nc, m) as block:

            @block.scalar
            def _(act):
                for j in range(2):
                    nc.scalar.activation(sq[:, j, :, :], srcs[j], ACT.Square).then_inc(squared, 1)
                act.wait_ge(summed, 2)
                nc.scalar.activation(ss[:, :, :], ss[:, :, :], ACT.Sqrt, scale=1.0 / 64).then_inc(rooted, 1)

            @block.vector
            def _(dve):
                chain = Chain(dve, vec)
                for j in range(2):
                    dve.wait_ge(squared, j + 1)
                    nc.vector.tensor_reduce(ss[:, j, :], sq[:, j, :, :].rearrange("p t (h d) -> p (t h) d", h=H),
                                            AX.X, ALU.add).then_inc(summed, 1)
                dve.wait_ge(rooted, 1)
                chain.step(nc.vector.tensor_scalar(ss[:, :, :], ss[:, :, :], RMS_EPS, None, ALU.max))
                chain.step(nc.vector.reciprocal(ss[:, :, :], ss[:, :, :]))
                for j in range(2):
                    r = ss[:, j, :].rearrange("p (t h) -> p t h", h=H)
                    for h in range(H):
                        x = srcs[j][:, :, h * 64:(h + 1) * 64]
                        nc.vector.tensor_tensor(x, x, r[:, :, h:h + 1].to_broadcast([P, TT, 64]), ALU.mult).then_inc(ready, 1)
                for n in range(TT):
                    dve.wait_ge(transposed, n + 1)
                    nc.vector.tensor_scalar(qT[:, :, n * P:(n + 1) * P], tps[n % 2][:, 0, :, :], gk[:, 2:3], None, ALU.mult)
                    nc.vector.tensor_copy(klT[:, :, n * P:(n + 1) * P], tps[n % 2][:, 1, :, :]).then_inc(evacuated, 1)

            @block.tensor
            def _(pe):
                pe.wait_ge(ready, 2 * H)
                for n in range(TT):
                    if n >= 2:
                        pe.wait_ge(evacuated, n - 1)
                    for j in range(2):
                        for k in range(KD):
                            last = nc.tensor.transpose(tps[n % 2][:, j, k, :], srcs[j][:, n, k * P:(k + 1) * P], m.ident[:, :])
                    last.then_inc(transposed, 1)


def resampler_attention_block(nc, m, t, H, DH, qT, klT, kv_tok, w1, w2, wk, mbias):
    ctx, sb, ps, sem = scope(nc, m)
    HD = H * DH
    W = H * SEQ
    hpc = P // DH
    with ctx:
        ctok = sb("ctx_tok", [P, 2, MT, CA])
        stats, mv, rstd = sb("stats", [P, MT, 6]), sb("mv", [P, MT, 2]), sb("rstd", [P, MT])
        xT1, xT2 = sb("xT1", [P, MPAD]), sb("xT2", [CL, MPAD])
        q1, q2 = sb("q1", [P, W]), sb("q2", [CL, W])
        qz = sb("q_by_head", [P, KD, hpc, SEQ])
        kl = sb("kl", [P, KD, SEQ])
        vl = sb("vl", [SEQ, HD])
        mb = sb("mask_now", [P, MT])
        sq = sb("sq", [P, 2, HD])
        rk = sb("rk", [P, MT, H])
        sc = sb("scaled", [P, 2, W])
        e = sb("e", [P, 2, W])
        el = sb("e_latents", [SEQ, W])
        pt1, pt2 = sb("pt1", [P, W]), sb("pt2", [CL, W])
        rsum = sb("rsum", [SEQ, H])
        o = sb("o", [SEQ, HD])
        e64 = sb("sum_col", [CL, 1])
        one = sb("one_col", [SEQ, 1])
        own = sb("own_head", [P, hpc, SEQ])
        ringT = [ps(f"ringT{i}", [P, HALF]) for i in range(2)]
        ringK = [ps(f"ringK{i}", [P, HALF]) for i in range(2)]
        acc1, acc2 = ps("acc1", [P, W]), ps("acc2", [CL, W])
        o_ps, misc = ps("o_ps", [SEQ, HALF]), ps("misc", [P, HALF])
        loaded, zeroed = sem("loaded"), sem("zeroed")
        ctx_in = [sem(f"ctx_in{u}") for u in range(2)]
        norm_var, norm_std = sem("norm_var"), sem("norm_std")
        x_ready = sem("x_ready")
        staged = sem("staged")
        v_staged = sem("v_staged")
        t_full, t_free = sem("t_full"), sem("t_free")
        k_full, k_squared = sem("k_full"), sem("k_squared")
        k_summed = sem("k_summed")
        rms_root, rk_ready = sem("rms_root"), sem("rk_ready")
        s_full, s_free = sem("s_full"), sem("s_free")
        e_ready, e_used = sem("e_ready"), sem("e_used")
        lat_full, lat_ready = sem("lat_full"), sem("lat_ready")
        pooled_out = sem("pooled_out")
        o_full, sums_ready = sem("o_full"), sem("sums_ready")
        o_ready = sem("o_ready")
        oT_full, oT_out = sem("oT_full"), sem("oT_out")
        vec = sem("vec")
        NT = MT + 1
        PER = 2 * MT + 3
        with engines_block(nc, m) as block:

            def each_batch(eng, body):
                with eng.Fori(0, BATCH // 2) as i:
                    for u in range(2):
                        body(i * 2 + u, i, u)

            @block.sync
            def _(sp):
                sp.dma_start(e64[:, :], t["e64"]).then_inc(loaded, 16)
                sp.dma_start(own[:, :, :], t["own64"]).then_inc(loaded, 16)

                def body(b, i, u):
                    sp.wait_ge(pooled_out, b * 2 + 2)
                    sp.dma_start(flat(ctok[:, u, :, :]),
                                 t["ctok"][bass.ds(b, 1)].rearrange("o p t n -> p (o t n)")).then_inc(ctx_in[u], 16)

                each_batch(sp, body)

            @block.gpsimd
            def _(pool):
                pool.sem_inc(s_free, 1)
                nc.gpsimd.memset(one[:, :], 1.0).then_inc(zeroed, 1)
                pool.wait_ge(loaded, 32)

                def body(b, i, u):
                    pool.wait_ge(pooled_out, b * 2 + 4)
                    hold_waits(pool, m)
                    now = bass.ds(b * SEQ, SEQ)
                    for c in range(KD):
                        nc.gpsimd.tensor_tensor(qz[:, c, :, :], qT[:, c, now].unsqueeze(1).to_broadcast([P, hpc, SEQ]),
                                                own[:, :, :], ALU.mult)
                    nc.gpsimd.tensor_copy(mb[:, :], mbias[:, bass.ds(b, 1), :].rearrange("p o t -> p (o t)"))
                    nc.gpsimd.tensor_copy(kl[:, :, :], klT[:, :, now]).then_inc(staged, 1)

                each_batch(pool, body)

            @block.tensor
            def _(pe):
                pe.wait_ge(zeroed, 1)
                pe.wait_ge(loaded, 32)

                def body(b, i, u):
                    pe.wait_ge(t_free, b * NT + 1)
                    for h in range(H):
                        src = qT[:, h // hpc, bass.ds(b * SEQ, SEQ)]
                        nc.tensor.matmul(ringT[0][:, h * SEQ:(h + 1) * SEQ], wk[:, h, 0:P], src, start=True, stop=True)
                        last = nc.tensor.matmul(ringT[0][0:CL, W + h * SEQ:W + (h + 1) * SEQ], wk[:, h, P:CA], src,
                                                start=True, stop=True)
                    last.then_inc(t_full, 1)
                    pe.wait_ge(staged, b + 1)
                    pe.wait_ge(oT_out, b + 1)
                    hold_waits(pe, m)
                    for c in range(KD):
                        last = nc.tensor.matmul(misc[0:SEQ, c * P:(c + 1) * P], kl[:, c, :], flat(qz[:, c, :, :]),
                                                start=True, stop=True)
                    last.then_inc(lat_full, 1)

                    def turn(n):
                        pe.wait_ge(x_ready, b * MT + n + 1)
                        pe.wait_ge(t_free, b * NT + n + 2)
                        bank = ringT[(n + 1) % 2]
                        nc.tensor.transpose(bank[:, 0:P], ctok[:, u, n, 0:P], m.ident[:, :])
                        nc.tensor.transpose(bank[0:CL, P:2 * P], ctok[:, u, n, P:CA], m.ident[:, :]).then_inc(t_full, 1)

                    def keys(n):
                        pe.wait_ge(t_free, b * NT + n + 4)
                        if n < 2:
                            pe.wait_ge(s_free, b * MT + 1)
                        else:
                            pe.wait_ge(k_squared, b * MT + n - 1)
                        cols = slice(n * P, (n + 1) * P)
                        nc.tensor.matmul(ringK[n % 2][:, 0:HD], xT1[:, cols], w1[:, 0:HD], start=True, stop=False)
                        nc.tensor.matmul(ringK[n % 2][:, 0:HD], xT2[:, cols], w2[:, 0:HD],
                                         start=False, stop=True).then_inc(k_full, 1)

                    turn(0)
                    for n in range(1, MT):
                        turn(n)
                        keys(n - 1)
                    keys(MT - 1)

                    def scores(n):
                        if n < 2:
                            pe.wait_ge(k_squared, b * MT + MT - 1 + n)
                        else:
                            pe.wait_ge(s_free, b * MT + n)
                        bank = ringK[(MT + n) % 2]
                        cols = slice(n * P, (n + 1) * P)
                        nc.tensor.matmul(bank[:, 0:W], xT1[:, cols], q1[:, :], start=True, stop=False)
                        nc.tensor.matmul(bank[:, 0:W], xT2[:, cols], q2[:, :], start=False, stop=True).then_inc(s_full, 1)

                    def pool_tile(n):
                        pe.wait_ge(e_ready, b * MT + n + 1)
                        if n == 0:
                            pe.wait_ge(pooled_out, b * 2 + 4)
                        nc.tensor.matmul(acc1[:, :], ctok[:, u, n, 0:P], e[:, n % 2, :], start=(n == 0), stop=(n == MT - 1))
                        nc.tensor.matmul(acc2[:, :], ctok[:, u, n, P:CA], e[:, n % 2, :], start=(n == 0),
                                         stop=(n == MT - 1)).then_inc(e_used, 1)

                    scores(0)
                    scores(1)
                    for n in range(MT):
                        pool_tile(n)
                        if n + 2 < MT:
                            scores(n + 2)

                    pe.wait_ge(pooled_out, b * 2 + 6)
                    pe.wait_ge(lat_ready, b + 1)
                    pe.wait_ge(v_staged, b + 1)
                    pe.wait_ge(o_ready, b + 1)
                    hold_waits(pe, m)
                    for h in range(H):
                        rows = slice(h * SEQ, (h + 1) * SEQ)
                        vcols = slice(HD + h * DH, HD + (h + 1) * DH)
                        dst = o_ps[:, h * DH:(h + 1) * DH]
                        nc.tensor.matmul(dst, pt1[:, rows], w1[:, vcols], start=True, stop=False)
                        nc.tensor.matmul(dst, pt2[:, rows], w2[:, vcols], start=False, stop=False)
                        nc.tensor.matmul(dst, el[:, rows], vl[:, h * DH:(h + 1) * DH], start=False, stop=True)
                        dst = o_ps[:, HD + h:HD + h + 1]
                        nc.tensor.matmul(dst, pt2[:, rows], e64[:, :], start=True, stop=False)
                        last = nc.tensor.matmul(dst, el[:, rows], one[:, :], start=False, stop=True)
                    last.then_inc(o_full, 1)
                    pe.wait_ge(o_ready, b + 2)
                    hold_waits(pe, m)
                    for c in range(KD):
                        last = nc.tensor.transpose(misc[:, W + c * SEQ:W + (c + 1) * SEQ], o[:, c * P:(c + 1) * P],
                                                   m.ident[0:SEQ, 0:SEQ])
                    last.then_inc(oT_full, 1)

                each_batch(pe, body)

            @block.scalar
            def _(act):
                act.sem_inc(t_free, 2)
                act.sem_inc(oT_out, 1)
                act.sem_inc(e_used, 2)
                act.sem_inc(pooled_out, 4)

                def body(b, i, u):
                    act.wait_ge(norm_var, b + 1)
                    nc.scalar.activation(rstd[:, :], rstd[:, :], ACT.Sqrt).then_inc(norm_std, 1)
                    act.wait_ge(t_full, b * NT + 1)
                    nc.scalar.copy(q1[:, :], ringT[0][:, 0:W])
                    nc.scalar.copy(q2[:, :], ringT[0][0:CL, W:2 * W]).then_inc(t_free, 1)
                    nc.scalar.copy(vl[:, :], kv_tok[u * SEQ:(u + 1) * SEQ, bass.ds(i, 1), HD:2 * HD]
                                   .rearrange("p o n -> p (o n)")).then_inc(v_staged, 1)

                    def square(n):
                        act.wait_ge(k_full, b * MT + n + 1)
                        act.wait_ge(k_summed, b * MT + n + 1)
                        nc.scalar.activation(sq[:, n % 2, :], ringK[n % 2][:, 0:HD], ACT.Square).then_inc(k_squared, 1)

                    for n in range(MT):
                        act.wait_ge(t_full, b * NT + n + 2)
                        bank = ringT[(n + 1) % 2]
                        nc.scalar.copy(xT1[:, n * P:(n + 1) * P], bank[:, 0:P])
                        nc.scalar.copy(xT2[:, n * P:(n + 1) * P], bank[0:CL, P:2 * P]).then_inc(t_free, 1)
                        if n:
                            square(n - 1)
                    square(MT - 1)
                    act.wait_ge(k_summed, b * MT + MT + 2)
                    nc.scalar.activation(flat(rk[:, :, :]), flat(rk[:, :, :]), ACT.Sqrt, scale=1.0 / DH).then_inc(rms_root, 1)
                    act.wait_ge(lat_full, b + 1)
                    nc.scalar.activation(el[:, :], misc[0:SEQ, 0:W], ACT.Exp).then_inc(lat_ready, 1)
                    for n in range(MT):
                        act.wait_ge(s_free, b * MT + n + 2)
                        act.wait_ge(e_used, b * MT + (n + 1))
                        nc.scalar.activation(e[:, n % 2, :], sc[:, n % 2, :], ACT.Exp,
                                             bias=mb[:, n:n + 1]).then_inc(e_ready, 1)
                    act.wait_ge(e_used, b * MT + MT + 2)
                    nc.scalar.copy(pt1[:, :], acc1[:, :]).then_inc(pooled_out, 1)
                    act.wait_ge(oT_full, b + 1)
                    nc.scalar.copy(m.featT[:, 0:KD, bass.ds(b * SEQ, SEQ)],
                                   misc[:, W:W + KD * SEQ].rearrange("p (c n) -> p c n", c=KD)).then_inc(oT_out, 1)

                each_batch(act, body)

            @block.vector
            def _(dve):
                dve.sem_inc(k_summed, 2)
                dve.sem_inc(o_ready, 1)

                def body(b, i, u):
                    chain = Chain(dve, vec, b * PER, PER)
                    dve.wait_ge(ctx_in[u], i * 16 + 16)
                    for n in range(MT):
                        nc.vector.bn_stats(stats[:, n, :], ctok[:, u, n, 0:DC]).then_inc(vec, 1)
                        chain.n += 1
                    dve.wait_ge(vec, b * PER + MT)
                    hold_waits(dve, m)
                    for n in range(MT):
                        nc.vector.bn_aggr(mv[:, n, :], stats[:, n, :]).then_inc(vec, 1)
                        chain.n += 1
                    dve.wait_ge(vec, b * PER + chain.n)
                    nc.vector.tensor_scalar(rstd[:, :], mv[:, :, 1], LN_EPS, None, ALU.add).then_inc(norm_var, 1)
                    dve.wait_ge(norm_std, b + 1)
                    chain.step(nc.vector.reciprocal(rstd[:, :], rstd[:, :]))
                    for n in range(MT):
                        nc.vector.tensor_scalar(ctok[:, u, n, 0:DC], ctok[:, u, n, 0:DC], mv[:, n, 0:1],
                                                rstd[:, n:n + 1], ALU.subtract, ALU.mult).then_inc(x_ready, 1)
                    for n in range(MT):
                        dve.wait_ge(k_squared, b * MT + n + 1)
                        nc.vector.tensor_reduce(rk[:, n, :], sq[:, n % 2, :].rearrange("p (h d) -> p h d", h=H),
                                                AX.X, ALU.add).then_inc(k_summed, 1)
                    dve.wait_ge(rms_root, b + 1)
                    chain.step(nc.vector.tensor_scalar(flat(rk[:, :, :]), flat(rk[:, :, :]), RMS_EPS, None, ALU.max))
                    chain.step(nc.vector.reciprocal(flat(rk[:, :, :]), flat(rk[:, :, :])))
                    chain.close()
                    for n in range(MT):
                        dve.wait_ge(s_full, b * MT + n + 1)
                        if n >= 2:
                            dve.wait_ge(e_ready, b * MT + n - 1)
                        nc.vector.tensor_tensor(sc[:, n % 2, :].rearrange("p (h n) -> p h n", h=H),
                                                ringK[(MT + n) % 2][:, 0:W].rearrange("p (h n) -> p h n", h=H),
                                                rk[:, n, :].unsqueeze(2).to_broadcast([P, H, SEQ]), ALU.mult).then_inc(s_free, 1)
                    dve.wait_ge(e_used, b * MT + MT + 2)
                    nc.vector.tensor_copy(pt2[:, :], acc2[:, :]).then_inc(pooled_out, 1)
                    dve.wait_ge(o_full, b + 1)
                    nc.vector.reciprocal(rsum[:, :], o_ps[:, HD:HD + H]).then_inc(sums_ready, 1)
                    dve.wait_ge(sums_ready, b + 1)
                    nc.vector.tensor_tensor(o[:, :].rearrange("p (h d) -> p h d", h=H),
                                            o_ps[:, 0:HD].rearrange("p (h d) -> p h d", h=H),
                                            rsum[:, :].unsqueeze(2).to_broadcast([SEQ, H, DH]), ALU.mult).then_inc(o_ready, 1)

                each_batch(dve, body)


def build(nc, t, out):
    with ExitStack() as ctx:
        m = alloc_memory(nc, ctx)
        load_x_block(nc, m, t["x"], t["ident"])
        project_and_norm_block(nc, m, 0)
        for layer in range(FIRST_LAYER, LAST_LAYER + 1):
            last = layer == LAST_LAYER
            if layer == 0:
                cross_attention_blocks(nc, m, 16, 64, dict(wq=t["a_wq"], bq=None, wk=t["a_wk"], wv1=t["a_wv1"],
                                       wv2=t["a_wv2"], wo=t["a_wo"], bo=t["a_bo"]), t)
                project_and_norm_block(nc, m, 8, bias=True, norm=not last)
            elif layer == 1:
                latent_attention_layer(nc, m, t)
                project_and_norm_block(nc, m, 2, norm=not last)
            elif layer == 4:
                biased_attention_layer(nc, m, t)
                project_and_norm_block(nc, m, 2, bias=True, norm=not last)
            elif layer == 7:
                linear_attention_layer(nc, m, t)
                project_and_norm_block(nc, m, 2, norm=not last)
            elif layer in (6, 9):
                k = "g" if layer == 6 else "j"
                cross_attention_blocks(nc, m, 16, 16, dict(wq=t[k + "_wq"], bq=t[k + "_bq"], wk=t[k + "_wk"],
                                       wv1=t[k + "_wv1"], wv2=t[k + "_wv2"], wo=t[k + "_wo"], bo=t[k + "_bo"],
                                       wkb=t[k + "_wkb"], bvb=t[k + "_bvb"]), t)
                project_and_norm_block(nc, m, 2, bias=True, norm=not last)
            elif layer == 2:
                switch_head_layer(nc, m, t)
                project_and_norm_block(nc, m, 3, last_rows=64, norm=not last)
            elif layer == 3:
                resampler_layer(nc, m, t)
                project_and_norm_block(nc, m, 2, bias=True, norm=not last)
            elif layer == 5:
                with nc.sbuf_tensor("mod_factor", [P, TT], F32) as factor:
                    mixture_of_depths_layer(nc, m, t, factor)
                    project_and_norm_block(nc, m, 8, bias=True, gated=factor, norm=not last)
            elif layer in (8, 11):
                groups, n, k = (1, 16, "i") if layer == 8 else (2, 32, "l")
                N = groups * n
                total = N + (layer == 8)
                with ExitStack() as own:
                    w_gate, rev, weights = (own.enter_context(nc.sbuf_tensor(f"{k}_{x}", shape, F32)) for x, shape in
                                            (("gate", [P, KD, N]), ("rev", [P, n]), ("weights", [P, TT, total])))
                    b_gate = own.enter_context(nc.sbuf_tensor(f"{k}_bgate", [1, N], F32))
                    loads = [(w_gate[:, :, :], t[k + "_gate"]), (rev[:, :], t[f"rev{n}"])]
                    if layer == 8:
                        loads.append((b_gate[:, :], t["i_bgate"]))
                    routing_block(nc, m, w_gate, loads, groups, n, weights, rev,
                                  bias=b_gate[0:1, :] if layer == 8 else None, softmax=layer == 11, shared=layer == 8)
                    experts_block(nc, m, total, t[k + "_experts"], weights, add_xn=layer == 8)
                if not last:
                    project_and_norm_block(nc, m, 0)
            elif layer == 10:
                with nc.sbuf_tensor("s4d_kernel", [P, KD, SEQ], F32) as kern:
                    state_space_kernel_block(nc, m, t, kern)
                    causal_convolution_block(nc, m, t, kern)
                project_and_norm_block(nc, m, 2, bias=True, norm=not last)
        store_x_block(nc, m, out)


def rows_to_partitions(w):
    w = np.asarray(w)
    return np.ascontiguousarray(w.reshape(w.shape[0] // P, P, w.shape[1]).transpose(1, 0, 2))


def column(b):
    return np.ascontiguousarray(np.asarray(b).reshape(-1, P).T)


def per_head_keys(wk, bk, heads, dh):
    w = np.zeros((CA, heads * dh), np.float32)
    w[:DC] = wk
    if bk is not None:
        w[DC] = bk
    out = np.zeros((P, heads, CA), np.float32)
    for h in range(heads):
        r = (h * dh) % P
        out[r:r + dh, h, :] = w[:, h * dh:(h + 1) * dh].T
    return out


def keys_twice(w):
    return np.concatenate([w[:, :, :P], w[:, :, P:DC], w[:, :, P:DC]], 2)


def with_row(w, b):
    out = np.zeros((w.shape[0] + 1, w.shape[1]), np.float32)
    out[:-1] = w
    if b is not None:
        out[-1] = b
    return out


def lay_out(a):
    t = {}
    t["x"] = np.ascontiguousarray(a["x"].reshape(TT, P, D).transpose(1, 0, 2))
    t["ident"] = np.eye(P, dtype=np.float32)
    aug = np.zeros((BATCH, MPAD, CA), np.float32)
    aug[:, :KEYS, :DC] = a["ctx_768"]
    aug[:, :KEYS, DC] = 1.0
    ctxT = aug.transpose(0, 2, 1)[:, :DC]
    t["ctxT1"] = np.ascontiguousarray(ctxT[:, :P, :KEYS])
    t["ctxT2"] = np.ascontiguousarray(ctxT[:, P:, :KEYS])
    low = np.concatenate([ctxT[:, P:]] * 2, 1)
    tiles = [x.reshape(BATCH, P, MT, P).transpose(0, 2, 1, 3) for x in (ctxT[:, :P], low)]
    rows = aug[:, :, :DC].reshape(BATCH, MT, P, DC)
    t["ctx_tiles"] = np.concatenate([*tiles, rows], 3).reshape(BATCH * MT, P, 2 * P + DC)
    t["ctok"] = np.ascontiguousarray(aug.reshape(BATCH, MT, P, CA).transpose(0, 2, 1, 3))
    e64 = np.zeros((CL, 1), np.float32)
    e64[-1] = 1.0
    t["e64"] = e64

    t["a_wq"] = rows_to_partitions(a["L0_xattn_Wq"])
    t["a_wk"] = keys_twice(per_head_keys(a["L0_xattn_Wk"], None, 16, 64))
    wv = a["L0_xattn_Wv"]
    t["a_wv1"], t["a_wv2"] = wv[:P], np.concatenate([wv[P:]] * 2)
    t["a_wo"] = rows_to_partitions(a["L0_xattn_Wo"])
    t["a_bo"] = a["L0_xattn_bo"][None, :]

    swap = np.arange(D) ^ 1
    t["b_wq"], t["b_wqs"] = rows_to_partitions(a["L0_attn_wq"]), rows_to_partitions(a["L0_attn_wq"][:, swap])
    t["b_wd"] = rows_to_partitions(a["L0_attn_w_down"])
    t["b_wk"], t["b_wks"] = rows_to_partitions(a["L0_attn_wk_up"]), rows_to_partitions(a["L0_attn_wk_up"][:, swap])
    t["b_wv"] = rows_to_partitions(a["L0_attn_wv_up"])
    t["b_wo"] = rows_to_partitions(a["L0_attn_wo"])
    inv = 1.0 / 10000.0 ** (np.arange(0, 16, 2, dtype=np.float32) / 16)
    ang = np.outer(np.arange(SEQ, dtype=np.float32), inv)
    pair = (np.arange(P) % 16) // 2
    t["rope_cos"] = np.ascontiguousarray(np.cos(ang).astype(np.float32).T[pair])
    sign = np.where(np.arange(P) % 2 == 0, -1.0, 1.0).astype(np.float32)
    t["rope_sin"] = np.ascontiguousarray(np.sin(ang).astype(np.float32).T[pair] * sign[:, None])
    for dh in (16, 64):
        own = np.arange(P)[:, None] // dh == np.arange(P // dh)[None, :]
        t[f"own{dh}"] = np.ascontiguousarray(np.repeat(own[:, :, None], SEQ, 2).astype(np.float32))
    pos = np.arange(P) % SEQ
    t["causal"] = (np.arange(SEQ)[None, :] <= pos[:, None]).astype(np.float32)
    t["before"] = (np.arange(SEQ)[None, :] < pos[:, None]).astype(np.float32)

    order = np.arange(3 * D).reshape(16, 3, 16).transpose(1, 0, 2).reshape(3, D)
    for n, k in enumerate("qkv"):
        t[f"e_w{k}"] = rows_to_partitions(a["L1_attn_Wqkv"][:, order[n]])
    t["e_bq"], t["e_bk"] = column(a["L1_attn_bqkv"][order[0]]), column(a["L1_attn_bqkv"][order[1]])
    t["e_bv"] = a["L1_attn_bqkv"][order[2]][None, :]
    t["e_wo"], t["e_bo"] = rows_to_partitions(a["L1_attn_Wout"]), a["L1_attn_bout"][None, :]

    for k, n, names in (("g", "L2_xattn_", ("Wq", "bq", "Wk", "bk", "Wv", "bv", "Wo", "bo")),
                        ("j", "L3_xattn_", ("w_q", "b_q", "w_k", "b_k", "w_v", "b_v", "w_o", "b_o"))):
        wq, bq, wk, bk, wv, bv, wo, bo = (a[n + x] for x in names)
        t[k + "_wq"], t[k + "_bq"] = rows_to_partitions(wq), column(bq)
        w = per_head_keys(wk, bk, 16, 16)
        t[k + "_wk"], t[k + "_wkb"] = keys_twice(w), w[:, :, DC]
        t[k + "_wv1"], t[k + "_wv2"] = wv[:P], np.concatenate([wv[P:]] * 2)
        t[k + "_bvb"] = np.tile(bv, (P, 1))
        t[k + "_wo"], t[k + "_bo"] = rows_to_partitions(wo), bo[None, :]

    for k in ("q", "k", "v", "o"):
        t["h_w" + k] = rows_to_partitions(a["L2_attn_W_" + k].T)

    t["c_wq"], t["c_wk"] = rows_to_partitions(a["L0_ffn_Wq"]), rows_to_partitions(a["L0_ffn_Wk"])
    wx = a["L0_ffn_Wv"].transpose(1, 0, 2).reshape(D, -1)
    t["c_wx"] = rows_to_partitions(np.concatenate([wx, a["L0_ffn_Ws"], a["L0_ffn_Wd"]], 1))
    wo = np.zeros((3 * P, D), np.float32)
    wo[:5 * 64] = a["L0_ffn_Wo"].reshape(5 * 64, D)
    t["c_wo"] = rows_to_partitions(wo)
    for n in (5, 16, 32):
        t[f"rev{n}"] = np.tile(np.arange(n, 0, -1, dtype=np.float32), (P, 1))

    t["d_wq"], t["d_wlkv"] = rows_to_partitions(a["L1_xattn_Wq"].T), rows_to_partitions(a["L1_xattn_Wlkv"].T)
    w = with_row(a["L1_xattn_Wkv"].T, None)
    t["d_w1"], t["d_w2"] = w[:P], w[P:]
    t["d_wk"] = per_head_keys(a["L1_xattn_Wkv"][:D].T, None, 4, 64)
    gk = np.zeros((P, 4), np.float32)
    gk[:, 0], gk[:, 1] = np.tile(a["L1_xattn_qn_g"], 2), np.tile(a["L1_xattn_kn_g"], 2)
    t["d_gk"] = gk
    two = np.zeros((4, P), np.float32)
    for n, x in enumerate(("g", "b")):
        v = a[f"L1_xattn_ln_x_{x}"]
        two[2 * n], two[2 * n + 1, :DC - P] = v[:P], v[P:]
        t[f"d_{x}_row"] = np.tile(v, (P, 1))
    t["d_gates"] = np.concatenate([column(a["L1_xattn_ln_l_g"]), column(a["L1_xattn_ln_l_b"]), two[:2].T], 1)
    t["d_bcol"] = two[2:].T
    mask = np.zeros((BATCH, MPAD, 4), np.uint8)
    mask[:, :KEYS, 0] = a["mask_BxS2_bk0"].view(np.uint8)
    t["d_mask"] = mask.view(np.int32).reshape(BATCH, MT, P).transpose(2, 0, 1)
    t["d_wo"], t["d_bo"] = rows_to_partitions(a["L1_xattn_Wo"].T), a["L1_xattn_bo"][None, :]

    t["f_w1"], t["f_b1"] = rows_to_partitions(a["L1_ffn_W1"]), column(a["L1_ffn_b1"])
    t["f_wr"] = column(a["L1_ffn_w_router"])
    t["f_w2"], t["f_b2"] = rows_to_partitions(a["L1_ffn_W2"]), a["L1_ffn_b2"][None, :]

    def pack(wg, wu, wd):
        up = [w.reshape(-1, KD, P, P).transpose(0, 2, 1, 3).reshape(-1, P, KD * P) for w in (wg, wu)]
        return np.concatenate([*up, wd], 2)

    t["i_gate"], t["i_bgate"] = rows_to_partitions(a["L2_ffn_gate_w"]), a["L2_ffn_gate_b"][None, :]
    t["i_experts"] = np.concatenate([
        pack(*(a["L2_ffn_experts_" + w] for w in ("wg", "wu", "wd"))),
        pack(*(a["L2_ffn_shared_" + w][None] for w in ("wg", "wu", "wd")))])
    t["l_gate"] = rows_to_partitions(np.concatenate([a["L3_ffn_router_w0"], a["L3_ffn_router_w1"]], 1))
    t["l_experts"] = np.concatenate([pack(*(a[f"L3_ffn_{w}{g}"] for w in ("wg", "wu", "wd"))) for g in range(2)])

    t["k_ldt"] = column(a["L3_attn_log_dt"])
    for k, x in (("lar", "log_A_real"), ("aim", "A_imag"), ("cre", "C_real"), ("cim", "C_imag")):
        t["k_" + k] = rows_to_partitions(a["L3_attn_" + x])
    t["k_w"], t["k_b"] = rows_to_partitions(a["L3_attn_W"].T), a["L3_attn_b"][None, :]
    return t


def kernel(**inputs):
    import concourse.bacc as bacc
    from concourse.bass_utils import run_bass_kernel_spmd

    nc = bacc.Bacc("TRN2", target_bir_lowering=False, num_devices=1)
    arrays, t = {}, {}
    for name, a in lay_out({k: np.asarray(v) for k, v in inputs.items()}).items():
        a = np.ascontiguousarray(a)
        arrays[f"in_{name}_dram"] = a
        t[name] = nc.dram_tensor(f"in_{name}_dram", a.shape, mybir.dt.from_np(a.dtype), kind="ExternalInput").ap()
    out = nc.dram_tensor("out_0_dram", (P, TT, D), F32, kind="ExternalOutput").ap()
    build(nc, t, out)
    r = run_bass_kernel_spmd(nc, [arrays], core_ids=[0])
    got = r.results[0]["out_0_dram"]
    return np.ascontiguousarray(got.transpose(1, 0, 2)).reshape(BATCH, SEQ, D)
```

```python
from contextlib import ExitStack, contextmanager

import concourse.bass as bass
import numpy as np
from concourse import mybir

F32 = mybir.dt.float32
BF16 = mybir.dt.bfloat16
I32 = mybir.dt.int32
ALU = mybir.AluOpType
ACT = mybir.ActivationFunctionType
AX = mybir.AxisListType

FIRST_LAYER, LAST_LAYER = 0, 11

P = 128
BATCH, SEQ, D = 16, 64, 256
KEYS, DC = 1601, 192
TOK = BATCH * SEQ
TT = TOK // P
KD = D // P
MT = -(-KEYS // P)
MPAD = MT * P
CA = DC + 1
CL = CA - P
HALF = 512
LN_EPS = 1e-5
CLIP = 1e-6


class Mem:
    pass


def alloc_memory(nc, ctx):
    m = Mem()
    m.ctx = ctx

    def sb(name, shape, dt=F32):
        return ctx.enter_context(nc.sbuf_tensor(name, shape, dt))

    m.x = sb("x_tok", [P, TT, D])
    m.xn = sb("xn_tok", [P, TT, D])
    m.xnT = sb("xn_T", [P, KD, TOK])
    m.featT = sb("feat_T", [P, 8, TOK])
    m.wo = sb("w_out", [P, 8, D])
    m.bo = sb("b_out", [1, D])
    m.ident = sb("ident", [P, P])
    m.ones = sb("ones_row", [1, P])
    m.bf_in = ctx.enter_context(nc.semaphore("bf_in"))
    m.bf_in_count = 0
    m.held = ctx.enter_context(nc.semaphore("held"))
    m.n_blocks = 0
    m.retired = []
    return m


def scope(nc, m):
    m.n_blocks += 1
    tag = f"b{m.n_blocks}_"
    ctx = ExitStack()

    def sb(name, shape, dt=F32):
        return ctx.enter_context(nc.sbuf_tensor(tag + name, shape, dt))

    def ps(name, shape, dt=F32):
        return ctx.enter_context(nc.psum_tensor(tag + name, shape, dt))

    def sem(name):
        s = nc.alloc_semaphore(name=tag + name)
        own.append(s)
        return s

    own = []
    ctx.callback(lambda: m.retired.extend(own))
    return ctx, sb, ps, sem


@contextmanager
def engines_block(nc, m):
    cleared, m.retired = m.retired, []
    for s in cleared:
        nc.gpsimd.sem_clear(s)
    with nc.Block() as block:
        yield block
    for s in cleared:
        nc.release_semaphore(s)


class Chain:

    def __init__(self, eng, sem, base=None, per=None):
        self.eng, self.sem, self.base, self.n, self.per = eng, sem, base, 0, per

    def step(self, ins):
        self.n += 1
        ins.then_inc(self.sem, 1)
        self.eng.wait_ge(self.sem, self.n if self.base is None else self.base + self.n)

    def close(self):
        assert self.n == self.per, (self.n, self.per)


def hold_waits(eng, m):
    eng.sem_inc(m.held, 1)


def flat(ap):
    return ap.rearrange("p a b -> p (a b)")


def load_x_block(nc, m, x_in, ident_in):
    ctx, sb, ps, sem = scope(nc, m)
    with ctx:
        loaded = sem("loaded")
        with engines_block(nc, m) as block:

            @block.sync
            def _(sp):
                sp.dma_start(m.x[:, :, :], x_in).then_inc(loaded, 16)
                sp.dma_start(m.ident[:, :], ident_in).then_inc(loaded, 16)
                sp.wait_ge(loaded, 32)

            @block.vector
            def _(dve):
                nc.vector.memset(m.ones[:, :], 1.0)


def store_x_block(nc, m, x_out):
    ctx, sb, ps, sem = scope(nc, m)
    with ctx:
        stored = sem("stored")
        with engines_block(nc, m) as block:

            @block.sync
            def _(sp):
                sp.dma_start(x_out, m.x[:, :, :]).then_inc(stored, 16)
                sp.wait_ge(stored, 16)


def project_and_norm_block(nc, m, chunks, last_rows=P, bias=False, gated=None, norm=True):
    ctx, sb, ps, sem = scope(nc, m)
    with ctx:
        stats = sb("stats", [P, TT, 6])
        mv = sb("mean_var", [P, TT, 2])
        rstd = sb("rstd", [P, TT])
        proj = [ps(f"proj{i}", [P, D]) for i in range(2)]
        tps = [ps(f"tps{i}", [P, KD, P]) for i in range(2)]
        projected = sem("projected")
        added = sem("added")
        vec = sem("vec")
        var_ready = sem("var_ready")
        std_ready = sem("std_ready")
        xn_ready = sem("xn_ready")
        transposed = sem("transposed")
        evacuated = sem("evacuated")
        with engines_block(nc, m) as block:

            @block.tensor
            def _(pe):
                if chunks:
                    for t in range(TT):
                        if t >= 2:
                            pe.wait_ge(added, t - 1)
                        for c in range(chunks):
                            k = last_rows if c == chunks - 1 else P
                            last = nc.tensor.matmul(
                                proj[t % 2][:, :], m.featT[0:k, c, t * P:(t + 1) * P], m.wo[0:k, c, :],
                                start=(c == 0), stop=(c == chunks - 1 and not bias))
                        if bias:
                            last = nc.tensor.matmul(proj[t % 2][:, :], m.ones[0:1, :], m.bo[0:1, :],
                                                    start=False, stop=True)
                        last.then_inc(projected, 1)
                if norm:
                    for t in range(TT):
                        pe.wait_ge(xn_ready, t + 1)
                        if t >= 2:
                            pe.wait_ge(evacuated, t - 1)
                        for k in range(KD):
                            last = nc.tensor.transpose(tps[t % 2][:, k, :], m.xn[:, t, k * P:(k + 1) * P],
                                                       m.ident[:, :])
                        last.then_inc(transposed, 1)

            @block.vector
            def _(dve):
                chain = Chain(dve, vec)
                for t in range(TT):
                    if chunks:
                        dve.wait_ge(projected, t + 1)
                        if gated is not None:
                            chain.step(nc.vector.tensor_tensor(m.x[:, t, :], m.x[:, t, :], m.xn[:, t, :], ALU.add))
                            nc.vector.scalar_tensor_tensor(m.x[:, t, :], proj[t % 2][:, :], gated[:, t:t + 1],
                                                           m.x[:, t, :], ALU.mult, ALU.add).then_inc(added, 1)
                        else:
                            nc.vector.tensor_tensor(m.x[:, t, :], m.x[:, t, :], proj[t % 2][:, :],
                                                    ALU.add).then_inc(added, 1)
                        dve.wait_ge(added, t + 1)
                    if norm:
                        chain.step(nc.vector.bn_stats(stats[:, t, :], m.x[:, t, :]))
                        last = nc.vector.bn_aggr(mv[:, t, :], stats[:, t, :])
                if norm:
                    chain.step(last)
                    nc.vector.tensor_scalar(rstd[:, :], mv[:, :, 1], LN_EPS, None, ALU.add).then_inc(var_ready, 1)
                    dve.wait_ge(std_ready, 1)
                    chain.step(nc.vector.reciprocal(rstd[:, :], rstd[:, :]))
                    for t in range(TT):
                        nc.vector.tensor_scalar(m.xn[:, t, :], m.x[:, t, :], mv[:, t, 0:1], rstd[:, t:t + 1],
                                                ALU.subtract, ALU.mult).then_inc(xn_ready, 1)

            @block.scalar
            def _(act):
                if norm:
                    act.wait_ge(var_ready, 1)
                    nc.scalar.activation(rstd[:, :], rstd[:, :], ACT.Sqrt).then_inc(std_ready, 1)
                    for t in range(TT):
                        act.wait_ge(transposed, t + 1)
                        nc.scalar.copy(m.xnT[:, :, t * P:(t + 1) * P], tps[t % 2][:, :, :]).then_inc(evacuated, 1)


def feature_major_block(nc, m, jobs, loads, later=()):
    ctx, sb, ps, sem = scope(nc, m)
    pieces = [(j, c, h) for j in range(len(jobs)) for c in range(jobs[j][1]) for h in range(TOK // HALF)]
    on_act = [jobs[j][5][0] == "gelu" or (jobs[j][5][0] == "linear" and n % 2 == 0)
              for n, (j, c, h) in enumerate(pieces)]
    done_before = [sum(1 for k in range(n) if on_act[k] == on_act[n]) for n in range(len(pieces))]
    with ctx:
        ring = [ps(f"ring{i}", [P, HALF]) for i in range(4)]
        low = sb("low", [P, 2, HALF])
        loaded = sem("loaded")
        filled = sem("filled")
        act_done = sem("act_done")
        dve_done = sem("dve_done")
        vec = sem("vec")
        low_ready = sem("low_ready")
        later_in = sem("later_in")
        exp_ready = sem("exp_ready")
        with engines_block(nc, m) as block:

            @block.sync
            def _(sp):
                for buf, dram in loads:
                    sp.dma_start(buf, dram).then_inc(loaded, 16)
                for buf, dram in later:
                    sp.dma_start(buf, dram).then_inc(later_in, 16)
                if later:
                    sp.wait_ge(later_in, 16 * len(later))

            @block.tensor
            def _(pe):
                if loads:
                    pe.wait_ge(loaded, 16 * len(loads))
                for n, (j, c, h) in enumerate(pieces):
                    dst, chunks, w, src, kc, post = jobs[j]
                    if j and c == 0 and h == 0 and src is jobs[j - 1][0]:
                        for q in (k for k in range(n) if pieces[k][0] == j - 1):
                            pe.wait_ge(act_done if on_act[q] else dve_done, done_before[q] + 1)
                    if n >= 4:
                        pe.wait_ge(act_done if on_act[n - 4] else dve_done, done_before[n - 4] + 1)
                    for k in range(kc):
                        last = nc.tensor.matmul(ring[n % 4][:, :], w[:, k, c * P:(c + 1) * P],
                                                src[:, k, h * HALF:(h + 1) * HALF],
                                                start=(k == 0), stop=(k == kc - 1))
                    last.then_inc(filled, 1)

            @block.scalar
            def _(act):
                if loads:
                    act.wait_ge(loaded, 16 * len(loads))
                n_low = 0
                for n, (j, c, h) in enumerate(pieces):
                    dst, chunks, w, src, kc, post = jobs[j]
                    out = dst[:, c, h * HALF:(h + 1) * HALF]
                    if post[0] == "elu1":
                        n_low += 1
                        act.wait_ge(low_ready, n_low)
                        nc.scalar.activation(low[:, (n_low - 1) % 2, :], low[:, (n_low - 1) % 2, :],
                                             ACT.Exp).then_inc(exp_ready, 1)
                    if not on_act[n]:
                        continue
                    act.wait_ge(filled, n + 1)
                    if post[0] == "gelu":
                        nc.scalar.activation(out, ring[n % 4][:, :], ACT.Gelu_apprx_tanh,
                                             bias=post[1][:, c:c + 1]).then_inc(act_done, 1)
                    else:
                        nc.scalar.activation(out, ring[n % 4][:, :], ACT.Copy,
                                             scale=float(post[1])).then_inc(act_done, 1)

            @block.vector
            def _(dve):
                if loads:
                    dve.wait_ge(loaded, 16 * len(loads))
                n_low = 0
                for n, (j, c, h) in enumerate(pieces):
                    if on_act[n]:
                        continue
                    dst, chunks, w, src, kc, post = jobs[j]
                    out = dst[:, c, h * HALF:(h + 1) * HALF]
                    dve.wait_ge(filled, n + 1)
                    if post[0] == "bias":
                        nc.vector.tensor_scalar(out, ring[n % 4][:, :], post[1][:, c:c + 1], float(post[2]),
                                                ALU.add, ALU.mult).then_inc(dve_done, 1)
                    elif post[0] == "elu1":
                        nc.vector.tensor_scalar(low[:, n_low % 2, :], ring[n % 4][:, :], 0.0, None,
                                                ALU.min).then_inc(low_ready, 1)
                        n_low += 1
                        dve.wait_ge(exp_ready, n_low)
                        nc.vector.scalar_tensor_tensor(out, ring[n % 4][:, :], 0.0, low[:, (n_low - 1) % 2, :],
                                                       ALU.max, ALU.add).then_inc(dve_done, 1)
                    else:
                        nc.vector.tensor_scalar(out, ring[n % 4][:, :], float(post[1]), None,
                                                ALU.mult).then_inc(dve_done, 1)


RAW = 2 * P + DC


class Ring:

    def __init__(self, first, turn, turns, last):
        assert len(turn) % 2 == 0
        self.turn = len(turn)
        self.at = {key: n for n, key in enumerate(first + turn)}
        self.at.update({key: n + len(first) + turns * len(turn) for n, key in enumerate(last)})

    def __call__(self, i, *key):
        n = self.at[key]
        return n % 2, i * (self.turn // 2) + n // 2


def cross_attention_blocks(nc, m, heads, dh, d, t):
    F32R = mybir.dt.float32r
    nch = heads * dh // P
    hpc = P // dh
    scale = dh ** -0.5
    KT = [min(P, KEYS - n * P) for n in range(MT)]
    ctx, sb, ps, sem = scope(nc, m)
    with ctx:
        wk = sb("wk", [P, nch, 2 * P])
        wv1 = sb("wv1", [P, heads * dh])
        wv2 = sb("wv2", [P, heads * dh])
        own = sb("own_head", [P, hpc, SEQ])
        qT = m.featT
        inner, sb2, _, _ = scope(nc, m)
        with inner:
            wq = sb2("wq", [P, KD, heads * dh])
            feature_major_block(nc, m, [(qT, nch, wq, m.xnT, KD, ("linear", scale))], [(wq[:, :, :], d["wq"])],
                                later=((wk[:, :, :], d["wk"]), (wv1[:, :], d["wv1"]), (wv2[:, :], d["wv2"]),
                                       (m.wo[:, 0:nch, :], d["wo"]), (m.bo[:, :], d["bo"]), (own[:, :, :], d["own"])))

        z = sb("q_own", [P, nch, hpc, SEQ])
        raw = sb("raw", [P, 2, RAW])
        kHX = sb("kHX", [P, 2, 2 * P], F32R)
        kL0 = sb("kL0", [P, 2, P], F32R)
        kS = sb("kS", [P, 2, P], F32R)
        vHL = sb("vHL", [P, 2, 3 * P], F32R)
        cb1 = sb("ctx_bf1", [P, KEYS], BF16)
        cb2 = sb("ctx_bf2", [SEQ, KEYS], BF16)
        qb1 = sb("q_bf1", [P, TOK], BF16)
        qb2 = sb("q_bf2", [SEQ, TOK], BF16)
        qH0 = sb("qH0", [P, 2, TOK], F32R)
        qL0 = sb("qL0", [P, 2, TOK], F32R)
        qH1 = sb("qH1", [P, 2, TOK], F32R)
        qS = sb("qS", [P, 2, TOK], F32R)
        e = sb("e", [P, 2, TOK])
        eH = sb("eH", [P, 2, TOK], F32R)
        eL = sb("eL", [P, 2, TOK], F32R)
        es = sb("e_sum", [P, 2, TOK])
        pt1, pt2 = m.xnT[:, 0, :], m.xnT[:, 1, :]
        mx = sb("max_parts", [P, 8, 2])
        nmx = sb("neg_max", [P, 8])
        num, den = sb("num", [P, nch, SEQ]), sb("den", [P, nch, SEQ])
        ones = sb("ones_mat", [P, P])
        pair = [ps("pair0", [P, 2, HALF]), ps("pair1", [P, 2, HALF])]
        acc1 = ps("acc1", [P, 2, HALF])
        acc2 = ps("acc2", [P, 2, HALF])

        set_up = sem("set_up")
        raw_in = [sem(f"raw_in{k}") for k in range(2)]
        bf_in, bf_before = m.bf_in, m.bf_in_count
        m.bf_in_count += (BATCH + 1) * 32
        k_hi, k_lo = sem("k_hi"), sem("k_lo")
        v_hi, v_lo = sem("v_hi"), sem("v_lo")
        full = [sem(f"full{p}") for p in range(2)]
        free = [sem(f"free{p}") for p in range(2)]
        q_hi = sem("q_hi")
        q_own = sem("q_own")
        q_cast = sem("q_cast")
        max_ready = sem("max_ready")
        shifted = sem("shifted")
        summed = sem("summed")
        taken = sem("taken")
        inverted = sem("inverted")
        divided = sem("divided")
        eH_ready = sem("eH_ready")
        eL_ready = sem("eL_ready")
        es_added = sem("es_added")
        pooled = sem("pooled")
        pooled_out = sem("pooled_out")
        REST = KEYS - TOK

        LAST = BATCH - 1

        def next_items(c, tile=None):
            out = {1: [(c, "qA"), (c, "qB")], 11: [(c, "neg")]}
            out.update({n: [(c, "m0", n - 3), (c, "m1", n - 3)] for n in range(3, 11)})
            return out.get(tile, []) if tile is not None else [x for n in range(MT) for x in out.get(n, [])]

        def batch_items(c):
            for n in range(MT):
                yield (c, "s", n)
                yield from next_items(c, n) if c != LAST else []
                yield from [(c, x) for k, x in ((2, "S"), (3, "O")) if k == n and c]

        end = [("end", x) for x in "SO"]
        ring = Ring(next_items("start") + list(batch_items(0)), list(batch_items(1)) + list(batch_items(2)),
                    BATCH // 2 - 1, list(batch_items(LAST)) + end)

        def each_batch(eng, body):
            body(0, 0)
            with eng.Fori(0, BATCH // 2 - 1) as i:
                body(i, 1)
                body(i, 2)
            body(0, LAST)

        def tile(i, c, n):
            return i * (2 * MT) + (c * MT + n)

        with engines_block(nc, m) as block:

            @block.sync
            def _(sp):
                with sp.Fori(0, BATCH // 2) as i:
                    for k in range(2 * MT):
                        g = i * (2 * MT) + k
                        sp.wait_ge(v_lo, g + 1)
                        sp.dma_start(raw[:, k % 2, :], t["ctx_tiles"][bass.ds(g, 1)]
                                     .rearrange("o p n -> p (o n)")).then_inc(raw_in[k % 2], 16)

            @block.gpsimd
            def _(pool):
                pool.sem_inc(free[0], 1)
                pool.sem_inc(free[1], 1)
                pool.sem_inc(es_added, 2)
                pool.sem_inc(divided, 1)
                nc.gpsimd.memset(ones[:, :], 1.0).then_inc(set_up, 1)
                for k in range(2):
                    nc.gpsimd.memset(kS[:, k, :].bitcast(F32), 0.0).then_inc(set_up, 1)
                    nc.gpsimd.memset(qS[:, k, :].bitcast(F32), 0.0).then_inc(set_up, 1)
                pool.wait_ge(set_up, 5)
                for row in (SEQ, SEQ + 32):
                    nc.gpsimd.memset(kS[row:row + 1, :, :].bitcast(F32), 1.0).then_inc(set_up, 1)

                def load_bf(b):
                    pool.dma_start(cb1[:, :], t["ctxT1"][bass.ds(b, 1)].rearrange("o p n -> p (o n)")).then_inc(bf_in, 16)
                    pool.dma_start(cb2[0:SEQ, :], t["ctxT2"][bass.ds(b, 1)].rearrange("o p n -> p (o n)")).then_inc(bf_in, 16)

                def keep_own(b):
                    wide = [P, nch, hpc, SEQ]
                    nc.gpsimd.tensor_tensor(z[:, :, :, :], own[:, :, :].unsqueeze(1).to_broadcast(wide),
                                            qT[:, 0:nch, bass.ds(b * SEQ, SEQ)].unsqueeze(2).to_broadcast(wide),
                                            ALU.mult).then_inc(q_own, 1)

                def divide(b):
                    pool.wait_ge(inverted, b * 2 + 2)
                    hold_waits(pool, m)
                    nc.gpsimd.tensor_tensor(m.featT[:, 0:nch, bass.ds(b * SEQ, SEQ)], num[:, :, :], den[:, :, :],
                                            ALU.mult).then_inc(divided, 1)

                load_bf(0)
                pool.wait_ge(set_up, 7)
                keep_own(0)
                pool.wait_ge(max_ready, 1)
                load_bf(1)

                def body(i, c):
                    b, u, follows = i * 2 + c, c % 2, c != LAST
                    if follows:
                        pool.wait_ge(q_hi, b * 2 + 2)
                        hold_waits(pool, m)
                        keep_own(b + 1)
                    for n in range(MT):
                        p, k = ring(i, c, "s", n)
                        pool.wait_ge(free[p], k + 2)
                        g, s = tile(i, c, n), (c * MT + n) % 2
                        if n == 1:
                            nc.gpsimd.tensor_tensor(es[:, u, :], e[:, 1 - s, :], e[:, s, :], ALU.add).then_inc(es_added, 2)
                        if n > 1:
                            pool.wait_ge(es_added, g + 2)
                            nc.gpsimd.tensor_tensor(es[0:KT[n], u, :], es[0:KT[n], u, :], e[0:KT[n], s, :],
                                                    ALU.add).then_inc(es_added, 1)
                        if n == 12 and c:
                            divide(b - 1)
                        if n == 11 and follows:
                            pool.wait_ge(max_ready, b + 2)
                            load_bf(b + 2)

                each_batch(pool, body)
                divide(LAST)

            @block.tensor
            def _(pe):
                pe.wait_ge(set_up, 7)

                def fill(i, *key):
                    p, k = ring(i, *key)
                    pe.wait_ge(free[p], k + 1)
                    return pair[p], full[p]

                def project(i, who, b):
                    pe.wait_ge(q_own, b + 1)
                    for name, c0 in (("qA", 0), ("qB", P)):
                        dst, done = fill(i, who, name)
                        for ch in range(nch):
                            last = nc.tensor.matmul(flat(dst[:, :, :])[:, ch * hpc * SEQ:(ch + 1) * hpc * SEQ],
                                                    wk[:, ch, c0:c0 + P], flat(z[:, ch, :, :]), start=True, stop=True)
                        last.then_inc(done, 1)

                def max_part(i, who, j, half, b):
                    if j == 0 and half == 0:
                        pe.wait_ge(q_cast, b * 2 + 2)
                        pe.wait_ge(bf_in, b * 32 + bf_before + 32)
                    dst, done = fill(i, who, f"m{half}", j)
                    for h, a, x in (((0, 0, HALF), (1, HALF, TOK)), ((0, TOK, TOK + HALF), (1, TOK + HALF, KEYS)))[half]:
                        nc.tensor.matmul(dst[:, h, 0:x - a], qb1[:, j * P:(j + 1) * P], cb1[:, a:x], start=True, stop=False)
                        last = nc.tensor.matmul(dst[:, h, 0:x - a], qb2[:, j * P:(j + 1) * P], cb2[:, a:x],
                                                start=False, stop=True)
                    last.then_inc(done, 1)

                def shift_row(i, who, b):
                    pe.wait_ge(max_ready, b + 1)
                    dst, done = fill(i, who, "neg")
                    for j in range(8):
                        last = nc.tensor.matmul(flat(dst[0:1, :, :])[:, j * P:(j + 1) * P], nmx[:, j:j + 1], m.ident[:, :],
                                                start=True, stop=True)
                    last.then_inc(done, 1)

                def scores(i, c, n):
                    g, s, u, b = tile(i, c, n), (c * MT + n) % 2, c % 2, i * 2 + c
                    if n == 0:
                        pe.wait_ge(summed, b + 1)
                    pe.wait_ge(k_lo, g + 1)
                    dst, done = fill(i, c, "s", n)
                    for h in range(2):
                        cols = slice(h * HALF, (h + 1) * HALF)
                        out = dst[0:KT[n], h, :]
                        for x, (w, q) in enumerate((
                                (kHX[:, s, 0:KT[n]], qH0[:, u, cols]), (kHX[:, s, 0:KT[n]], qL0[:, u, cols]),
                                (kL0[:, s, 0:KT[n]], qH0[:, u, cols]), (kHX[:, s, P:P + KT[n]], qH1[:, u, cols]),
                                (kS[0:SEQ + 33, s, 0:KT[n]], qS[0:SEQ + 33, u, cols]))):
                            last = nc.tensor.matmul(out, w, q, start=(x == 0), stop=(x == 4))
                    last.then_inc(done, 1)

                def pool_tile(i, c, n):
                    g, s, b = tile(i, c, n), (c * MT + n) % 2, i * 2 + c
                    pe.wait_ge(eL_ready, g + 3)
                    pe.wait_ge(v_lo, g + 3)
                    if n == 0:
                        pe.wait_ge(pooled_out, b * 2 + 2)
                    r = slice(0, KT[n])
                    for h in range(2):
                        cols = slice(h * HALF, (h + 1) * HALF)
                        hi, lo = eH[r, s, cols], eL[r, s, cols]
                        low = vHL[r, s, P:2 * P]
                        nc.tensor.matmul(acc1[:, h, :], vHL[r, s, 0:P], hi, start=(n == 0), stop=False)
                        nc.tensor.matmul(acc1[:, h, :], vHL[r, s, 0:P], lo, start=False, stop=False)
                        nc.tensor.matmul(acc1[:, h, :], vHL[r, s, 2 * P:3 * P], hi, start=False, stop=(n == MT - 1))
                        nc.tensor.matmul(acc2[:, h, :], low, hi, start=(n == 0), stop=False)
                        last = nc.tensor.matmul(acc2[:, h, :], low, lo, start=False, stop=(n == MT - 1))
                    last.then_inc(pooled, 1)

                def sum_up(i, who, c):
                    pe.wait_ge(es_added, tile(i, c, MT - 1) + 3)
                    dst, done = fill(i, who, "S")
                    for h in range(2):
                        last = nc.tensor.matmul(dst[:, h, :], ones[:, :], es[:, c % 2, h * HALF:(h + 1) * HALF],
                                                start=True, stop=True)
                    last.then_inc(done, 1)

                def outputs(i, who, c):
                    pe.wait_ge(pooled_out, (i * 2 + c) * 2 + 4)
                    dst, done = fill(i, who, "O")
                    for ch in range(nch):
                        cols, rows = slice(ch * P, (ch + 1) * P), slice(ch * hpc * SEQ, (ch + 1) * hpc * SEQ)
                        out = flat(dst[:, :, :])[:, rows]
                        nc.tensor.matmul(out, wv1[:, cols], pt1[:, rows], start=True, stop=False)
                        last = nc.tensor.matmul(out, wv2[:, cols], pt2[:, rows], start=False, stop=True)
                    last.then_inc(done, 1)

                project(0, "start", 0)
                for j in range(8):
                    max_part(0, "start", j, 0, 0)
                    max_part(0, "start", j, 1, 0)
                shift_row(0, "start", 0)

                def body(i, c):
                    b, follows = i * 2 + c, c != LAST
                    for n in range(MT):
                        scores(i, c, n)
                        if n == 0 and c:
                            pool_tile(i, c - 1, MT - 1)
                        if n == 1 and follows:
                            project(i, c, b + 1)
                        if 3 <= n <= 10 and follows:
                            max_part(i, c, n - 3, 0, b + 1)
                        if n:
                            pool_tile(i, c, n - 1)
                        if 3 <= n <= 10 and follows:
                            max_part(i, c, n - 3, 1, b + 1)
                        if n == 11 and follows:
                            shift_row(i, c, b + 1)
                        if n == 2 and c:
                            sum_up(i, c, c - 1)
                        if n == 3 and c:
                            outputs(i, c, c - 1)

                each_batch(pe, body)
                pool_tile(0, LAST, MT - 1)
                sum_up(0, "end", LAST)
                outputs(0, "end", LAST)

            @block.scalar
            def _(act):
                act.sem_inc(pooled_out, 2)
                act.wait_ge(set_up, 7)

                def split_keys(g, s, k):
                    act.wait_ge(raw_in[s], k)
                    nc.scalar.copy(kHX[:, s, :], raw[:, s, 0:2 * P])
                    nc.scalar.copy(kS[0:SEQ, s, :], raw[0:SEQ, s, P:2 * P]).then_inc(k_hi, 1)

                def split_values(g, s):
                    act.wait_ge(pooled, g + 1)
                    nc.scalar.copy(vHL[:, s, 0:DC], raw[:, s, 2 * P:RAW]).then_inc(v_hi, 1)

                def round_q(i, who, b, s):
                    for x, dst, low, rows in (("qA", qH0, qb1, P), ("qB", qH1, qb2, SEQ)):
                        p, k = ring(i, who, x)
                        act.wait_ge(full[p], k + 1)
                        nc.scalar.copy(dst[:, s, :], flat(pair[p][:, :, :])).then_inc(q_hi, 1)
                        act.wait_ge(q_hi, b * 2 + (1 if x == "qA" else 2))
                        nc.scalar.copy(low[0:rows, :], dst[0:rows, s, :].bitcast(F32)).then_inc(q_cast, 1)

                round_q(0, "start", 0, 0)
                split_keys(0, 0, 16)
                split_values(0, 0)
                split_keys(1, 1, 16)

                def copy_pooled(i, c):
                    act.wait_ge(pooled, tile(i, c, MT - 1) + 3)
                    nc.scalar.copy(pt1, flat(acc1[:, :, :])).then_inc(pooled_out, 1)

                def take_blocks(i, who, name, dst):
                    p, k = ring(i, who, name)
                    act.wait_ge(full[p], k + 1)
                    hold_waits(act, m)
                    for h in range(hpc):
                        r = slice(h * dh, (h + 1) * dh)
                        last = nc.scalar.copy(dst[r, :, :], flat(pair[p][r, :, :]).rearrange("p (c n) -> p c n", c=nch)
                                              [:, :, h * SEQ:(h + 1) * SEQ])
                    last.then_inc(free[p], 1)
                    return free[p], k + 2

                def take_sums(i, who, b):
                    act.wait_ge(divided, b + 1)
                    take_blocks(i, who, "S", den)

                def take_outputs(i, who, b):
                    act.wait_ge(*take_blocks(i, who, "O", num))
                    act.sem_inc(taken, 1)

                def body(i, c):
                    b, u, follows = i * 2 + c, c % 2, c != LAST
                    for n in range(MT):
                        g, s = tile(i, c, n), (c * MT + n) % 2
                        r = slice(0, KT[n])
                        p, k = ring(i, c, "s", n)
                        act.wait_ge(full[p], k + 1)
                        act.wait_ge(eL_ready, g + 1)
                        act.wait_ge(es_added, g + 1)
                        nc.scalar.activation(e[r, s, :], flat(pair[p][r, :, :]), ACT.Exp).then_inc(free[p], 1)
                        act.wait_ge(free[p], k + 2)
                        act.wait_ge(pooled, g + 1)
                        nc.scalar.copy(eH[r, s, :], e[r, s, :]).then_inc(eH_ready, 1)
                        if n == 0 and c:
                            copy_pooled(i, c - 1)
                        if n == 1 and follows:
                            round_q(i, c, b + 1, 1 - u)
                        if follows or n < MT - 2:
                            split_keys(g + 2, s, i * (MT * 16) + ((c * MT + n + 2) // 2 + 1) * 16)
                        if follows or n < MT - 1:
                            split_values(g + 1, 1 - s)
                        if n == 2 and c:
                            take_sums(i, c, b - 1)
                        if n == 3 and c:
                            take_outputs(i, c, b - 1)

                each_batch(act, body)
                copy_pooled(0, LAST)
                take_sums(0, "end", LAST)
                take_outputs(0, "end", LAST)

            @block.vector
            def _(dve):
                dve.sem_inc(v_lo, 2)
                dve.sem_inc(eL_ready, 2)
                dve.sem_inc(pooled, 2)
                dve.wait_ge(set_up, 7)

                def split_keys(g, s):
                    dve.wait_ge(k_hi, g + 1)
                    nc.vector.tensor_tensor(kL0[:, s, :], raw[:, s, 0:P], kHX[:, s, 0:P].bitcast(F32), ALU.subtract)
                    low = kHX[SEQ:P, s, P:2 * P]
                    nc.vector.tensor_tensor(low, raw[SEQ:P, s, P:2 * P], low.bitcast(F32), ALU.subtract).then_inc(k_lo, 1)

                def split_values(g, s):
                    dve.wait_ge(v_hi, g + 1)
                    nc.vector.tensor_tensor(vHL[:, s, 2 * P:3 * P], raw[:, s, 2 * P:3 * P], vHL[:, s, 0:P].bitcast(F32),
                                            ALU.subtract)
                    nc.vector.tensor_tensor(vHL[:, s, DC:2 * P], raw[:, s, 3 * P:RAW], vHL[:, s, P:DC].bitcast(F32),
                                            ALU.subtract).then_inc(v_lo, 1)

                def split_q(i, who, b, s):
                    for x, (name, hi, lo, r) in enumerate((("qA", qH0, qL0, P), ("qB", qH1, qS, SEQ))):
                        p, k = ring(i, who, name)
                        dve.wait_ge(q_hi, b * 2 + x + 1)
                        nc.vector.tensor_tensor(lo[0:r, s, :], flat(pair[p][0:r, :, :]), hi[0:r, s, :].bitcast(F32),
                                                ALU.subtract).then_inc(free[p], 1)

                def max_part(i, who, j, half):
                    p, k = ring(i, who, f"m{half}", j)
                    dve.wait_ge(full[p], k + 1)
                    nc.vector.tensor_reduce(mx[:, j, half:half + 1], flat(pair[p][:, :, :])[:, 0:(TOK, REST)[half]],
                                            AX.X, ALU.max).then_inc(free[p], 1)

                def max_all(i, who):
                    for half in range(2):
                        p, k = ring(i, who, f"m{half}", 7)
                        dve.wait_ge(free[p], k + 2)
                    nc.vector.tensor_reduce(nmx[:, :], mx[:, :, :], AX.X, ALU.max, negate=True).then_inc(max_ready, 1)

                def shift_row(i, who, b, s):
                    p, k = ring(i, who, "neg")
                    dve.wait_ge(full[p], k + 1)
                    row, hi, lo = flat(pair[p][0:1, :, :]), qS[SEQ:SEQ + 1, s, :], qS[SEQ + 32:SEQ + 33, s, :]
                    nc.vector.tensor_copy(hi, row).then_inc(shifted, 1)
                    dve.wait_ge(shifted, b + 1)
                    nc.vector.tensor_tensor(lo, row, hi.bitcast(F32), ALU.subtract).then_inc(summed, 1)
                    dve.wait_ge(summed, b + 1)
                    dve.sem_inc(free[p], 1)

                split_q(0, "start", 0, 0)
                split_keys(0, 0)
                split_values(0, 0)
                split_keys(1, 1)
                for j in range(8):
                    max_part(0, "start", j, 0)
                    max_part(0, "start", j, 1)
                max_all(0, "start")
                shift_row(0, "start", 0, 0)

                def copy_pooled(i, c):
                    dve.wait_ge(pooled, tile(i, c, MT - 1) + 3)
                    nc.vector.tensor_copy(pt2, flat(acc2[:, :, :])).then_inc(pooled_out, 1)

                def invert_sums(b, half):
                    dve.wait_ge(taken, b + 1)
                    part = den[:, half * (nch // 2):(half + 1) * (nch // 2), :]
                    nc.vector.reciprocal(part, part).then_inc(inverted, 1)

                def body(i, c):
                    b, u, follows = i * 2 + c, c % 2, c != LAST
                    for n in range(MT):
                        g, s = tile(i, c, n), (c * MT + n) % 2
                        r = slice(0, KT[n])
                        if 3 <= n <= 10 and follows:
                            max_part(i, c, n - 3, 0)
                        dve.wait_ge(eH_ready, g + 1)
                        nc.vector.tensor_tensor(eL[r, s, :], e[r, s, :], eH[r, s, :].bitcast(F32),
                                                ALU.subtract).then_inc(eL_ready, 1)
                        if n == 0 and c:
                            copy_pooled(i, c - 1)
                        if n == 1 and follows:
                            split_q(i, c, b + 1, 1 - u)
                        if follows or n < MT - 2:
                            split_keys(g + 2, s)
                        if follows or n < MT - 1:
                            split_values(g + 1, 1 - s)
                        if 3 <= n <= 10 and follows:
                            max_part(i, c, n - 3, 1)
                        if n == 10 and follows:
                            max_all(i, c)
                        if n == 11 and follows:
                            shift_row(i, c, b + 1, 1 - u)
                        if n >= MT - 2 and c:
                            invert_sums(b - 1, n - (MT - 2))

                each_batch(dve, body)
                copy_pooled(0, LAST)
                invert_sums(LAST, 0)
                invert_sums(LAST, 1)


def narrow_cross_attention_blocks(nc, m, d, t):
    F32R = mybir.dt.float32r
    heads, dh = 16, 16
    HPC = P // dh
    HD = heads * dh
    REST = KEYS - TOK
    KT = [min(P, KEYS - n * P) for n in range(MT)]
    LAST = BATCH - 1
    ctx, sb, ps, sem = scope(nc, m)
    with ctx:
        qT = m.featT
        bq = sb("bq", [P, KD])
        w = sb("w_raw", [P, 2, 2 * HD])
        biases = sb("bk_bv", [P, 2, KD])
        own = sb("own_head", [P, HPC, SEQ])
        inner, sb2, _, _ = scope(nc, m)
        with inner:
            wq = sb2("wq", [P, KD, HD])
            feature_major_block(nc, m, [(qT, KD, wq, m.xnT, KD, ("bias", bq, dh ** -0.5))],
                                [(wq[:, :, :], d["wq"]), (bq[:, :], d["bq"])],
                                later=((w[:, :, :], d["w"]), (biases[:, :, :], d["biases"]), (own[:, :, :], t["own16"]),
                                       (m.wo[:, 0:KD, :], d["wo"]), (m.bo[:, :], d["bo"])))

        wH = sb("w_hi", [P, 2, 2 * HD], F32R)
        wL = sb("w_lo", [P, 2, 2 * HD], F32R)
        wb = sb("wk_bf", [P, 2, HD], BF16)
        ones = sb("ones_mat", [P, P])
        onesS = sb("ones_rows", [33, P], F32R)
        raw = sb("raw", [P, 2, 2, 2 * P])
        cX = sb("cX", [P, 2, 2, 2 * P], F32R)
        cL0 = sb("cL0", [P, 2, 2, P], F32R)
        kf = sb("keys", [P, 2, KD, 2 * P])
        vf = sb("values", [P, 2, 2, HD])
        kH, kL = sb("kH", [P, 2, KD, 2 * P], F32R), sb("kL", [P, 2, KD, 2 * P], F32R)
        vH, vL = sb("vH", [P, 2, 2, HD], F32R), sb("vL", [P, 2, 2, HD], F32R)
        cb1, cb2 = sb("ctx_bf1", [P, KEYS], BF16), sb("ctx_bf2", [SEQ, KEYS], BF16)
        kb = sb("keys_bf", [P, KD, KEYS], BF16)
        z = sb("q_own", [P, KD, HPC, SEQ])
        qb = sb("q_bf", [P, TOK], BF16)
        qH, qL = sb("qH", [P, 2, TOK], F32R), sb("qL", [P, 2, TOK], F32R)
        qS = sb("shift", [33, 2, TOK], F32R)
        e = sb("e", [P, 2, TOK])
        eH, eL = sb("eH", [P, 2, TOK], F32R), sb("eL", [P, 2, TOK], F32R)
        es = sb("e_sum", [P, 2, TOK])
        kept = m.xnT[:, 0, :].rearrange("p (c n) -> p c n", c=KD)
        den, num = sb("den", [P, KD, SEQ]), sb("num", [P, KD, SEQ])
        mx, nmx = sb("max_parts", [P, 8, 2]), sb("neg_max", [P, 8])
        pair = [ps("pair0", [P, 2, HALF]), ps("pair1", [P, 2, HALF])]
        k_ps, v_ps = ps("k_ps", [P, KD, 2 * P]), ps("v_ps", [P, 2, HD])
        acc = ps("acc", [P, 2, HALF])

        set_up = sem("set_up")
        w_hi, w_ready = sem("w_hi"), sem("w_ready")
        raw_in = [sem(f"raw_in{k}") for k in range(2)]
        bf_in, bf_before = m.bf_in, m.bf_in_count
        m.bf_in_count += (BATCH + 1) * 32
        c_hi, c_lo = sem("c_hi"), sem("c_lo")
        projected = sem("projected")
        k_out = sem("k_out")
        evacuated = sem("evacuated")
        k_hi, k_lo = sem("k_hi"), sem("k_lo")
        v_hi, v_lo = sem("v_hi"), sem("v_lo")
        full = [sem(f"full{p}") for p in range(2)]
        free = [sem(f"free{p}") for p in range(2)]
        q_own = sem("q_own")
        q_hi, q_lo, q_cast = sem("q_hi"), sem("q_lo"), sem("q_cast")
        kb_ready = sem("kb_ready")
        max_ready = sem("max_ready")
        shift_hi, shift_lo = sem("shift_hi"), sem("shift_lo")
        eH_ready = sem("eH_ready")
        eL_ready = sem("eL_ready")
        es_added = sem("es_added")
        pooled = sem("pooled")
        vec = sem("vec")
        inverted, divided = sem("inverted"), sem("divided")
        acc_read = sem("acc_read")

        def next_items(c, tile=None):
            out = {n: [(c, "kb", n)] * (n <= 3) + [(c, "m0", n - 3), (c, "m1", n - 3)] * (n >= 3) for n in range(11)}
            out[11] = [(c, "neg")]
            return out.get(tile, []) if tile is not None else [x for n in range(MT) for x in out.get(n, [])]

        def batch_items(c):
            for n in range(MT):
                yield (c, "s", n)
                yield from next_items(c, n) if c != LAST else []
                yield from [(c, "S")] if n == 2 and c else []

        UNROLL, REMAIN = 4, range(LAST - 2, LAST + 1)
        TURNS = (BATCH - 1 - len(REMAIN)) // UNROLL
        ring = Ring(next_items("start") + list(batch_items(0)), [x for c in range(1, UNROLL + 1) for x in batch_items(c)],
                    TURNS, [x for c in REMAIN for x in batch_items(c)] + [("end", "S")])

        def each_batch(eng, body):
            body(0, 0)
            with eng.Fori(0, TURNS) as i:
                for c in range(1, UNROLL + 1):
                    body(i, c)
            for c in REMAIN:
                body(0, c)

        def tile(i, c, n):
            return i * (UNROLL * MT) + (c * MT + n)

        def pair_ahead(i, c, n):
            k = c * MT + n
            if k % 2 or k + 2 >= BATCH * MT:
                return None
            return i * (UNROLL * MT // 2) + (k + 2) // 2, (k + 2) // 2 % 2

        def pair_read_ahead(i, c, n):
            k = c * MT + n
            if k % 2 == 0 or k + 3 >= BATCH * MT:
                return None
            return i * (UNROLL * MT // 2) + (k + 3) // 2, (k + 3) // 2 % 2

        with engines_block(nc, m) as block:

            @block.sync
            def _(sp):
                with sp.Fori(0, BATCH * MT // 4) as i:
                    for k in range(2):
                        q = i * 2 + k
                        sp.wait_ge(c_lo, q + 1)
                        sp.dma_start(raw[:, k, :, :], t["ctx_tiles"][bass.ds(i * 4 + k * 2, 2), :, 0:2 * P]
                                     .rearrange("o p n -> p o n")).then_inc(raw_in[k], 16)

            @block.gpsimd
            def _(pool):
                pool.sem_inc(c_lo, 2)
                pool.sem_inc(free[0], 1)
                pool.sem_inc(free[1], 1)
                pool.sem_inc(es_added, 2)
                nc.gpsimd.memset(ones[:, :], 1.0).then_inc(set_up, 1)
                nc.gpsimd.memset(onesS[:, :].bitcast(F32), 0.0).then_inc(set_up, 1)
                nc.gpsimd.memset(qS[:, :, :].bitcast(F32), 0.0).then_inc(set_up, 1)
                pool.wait_ge(set_up, 3)
                nc.gpsimd.memset(onesS[0:1, :].bitcast(F32), 1.0).then_inc(set_up, 1)
                nc.gpsimd.memset(onesS[32:33, :].bitcast(F32), 1.0).then_inc(set_up, 1)

                def load_bf(b):
                    pool.dma_start(cb1[:, :], t["ctxT1"][bass.ds(b, 1)].rearrange("o p n -> p (o n)")).then_inc(bf_in, 16)
                    pool.dma_start(cb2[:, :], t["ctxT2"][bass.ds(b, 1)].rearrange("o p n -> p (o n)")).then_inc(bf_in, 16)

                def keep_own(b):
                    for c in range(KD):
                        last = nc.gpsimd.tensor_tensor(
                            z[:, c, :, :], own[:, :, :],
                            qT[:, c:c + 1, bass.ds(b * SEQ, SEQ)].to_broadcast([P, HPC, SEQ]), ALU.mult)
                    last.then_inc(q_own, 1)

                load_bf(0)
                pool.wait_ge(set_up, 5)
                keep_own(0)
                pool.wait_ge(kb_ready, 4)
                load_bf(1)

                def body(i, c):
                    b, u, follows = i * UNROLL + c, c % 2, c != LAST
                    for n in range(MT):
                        p, k = ring(i, c, "s", n)
                        pool.wait_ge(free[p], k + 2)
                        g, s = tile(i, c, n), (c * MT + n) % 2
                        if n == 1:
                            nc.gpsimd.tensor_tensor(es[:, u, :], e[:, 1 - s, :], e[:, s, :], ALU.add).then_inc(es_added, 2)
                        if n > 1:
                            pool.wait_ge(es_added, g + 2)
                            nc.gpsimd.tensor_tensor(es[0:KT[n], u, :], es[0:KT[n], u, :], e[0:KT[n], s, :],
                                                    ALU.add).then_inc(es_added, 1)
                        if n == 1 and follows:
                            pool.wait_ge(q_cast, b + 1)
                            pool.wait_ge(q_lo, b + 1)
                            hold_waits(pool, m)
                            keep_own(b + 1)
                        if n == 4 and follows:
                            pool.wait_ge(kb_ready, b * 4 + 8)
                            load_bf(b + 2)

                each_batch(pool, body)

            @block.tensor
            def _(pe):
                pe.wait_ge(w_ready, 1)
                pe.wait_ge(set_up, 5)

                def fill(i, *key):
                    p, k = ring(i, *key)
                    pe.wait_ge(free[p], k + 1)
                    return pair[p], full[p]

                def project(q, s):
                    pe.wait_ge(c_lo, q + 3)
                    pe.wait_ge(evacuated, q + 1)
                    cH, cHL, cL, c1 = cX[:, s, :, 0:P], cX[:, s, :, P:2 * P], cL0[:, s, :, :], cX[0:SEQ, s, :, P:2 * P]
                    for c in range(KD):
                        cols = slice(c * P, (c + 1) * P)
                        out = k_ps[:, c, :].rearrange("p (o n) -> p o n", o=2)
                        for x, (a, v) in enumerate(((wH[:, 0, cols], cH), (wL[:, 0, cols], cH), (wH[:, 0, cols], cL),
                                                    (wH[:, 1, cols], cHL), (wL[0:SEQ, 1, cols], c1))):
                            nc.tensor.matmul(out, a, v, start=(x == 0), stop=(x == 4))
                    cols = slice(HD, 2 * HD)
                    for o in range(2):
                        for x, (a, v) in enumerate(((cH, wH[:, 0, cols]), (cH, wL[:, 0, cols]), (cL, wH[:, 0, cols]),
                                                    (cHL, wH[:, 1, cols]), (c1, wL[0:SEQ, 1, cols]))):
                            last = nc.tensor.matmul(v_ps[:, o, :], a[:, o, :], v, start=(x == 0), stop=(x == 4))
                    last.then_inc(projected, 1)

                def project_bf(i, who, n, b):
                    if n == 0:
                        pe.wait_ge(bf_in, b * 32 + bf_before + 32)
                    dst, done = fill(i, who, "kb", n)
                    c = n // 2
                    for h, a, x in (((0, 0, HALF), (1, HALF, TOK)), ((0, TOK, TOK + HALF), (1, TOK + HALF, KEYS)))[n % 2]:
                        nc.tensor.matmul(dst[:, h, 0:x - a], wb[:, 0, c * P:(c + 1) * P], cb1[:, a:x], start=True, stop=False)
                        last = nc.tensor.matmul(dst[:, h, 0:x - a], wb[0:SEQ, 1, c * P:(c + 1) * P], cb2[:, a:x],
                                                start=False, stop=True)
                    last.then_inc(done, 1)

                def max_part(i, who, j, half, b):
                    if half == 0 and j % 4 == 0:
                        pe.wait_ge(q_cast, b + 1)
                        pe.wait_ge(kb_ready, b * 4 + 2 + j // 2)
                    dst, done = fill(i, who, f"m{half}", j)
                    for h, a, x in (((0, 0, HALF), (1, HALF, TOK)), ((0, TOK, TOK + HALF), (1, TOK + HALF, KEYS)))[half]:
                        last = nc.tensor.matmul(dst[:, h, 0:x - a], qb[:, j * P:(j + 1) * P], kb[:, j // 4, a:x],
                                                start=True, stop=True)
                    last.then_inc(done, 1)

                def shift_row(i, who, b):
                    pe.wait_ge(max_ready, b + 1)
                    dst, done = fill(i, who, "neg")
                    for j in range(8):
                        last = nc.tensor.matmul(flat(dst[0:1, :, :])[:, j * P:(j + 1) * P], nmx[:, j:j + 1], m.ident[:, :],
                                                start=True, stop=True)
                    last.then_inc(done, 1)

                def scores(i, c, n):
                    u, b = c % 2, i * UNROLL + c
                    k = c * MT + n
                    s, own_pair = k // 2 % 2, i * (UNROLL * MT // 2) + k // 2
                    if n == 0:
                        pe.wait_ge(q_lo, b + 1)
                        pe.wait_ge(shift_lo, b + 1)
                    pe.wait_ge(k_lo, own_pair + 1)
                    dst, done = fill(i, c, "s", n)
                    for h in range(2):
                        cols, r = slice(h * HALF, (h + 1) * HALF), slice(0, KT[n])
                        keys = slice(k % 2 * P, k % 2 * P + KT[n])
                        for x, (a, v) in enumerate(((kH[:, s, h, keys], qH[:, u, cols]), (kH[:, s, h, keys], qL[:, u, cols]),
                                                    (kL[:, s, h, keys], qH[:, u, cols]), (onesS[:, r], qS[:, u, cols]))):
                            last = nc.tensor.matmul(dst[r, h, :], a, v, start=(x == 0), stop=(x == 3))
                    last.then_inc(done, 1)

                def pool_tile(i, c, n):
                    g, s, b = tile(i, c, n), (c * MT + n) % 2, i * UNROLL + c
                    pe.wait_ge(eL_ready, g + 3)
                    pe.wait_ge(v_lo, g + 5)
                    if n == 0:
                        pe.wait_ge(acc_read, b + 1)
                    r, vs, vo = slice(0, KT[n]), (c * MT + n) // 2 % 2, (c * MT + n) % 2
                    for h in range(2):
                        cols, f = slice(h * HALF, (h + 1) * HALF), slice(h * P, (h + 1) * P)
                        nc.tensor.matmul(acc[:, h, :], vH[r, vs, vo, f], eH[r, s, cols], start=(n == 0), stop=False)
                        nc.tensor.matmul(acc[:, h, :], vH[r, vs, vo, f], eL[r, s, cols], start=False, stop=False)
                        last = nc.tensor.matmul(acc[:, h, :], vL[r, vs, vo, f], eH[r, s, cols], start=False, stop=(n == MT - 1))
                    last.then_inc(pooled, 1)

                def sum_up(i, who, c):
                    pe.wait_ge(es_added, tile(i, c, MT - 1) + 3)
                    dst, done = fill(i, who, "S")
                    for h in range(2):
                        last = nc.tensor.matmul(dst[:, h, :], ones[:, :], es[:, c % 2, h * HALF:(h + 1) * HALF],
                                                start=True, stop=True)
                    last.then_inc(done, 1)

                project(0, 0)
                for n in range(4):
                    project_bf(0, "start", n, 0)
                for j in range(8):
                    max_part(0, "start", j, 0, 0)
                    max_part(0, "start", j, 1, 0)
                shift_row(0, "start", 0)

                def body(i, c):
                    b, follows = i * UNROLL + c, c != LAST
                    for n in range(MT):
                        scores(i, c, n)
                        if n <= 3 and follows:
                            project_bf(i, c, n, b + 1)
                        if 3 <= n <= 10 and follows:
                            max_part(i, c, n - 3, 0, b + 1)
                        if n == 0 and c:
                            pool_tile(i, c - 1, MT - 1)
                        if n:
                            pool_tile(i, c, n - 1)
                        if 3 <= n <= 10 and follows:
                            max_part(i, c, n - 3, 1, b + 1)
                        if pair_ahead(i, c, n):
                            project(*pair_ahead(i, c, n))
                        if n == 11 and follows:
                            shift_row(i, c, b + 1)
                        if n == 2 and c:
                            sum_up(i, c, c - 1)

                each_batch(pe, body)
                pool_tile(0, LAST, MT - 1)
                sum_up(0, "end", LAST)

            @block.scalar
            def _(act):
                act.sem_inc(evacuated, 1)
                act.wait_ge(set_up, 5)
                nc.scalar.copy(flat(wH[:, :, :]), flat(w[:, :, :])).then_inc(w_hi, 1)
                nc.scalar.copy(wb[:, :, :], w[:, :, 0:HD]).then_inc(w_hi, 1)

                def split_context(q, s):
                    act.wait_ge(raw_in[s], (q + 2 - s) * 8)
                    if not isinstance(q, int) or q >= 2:
                        act.wait_ge(projected, q - 1)
                    nc.scalar.copy(cX[:, s, :, :], raw[:, s, :, :]).then_inc(c_hi, 1)

                def round_projected(q, s):
                    act.wait_ge(projected, q + 1)
                    for ch in range(KD):
                        nc.scalar.activation(kf[:, s, ch, :], k_ps[:, ch, :], ACT.Identity,
                                             bias=biases[:, 0, ch:ch + 1]).then_inc(k_out, 1)
                    act.wait_ge(v_lo, q * 2 + 2)
                    nc.scalar.copy(vf[:, s, :, :], v_ps[:, :, :]).then_inc(evacuated, 1)
                    act.wait_ge(k_out, q * 2 + 2)
                    nc.scalar.copy(kH[:, s, :, :], kf[:, s, :, :]).then_inc(k_hi, 1)

                def round_values(i, c, n):
                    g, k = tile(i, c, n), c * MT + n
                    act.wait_ge(evacuated, i * (UNROLL * MT // 2) + k // 2 + 2)
                    if not isinstance(g, int) or g >= 4:
                        act.wait_ge(pooled, g - 1)
                    nc.scalar.copy(vH[:, k // 2 % 2, k % 2, :], vf[:, k // 2 % 2, k % 2, :]).then_inc(v_hi, 1)

                def keys_bf(i, who, n):
                    p, k = ring(i, who, "kb", n)
                    act.wait_ge(full[p], k + 1)
                    a, x = ((0, TOK), (TOK, KEYS))[n % 2]
                    nc.scalar.activation(kb[:, n // 2, a:x], flat(pair[p][:, :, :])[:, 0:x - a], ACT.Identity,
                                         bias=biases[:, 0, n // 2:n // 2 + 1]).then_inc(free[p], 1)
                    act.wait_ge(free[p], k + 2)
                    act.sem_inc(kb_ready, 1)

                def round_q(b, s):
                    act.wait_ge(q_own, b + 1)
                    nc.scalar.copy(qH[:, s, :], z[:, :, :, :].rearrange("p c h q -> p (c h q)")).then_inc(q_hi, 1)

                def cast_q(b):
                    act.wait_ge(q_own, b + 1)
                    nc.scalar.copy(qb[:, :], z[:, :, :, :].rearrange("p c h q -> p (c h q)")).then_inc(q_cast, 1)

                split_context(0, 0)
                split_context(1, 1)
                round_q(0, 0)
                cast_q(0)
                round_projected(0, 0)
                round_values(0, 0, 0)
                for n in range(4):
                    keys_bf(0, "start", n)

                def body(i, c):
                    b, u, follows = i * UNROLL + c, c % 2, c != LAST
                    for n in range(MT):
                        g, s = tile(i, c, n), (c * MT + n) % 2
                        r = slice(0, KT[n])
                        p, k = ring(i, c, "s", n)
                        act.wait_ge(full[p], k + 1)
                        act.wait_ge(eL_ready, g + 1)
                        act.wait_ge(es_added, g + 1)
                        nc.scalar.activation(e[r, s, :], flat(pair[p][r, :, :]), ACT.Exp).then_inc(free[p], 1)
                        act.wait_ge(free[p], k + 2)
                        act.wait_ge(pooled, g + 1)
                        nc.scalar.copy(eH[r, s, :], e[r, s, :]).then_inc(eH_ready, 1)
                        if n <= 3 and follows:
                            keys_bf(i, c, n)
                        if follows or n < MT - 1:
                            round_values(i, c, n + 1)
                        if pair_ahead(i, c, n):
                            round_projected(*pair_ahead(i, c, n))
                        if pair_read_ahead(i, c, n):
                            split_context(*pair_read_ahead(i, c, n))
                        if n == 2 and follows:
                            cast_q(b + 1)
                        if n == 9 and follows:
                            round_q(b + 1, 1 - u)

                each_batch(act, body)

            @block.vector
            def _(dve):
                dve.sem_inc(v_lo, 4)
                dve.sem_inc(eL_ready, 2)
                dve.sem_inc(pooled, 2)
                dve.sem_inc(acc_read, 1)
                dve.sem_inc(vec, 1)
                dve.wait_ge(set_up, 5)
                dve.wait_ge(w_hi, 2)
                nc.vector.tensor_tensor(flat(wL[:, :, :]), flat(w[:, :, :]), flat(wH[:, :, :]).bitcast(F32),
                                        ALU.subtract).then_inc(w_ready, 1)

                def split_context(q, s):
                    dve.wait_ge(c_hi, q + 1)
                    nc.vector.tensor_tensor(cL0[:, s, :, :], raw[:, s, :, 0:P], cX[:, s, :, 0:P].bitcast(F32), ALU.subtract)
                    low = cX[SEQ:P, s, :, P:2 * P]
                    nc.vector.tensor_tensor(low, raw[SEQ:P, s, :, P:2 * P], low.bitcast(F32), ALU.subtract).then_inc(c_lo, 1)

                def split_projected(q, s):
                    dve.wait_ge(k_hi, q + 1)
                    nc.vector.tensor_tensor(kL[:, s, :, :], kf[:, s, :, :], kH[:, s, :, :].bitcast(F32),
                                            ALU.subtract).then_inc(k_lo, 1)

                def split_values(i, c, n):
                    g, k = tile(i, c, n), c * MT + n
                    s, o = k // 2 % 2, k % 2
                    dve.wait_ge(v_hi, g + 1)
                    nc.vector.tensor_tensor(vL[:, s, o, :], vf[:, s, o, :], vH[:, s, o, :].bitcast(F32),
                                            ALU.subtract).then_inc(v_lo, 1)

                def split_q(b, s):
                    dve.wait_ge(q_hi, b + 1)
                    nc.vector.tensor_tensor(qL[:, s, :], z[:, :, :, :].rearrange("p c h q -> p (c h q)"),
                                            qH[:, s, :].bitcast(F32), ALU.subtract).then_inc(q_lo, 1)

                def max_part(i, who, j, half):
                    p, k = ring(i, who, f"m{half}", j)
                    dve.wait_ge(full[p], k + 1)
                    nc.vector.tensor_reduce(mx[:, j, half:half + 1], flat(pair[p][:, :, :])[:, 0:(TOK, REST)[half]],
                                            AX.X, ALU.max).then_inc(free[p], 1)

                def max_all(i, who):
                    for half in range(2):
                        p, k = ring(i, who, f"m{half}", 7)
                        dve.wait_ge(free[p], k + 2)
                    nc.vector.tensor_reduce(nmx[:, :], mx[:, :, :], AX.X, ALU.max, negate=True).then_inc(max_ready, 1)

                def shift_row(i, who, b, s):
                    p, k = ring(i, who, "neg")
                    row, hi = flat(pair[p][0:1, :, :]), qS[0:1, s, :]
                    dve.wait_ge(full[p], k + 1)
                    nc.vector.tensor_copy(hi, row).then_inc(shift_hi, 1)
                    dve.wait_ge(shift_hi, b + 1)
                    nc.vector.tensor_tensor(qS[32:33, s, :], row, hi.bitcast(F32), ALU.subtract).then_inc(shift_lo, 1)
                    dve.wait_ge(shift_lo, b + 1)
                    dve.sem_inc(free[p], 1)

                STEPS = 4

                def own_of(dst, src, b, n, read):
                    dve.wait_ge(vec, b * STEPS + n + 1)
                    nc.vector.tensor_tensor(kept.rearrange("p c (h q) -> p c h q", q=SEQ),
                                            src.rearrange("p c (h q) -> p c h q", q=SEQ),
                                            own[:, :, :].unsqueeze(1).to_broadcast([P, KD, HPC, SEQ]),
                                            ALU.mult).then_inc(vec, 1)
                    dve.wait_ge(vec, b * STEPS + n + 2)
                    dve.sem_inc(read, 1)
                    return nc.vector.tensor_reduce(dst[:, :, :], kept.rearrange("p c (h q) -> p c q h", q=SEQ),
                                                   AX.X, ALU.add)

                def take_pooled(i, c):
                    b = i * UNROLL + c
                    dve.wait_ge(pooled, tile(i, c, MT - 1) + 3)
                    own_of(num, acc[:, :, :], b, 0, acc_read).then_inc(vec, 1)

                def outputs(i, who, c):
                    b = i * UNROLL + c
                    p, k = ring(i, who, "S")
                    dve.wait_ge(full[p], k + 1)
                    own_of(den, pair[p][:, :, :], b, 2, free[p]).then_inc(vec, 1)
                    dve.wait_ge(vec, b * STEPS + 5)
                    nc.vector.reciprocal(den[:, :, :], den[:, :, :]).then_inc(inverted, 1)
                    dve.wait_ge(inverted, b + 1)
                    nc.vector.tensor_tensor(num[:, :, :], num[:, :, :], den[:, :, :], ALU.mult).then_inc(divided, 1)
                    dve.wait_ge(divided, b + 1)
                    hold_waits(dve, m)
                    for ch in range(KD):
                        nc.vector.tensor_scalar(m.featT[:, ch, bass.ds(b * SEQ, SEQ)], num[:, ch, :],
                                                biases[:, 1, ch:ch + 1], None, ALU.add)

                split_context(0, 0)
                split_context(1, 1)
                split_q(0, 0)
                split_projected(0, 0)
                split_values(0, 0, 0)
                for j in range(8):
                    max_part(0, "start", j, 0)
                    max_part(0, "start", j, 1)
                max_all(0, "start")
                shift_row(0, "start", 0, 0)

                def body(i, c):
                    b, u, follows = i * UNROLL + c, c % 2, c != LAST
                    for n in range(MT):
                        g, s = tile(i, c, n), (c * MT + n) % 2
                        r = slice(0, KT[n])
                        if 3 <= n <= 10 and follows:
                            max_part(i, c, n - 3, 0)
                            max_part(i, c, n - 3, 1)
                        dve.wait_ge(eH_ready, g + 1)
                        nc.vector.tensor_tensor(eL[r, s, :], e[r, s, :], eH[r, s, :].bitcast(F32),
                                                ALU.subtract).then_inc(eL_ready, 1)
                        if n == 0 and c:
                            take_pooled(i, c - 1)
                        if follows or n < MT - 1:
                            split_values(i, c, n + 1)
                        if pair_ahead(i, c, n):
                            split_projected(*pair_ahead(i, c, n))
                        if pair_read_ahead(i, c, n):
                            split_context(*pair_read_ahead(i, c, n))
                        if n == 10 and follows:
                            max_all(i, c)
                        if n == 10 and follows:
                            split_q(b + 1, 1 - u)
                        if n == 11 and follows:
                            shift_row(i, c, b + 1, 1 - u)
                        if n == 2 and c:
                            outputs(i, c, c - 1)

                each_batch(dve, body)
                take_pooled(0, LAST)
                outputs(0, "end", LAST)


def token_major_block(nc, m, jobs, loads):
    ctx, sb, ps, sem = scope(nc, m)
    with ctx:
        ring = [ps(f"ring{i}", [P, HALF]) for i in range(4)]
        loaded = sem("loaded")
        filled = sem("filled")
        act_done = sem("act_done")
        dve_done = sem("dve_done")
        pieces = [(j, t) for t in range(TT) for j in range(len(jobs))]
        with engines_block(nc, m) as block:

            @block.sync
            def _(sp):
                for buf, dram in loads:
                    sp.dma_start(buf, dram).then_inc(loaded, 16)

            @block.tensor
            def _(pe):
                if loads:
                    pe.wait_ge(loaded, 16 * len(loads))
                for n, (j, t) in enumerate(pieces):
                    dst, w, src, kc, bias = jobs[j]
                    cols = dst.shape[-1]
                    if n >= 4:
                        pe.wait_ge(act_done if n % 2 == 0 else dve_done, (n - 4) // 2 + 1)
                    for k in range(kc):
                        last = nc.tensor.matmul(ring[n % 4][:, 0:cols], src[:, k, t * P:(t + 1) * P], w[:, k, :],
                                                start=(k == 0), stop=(k == kc - 1 and bias is None))
                    if bias is not None:
                        last = nc.tensor.matmul(ring[n % 4][:, 0:cols], m.ones[0:1, :], bias, start=False, stop=True)
                    last.then_inc(filled, 1)

            @block.scalar
            def _(act):
                for n, (j, t) in enumerate(pieces):
                    if n % 2 == 0:
                        dst = jobs[j][0]
                        act.wait_ge(filled, n + 1)
                        nc.scalar.copy(dst[:, t, :], ring[n % 4][:, 0:dst.shape[-1]]).then_inc(act_done, 1)

            @block.vector
            def _(dve):
                for n, (j, t) in enumerate(pieces):
                    if n % 2 == 1:
                        dst = jobs[j][0]
                        dve.wait_ge(filled, n + 1)
                        nc.vector.tensor_copy(dst[:, t, :], ring[n % 4][:, 0:dst.shape[-1]]).then_inc(dve_done, 1)


def self_attention_block(nc, m, heads, dh, qT, kT, v, loads, mask_dram, causal_dram=None, o_out=None):
    nch = heads * dh // P
    hpc = P // dh
    W = heads * SEQ
    ctx, sb, ps, sem = scope(nc, m)
    with ctx:
        own = sb("own_head", [P, hpc, SEQ])
        qs = sb("q_now", [P, 2, nch, P])
        kz = sb("k_by_head", [P, 2, 2, nch, hpc * SEQ])
        vz = sb("v_by_head", [P, 2, heads // 2, 2 * dh])
        ex = sb("weights", [P, heads, SEQ])
        exT = sb("weights_T", [P, heads // 2, P])
        o = sb("o_now", [P, heads, dh])
        mx = sb("row_max", [P, heads])
        rs = sb("row_sum", [P, heads])
        tri = sb("causal", [P, SEQ]) if causal_dram is not None else None
        s_ps = [ps(f"scores{u}", [P, W]) for u in range(2)]
        t_ps = ps("weights_T_ps", [P, W])
        o_ps = ps("o_ps", [P, heads * dh])
        ot_ps = ps("oT_ps", [P, nch, P]) if o_out is None else None
        loaded = sem("loaded")
        zeroed = sem("zeroed")
        q_staged, k_staged = sem("q_staged"), sem("k_staged")
        v_ready = sem("v_ready")
        scored = sem("scored")
        shifted = sem("shifted")
        exped = sem("exped")
        transposed = sem("transposed")
        exT_ready = sem("exT_ready")
        weighed = sem("weighed")
        o_ready = sem("o_ready")
        o_transposed = sem("o_transposed")
        o_out_done = sem("o_out_done")
        vec = sem("vec")
        n_loads = len(loads) + 1 + (causal_dram is not None)
        VSTEPS = 3

        def turns(eng, body):
            for t in (0, 1):
                body(t, t)
            with eng.Fori(1, TT // 2 - 1) as i:
                for u in range(2):
                    body(i * 2 + u, u)
            for t in (TT - 2, TT - 1):
                body(t, t % 2)

        def there(t, ahead):
            return not isinstance(t, int) or 0 <= t + ahead < TT

        with engines_block(nc, m) as block:

            @block.sync
            def _(sp):
                sp.dma_start(own[:, :, :], mask_dram).then_inc(loaded, 16)
                if causal_dram is not None:
                    sp.dma_start(tri[:, :], causal_dram).then_inc(loaded, 16)
                for buf, dram in loads:
                    sp.dma_start(buf, dram).then_inc(loaded, 16)

            @block.gpsimd
            def _(pool):
                pool.sem_inc(scored, 2)
                pool.sem_inc(weighed, 1)
                pool.wait_ge(loaded, 16 * n_loads)
                nc.gpsimd.memset(vz[:, :, :, :], 0.0).then_inc(zeroed, 1)

                def body(t, u):
                    pool.wait_ge(scored, t + 1)
                    for e in range(2):
                        for c in range(nch):
                            last = nc.gpsimd.tensor_tensor(
                                kz[:, u, e, c, :].rearrange("p (h n) -> p h n", h=hpc),
                                kT[:, c, bass.ds(t * P + e * SEQ, SEQ)].unsqueeze(1).to_broadcast([P, hpc, SEQ]),
                                own[:, :, :], ALU.mult)
                    last.then_inc(k_staged, 1)

                turns(pool, body)

            @block.tensor
            def _(pe):
                def scores(t, u):
                    pe.wait_ge(q_staged, t + 1)
                    pe.wait_ge(k_staged, t + 1)
                    pe.wait_ge(shifted, t + 1)
                    for e in range(2):
                        for c in range(nch):
                            last = nc.tensor.matmul(s_ps[u][e * SEQ:(e + 1) * SEQ, c * hpc * SEQ:(c + 1) * hpc * SEQ],
                                                    qs[:, u, c, e * SEQ:(e + 1) * SEQ], kz[:, u, e, c, :],
                                                    start=True, stop=True)
                    last.then_inc(scored, 1)

                def transpose_outputs(t):
                    pe.wait_ge(o_out_done, t + 1)
                    pe.wait_ge(o_ready, t + 2)
                    for c in range(nch):
                        last = nc.tensor.transpose(
                            ot_ps[:, c, :], o[:, c * hpc:(c + 1) * hpc, :].rearrange("p h d -> p (h d)"), m.ident[:, :])
                    last.then_inc(o_transposed, 1)

                scores(0, 0)
                scores(1, 1)

                def body(t, u):
                    pe.wait_ge(exT_ready, t + 1)
                    if causal_dram is None:
                        pe.wait_ge(exped, t + 1)
                    else:
                        pe.wait_ge(shifted, t + 3)
                    for j in range(heads // 2):
                        last = nc.tensor.transpose(t_ps[:, j * P:(j + 1) * P],
                                                   ex[:, 2 * j:2 * j + 2, :].rearrange("p h n -> p (h n)"), m.ident[:, :])
                    last.then_inc(transposed, 1)
                    if o_out is None and there(t, -1):
                        transpose_outputs(t - 1)
                    if there(t, 2):
                        scores(t + 2, u)
                    pe.wait_ge(v_ready, t + 1)
                    pe.wait_ge(o_ready, t + 1)
                    pe.wait_ge(exT_ready, t + 2)
                    hold_waits(pe, m)
                    for e in range(2):
                        for j in range(heads // 2):
                            last = nc.tensor.matmul(o_ps[e * SEQ:(e + 1) * SEQ, j * 2 * dh:(j + 1) * 2 * dh],
                                                    exT[:, j, e * SEQ:(e + 1) * SEQ], vz[:, e, j, :],
                                                    start=True, stop=True)
                    last.then_inc(weighed, 1)

                turns(pe, body)
                if o_out is None:
                    transpose_outputs(TT - 1)

            @block.scalar
            def _(act):
                act.wait_ge(zeroed, 1)
                act.sem_inc(exT_ready, 1)
                act.sem_inc(o_out_done, 1)

                def stage_q(t, u):
                    act.wait_ge(scored, t + 1)
                    nc.scalar.copy(qs[:, u, :, :], qT[:, 0:nch, bass.ds(t * P, P)]).then_inc(q_staged, 1)

                def exponentials(t):
                    act.wait_ge(shifted, t + 3)
                    nc.scalar.activation(ex[:, :, :], ex[:, :, :], ACT.Exp).then_inc(exped, 1)

                def copy_outputs(t):
                    act.wait_ge(o_transposed, t + 1)
                    nc.scalar.copy(m.featT[:, 0:nch, bass.ds(t * P, P)], ot_ps[:, :, :]).then_inc(o_out_done, 1)

                stage_q(0, 0)
                stage_q(1, 1)
                if causal_dram is None:
                    exponentials(0)

                def body(t, u):
                    if there(t, 2):
                        stage_q(t + 2, u)
                    act.wait_ge(weighed, t + 1)
                    for e in range(2):
                        for par in range(2):
                            src = v[e * SEQ:(e + 1) * SEQ, bass.ds(t, 1), :].rearrange(
                                "p o (j two d) -> p (o j) two d", two=2, d=dh)[:, :, par, :]
                            last = nc.scalar.copy(
                                vz[par * SEQ:(par + 1) * SEQ, e, :, par * dh:(par + 1) * dh], src)
                    last.then_inc(v_ready, 1)
                    act.wait_ge(transposed, t + 1)
                    nc.scalar.copy(flat(exT[:, :, :]), t_ps[:, :]).then_inc(exT_ready, 1)
                    if o_out is None and there(t, -1):
                        copy_outputs(t - 1)
                    if causal_dram is None and there(t, 1):
                        exponentials(t + 1)

                turns(act, body)
                if o_out is None:
                    copy_outputs(TT - 1)

            @block.vector
            def _(dve):
                dve.sem_inc(shifted, 2)
                dve.sem_inc(o_ready, 1)
                dve.sem_inc(vec, 1)
                if causal_dram is not None:
                    dve.wait_ge(loaded, 16 * n_loads)

                def weights(t, u):
                    s3 = s_ps[u][:, :].rearrange("p (h n) -> p h n", h=heads)
                    dve.wait_ge(scored, t + 3)
                    if causal_dram is None:
                        nc.vector.tensor_reduce(mx[:, :], s3, AX.X, ALU.max).then_inc(vec, 1)
                        dve.wait_ge(vec, t * VSTEPS + 2)
                        if there(t, -1):
                            dve.wait_ge(transposed, t)
                        nc.vector.tensor_tensor(ex[:, :, :], s3, mx[:, :].unsqueeze(2).to_broadcast([P, heads, SEQ]),
                                                ALU.subtract).then_inc(shifted, 1)
                    else:
                        if there(t, -1):
                            dve.wait_ge(transposed, t)
                        nc.vector.tensor_tensor(ex[:, :, :], s3, tri[:, :].unsqueeze(1).to_broadcast([P, heads, SEQ]),
                                                ALU.mult).then_inc(shifted, 1)

                def sums(t):
                    if causal_dram is None:
                        dve.wait_ge(exped, t + 1)
                        nc.vector.tensor_reduce(rs[:, :], ex[:, :, :], AX.X, ALU.add).then_inc(vec, 1)
                    else:
                        dve.wait_ge(shifted, t + 3)
                        nc.vector.tensor_reduce(mx[:, :], ex[:, :, :], AX.X, ALU.add).then_inc(vec, 1)
                        dve.wait_ge(vec, t * VSTEPS + 2)
                        nc.vector.tensor_scalar(rs[:, :], mx[:, :], CLIP, None, ALU.max).then_inc(vec, 1)
                    dve.wait_ge(vec, t * VSTEPS + 3)
                    nc.vector.reciprocal(rs[:, :], rs[:, :]).then_inc(vec, 1)

                weights(0, 0)
                sums(0)

                def body(t, u):
                    if there(t, 1):
                        weights(t + 1, 1 - u)
                    if causal_dram is None and there(t, 1):
                        dve.wait_ge(vec, t * VSTEPS + 5)
                    else:
                        dve.wait_ge(vec, t * VSTEPS + 4)
                    dve.wait_ge(weighed, t + 2)
                    if o_out is None:
                        if there(t, -1):
                            dve.wait_ge(o_transposed, t)
                        dst = o[:, :, :]
                    else:
                        dst = o_out[:, bass.ds(t, 1), :].rearrange("p o (h d) -> p (o h) d", h=heads)
                    nc.vector.tensor_tensor(dst, o_ps[:, :].rearrange("p (h d) -> p h d", h=heads),
                                            rs[:, :].unsqueeze(2).to_broadcast([P, heads, dh]), ALU.mult).then_inc(o_ready, 1)
                    if there(t, 1):
                        dve.wait_ge(o_ready, t + 2)
                        sums(t + 1)

                turns(dve, body)


def qkv_memory(nc, m, nch, cols):
    ctx, sb, ps, sem = scope(nc, m)
    return ctx, sb, sb("qT", [P, nch, TOK]), sb("kT", [P, nch, TOK]), sb("v", [P, TT, cols])


def latent_attention_layer(nc, m, t):
    ctx, sb, qT, kT, v = qkv_memory(nc, m, KD, D)
    with ctx:
        wq, wqs, wd = (sb(n, [P, KD, c]) for n, c in (("wq", D), ("wqs", D), ("wd", P)))
        wk, wks, wv = (sb(n, [P, 1, D]) for n in ("wk", "wks", "wv"))
        qsT, ksT = sb("qsT", [P, KD, TOK]), sb("ksT", [P, KD, TOK])
        lat = sb("lat", [P, 1, TOK])
        cos, sin = sb("cos", [P, SEQ]), sb("sin", [P, SEQ])
        scale = 0.25
        feature_major_block(
            nc, m,
            [(qT, KD, wq, m.xnT, KD, ("linear", scale)), (qsT, KD, wqs, m.xnT, KD, ("linear", scale)),
             (lat, 1, wd, m.xnT, KD, ("linear", 1.0)), (kT, KD, wk, lat, 1, ("linear", 1.0)),
             (ksT, KD, wks, lat, 1, ("linear", 1.0))],
            [(wq[:, :, :], t["b_wq"]), (wqs[:, :, :], t["b_wqs"]), (wd[:, :, :], t["b_wd"]), (wk[:, :, :], t["b_wk"]),
             (wks[:, :, :], t["b_wks"]), (wv[:, :, :], t["b_wv"]), (cos[:, :], t["rope_cos"]), (sin[:, :], t["rope_sin"])])
        rotate_block(nc, m, qT, qsT, kT, ksT, cos, sin)
        token_major_block(nc, m, [(v, wv, lat, 1, None)], [])
        self_attention_block(nc, m, 16, 16, qT, kT, v, [(m.wo[:, 0:KD, :], t["b_wo"])], t["own16"])


def rotate_block(nc, m, qT, qsT, kT, ksT, cos, sin):
    ctx, sb, ps, sem = scope(nc, m)

    def rows(x, c):
        return x[:, c, :].rearrange("p (b n) -> p b n", b=BATCH)

    def table(x):
        return x[:, :].unsqueeze(1).to_broadcast([P, BATCH, SEQ])

    with ctx:
        q_steps, k_steps = sem("q_steps"), sem("k_steps")
        with engines_block(nc, m) as block:

            @block.vector
            def _(dve):
                chain = Chain(dve, q_steps)
                for c in range(KD):
                    nc.vector.tensor_tensor(rows(qT, c), rows(qT, c), table(cos), ALU.mult).then_inc(q_steps, 1)
                    chain.n += 1
                    chain.step(nc.vector.tensor_tensor(rows(qsT, c), rows(qsT, c), table(sin), ALU.mult))
                    chain.step(nc.vector.tensor_tensor(qT[:, c, :], qT[:, c, :], qsT[:, c, :], ALU.add))

            @block.gpsimd
            def _(pool):
                chain = Chain(pool, k_steps)
                for c in range(KD):
                    nc.gpsimd.tensor_tensor(rows(kT, c), rows(kT, c), table(cos), ALU.mult).then_inc(k_steps, 1)
                    chain.n += 1
                    chain.step(nc.gpsimd.tensor_tensor(rows(ksT, c), rows(ksT, c), table(sin), ALU.mult))
                    chain.step(nc.gpsimd.tensor_tensor(kT[:, c, :], kT[:, c, :], ksT[:, c, :], ALU.add))


def biased_attention_layer(nc, m, t):
    ctx, sb, qT, kT, v = qkv_memory(nc, m, KD, D)
    with ctx:
        wq, wk, wv = (sb(n, [P, KD, D]) for n in ("wq", "wk", "wv"))
        bq, bk, bv = sb("bq", [P, KD]), sb("bk", [P, KD]), sb("bv", [1, D])
        feature_major_block(
            nc, m, [(qT, KD, wq, m.xnT, KD, ("bias", bq, 0.25)), (kT, KD, wk, m.xnT, KD, ("bias", bk, 1.0))],
            [(wq[:, :, :], t["e_wq"]), (wk[:, :, :], t["e_wk"]), (wv[:, :, :], t["e_wv"]), (bq[:, :], t["e_bq"]),
             (bk[:, :], t["e_bk"]), (bv[:, :], t["e_bv"]), (m.bo[:, :], t["e_bo"])])
        token_major_block(nc, m, [(v, wv, m.xnT, KD, bv[0:1, :])], [])
        self_attention_block(nc, m, 16, 16, qT, kT, v, [(m.wo[:, 0:KD, :], t["e_wo"])], t["own16"])


def linear_attention_layer(nc, m, t):
    ctx, sb, qT, kT, v = qkv_memory(nc, m, KD, D)
    with ctx:
        wq, wk, wv = (sb(n, [P, KD, D]) for n in ("wq", "wk", "wv"))
        feature_major_block(
            nc, m, [(qT, KD, wq, m.xnT, KD, ("elu1",)), (kT, KD, wk, m.xnT, KD, ("elu1",))],
            [(wq[:, :, :], t["h_wq"]), (wk[:, :, :], t["h_wk"]), (wv[:, :, :], t["h_wv"])])
        token_major_block(nc, m, [(v, wv, m.xnT, KD, None)], [])
        self_attention_block(nc, m, 16, 16, qT, kT, v, [(m.wo[:, 0:KD, :], t["h_wo"])], t["own16"], t["causal"])

FAR = 3.0e38


def top2_steps(nc, chain, logits, rev, masks, tmp, eq, mx):
    _, groups, n = logits.shape

    def spread(x):
        return x[:, :].unsqueeze(2).to_broadcast([P, groups, n])

    ranks = rev[:, :].unsqueeze(1).to_broadcast([P, groups, n])
    for k, (src, out) in enumerate(((logits, masks), (tmp, eq))):
        chain.step(nc.vector.tensor_reduce(mx[:, :], src, AX.X, ALU.max))
        chain.step(nc.vector.tensor_tensor(eq, src, spread(mx), ALU.is_equal))
        chain.step(nc.vector.tensor_tensor(eq, eq, ranks, ALU.mult))
        chain.step(nc.vector.tensor_reduce(mx[:, :], eq, AX.X, ALU.max))
        chain.step(nc.vector.tensor_tensor(out, eq, spread(mx), ALU.is_equal))
        if k == 0:
            chain.step(nc.vector.scalar_tensor_tensor(tmp, out, -FAR, logits, ALU.mult, ALU.add))
    chain.step(nc.vector.tensor_tensor(masks, masks, eq, ALU.add))


def switch_head_layer(nc, m, t):
    H, DH, E = 8, 64, 5
    NX = E * DH
    NG = H * E
    with ExitStack() as whole:
        def big(name, shape):
            return whole.enter_context(nc.sbuf_tensor(name, shape, F32))

        qT, kT = big("c_qT", [P, 4, TOK]), big("c_kT", [P, 4, TOK])
        v = big("c_v", [P, TT, H * DH])
        xvg = big("c_xvg", [P, TT, NX + 2 * NG])
        mask = big("c_mask", [P, TT * 2 * H, E])
        o = big("c_o", [P, TT, H * DH])
        rev = big("c_rev", [P, E])
        wv = big("c_wv", [P, TT, NG])
        ctx, sb, ps, sem = scope(nc, m)
        with ctx:
            wq, wk = sb("wq", [P, KD, H * DH]), sb("wk", [P, KD, H * DH])
            wx = sb("wx", [P, KD, NX + 2 * NG])
            feature_major_block(
                nc, m, [(qT, 4, wq, m.xnT, KD, ("linear", DH ** -0.5)), (kT, 4, wk, m.xnT, KD, ("linear", 1.0))],
                [(wq[:, :, :], t["c_wq"]), (wk[:, :, :], t["c_wk"]), (wx[:, :, :], t["c_wx"]), (rev[:, :], t["rev5"])])
            token_major_block(nc, m, [(xvg, wx, m.xnT, KD, None)], [])
        switch_gates_block(nc, m, xvg, mask, wv, rev, H, E, NX)
        switch_mix_block(nc, m, H, DH, E, "values",
                         lambda i: xvg[:, bass.ds(i, 1), 0:NX].rearrange("p o (e d) -> p (o e) d", e=E)
                         .unsqueeze(2).to_broadcast([P, E, H, DH]),
                         lambda i: wv[:, bass.ds(i, 1), :].rearrange("p o (h e) -> p (o e) h", e=E)
                         .unsqueeze(3).to_broadcast([P, E, H, DH]),
                         "p e h d -> p (h d) e", v)
        self_attention_block(nc, m, H, DH, qT, kT, v, [(m.wo[:, 0:3, :], t["c_wo"])], t["own64"], None, o)
        ctx, sb, ps, sem = scope(nc, m)
        with ctx:
            a = sb("by_expert", [P, TT, NX])
            switch_mix_block(nc, m, H, DH, E, "outputs",
                             lambda i: o[:, bass.ds(i, 1), :].rearrange("p o (h d) -> p o h d", h=H)
                             .to_broadcast([P, E, H, DH]),
                             lambda i: mask[:, bass.ds(i * (2 * H) + H, H), :].rearrange("p h e -> p e h")
                             .unsqueeze(3).to_broadcast([P, E, H, DH]),
                             "p e h d -> p e d h", a)
            to_features_block(nc, m, a, NX)


def switch_gates_block(nc, m, xvg, mask, wv, rev, H, E, NX):
    G = TT * 2 * H
    ctx, sb, ps, sem = scope(nc, m)
    with ctx:
        logits, tmp, eq = (sb(n, [P, G, E]) for n in ("logits", "tmp", "eq"))
        mx = sb("mx", [P, G])
        gathered, gated = sem("gathered"), sem("gated")
        vec = sem("vec")
        gates = xvg[:, :, NX:NX + 2 * H * E]
        with engines_block(nc, m) as block:

            @block.scalar
            def _(act):
                nc.scalar.copy(logits[:, :, :].rearrange("p (t g) e -> p t (g e)", t=TT), gates).then_inc(gathered, 1)
                nc.scalar.activation(wv[:, :, :], gates[:, :, 0:H * E], ACT.Sigmoid).then_inc(gated, 1)

            @block.vector
            def _(dve):
                dve.wait_ge(gathered, 1)
                chain = Chain(dve, vec)
                top2_steps(nc, chain, logits[:, :, :], rev, mask[:, :, :], tmp[:, :, :], eq[:, :, :], mx)
                dve.wait_ge(gated, 1)
                nc.vector.tensor_tensor(wv[:, :, :], wv[:, :, :],
                                        mask[:, :, :].rearrange("p (t g) e -> p t (g e)", t=TT)[:, :, 0:H * E], ALU.mult)


def switch_mix_block(nc, m, H, DH, E, what, left, right, order, dst):
    ctx, sb, ps, sem = scope(nc, m)
    with ctx:
        prod = sb("prod", [P, 2, E, H, DH])
        multiplied, summed = sem("multiplied"), sem("summed")
        by_dve = sem("by_dve")
        POOLS = E - 2
        with engines_block(nc, m) as block:

            @block.gpsimd
            def _(pool):
                pool.sem_inc(summed, 2)
                with pool.Fori(0, TT // 2) as i:
                    for u in range(2):
                        n = i * 2 + u
                        pool.wait_ge(summed, n + 1)
                        hold_waits(pool, m)
                        for e in range(POOLS):
                            last = nc.gpsimd.tensor_tensor(prod[:, u, e, :, :], left(n)[:, e], right(n)[:, e], ALU.mult)
                        last.then_inc(multiplied, 1)

            @block.vector
            def _(dve):
                with dve.Fori(0, TT // 2) as i:
                    for u in range(2):
                        n = i * 2 + u
                        dve.wait_ge(summed, n + 1)
                        hold_waits(dve, m)
                        for e in range(POOLS, E):
                            last = nc.vector.tensor_tensor(prod[:, u, e, :, :], left(n)[:, e], right(n)[:, e], ALU.mult)
                        last.then_inc(by_dve, 1)
                        dve.wait_ge(by_dve, n + 1)
                        dve.wait_ge(multiplied, n + 1)
                        src = prod[:, u, :, :, :].rearrange(order)
                        out = dst[:, bass.ds(n, 1), :]
                        if len(src.shape) == 4:
                            out = out.rearrange("p o (e d) -> p (o e) d", e=E)
                        else:
                            out = out.rearrange("p o n -> p (o n)")
                        nc.vector.tensor_reduce(out, src, AX.X, ALU.add).then_inc(summed, 1)


def to_features_block(nc, m, a, cols):
    chunks = -(-cols // P)
    ctx, sb, ps, sem = scope(nc, m)
    with ctx:
        tps = [ps(f"tps{i}", [P, chunks, P]) for i in range(2)]
        transposed, evacuated = sem("transposed"), sem("evacuated")
        with engines_block(nc, m) as block:

            @block.tensor
            def _(pe):
                for n in range(TT):
                    if n >= 2:
                        pe.wait_ge(evacuated, 2 * (n - 1))
                    for c in range(chunks):
                        k = min(P, cols - c * P)
                        last = nc.tensor.transpose(tps[n % 2][0:k, c, :], a[:, n, c * P:c * P + k], m.ident[:, :])
                    last.then_inc(transposed, 1)

            @block.scalar
            def _(act):
                for n in range(TT):
                    act.wait_ge(transposed, n + 1)
                    full = cols // P
                    nc.scalar.copy(m.featT[:, 0:full, n * P:(n + 1) * P], tps[n % 2][:, 0:full, :]).then_inc(evacuated, 1)
                    k = cols - full * P
                    nc.scalar.copy(m.featT[0:k, full, n * P:(n + 1) * P], tps[n % 2][0:k, full, :]).then_inc(evacuated, 1)


def mixture_of_depths_layer(nc, m, t, factor):
    CAP = SEQ // 2
    ctx, sb, ps, sem = scope(nc, m)
    with ctx:
        w1, b1 = sb("w1", [P, KD, 1024]), sb("b1", [P, 8])
        wr = sb("wr", [P, KD])
        before = sb("before", [P, SEQ])
        feature_major_block(
            nc, m, [(m.featT, 8, w1, m.xnT, KD, ("gelu", b1))],
            [(w1[:, :, :], t["f_w1"]), (b1[:, :], t["f_b1"]), (wr[:, :], t["f_wr"]), (before[:, :], t["before"]),
             (m.wo[:, :, :], t["f_w2"]), (m.bo[:, :], t["f_b2"])])
        row = sb("score_row", [1, TOK])
        col = sb("score_col", [P, TT])
        above, equal = sb("above", [P, TT, SEQ]), sb("equal", [P, TT, SEQ])
        rank = sb("rank", [P, TT])
        row_ps, all_ps, col_ps = ps("row_ps", [1, TOK]), ps("all_ps", [P, TOK]), ps("col_ps", [P, TT])
        row_done, row_ready, spread_done, col_ready, sig_ready = (
            sem(n) for n in ("row_done", "row_ready", "spread_done", "col_ready", "sig_ready"))
        vec = sem("vec")
        with engines_block(nc, m) as block:

            @block.tensor
            def _(pe):
                for h in range(2):
                    for k in range(KD):
                        last = nc.tensor.matmul(row_ps[0:1, h * HALF:(h + 1) * HALF], wr[:, k:k + 1],
                                                m.xnT[:, k, h * HALF:(h + 1) * HALF], start=(k == 0), stop=(k == KD - 1))
                last.then_inc(row_done, 1)
                pe.wait_ge(row_ready, 1)
                for h in range(2):
                    nc.tensor.matmul(all_ps[:, h * HALF:(h + 1) * HALF], m.ones[0:1, :], row[0:1, h * HALF:(h + 1) * HALF],
                                     start=True, stop=True)
                for n in range(TT):
                    last = nc.tensor.matmul(col_ps[:, n:n + 1], row[0:1, n * P:(n + 1) * P], m.ones[0:1, 0:1],
                                            start=True, stop=True)
                last.then_inc(spread_done, 1)

            @block.scalar
            def _(act):
                act.wait_ge(row_done, 1)
                nc.scalar.copy(row[:, :], row_ps[:, :]).then_inc(row_ready, 1)
                act.wait_ge(col_ready, 1)
                nc.scalar.activation(factor[:, :], col[:, :], ACT.Sigmoid).then_inc(sig_ready, 1)

            @block.vector
            def _(dve):
                chain = Chain(dve, vec)
                dve.wait_ge(spread_done, 1)
                nc.vector.tensor_copy(col[:, :], col_ps[:, :]).then_inc(col_ready, 1)
                dve.wait_ge(col_ready, 1)
                for op, dst in ((ALU.is_gt, above), (ALU.is_equal, equal)):
                    for e in range(2):
                        rows = slice(e * SEQ, (e + 1) * SEQ)
                        chain.step(nc.vector.tensor_tensor(
                            dst[rows, :, :], all_ps[rows, :].rearrange("p (t e n) -> p t e n", e=2, n=SEQ)[:, :, e, :],
                            col[rows, :].unsqueeze(2).to_broadcast([SEQ, TT, SEQ]), op))
                chain.step(nc.vector.tensor_tensor(equal[:, :, :], equal[:, :, :],
                                                   before[:, :].unsqueeze(1).to_broadcast([P, TT, SEQ]), ALU.mult))
                chain.step(nc.vector.tensor_tensor(above[:, :, :], above[:, :, :], equal[:, :, :], ALU.add))
                chain.step(nc.vector.tensor_reduce(rank[:, :], above[:, :, :], AX.X, ALU.add))
                dve.wait_ge(sig_ready, 1)
                nc.vector.scalar_tensor_tensor(factor[:, :], rank[:, :], float(CAP), factor[:, :], ALU.is_lt, ALU.mult)


def routing_block(nc, m, w_gate, loads, groups, n, weights, rev, bias=None, softmax=False, shared=False):
    G = TT * groups
    N = groups * n
    ctx, sb, ps, sem = scope(nc, m)
    with ctx:
        logits, tmp, eq, mask, val = (sb(x, [P, G, n]) for x in ("logits", "tmp", "eq", "mask", "val"))
        mx, sums = sb("mx", [P, G]), sb("sums", [P, G])
        lps = ps("lps", [P, TT, N])
        loaded, projected, logits_ready, shifted, valued = (
            sem(x) for x in ("loaded", "projected", "logits_ready", "shifted", "valued"))
        vec = sem("vec")

        def spread(x):
            return x[:, :].unsqueeze(2).to_broadcast([P, G, n])

        with engines_block(nc, m) as block:

            @block.sync
            def _(sp):
                for buf, dram in loads:
                    sp.dma_start(buf, dram).then_inc(loaded, 16)

            @block.tensor
            def _(pe):
                pe.wait_ge(loaded, 16 * len(loads))
                for i in range(TT):
                    for k in range(KD):
                        last = nc.tensor.matmul(lps[:, i, :], m.xnT[:, k, i * P:(i + 1) * P], w_gate[:, k, :],
                                                start=(k == 0), stop=(k == KD - 1 and bias is None))
                    if bias is not None:
                        last = nc.tensor.matmul(lps[:, i, :], m.ones[0:1, :], bias, start=False, stop=True)
                last.then_inc(projected, 1)

            @block.scalar
            def _(act):
                act.wait_ge(projected, 1)
                nc.scalar.copy(logits[:, :, :].rearrange("p g n -> p (g n)"), flat(lps[:, :, :])).then_inc(logits_ready, 1)
                if softmax:
                    act.wait_ge(shifted, 1)
                    nc.scalar.activation(val[:, :, :], val[:, :, :], ACT.Exp).then_inc(valued, 1)
                else:
                    act.wait_ge(logits_ready, 1)
                    nc.scalar.activation(val[:, :, :], logits[:, :, :], ACT.Sigmoid).then_inc(valued, 1)

            @block.vector
            def _(dve):
                chain = Chain(dve, vec)
                dve.wait_ge(logits_ready, 1)
                if loads:
                    dve.wait_ge(loaded, 16 * len(loads))
                if softmax:
                    chain.step(nc.vector.tensor_reduce(mx[:, :], logits[:, :, :], AX.X, ALU.max))
                    nc.vector.tensor_tensor(val[:, :, :], logits[:, :, :], spread(mx), ALU.subtract).then_inc(shifted, 1)
                    dve.wait_ge(shifted, 1)
                top2_steps(nc, chain, logits[:, :, :], rev, mask[:, :, :], tmp[:, :, :], eq[:, :, :], mx)
                dve.wait_ge(valued, 1)
                out = weights[:, :, 0:N].rearrange("p t (g n) -> p t g n", g=groups)
                if softmax:
                    chain.step(nc.vector.tensor_reduce(sums[:, :], val[:, :, :], AX.X, ALU.add))
                    chain.step(nc.vector.reciprocal(sums[:, :], sums[:, :]))
                    chain.step(nc.vector.tensor_tensor(val[:, :, :], val[:, :, :], spread(sums), ALU.mult))
                    chain.step(nc.vector.scalar_tensor_tensor(val[:, :, :], val[:, :, :], 0.5, mask[:, :, :], ALU.mult, ALU.mult))
                else:
                    chain.step(nc.vector.tensor_tensor(val[:, :, :], val[:, :, :], mask[:, :, :], ALU.mult))
                    chain.step(nc.vector.tensor_reduce(sums[:, :], val[:, :, :], AX.X, ALU.add))
                    chain.step(nc.vector.reciprocal(sums[:, :], sums[:, :]))
                    chain.step(nc.vector.tensor_tensor(val[:, :, :], val[:, :, :], spread(sums), ALU.mult))
                chain.step(nc.vector.tensor_copy(out, val[:, :, :].rearrange("p (t g) n -> p t g n", t=TT)))
                if shared:
                    nc.vector.memset(weights[:, :, N:N + 1], 1.0)


def experts_block(nc, m, n_experts, packed, weights, add_xn):
    F32R = mybir.dt.float32r
    W = 6 * P
    ctx, sb, ps, sem = scope(nc, m)
    with ctx:
        w = sb("w", [P, 2, W])
        wH, wL = sb("wH", [P, 2, W], F32R), sb("wL", [P, 2, W], F32R)
        xH, xL = sb("xH", [P, KD, TOK], F32R), sb("xL", [P, KD, TOK], F32R)
        act_g = sb("silu", [P, 2, HALF])
        hT = sb("hT", [P, 2, HALF])
        hH, hL = sb("hH", [P, 2, HALF], F32R), sb("hL", [P, 2, HALF], F32R)
        g_ps, u_ps = ps("g_ps", [P, 2, HALF]), ps("u_ps", [P, 2, HALF])
        y_ps = [ps(f"y{i}", [P, HALF]) for i in range(4)]
        w_in = [sem(f"w_in{u}") for u in range(2)]
        x_hi, x_lo = sem("x_hi"), sem("x_lo")
        w_hi = sem("w_hi")
        w_lo = sem("w_lo")
        gu_done = sem("gu_done")
        silu_done = sem("silu_done")
        h_ready = sem("h_ready")
        h_hi, h_lo = sem("h_hi"), sem("h_lo")
        y_done = sem("y_done")
        y_added = sem("y_added")
        xn_added = sem("xn_added")

        def three(out, aH, aL, bH, bL, start, stop):
            nc.tensor.matmul(out, aH, bH, start=start, stop=False)
            nc.tensor.matmul(out, aL, bH, start=False, stop=False)
            return nc.tensor.matmul(out, aH, bL, start=False, stop=stop)

        def sync_turn(sp, e, u):
            sp.wait_ge(w_lo, e + 1)
            sp.dma_start(w[:, u, :], packed[bass.ds(e, 1)].rearrange("o p n -> p (o n)")).then_inc(w_in[u], 16)

        def up(pe, e, u, h):
            pe.wait_ge(h_ready, e * 2 + h + 1)
            for dst, col in ((g_ps, 0), (u_ps, 2 * P)):
                for k in range(KD):
                    a, b = slice(col + k * P, col + (k + 1) * P), slice(h * HALF, (h + 1) * HALF)
                    last = three(dst[:, h, :], wH[:, u, a], wL[:, u, a], xH[:, k, b], xL[:, k, b], k == 0, k == KD - 1)
            last.then_inc(gu_done, 1)

        def down(pe, e, u, h):
            pe.wait_ge(h_lo, e * 2 + h + 1)
            for n in range(4 * h, 4 * h + 4):
                pe.wait_ge(y_added, e * TT + n + 1)
                r = slice((n % 4) * P, (n % 4 + 1) * P)
                a, b = hH[:, h, r], hL[:, h, r]
                three(y_ps[n % 4][:, 0:D], a, b, wH[:, u, 4 * P:W], wL[:, u, 4 * P:W], True, True).then_inc(y_done, 1)

        def pe_turn(pe, e, u, first=False):
            pe.wait_ge(w_lo, e + 3)
            up(pe, e, u, 0)
            if not first:
                down(pe, e - 1, 1 - u, 1)
            up(pe, e, u, 1)
            down(pe, e, u, 0)

        def split_weights(act, e, u):
            act.wait_ge(w_in[u], (e + 2 - u) * 8)
            act.wait_ge(y_done, e * TT + 8)
            nc.scalar.copy(wH[:, u, :], w[:, u, :]).then_inc(w_hi, 1)

        def act_turn(act, e, u, last=False):
            for h in range(2):
                act.wait_ge(gu_done, e * 2 + h + 1)
                act.wait_ge(h_ready, e * 2 + h + 1)
                nc.scalar.activation(act_g[:, h, :], g_ps[:, h, :], ACT.Silu).then_inc(silu_done, 1)
                act.wait_ge(h_ready, e * 2 + h + 3)
                act.wait_ge(y_done, e * TT + 4 * h + 12)
                nc.scalar.copy(hH[:, h, :], hT[:, h, :]).then_inc(h_hi, 1)
                if h == 0 and not last:
                    split_weights(act, e + 1, 1 - u)

        def pool_turn(pool, e, u):
            pool.wait_ge(w_hi, e + 1)
            hold_waits(pool, m)
            nc.gpsimd.tensor_tensor(wL[:, u, :], w[:, u, :], wH[:, u, :].bitcast(F32), ALU.subtract).then_inc(w_lo, 1)

        def add_tiles(dve, e, h):
            for n in range(4 * h, 4 * h + 4):
                dve.wait_ge(y_done, e * TT + n + 17)
                dve.wait_ge(y_added, e * TT + n + 1)
                nc.vector.scalar_tensor_tensor(m.x[:, n, :], y_ps[n % 4][:, 0:D],
                                               weights[:, n, bass.ds(e, 1)], m.x[:, n, :],
                                               ALU.mult, ALU.add).then_inc(y_added, 1)

        def dve_turn(dve, e, u, first=False):
            for h in range(2):
                dve.wait_ge(silu_done, e * 2 + h + 1)
                nc.vector.tensor_tensor(hT[:, h, :], act_g[:, h, :], u_ps[:, h, :], ALU.mult).then_inc(h_ready, 1)
                if h == 1 or not first:
                    add_tiles(dve, e if h else e - 1, 1 - h)
                dve.wait_ge(h_hi, e * 2 + h + 1)
                nc.vector.tensor_tensor(hL[:, h, :], hT[:, h, :], hH[:, h, :].bitcast(F32), ALU.subtract).then_inc(h_lo, 1)

        def turns(eng, body, **ends):
            left = (n_experts - 1) % 2 or 2
            body(eng, 0, 0, **{k: v for k, v in ends.items() if k == "first"})
            with eng.Fori(0, (n_experts - 1 - left) // 2) as i:
                for v in (1, 2):
                    body(eng, i * 2 + v, v % 2)
            for e in range(n_experts - left, n_experts):
                body(eng, e, e % 2, **({"last": True} if "last" in ends and e == n_experts - 1 else {}))

        with engines_block(nc, m) as block:

            @block.sync
            def _(sp):
                sp.sem_inc(y_done, 16)
                turns(sp, sync_turn)

            @block.gpsimd
            def _(pool):
                pool.sem_inc(w_lo, 2)
                pool.wait_ge(x_hi, 1)
                nc.gpsimd.tensor_tensor(flat(xL[:, :, :]), flat(m.xnT[:, :, :]), flat(xH[:, :, :]).bitcast(F32),
                                        ALU.subtract).then_inc(x_lo, 1)
                turns(pool, pool_turn)

            @block.tensor
            def _(pe):
                pe.wait_ge(x_lo, 1)
                turns(pe, pe_turn, first=True)
                down(pe, n_experts - 1, (n_experts - 1) % 2, 1)

            @block.scalar
            def _(act):
                nc.scalar.copy(flat(xH[:, :, :]), flat(m.xnT[:, :, :])).then_inc(x_hi, 1)
                split_weights(act, 0, 0)
                turns(act, act_turn, last=True)

            @block.vector
            def _(dve):
                dve.sem_inc(h_ready, 2)
                dve.sem_inc(y_added, 4)
                if add_xn:
                    nc.vector.tensor_tensor(flat(m.x[:, :, :]), flat(m.x[:, :, :]), flat(m.xn[:, :, :]),
                                            ALU.add).then_inc(xn_added, 1)
                    dve.wait_ge(xn_added, 1)
                turns(dve, dve_turn, first=True)
                add_tiles(dve, n_experts - 1, 1)


TWO_PI = 2.0 * np.pi
TWO_PI_HI = 6.28125
TWO_PI_LO = TWO_PI - TWO_PI_HI
ROUND = 1.5 * 2.0 ** 23
N2 = 32


def state_space_kernel_block(nc, m, t, kern):
    ctx, sb, ps, sem = scope(nc, m)
    with ctx:
        S = [P, KD, N2]
        ldt, dt = sb("ldt", [P, KD]), sb("dt", [P, KD])
        are, aim, cre, cim = (sb(x, S) for x in ("are", "aim", "cre", "cim"))
        a, th, em1, ang, turns_, sb1, sb2 = (sb(x, S) for x in ("a", "th", "em1", "ang", "turns", "sin1", "sin2"))
        zr, zi, wr, u, v, w, qr, qi = (sb(x, S) for x in ("zr", "zi", "wr", "u", "v", "w", "qr", "qi"))
        Vr, Vi = sb("Vr", [P, KD, SEQ, N2]), sb("Vi", [P, KD, SEQ, N2])
        temps = [sb(f"temp{k}", [P, KD, SEQ // 2, N2]) for k in range(4)]
        loaded, exp_ready, small_ready, tanh_ready, ang_ready, sin_ready = (
            sem(x) for x in ("loaded", "exp_ready", "small_ready", "tanh_ready", "ang_ready", "sin_ready"))
        vec = sem("vec")
        with engines_block(nc, m) as block:

            @block.sync
            def _(sp):
                for buf, x in ((ldt, "k_ldt"), (are, "k_lar"), (aim, "k_aim"), (cre, "k_cre"), (cim, "k_cim")):
                    dst = buf[:, :] if x == "k_ldt" else buf[:, :, :]
                    sp.dma_start(dst, t[x]).then_inc(loaded, 16)

            @block.scalar
            def _(act):
                act.wait_ge(loaded, 5 * 16)
                nc.scalar.activation(dt[:, :], ldt[:, :], ACT.Exp).then_inc(exp_ready, 1)
                nc.scalar.activation(are[:, :, :], are[:, :, :], ACT.Exp).then_inc(exp_ready, 1)
                act.wait_ge(small_ready, 1)
                nc.scalar.activation(th[:, :, :], a[:, :, :], ACT.Tanh, scale=0.5).then_inc(tanh_ready, 1)
                act.wait_ge(ang_ready, 1)
                nc.scalar.activation(sb1[:, :, :], ang[:, :, :], ACT.Sin).then_inc(sin_ready, 1)
                nc.scalar.activation(sb2[:, :, :], ang[:, :, :], ACT.Sin, scale=0.5).then_inc(sin_ready, 1)

            @block.vector
            def _(dve):
                chain = Chain(dve, vec)

                def tt(out, x, y, op):
                    chain.step(nc.vector.tensor_tensor(out, x, y, op))

                def ts(out, x, s1, s2, op0, op1):
                    chain.step(nc.vector.tensor_scalar(out, x, s1, s2, op0, op1))

                def spread(x):
                    return x[:, :].unsqueeze(2).to_broadcast(S)

                F = (slice(None),) * 3
                dve.wait_ge(exp_ready, 2)
                ts(are[F], are[F], -1.0, None, ALU.mult, ALU.bypass)
                nc.vector.tensor_tensor(a[F], are[F], spread(dt), ALU.mult).then_inc(small_ready, 1)
                tt(ang[F], aim[F], spread(dt), ALU.mult)
                ts(turns_[F], ang[F], 1.0 / TWO_PI, ROUND, ALU.mult, ALU.add)
                ts(turns_[F], turns_[F], -ROUND, None, ALU.add, ALU.bypass)
                chain.step(nc.vector.scalar_tensor_tensor(ang[F], turns_[F], -TWO_PI_HI, ang[F], ALU.mult, ALU.add))
                chain.step(nc.vector.scalar_tensor_tensor(ang[F], turns_[F], -TWO_PI_LO, ang[F], ALU.mult, ALU.add))
                nc.vector.tensor_scalar(ang[F], ang[F], 3.1415925, -3.1415925, ALU.min, ALU.max).then_inc(ang_ready, 1)
                dve.wait_ge(tanh_ready, 1)
                ts(u[F], th[F], -1.0, 1.0, ALU.mult, ALU.add)
                chain.step(nc.vector.reciprocal(u[F], u[F]))
                chain.step(nc.vector.scalar_tensor_tensor(em1[F], th[F], 2.0, u[F], ALU.mult, ALU.mult))
                ts(v[F], em1[F], 1.0, None, ALU.add, ALU.bypass)
                dve.wait_ge(sin_ready, 2)
                tt(zi[F], v[F], sb1[F], ALU.mult)
                tt(w[F], sb2[F], sb2[F], ALU.mult)
                tt(w[F], w[F], v[F], ALU.mult)
                chain.step(nc.vector.scalar_tensor_tensor(wr[F], w[F], -2.0, em1[F], ALU.mult, ALU.add))
                ts(zr[F], wr[F], 1.0, None, ALU.add, ALU.bypass)
                tt(u[F], are[F], are[F], ALU.mult)
                tt(v[F], aim[F], aim[F], ALU.mult)
                tt(u[F], u[F], v[F], ALU.add)
                chain.step(nc.vector.reciprocal(u[F], u[F]))
                tt(v[F], wr[F], are[F], ALU.mult)
                tt(w[F], zi[F], aim[F], ALU.mult)
                tt(v[F], v[F], w[F], ALU.add)
                tt(qr[F], v[F], u[F], ALU.mult)
                tt(v[F], zi[F], are[F], ALU.mult)
                tt(w[F], wr[F], aim[F], ALU.mult)
                tt(v[F], v[F], w[F], ALU.subtract)
                tt(qi[F], v[F], u[F], ALU.mult)

                def together(*steps):
                    for ins in steps:
                        ins.then_inc(vec, 1)
                        chain.n += 1
                    dve.wait_ge(vec, chain.n)

                def product(outr, outi, xr, xi, yr, yi, s):
                    together(*(nc.vector.tensor_tensor(a, b, c, ALU.mult) for a, b, c in
                               ((s[0], xr, yr), (s[1], xi, yi), (s[2], xr, yi), (s[3], xi, yr))))
                    together(nc.vector.tensor_tensor(outr, s[0], s[1], ALU.subtract),
                             nc.vector.tensor_tensor(outi, s[2], s[3], ALU.add))

                spare = (v[F], w[F], th[F], em1[F])
                product(Vr[:, :, 0, :], Vi[:, :, 0, :], cre[F], cim[F], qr[F], qi[F], spare)
                n = 1
                while n < SEQ:
                    yr, yi = (x[:, :, :].unsqueeze(2).to_broadcast([P, KD, n, N2]) for x in (zr, zi))
                    product(Vr[:, :, n:2 * n, :], Vi[:, :, n:2 * n, :], Vr[:, :, 0:n, :], Vi[:, :, 0:n, :], yr, yi,
                            [x[:, :, 0:n, :] for x in temps])
                    n *= 2
                    if n < SEQ:
                        product(u[F], qr[F], zr[F], zi[F], zr[F], zi[F], spare)
                        together(nc.vector.tensor_copy(zr[F], u[F]), nc.vector.tensor_copy(zi[F], qr[F]))
                chain.step(nc.vector.tensor_reduce(kern[:, :, :], Vr[:, :, :, :], AX.X, ALU.add))
                ts(kern[:, :, :], kern[:, :, :], 2.0, None, ALU.mult, ALU.bypass)


TAPS = 8


def causal_convolution_block(nc, m, t, kern):
    ctx, sb, ps, sem = scope(nc, m)
    with ctx:
        xpad = sb("xpad", [P, KD, BATCH, 2 * SEQ])
        y = sb("y", [P, KD, TOK])
        loaded, padded, zeroed, summed, copied = (sem(x) for x in ("loaded", "padded", "zeroed", "summed", "copied"))
        with engines_block(nc, m) as block:

            @block.sync
            def _(sp):
                sp.dma_start(m.wo[:, 0:KD, :], t["k_w"]).then_inc(loaded, 16)
                sp.dma_start(m.bo[:, :], t["k_b"]).then_inc(loaded, 16)
                sp.wait_ge(loaded, 32)

            @block.gpsimd
            def _(pool):
                for c in range(KD):
                    nc.gpsimd.memset(xpad[:, c, :, 0:SEQ], 0.0).then_inc(padded, 1)
                nc.gpsimd.memset(y[:, :, :], 0.0).then_inc(zeroed, 1)

            @block.scalar
            def _(act):
                for c in range(KD):
                    nc.scalar.copy(xpad[:, c, :, SEQ:2 * SEQ], m.xnT[:, c, :].rearrange("p (b n) -> p b n", b=BATCH)).then_inc(copied, 1)
                for c in range(KD):
                    act.wait_ge(summed, KD * SEQ + 2)
                    nc.scalar.activation(m.featT[:, c, :], y[:, c, :], ACT.Gelu)

            @block.vector
            def _(dve):
                dve.sem_inc(summed, 2)
                dve.wait_ge(copied, KD)
                dve.wait_ge(padded, KD)
                dve.wait_ge(zeroed, 1)
                for first in range(0, SEQ, TAPS):
                    reach = SEQ - first
                    with dve.Fori(0, TAPS) as i:
                        s = i + first
                        for c in range(KD):
                            dve.wait_ge(summed, s * KD + c + 1)
                            hold_waits(dve, m)
                            yc = y[:, c, :].rearrange("p (b n) -> p b n", b=BATCH)[:, :, first:SEQ]
                            nc.vector.scalar_tensor_tensor(yc, xpad[:, c, :, bass.ds(SEQ - i, reach)],
                                                           kern[:, c, bass.ds(s, 1)], yc, ALU.mult, ALU.add).then_inc(summed, 1)


MASKED = -30000.0
RMS_EPS = 1e-8


def resampler_layer(nc, m, t):
    H, DH = 4, 64
    HD = H * DH
    with ExitStack() as whole:
        def big(name, shape, dt=F32):
            return whole.enter_context(nc.sbuf_tensor("d_" + name, shape, dt))

        lnT = m.featT
        q_tok, kv_tok = big("q_tok", [P, TT, HD]), big("kv_tok", [P, TT, 2 * HD])
        qT, klT = big("qT", [P, KD, TOK]), big("klT", [P, KD, TOK])
        wq, wlkv = big("wq", [P, KD, HD]), big("wlkv", [P, KD, 2 * HD])
        w1, w2 = big("w1", [P, 2 * HD]), big("w2", [CL, 2 * HD])
        wk = big("wk", [P, H, CA])
        gk, gates = big("gk", [P, 4]), big("gates", [P, 6])
        g_row, b_row = big("g_row", [P, DC]), big("b_row", [P, DC])
        mask_in, mbias = big("mask_in", [P, BATCH, MT], I32), big("mbias", [P, BATCH, MT])
        resampler_prepare_block(nc, m, t, lnT, wq, wlkv, w1, w2, wk, gk, gates, g_row, b_row, mask_in, mbias)
        token_major_block(nc, m, [(q_tok, wq, lnT, KD, None), (kv_tok, wlkv, lnT, KD, None)], [])
        unit_rms_block(nc, m, q_tok, kv_tok, qT, klT, gk, H)
        resampler_attention_block(nc, m, t, H, DH, qT, klT, kv_tok, w1, w2, wk, mbias)


def resampler_prepare_block(nc, m, t, lnT, wq, wlkv, w1, w2, wk, gk, gates, g_row, b_row, mask_in, mbias):
    ctx, sb, ps, sem = scope(nc, m)
    H = 4
    with ctx:
        stats, mv, rstd = sb("stats", [P, TT, 6]), sb("mv", [P, TT, 2]), sb("rstd", [P, TT])
        ln = sb("ln", [P, TT, D])
        tmp = sb("tmp", [P, H, DC])
        bcol = sb("bcol", [P, 2])
        tps = [ps(f"tps{i}", [P, KD, P]) for i in range(2)]
        b_ps = ps("b_ps", [1, HALF])
        loaded, var_ready, std_ready, ln_ready, transposed, evacuated, folded = (
            sem(x) for x in ("loaded", "var_ready", "std_ready", "ln_ready", "transposed", "evacuated", "folded"))
        vec = sem("vec")
        loads = ((wq[:, :, :], "d_wq"), (wlkv[:, :, :], "d_wlkv"), (w1[:, :], "d_w1"), (w2[:, :], "d_w2"),
                 (wk[:, :, :], "d_wk"), (gk[:, :], "d_gk"), (gates[:, :], "d_gates"), (g_row[:, :], "d_g_row"),
                 (b_row[:, :], "d_b_row"), (mask_in[:, :, :], "d_mask"), (bcol[:, :], "d_bcol"),
                 (m.wo[:, 0:KD, :], "d_wo"), (m.bo[:, :], "d_bo"))
        with engines_block(nc, m) as block:

            @block.sync
            def _(sp):
                for buf, name in loads:
                    sp.dma_start(buf, t[name]).then_inc(loaded, 16)

            @block.vector
            def _(dve):
                chain = Chain(dve, vec)
                for n in range(TT):
                    chain.step(nc.vector.bn_stats(stats[:, n, :], m.xn[:, n, :]))
                    last = nc.vector.bn_aggr(mv[:, n, :], stats[:, n, :])
                chain.step(last)
                nc.vector.tensor_scalar(rstd[:, :], mv[:, :, 1], LN_EPS, None, ALU.add).then_inc(var_ready, 1)
                dve.wait_ge(loaded, 16 * len(loads))
                nc.vector.tensor_copy(mbias[:, :, :], mask_in[:, :, :]).then_inc(vec, 1)
                chain.n += 1
                for h in range(H):
                    nc.vector.tensor_tensor(tmp[:, h, :], wk[:, h, 0:DC], b_row[:, :], ALU.mult).then_inc(vec, 1)
                    chain.n += 1
                dve.wait_ge(vec, chain.n)
                nc.vector.tensor_reduce(wk[:, :, DC:CA], tmp[:, :, :], AX.X, ALU.add)
                for h in range(H):
                    nc.vector.tensor_tensor(wk[:, h, 0:DC], wk[:, h, 0:DC], g_row[:, :], ALU.mult)
                nc.vector.tensor_scalar(mbias[:, :, :], mbias[:, :, :], -MASKED, MASKED, ALU.mult, ALU.add)
                dve.wait_ge(folded, 1)
                nc.vector.tensor_scalar(w1[:, :], w1[:, :], gates[:, 4:5], None, ALU.mult)
                nc.vector.tensor_scalar(w2[0:CL - 1, :], w2[0:CL - 1, :], gates[0:CL - 1, 5:6], None, ALU.mult)
                nc.vector.tensor_copy(w2[CL - 1:CL, :], b_ps[:, :])
                nc.vector.scalar_tensor_tensor(gk[:, 2:3], gk[:, 0:1], DHEAD_SCALE, gk[:, 1:2], ALU.mult, ALU.mult)
                dve.wait_ge(std_ready, 1)
                chain.step(nc.vector.reciprocal(rstd[:, :], rstd[:, :]))
                for n in range(TT):
                    nc.vector.tensor_scalar(ln[:, n, :], m.xn[:, n, :], mv[:, n, 0:1], rstd[:, n:n + 1],
                                            ALU.subtract, ALU.mult).then_inc(ln_ready, 1)
                for n in range(TT):
                    dve.wait_ge(transposed, n + 1)
                    for k in range(KD):
                        last = nc.vector.tensor_scalar(lnT[:, k, n * P:(n + 1) * P], tps[n % 2][:, k, :],
                                                       gates[:, k:k + 1], gates[:, 2 + k:3 + k], ALU.mult, ALU.add)
                    last.then_inc(evacuated, 1)

            @block.scalar
            def _(act):
                act.wait_ge(var_ready, 1)
                nc.scalar.activation(rstd[:, :], rstd[:, :], ACT.Sqrt).then_inc(std_ready, 1)

            @block.tensor
            def _(pe):
                pe.wait_ge(loaded, 16 * len(loads))
                nc.tensor.matmul(b_ps[:, :], bcol[:, 0:1], w1[:, :], start=True, stop=False)
                nc.tensor.matmul(b_ps[:, :], bcol[0:CL - 1, 1:2], w2[0:CL - 1, :], start=False, stop=True).then_inc(folded, 1)
                for n in range(TT):
                    pe.wait_ge(ln_ready, n + 1)
                    if n >= 2:
                        pe.wait_ge(evacuated, n - 1)
                    for k in range(KD):
                        last = nc.tensor.transpose(tps[n % 2][:, k, :], ln[:, n, k * P:(k + 1) * P], m.ident[:, :])
                    last.then_inc(transposed, 1)


DHEAD_SCALE = 64 ** -0.5


def unit_rms_block(nc, m, q_tok, kv_tok, qT, klT, gk, H):
    ctx, sb, ps, sem = scope(nc, m)
    with ctx:
        HD = H * 64
        sq = sb("sq", [P, 2, TT, HD])
        ss = sb("ss", [P, 2, TT * H])
        tps = [ps(f"tps{i}", [P, 2, KD, P]) for i in range(2)]
        squared, summed, rooted, ready, transposed, evacuated = (
            sem(x) for x in ("squared", "summed", "rooted", "ready", "transposed", "evacuated"))
        vec = sem("vec")
        srcs = (q_tok[:, :, :], kv_tok[:, :, 0:HD])
        with engines_block(nc, m) as block:

            @block.scalar
            def _(act):
                for j in range(2):
                    nc.scalar.activation(sq[:, j, :, :], srcs[j], ACT.Square).then_inc(squared, 1)
                act.wait_ge(summed, 2)
                nc.scalar.activation(ss[:, :, :], ss[:, :, :], ACT.Sqrt, scale=1.0 / 64).then_inc(rooted, 1)

            @block.vector
            def _(dve):
                chain = Chain(dve, vec)
                for j in range(2):
                    dve.wait_ge(squared, j + 1)
                    nc.vector.tensor_reduce(ss[:, j, :], sq[:, j, :, :].rearrange("p t (h d) -> p (t h) d", h=H),
                                            AX.X, ALU.add).then_inc(summed, 1)
                dve.wait_ge(rooted, 1)
                chain.step(nc.vector.tensor_scalar(ss[:, :, :], ss[:, :, :], RMS_EPS, None, ALU.max))
                chain.step(nc.vector.reciprocal(ss[:, :, :], ss[:, :, :]))
                for j in range(2):
                    r = ss[:, j, :].rearrange("p (t h) -> p t h", h=H)
                    for h in range(H):
                        x = srcs[j][:, :, h * 64:(h + 1) * 64]
                        nc.vector.tensor_tensor(x, x, r[:, :, h:h + 1].to_broadcast([P, TT, 64]), ALU.mult).then_inc(ready, 1)
                for n in range(TT):
                    dve.wait_ge(transposed, n + 1)
                    nc.vector.tensor_scalar(qT[:, :, n * P:(n + 1) * P], tps[n % 2][:, 0, :, :], gk[:, 2:3], None, ALU.mult)
                    nc.vector.tensor_copy(klT[:, :, n * P:(n + 1) * P], tps[n % 2][:, 1, :, :]).then_inc(evacuated, 1)

            @block.tensor
            def _(pe):
                pe.wait_ge(ready, 2 * H)
                for n in range(TT):
                    if n >= 2:
                        pe.wait_ge(evacuated, n - 1)
                    for j in range(2):
                        for k in range(KD):
                            last = nc.tensor.transpose(tps[n % 2][:, j, k, :], srcs[j][:, n, k * P:(k + 1) * P], m.ident[:, :])
                    last.then_inc(transposed, 1)


def resampler_attention_block(nc, m, t, H, DH, qT, klT, kv_tok, w1, w2, wk, mbias):
    ctx, sb, ps, sem = scope(nc, m)
    HD = H * DH
    W = H * SEQ
    hpc = P // DH
    with ctx:
        ctok = sb("ctx_tok", [P, 2, MT, CA])
        stats, mv, rstd = sb("stats", [P, MT, 6]), sb("mv", [P, MT, 2]), sb("rstd", [P, MT])
        xT1, xT2 = sb("xT1", [P, MPAD]), sb("xT2", [CL, MPAD])
        q1, q2 = sb("q1", [P, W]), sb("q2", [CL, W])
        qz = sb("q_by_head", [P, KD, hpc, SEQ])
        kl = sb("kl", [P, KD, SEQ])
        vl = sb("vl", [SEQ, HD])
        mb = sb("mask_now", [P, MT])
        sq = sb("sq", [P, 2, HD])
        rk = sb("rk", [P, MT, H])
        sc = sb("scaled", [P, 2, W])
        e = sb("e", [P, 2, W])
        el = sb("e_latents", [SEQ, W])
        pt1, pt2 = sb("pt1", [P, W]), sb("pt2", [CL, W])
        rsum = sb("rsum", [SEQ, H])
        o = sb("o", [SEQ, HD])
        e64 = sb("sum_col", [CL, 1])
        one = sb("one_col", [SEQ, 1])
        own = sb("own_head", [P, hpc, SEQ])
        ringT = [ps(f"ringT{i}", [P, HALF]) for i in range(2)]
        ringK = [ps(f"ringK{i}", [P, HALF]) for i in range(2)]
        acc1, acc2 = ps("acc1", [P, W]), ps("acc2", [CL, W])
        o_ps, misc = ps("o_ps", [SEQ, HALF]), ps("misc", [P, HALF])
        loaded, zeroed = sem("loaded"), sem("zeroed")
        ctx_in = [sem(f"ctx_in{u}") for u in range(2)]
        norm_var, norm_std = sem("norm_var"), sem("norm_std")
        stats_done, var_done, inverted = sem("stats_done"), sem("var_done"), sem("inverted")
        x_ready = sem("x_ready")
        staged = sem("staged")
        v_staged = sem("v_staged")
        t_full, t_free = sem("t_full"), sem("t_free")
        k_full, k_squared = sem("k_full"), sem("k_squared")
        k_summed = sem("k_summed")
        rms_root = sem("rms_root")
        s_full, s_free = sem("s_full"), sem("s_free")
        e_ready, e_used = sem("e_ready"), sem("e_used")
        lat_full, lat_ready = sem("lat_full"), sem("lat_ready")
        pooled_out = sem("pooled_out")
        o_full, sums_ready = sem("o_full"), sem("sums_ready")
        o_ready = sem("o_ready")
        oT_full, oT_out = sem("oT_full"), sem("oT_out")
        vec = sem("vec")
        NT = MT + 1
        PER = 2
        with engines_block(nc, m) as block:

            def each_batch(eng, body):
                body(0, 0, 0)
                with eng.Fori(0, BATCH // 2 - 1) as i:
                    body(i * 2 + 1, i, 1)
                    body(i * 2 + 2, i + 1, 0)
                body(BATCH - 1, BATCH // 2 - 1, 1)

            def follows_one(b):
                return not isinstance(b, int) or b > 0

            @block.sync
            def _(sp):
                sp.dma_start(e64[:, :], t["e64"]).then_inc(loaded, 16)
                sp.dma_start(own[:, :, :], t["own64"]).then_inc(loaded, 16)

                sp.dma_start(flat(ctok[:, 0, :, :]), t["ctok"][0].rearrange("p t n -> p (t n)")).then_inc(ctx_in[0], 16)

                def body(b, i, u):
                    sp.wait_ge(pooled_out, b * 2 + 4)
                    sp.dma_start(flat(ctok[:, 1 - u, :, :]),
                                 t["ctok"][bass.ds(b + 1, 1)].rearrange("o p t n -> p (o t n)")).then_inc(ctx_in[1 - u], 16)

                each_batch(sp, body)

            @block.gpsimd
            def _(pool):
                pool.sem_inc(s_free, 1)
                nc.gpsimd.memset(one[:, :], 1.0).then_inc(zeroed, 1)
                pool.wait_ge(loaded, 32)

                def body(b, i, u):
                    pool.wait_ge(pooled_out, b * 2 + 4)
                    hold_waits(pool, m)
                    now = bass.ds(b * SEQ, SEQ)
                    for c in range(KD):
                        nc.gpsimd.tensor_tensor(qz[:, c, :, :], qT[:, c, now].unsqueeze(1).to_broadcast([P, hpc, SEQ]),
                                                own[:, :, :], ALU.mult)
                    nc.gpsimd.tensor_copy(mb[:, :], mbias[:, bass.ds(b, 1), :].rearrange("p o t -> p (o t)"))
                    nc.gpsimd.tensor_copy(kl[:, :, :], klT[:, :, now]).then_inc(staged, 1)

                each_batch(pool, body)

            @block.tensor
            def _(pe):
                pe.wait_ge(zeroed, 1)
                pe.wait_ge(loaded, 32)

                def weigh_values(b):
                    pe.wait_ge(pooled_out, b * 2 + 6)
                    pe.wait_ge(lat_ready, b + 1)
                    pe.wait_ge(v_staged, b + 1)
                    pe.wait_ge(o_ready, b + 1)
                    hold_waits(pe, m)
                    for h in range(H):
                        rows = slice(h * SEQ, (h + 1) * SEQ)
                        vcols = slice(HD + h * DH, HD + (h + 1) * DH)
                        dst = o_ps[:, h * DH:(h + 1) * DH]
                        nc.tensor.matmul(dst, pt1[:, rows], w1[:, vcols], start=True, stop=False)
                        nc.tensor.matmul(dst, pt2[:, rows], w2[:, vcols], start=False, stop=False)
                        nc.tensor.matmul(dst, el[:, rows], vl[:, h * DH:(h + 1) * DH], start=False, stop=True)
                        dst = o_ps[:, HD + h:HD + h + 1]
                        nc.tensor.matmul(dst, pt2[:, rows], e64[:, :], start=True, stop=False)
                        last = nc.tensor.matmul(dst, el[:, rows], one[:, :], start=False, stop=True)
                    last.then_inc(o_full, 1)

                def transpose_outputs(b):
                    pe.wait_ge(o_ready, b + 2)
                    hold_waits(pe, m)
                    for c in range(KD):
                        last = nc.tensor.transpose(misc[:, W + c * SEQ:W + (c + 1) * SEQ], o[:, c * P:(c + 1) * P],
                                                   m.ident[0:SEQ, 0:SEQ])
                    last.then_inc(oT_full, 1)

                def body(b, i, u):
                    pe.wait_ge(t_free, b * NT + 1)
                    for h in range(H):
                        src = qT[:, h // hpc, bass.ds(b * SEQ, SEQ)]
                        nc.tensor.matmul(ringT[0][:, h * SEQ:(h + 1) * SEQ], wk[:, h, 0:P], src, start=True, stop=True)
                        last = nc.tensor.matmul(ringT[0][0:CL, W + h * SEQ:W + (h + 1) * SEQ], wk[:, h, P:CA], src,
                                                start=True, stop=True)
                    last.then_inc(t_full, 1)
                    pe.wait_ge(staged, b + 1)
                    pe.wait_ge(oT_out, b + 1)
                    if follows_one(b):
                        pe.wait_ge(lat_ready, b)
                    hold_waits(pe, m)
                    for c in range(KD):
                        last = nc.tensor.matmul(misc[0:SEQ, c * P:(c + 1) * P], kl[:, c, :], flat(qz[:, c, :, :]),
                                                start=True, stop=True)
                    last.then_inc(lat_full, 1)

                    def turn(n):
                        pe.wait_ge(x_ready, b * MT + n + 1)
                        pe.wait_ge(t_free, b * NT + n + 2)
                        bank = ringT[(n + 1) % 2]
                        nc.tensor.transpose(bank[:, 0:P], ctok[:, u, n, 0:P], m.ident[:, :])
                        nc.tensor.transpose(bank[0:CL, P:2 * P], ctok[:, u, n, P:CA], m.ident[:, :]).then_inc(t_full, 1)

                    def keys(n):
                        pe.wait_ge(t_free, b * NT + n + 4)
                        if n < 2:
                            pe.wait_ge(s_free, b * MT + 1)
                        else:
                            pe.wait_ge(k_squared, b * MT + n - 1)
                        cols = slice(n * P, (n + 1) * P)
                        nc.tensor.matmul(ringK[n % 2][:, 0:HD], xT1[:, cols], w1[:, 0:HD], start=True, stop=False)
                        nc.tensor.matmul(ringK[n % 2][:, 0:HD], xT2[:, cols], w2[:, 0:HD],
                                         start=False, stop=True).then_inc(k_full, 1)

                    turn(0)
                    for n in range(1, MT):
                        turn(n)
                        keys(n - 1)
                        if n == 3 and follows_one(b):
                            weigh_values(b - 1)
                        if n == 6 and follows_one(b):
                            transpose_outputs(b - 1)
                    keys(MT - 1)

                    def scores(n):
                        if n < 2:
                            pe.wait_ge(k_squared, b * MT + MT - 1 + n)
                        else:
                            pe.wait_ge(s_free, b * MT + n)
                        bank = ringK[(MT + n) % 2]
                        cols = slice(n * P, (n + 1) * P)
                        nc.tensor.matmul(bank[:, 0:W], xT1[:, cols], q1[:, :], start=True, stop=False)
                        nc.tensor.matmul(bank[:, 0:W], xT2[:, cols], q2[:, :], start=False, stop=True).then_inc(s_full, 1)

                    def pool_tile(n):
                        pe.wait_ge(e_ready, b * MT + n + 1)
                        if n == 0:
                            pe.wait_ge(pooled_out, b * 2 + 4)
                        nc.tensor.matmul(acc1[:, :], ctok[:, u, n, 0:P], e[:, n % 2, :], start=(n == 0), stop=(n == MT - 1))
                        nc.tensor.matmul(acc2[:, :], ctok[:, u, n, P:CA], e[:, n % 2, :], start=(n == 0),
                                         stop=(n == MT - 1)).then_inc(e_used, 1)

                    scores(0)
                    scores(1)
                    for n in range(MT):
                        pool_tile(n)
                        if n + 2 < MT:
                            scores(n + 2)

                each_batch(pe, body)
                weigh_values(BATCH - 1)
                transpose_outputs(BATCH - 1)

            @block.scalar
            def _(act):
                act.sem_inc(t_free, 2)
                act.sem_inc(oT_out, 2)
                act.sem_inc(e_used, 2)
                act.sem_inc(pooled_out, 4)

                def copy_outputs(b):
                    act.wait_ge(oT_full, b + 1)
                    nc.scalar.copy(m.featT[:, 0:KD, bass.ds(b * SEQ, SEQ)],
                                   misc[:, W:W + KD * SEQ].rearrange("p (c n) -> p c n", c=KD)).then_inc(oT_out, 1)

                def root_var(b):
                    act.wait_ge(norm_var, b + 1)
                    nc.scalar.activation(rstd[:, :], rstd[:, :], ACT.Sqrt).then_inc(norm_std, 1)

                root_var(0)

                def body(b, i, u):
                    act.wait_ge(t_full, b * NT + 1)
                    nc.scalar.copy(q1[:, :], ringT[0][:, 0:W])
                    nc.scalar.copy(q2[:, :], ringT[0][0:CL, W:2 * W]).then_inc(t_free, 1)

                    def square(n):
                        act.wait_ge(k_full, b * MT + n + 1)
                        act.wait_ge(k_summed, b * MT + n + 1)
                        nc.scalar.activation(sq[:, n % 2, :], ringK[n % 2][:, 0:HD], ACT.Square).then_inc(k_squared, 1)

                    for n in range(MT):
                        act.wait_ge(t_full, b * NT + n + 2)
                        bank = ringT[(n + 1) % 2]
                        nc.scalar.copy(xT1[:, n * P:(n + 1) * P], bank[:, 0:P])
                        nc.scalar.copy(xT2[:, n * P:(n + 1) * P], bank[0:CL, P:2 * P]).then_inc(t_free, 1)
                        if n:
                            square(n - 1)
                        if n == 5:
                            if follows_one(b):
                                act.wait_ge(o_full, b)
                                hold_waits(act, m)
                            nc.scalar.copy(vl[:, :], kv_tok[u * SEQ:(u + 1) * SEQ, bass.ds(i, 1), HD:2 * HD]
                                           .rearrange("p o n -> p (o n)")).then_inc(v_staged, 1)
                        if n == 8 and follows_one(b):
                            copy_outputs(b - 1)
                    square(MT - 1)
                    root_var(b + 1)
                    act.wait_ge(k_summed, b * MT + MT + 2)
                    nc.scalar.activation(flat(rk[:, :, :]), flat(rk[:, :, :]), ACT.Sqrt, scale=1.0 / DH).then_inc(rms_root, 1)
                    act.wait_ge(lat_full, b + 1)
                    nc.scalar.activation(el[:, :], misc[0:SEQ, 0:W], ACT.Exp).then_inc(lat_ready, 1)
                    for n in range(MT):
                        act.wait_ge(s_free, b * MT + n + 2)
                        act.wait_ge(e_used, b * MT + (n + 1))
                        nc.scalar.activation(e[:, n % 2, :], sc[:, n % 2, :], ACT.Exp,
                                             bias=mb[:, n:n + 1]).then_inc(e_ready, 1)
                    act.wait_ge(e_used, b * MT + MT + 2)
                    nc.scalar.copy(pt1[:, :], acc1[:, :]).then_inc(pooled_out, 1)

                each_batch(act, body)
                copy_outputs(BATCH - 1)

            @block.vector
            def _(dve):
                dve.sem_inc(k_summed, 2)
                dve.sem_inc(o_ready, 1)

                def take_stats(u, tiles):
                    for n in tiles:
                        nc.vector.bn_stats(stats[:, n, :], ctok[:, u, n, 0:DC]).then_inc(stats_done, 1)

                def variances(b):
                    dve.wait_ge(stats_done, b * MT + MT)
                    hold_waits(dve, m)
                    for n in range(MT):
                        nc.vector.bn_aggr(mv[:, n, :], stats[:, n, :]).then_inc(var_done, 1)
                    dve.wait_ge(var_done, b * MT + MT)
                    nc.vector.tensor_scalar(rstd[:, :], mv[:, :, 1], LN_EPS, None, ALU.add).then_inc(norm_var, 1)

                def invert(b):
                    dve.wait_ge(norm_std, b + 1)
                    nc.vector.reciprocal(rstd[:, :], rstd[:, :]).then_inc(inverted, 1)
                    dve.wait_ge(inverted, b + 1)

                def normalize(u, n):
                    nc.vector.tensor_scalar(ctok[:, u, n, 0:DC], ctok[:, u, n, 0:DC], mv[:, n, 0:1],
                                            rstd[:, n:n + 1], ALU.subtract, ALU.mult).then_inc(x_ready, 1)

                def scale_outputs(b):
                    dve.wait_ge(o_full, b + 1)
                    nc.vector.reciprocal(rsum[:, :], o_ps[:, HD:HD + H]).then_inc(sums_ready, 1)
                    dve.wait_ge(sums_ready, b + 1)
                    nc.vector.tensor_tensor(o[:, :].rearrange("p (h d) -> p h d", h=H),
                                            o_ps[:, 0:HD].rearrange("p (h d) -> p h d", h=H),
                                            rsum[:, :].unsqueeze(2).to_broadcast([SEQ, H, DH]), ALU.mult).then_inc(o_ready, 1)

                dve.wait_ge(ctx_in[0], 16)
                take_stats(0, range(MT))
                variances(0)
                invert(0)
                for n in range(MT):
                    normalize(0, n)

                def body(b, i, u):
                    chain = Chain(dve, vec, b * PER, PER)
                    for n in range(MT):
                        dve.wait_ge(k_squared, b * MT + n + 1)
                        nc.vector.tensor_reduce(rk[:, n, :], sq[:, n % 2, :].rearrange("p (h d) -> p h d", h=H),
                                                AX.X, ALU.add).then_inc(k_summed, 1)
                        if n == 3 and follows_one(b):
                            scale_outputs(b - 1)
                        if n == 4:
                            dve.wait_ge(ctx_in[1 - u], (b + 2 + u) * 8)
                        if 4 <= n <= 9:
                            take_stats(1 - u, range((n - 4) * 2, (n - 3) * 2) if n < 9 else range(10, MT))
                        if n == 11:
                            variances(b + 1)
                    dve.wait_ge(rms_root, b + 1)
                    chain.step(nc.vector.tensor_scalar(flat(rk[:, :, :]), flat(rk[:, :, :]), RMS_EPS, None, ALU.max))
                    chain.step(nc.vector.reciprocal(flat(rk[:, :, :]), flat(rk[:, :, :])))
                    chain.close()
                    invert(b + 1)
                    for n in range(MT):
                        dve.wait_ge(s_full, b * MT + n + 1)
                        if n >= 2:
                            dve.wait_ge(e_ready, b * MT + n - 1)
                        nc.vector.tensor_tensor(sc[:, n % 2, :].rearrange("p (h n) -> p h n", h=H),
                                                ringK[(MT + n) % 2][:, 0:W].rearrange("p (h n) -> p h n", h=H),
                                                rk[:, n, :].unsqueeze(2).to_broadcast([P, H, SEQ]), ALU.mult).then_inc(s_free, 1)
                        normalize(1 - u, n)
                    dve.wait_ge(e_used, b * MT + MT + 2)
                    nc.vector.tensor_copy(pt2[:, :], acc2[:, :]).then_inc(pooled_out, 1)

                each_batch(dve, body)
                scale_outputs(BATCH - 1)


def build(nc, t, out):
    with ExitStack() as ctx:
        m = alloc_memory(nc, ctx)
        load_x_block(nc, m, t["x"], t["ident"])
        project_and_norm_block(nc, m, 0)
        for layer in range(FIRST_LAYER, LAST_LAYER + 1):
            last = layer == LAST_LAYER
            if layer == 0:
                cross_attention_blocks(nc, m, 16, 64, dict(wq=t["a_wq"], wk=t["a_wk"], wv1=t["a_wv1"], wv2=t["a_wv2"],
                                       wo=t["a_wo"], bo=t["a_bo"], own=t["own64"]), t)
                project_and_norm_block(nc, m, 8, bias=True, norm=not last)
            elif layer == 1:
                latent_attention_layer(nc, m, t)
                project_and_norm_block(nc, m, 2, norm=not last)
            elif layer == 4:
                biased_attention_layer(nc, m, t)
                project_and_norm_block(nc, m, 2, bias=True, norm=not last)
            elif layer == 7:
                linear_attention_layer(nc, m, t)
                project_and_norm_block(nc, m, 2, norm=not last)
            elif layer in (6, 9):
                k = "g" if layer == 6 else "j"
                narrow_cross_attention_blocks(nc, m, {x: t[f"{k}_{x}"] for x in ("wq", "bq", "w", "biases", "wo", "bo")}, t)
                project_and_norm_block(nc, m, 2, bias=True, norm=not last)
            elif layer == 2:
                switch_head_layer(nc, m, t)
                project_and_norm_block(nc, m, 3, last_rows=64, norm=not last)
            elif layer == 3:
                resampler_layer(nc, m, t)
                project_and_norm_block(nc, m, 2, bias=True, norm=not last)
            elif layer == 5:
                with nc.sbuf_tensor("mod_factor", [P, TT], F32) as factor:
                    mixture_of_depths_layer(nc, m, t, factor)
                    project_and_norm_block(nc, m, 8, bias=True, gated=factor, norm=not last)
            elif layer in (8, 11):
                groups, n, k = (1, 16, "i") if layer == 8 else (2, 32, "l")
                N = groups * n
                total = N + (layer == 8)
                with ExitStack() as own:
                    w_gate, rev, weights = (own.enter_context(nc.sbuf_tensor(f"{k}_{x}", shape, F32)) for x, shape in
                                            (("gate", [P, KD, N]), ("rev", [P, n]), ("weights", [P, TT, total])))
                    b_gate = own.enter_context(nc.sbuf_tensor(f"{k}_bgate", [1, N], F32))
                    loads = [(w_gate[:, :, :], t[k + "_gate"]), (rev[:, :], t[f"rev{n}"])]
                    if layer == 8:
                        loads.append((b_gate[:, :], t["i_bgate"]))
                    routing_block(nc, m, w_gate, loads, groups, n, weights, rev,
                                  bias=b_gate[0:1, :] if layer == 8 else None, softmax=layer == 11, shared=layer == 8)
                    experts_block(nc, m, total, t[k + "_experts"], weights, add_xn=layer == 8)
                if not last:
                    project_and_norm_block(nc, m, 0)
            elif layer == 10:
                with nc.sbuf_tensor("s4d_kernel", [P, KD, SEQ], F32) as kern:
                    state_space_kernel_block(nc, m, t, kern)
                    causal_convolution_block(nc, m, t, kern)
                project_and_norm_block(nc, m, 2, bias=True, norm=not last)
        store_x_block(nc, m, out)


def rows_to_partitions(w):
    w = np.asarray(w)
    return np.ascontiguousarray(w.reshape(w.shape[0] // P, P, w.shape[1]).transpose(1, 0, 2))


def column(b):
    return np.ascontiguousarray(np.asarray(b).reshape(-1, P).T)


def per_head_keys(wk, bk, heads, dh):
    w = np.zeros((CA, heads * dh), np.float32)
    w[:DC] = wk
    if bk is not None:
        w[DC] = bk
    out = np.zeros((P, heads, CA), np.float32)
    for h in range(heads):
        r = (h * dh) % P
        out[r:r + dh, h, :] = w[:, h * dh:(h + 1) * dh].T
    return out


def with_row(w, b):
    out = np.zeros((w.shape[0] + 1, w.shape[1]), np.float32)
    out[:-1] = w
    if b is not None:
        out[-1] = b
    return out


def lay_out(a):
    t = {}
    t["x"] = np.ascontiguousarray(a["x"].reshape(TT, P, D).transpose(1, 0, 2))
    t["ident"] = np.eye(P, dtype=np.float32)
    aug = np.zeros((BATCH, MPAD, CA), np.float32)
    aug[:, :KEYS, :DC] = a["ctx_768"]
    aug[:, :KEYS, DC] = 1.0
    ctxT = aug.transpose(0, 2, 1)[:, :DC]
    more = np.concatenate([ctxT, np.zeros_like(ctxT[:1])])[:, :, :KEYS]
    t["ctxT1"], t["ctxT2"] = np.ascontiguousarray(more[:, :P]), np.ascontiguousarray(more[:, P:])
    low = np.concatenate([ctxT[:, P:]] * 2, 1)
    tiles = [x.reshape(BATCH, P, MT, P).transpose(0, 2, 1, 3) for x in (ctxT[:, :P], low)]
    rows = aug[:, :, :DC].reshape(BATCH, MT, P, DC)
    t["ctx_tiles"] = np.concatenate([*tiles, rows], 3).reshape(BATCH * MT, P, 2 * P + DC)
    by_key = aug.reshape(BATCH, MT, P, CA).transpose(0, 2, 1, 3)
    t["ctok"] = np.concatenate([by_key, np.zeros_like(by_key[:1])])
    e64 = np.zeros((CL, 1), np.float32)
    e64[-1] = 1.0
    t["e64"] = e64

    t["a_wq"] = rows_to_partitions(a["L0_xattn_Wq"])
    wk = a["L0_xattn_Wk"].T
    t["a_wk"] = rows_to_partitions(np.concatenate([wk, wk[:, P:]], 1))
    wv = a["L0_xattn_Wv"]
    t["a_wv1"], t["a_wv2"] = wv[:P], np.concatenate([wv[P:]] * 2)
    t["a_wo"] = rows_to_partitions(a["L0_xattn_Wo"])
    t["a_bo"] = a["L0_xattn_bo"][None, :]

    swap = np.arange(D) ^ 1
    t["b_wq"], t["b_wqs"] = rows_to_partitions(a["L0_attn_wq"]), rows_to_partitions(a["L0_attn_wq"][:, swap])
    t["b_wd"] = rows_to_partitions(a["L0_attn_w_down"])
    t["b_wk"], t["b_wks"] = rows_to_partitions(a["L0_attn_wk_up"]), rows_to_partitions(a["L0_attn_wk_up"][:, swap])
    t["b_wv"] = rows_to_partitions(a["L0_attn_wv_up"])
    t["b_wo"] = rows_to_partitions(a["L0_attn_wo"])
    inv = 1.0 / 10000.0 ** (np.arange(0, 16, 2, dtype=np.float32) / 16)
    ang = np.outer(np.arange(SEQ, dtype=np.float32), inv)
    pair = (np.arange(P) % 16) // 2
    t["rope_cos"] = np.ascontiguousarray(np.cos(ang).astype(np.float32).T[pair])
    sign = np.where(np.arange(P) % 2 == 0, -1.0, 1.0).astype(np.float32)
    t["rope_sin"] = np.ascontiguousarray(np.sin(ang).astype(np.float32).T[pair] * sign[:, None])
    for dh in (16, 64):
        own = np.arange(P)[:, None] // dh == np.arange(P // dh)[None, :]
        t[f"own{dh}"] = np.ascontiguousarray(np.repeat(own[:, :, None], SEQ, 2).astype(np.float32))
    pos = np.arange(P) % SEQ
    t["causal"] = (np.arange(SEQ)[None, :] <= pos[:, None]).astype(np.float32)
    t["before"] = (np.arange(SEQ)[None, :] < pos[:, None]).astype(np.float32)

    order = np.arange(3 * D).reshape(16, 3, 16).transpose(1, 0, 2).reshape(3, D)
    for n, k in enumerate("qkv"):
        t[f"e_w{k}"] = rows_to_partitions(a["L1_attn_Wqkv"][:, order[n]])
    t["e_bq"], t["e_bk"] = column(a["L1_attn_bqkv"][order[0]]), column(a["L1_attn_bqkv"][order[1]])
    t["e_bv"] = a["L1_attn_bqkv"][order[2]][None, :]
    t["e_wo"], t["e_bo"] = rows_to_partitions(a["L1_attn_Wout"]), a["L1_attn_bout"][None, :]

    for k, n, names in (("g", "L2_xattn_", ("Wq", "bq", "Wk", "bk", "Wv", "bv", "Wo", "bo")),
                        ("j", "L3_xattn_", ("w_q", "b_q", "w_k", "b_k", "w_v", "b_v", "w_o", "b_o"))):
        wq, bq, wk, bk, wv, bv, wo, bo = (a[n + x] for x in names)
        t[k + "_wq"], t[k + "_bq"] = rows_to_partitions(wq), column(bq)
        w = np.concatenate([wk, wv], 1)
        t[k + "_w"] = np.stack([w[:P], np.concatenate([w[P:]] * 2)], 1)
        t[k + "_biases"] = np.stack([column(bk), column(bv)], 1)
        t[k + "_wo"], t[k + "_bo"] = rows_to_partitions(wo), bo[None, :]

    for k in ("q", "k", "v", "o"):
        t["h_w" + k] = rows_to_partitions(a["L2_attn_W_" + k].T)

    t["c_wq"], t["c_wk"] = rows_to_partitions(a["L0_ffn_Wq"]), rows_to_partitions(a["L0_ffn_Wk"])
    wx = a["L0_ffn_Wv"].transpose(1, 0, 2).reshape(D, -1)
    t["c_wx"] = rows_to_partitions(np.concatenate([wx, a["L0_ffn_Ws"], a["L0_ffn_Wd"]], 1))
    wo = np.zeros((3 * P, D), np.float32)
    wo[:5 * 64] = a["L0_ffn_Wo"].reshape(5 * 64, D)
    t["c_wo"] = rows_to_partitions(wo)
    for n in (5, 16, 32):
        t[f"rev{n}"] = np.tile(np.arange(n, 0, -1, dtype=np.float32), (P, 1))

    t["d_wq"], t["d_wlkv"] = rows_to_partitions(a["L1_xattn_Wq"].T), rows_to_partitions(a["L1_xattn_Wlkv"].T)
    w = with_row(a["L1_xattn_Wkv"].T, None)
    t["d_w1"], t["d_w2"] = w[:P], w[P:]
    t["d_wk"] = per_head_keys(a["L1_xattn_Wkv"][:D].T, None, 4, 64)
    gk = np.zeros((P, 4), np.float32)
    gk[:, 0], gk[:, 1] = np.tile(a["L1_xattn_qn_g"], 2), np.tile(a["L1_xattn_kn_g"], 2)
    t["d_gk"] = gk
    two = np.zeros((4, P), np.float32)
    for n, x in enumerate(("g", "b")):
        v = a[f"L1_xattn_ln_x_{x}"]
        two[2 * n], two[2 * n + 1, :DC - P] = v[:P], v[P:]
        t[f"d_{x}_row"] = np.tile(v, (P, 1))
    t["d_gates"] = np.concatenate([column(a["L1_xattn_ln_l_g"]), column(a["L1_xattn_ln_l_b"]), two[:2].T], 1)
    t["d_bcol"] = two[2:].T
    mask = np.zeros((BATCH, MPAD, 4), np.uint8)
    mask[:, :KEYS, 0] = a["mask_BxS2_bk0"].view(np.uint8)
    t["d_mask"] = mask.view(np.int32).reshape(BATCH, MT, P).transpose(2, 0, 1)
    t["d_wo"], t["d_bo"] = rows_to_partitions(a["L1_xattn_Wo"].T), a["L1_xattn_bo"][None, :]

    t["f_w1"], t["f_b1"] = rows_to_partitions(a["L1_ffn_W1"]), column(a["L1_ffn_b1"])
    t["f_wr"] = column(a["L1_ffn_w_router"])
    t["f_w2"], t["f_b2"] = rows_to_partitions(a["L1_ffn_W2"]), a["L1_ffn_b2"][None, :]

    def pack(wg, wu, wd):
        up = [w.reshape(-1, KD, P, P).transpose(0, 2, 1, 3).reshape(-1, P, KD * P) for w in (wg, wu)]
        return np.concatenate([*up, wd], 2)

    t["i_gate"], t["i_bgate"] = rows_to_partitions(a["L2_ffn_gate_w"]), a["L2_ffn_gate_b"][None, :]
    t["i_experts"] = np.concatenate([
        pack(*(a["L2_ffn_experts_" + w] for w in ("wg", "wu", "wd"))),
        pack(*(a["L2_ffn_shared_" + w][None] for w in ("wg", "wu", "wd")))])
    t["l_gate"] = rows_to_partitions(np.concatenate([a["L3_ffn_router_w0"], a["L3_ffn_router_w1"]], 1))
    t["l_experts"] = np.concatenate([pack(*(a[f"L3_ffn_{w}{g}"] for w in ("wg", "wu", "wd"))) for g in range(2)])

    t["k_ldt"] = column(a["L3_attn_log_dt"])
    for k, x in (("lar", "log_A_real"), ("aim", "A_imag"), ("cre", "C_real"), ("cim", "C_imag")):
        t["k_" + k] = rows_to_partitions(a["L3_attn_" + x])
    t["k_w"], t["k_b"] = rows_to_partitions(a["L3_attn_W"].T), a["L3_attn_b"][None, :]
    return t


def kernel(**inputs):
    import concourse.bacc as bacc
    from concourse.bass_utils import run_bass_kernel_spmd

    nc = bacc.Bacc("TRN2", target_bir_lowering=False, num_devices=1)
    arrays, t = {}, {}
    for name, a in lay_out({k: np.asarray(v) for k, v in inputs.items()}).items():
        a = np.ascontiguousarray(a)
        arrays[f"in_{name}_dram"] = a
        t[name] = nc.dram_tensor(f"in_{name}_dram", a.shape, mybir.dt.from_np(a.dtype), kind="ExternalInput").ap()
    out = nc.dram_tensor("out_0_dram", (P, TT, D), F32, kind="ExternalOutput").ap()
    build(nc, t, out)
    r = run_bass_kernel_spmd(nc, [arrays], core_ids=[0])
    got = r.results[0]["out_0_dram"]
    return np.ascontiguousarray(got.transpose(1, 0, 2)).reshape(BATCH, SEQ, D)
```
